# Optimizing a Trainium2 kernel written in Bass

```python
import numpy as np
import jax
import jax.numpy as jnp

def _softmax(x, axis=-1):
    return jax.nn.softmax(x, axis=axis)

def _gelu(x):
    return jax.nn.gelu(x, approximate=True)

def _silu(x):
    return jax.nn.silu(x)

def _sigmoid(x):
    return jax.nn.sigmoid(x)

def _layernorm(x, axis=-1, eps=1e-05):
    m = jnp.mean(x, axis=axis, keepdims=True)
    v = jnp.var(x, axis=axis, keepdims=True)
    return (x - m) / jnp.sqrt(v + eps)

def _scatter_add(tgt, idx, src, axis=0):
    return tgt.at[idx].add(src)

def _segment_sum(src, seg, n):
    return jax.ops.segment_sum(src, seg, n)
kernel_name = 'mk_perceiver_d4_seqx_r8_132036'

def setup_inputs(seed: int=0):
    np.random.seed(seed)
    _w = jnp.asarray

    def _rec_inputs():
        import jax
        import jax.numpy as jnp
        _rk = jax.random.key(seed)
        x = -0.000125 + 0.9999 * jax.random.normal(jax.random.fold_in(_rk, 1), (128, 32, 128), jnp.float32)
        _lenS = 32 - jax.random.randint(jax.random.fold_in(_rk, 7), (128,), 0, max(1, 32 // 4) + 1, jnp.int32)
        _lenS2 = 257 - jax.random.randint(jax.random.fold_in(_rk, 8), (128,), 0, max(1, 257 // 4) + 1, jnp.int32)
        _ctx_1024P = jax.random.normal(jax.random.fold_in(_rk, 11), (128, 16, 128), jnp.float32)
        _ctx_1024c = jax.random.dirichlet(jax.random.fold_in(_rk, 511), 0.3 * jnp.ones((16,), jnp.float32), (128, 257))
        _ctx_1024t = jnp.einsum('bsk,bkd->bsd', _ctx_1024c, _ctx_1024P)
        _ctx_1024t = _ctx_1024t * jax.lax.rsqrt(jnp.mean(jnp.square(_ctx_1024t)) + 1e-12) * 0.953939
        ctx_1024 = -0.000514642 + 1.00011 * (_ctx_1024t + 0.3 * jax.random.normal(jax.random.fold_in(_rk, 611), (128, 257, 128), jnp.float32))
        _validS = jnp.arange(32)[None, :] < _lenS[:, None]
        _validS2 = jnp.arange(257)[None, :] < _lenS2[:, None]
        _causal = jnp.tril(jnp.ones((32, 32), dtype=bool))
        mask_BxS2_bf1 = jnp.ones((128, 257), dtype=bool)
        return (x, ctx_1024, mask_BxS2_bf1)
    x, ctx_1024, mask_BxS2_bf1 = _rec_inputs()

    def _L0_xattn_setup():
        import jax, jax.numpy as jnp
        import numpy as np
        EPS = 1e-06
        NUM_HEADS = 16
        DIM_HEADS = 64

        def _ln(x, scale, bias):
            mu = jnp.mean(x, axis=-1, keepdims=True)
            var = jnp.mean(jnp.square(x - mu), axis=-1, keepdims=True)
            return (x - mu) * jax.lax.rsqrt(var + EPS) * scale + bias
        key = jax.random.key(seed)
        ks = jax.random.split(key, 8)
        b, n, m, dim, ctx_dim = (8, 512, 32, 128, 128)
        inner = NUM_HEADS * DIM_HEADS
        x = jax.random.normal(ks[0], (b, n, dim), dtype=jnp.float32)
        context = jax.random.normal(ks[1], (b, m, ctx_dim), dtype=jnp.float32)
        mask = jnp.ones((b, m), dtype=bool)
        Wq = jax.random.normal(ks[2], (dim, inner), dtype=jnp.float32) / np.sqrt(dim)
        Wkv = jax.random.normal(ks[3], (ctx_dim, 2 * inner), dtype=jnp.float32) / np.sqrt(ctx_dim)
        null_kv = jax.random.normal(ks[4], (2, DIM_HEADS), dtype=jnp.float32)
        Wo = jax.random.normal(ks[5], (inner, dim), dtype=jnp.float32) / np.sqrt(inner)
        return {'x': x, 'context': context, 'mask': mask, 'ln1_s': jnp.ones((dim,), jnp.float32), 'ln1_b': jnp.zeros((dim,), jnp.float32), 'lnc_s': jnp.ones((ctx_dim,), jnp.float32), 'lnc_b': jnp.zeros((ctx_dim,), jnp.float32), 'Wq': Wq, 'Wkv': Wkv, 'null_kv': null_kv, 'Wo': Wo, 'lno_s': jnp.ones((dim,), jnp.float32), 'lno_b': jnp.zeros((dim,), jnp.float32)}
    _L0_xattn_all = _L0_xattn_setup()
    _L0_xattn_in = {k: v for k, v in _L0_xattn_all.items() if k in ('ln1_s', 'ln1_b', 'lnc_s', 'lnc_b', 'Wq', 'Wkv', 'null_kv', 'Wo', 'lno_s', 'lno_b')}
    del _L0_xattn_all

    def _L0_attn_setup():
        import jax, jax.numpy as jnp
        import numpy as np
        B, T, C = (2, 256, 128)
        H, M = (16, 64)
        D = C // H
        key = jax.random.key(seed)
        ks = jax.random.split(key, 6)
        x = jax.random.normal(ks[0], (B, T, C), dtype=jnp.float32)
        Wqkv = jax.random.normal(ks[1], (3 * C, C), dtype=jnp.float32) / np.sqrt(C)
        bqkv = jax.random.normal(ks[2], (3 * C,), dtype=jnp.float32) * 0.02
        Wout = jax.random.normal(ks[3], (C, C), dtype=jnp.float32) / np.sqrt(C)
        bout = jax.random.normal(ks[4], (C,), dtype=jnp.float32) * 0.02
        proj = jax.random.normal(ks[5], (H, D, M), dtype=jnp.float32) / np.sqrt(D)
        return {'x': x, 'Wqkv': Wqkv, 'bqkv': bqkv, 'Wout': Wout, 'bout': bout, 'proj': proj}
    _L0_attn_all = _L0_attn_setup()
    _L0_attn_in = {k: v for k, v in _L0_attn_all.items() if k in ('Wqkv', 'bqkv', 'Wout', 'bout', 'proj')}
    del _L0_attn_all

    def _L0_ffn_setup():
        import jax, jax.numpy as jnp
        import numpy as np
        DIM = 128
        HIDDEN = 384
        SCALE = 1.0 / 127.0

        def _dequant(w_int, dtype):
            return w_int.astype(dtype) * jnp.asarray(SCALE, dtype)
        key = jax.random.key(seed)
        k_x, k_g, k_u, k_d = jax.random.split(key, 4)
        x = jax.random.normal(k_x, (4, 256, DIM), dtype=jnp.float32)
        w_gate = jax.random.randint(k_g, (HIDDEN, DIM), -127, 128, dtype=jnp.int32)
        w_up = jax.random.randint(k_u, (HIDDEN, DIM), -127, 128, dtype=jnp.int32)
        w_down = jax.random.randint(k_d, (DIM, HIDDEN), -127, 128, dtype=jnp.int32)
        return {'x': x, 'w_gate': w_gate, 'w_up': w_up, 'w_down': w_down}
    _L0_ffn_all = _L0_ffn_setup()
    _L0_ffn_in = {k: v for k, v in _L0_ffn_all.items() if k in ('w_gate', 'w_up', 'w_down')}
    del _L0_ffn_all

    def _L1_xattn_setup():
        import jax, jax.numpy as jnp
        import numpy as np
        import math
        D = 128
        H = 16
        B = 4
        S = 256

        def _split_heads(x):
            b, s, d = x.shape
            return x.reshape(b, s, H, d // H).transpose(0, 2, 1, 3)
        key = jax.random.key(seed)
        ks = jax.random.split(key, 11)
        s = 1.0 / math.sqrt(D)
        inp = {'queries': jax.random.normal(ks[0], (B, S, D), jnp.float32), 'keys': jax.random.normal(ks[1], (B, S, D), jnp.float32), 'values': jax.random.normal(ks[2], (B, S, D), jnp.float32), 'Wq': jax.random.normal(ks[3], (D, D), jnp.float32) * s, 'bq': jnp.zeros((D,), jnp.float32), 'Wk': jax.random.normal(ks[4], (D, D), jnp.float32) * s, 'bk': jnp.zeros((D,), jnp.float32), 'Wv': jax.random.normal(ks[5], (D, D), jnp.float32) * s, 'bv': jnp.zeros((D,), jnp.float32), 'Wo': jax.random.normal(ks[6], (D, D), jnp.float32) * s, 'bo': jnp.zeros((D,), jnp.float32)}
        return inp
    _L1_xattn_all = _L1_xattn_setup()
    _L1_xattn_in = {k: v for k, v in _L1_xattn_all.items() if k in ('Wq', 'bq', 'Wk', 'bk', 'Wv', 'bv', 'Wo', 'bo')}
    del _L1_xattn_all

    def _L1_attn_setup():
        import jax, jax.numpy as jnp
        import numpy as np
        B, T = (4, 256)
        D_MODEL = 128
        N_HEADS = 8
        HEAD_DIM = 32
        KV_LRANK = 64

        def _orthogonalize_per_head(w):
            chunks = w.reshape(N_HEADS, HEAD_DIM, D_MODEL)

            def ns(m):
                A = m @ m.T
                Bm = 1.5 * jnp.eye(HEAD_DIM, dtype=m.dtype) - 0.5 * A
                return Bm @ m
            return jax.vmap(ns)(chunks).reshape(w.shape)
        key = jax.random.key(seed)
        ks = jax.random.split(key, 6)

        def lin(k, out_dim, in_dim):
            bound = 1.0 / np.sqrt(in_dim)
            return jax.random.uniform(k, (out_dim, in_dim), jnp.float32, -bound, bound)
        Wq = _orthogonalize_per_head(lin(ks[0], N_HEADS * HEAD_DIM, D_MODEL))
        return {'x': jax.random.normal(ks[1], (B, T, D_MODEL), jnp.float32), 'Wq': Wq, 'Wkv_down': lin(ks[2], KV_LRANK, D_MODEL), 'Wk_up': lin(ks[3], N_HEADS * HEAD_DIM, KV_LRANK), 'Wv_up': lin(ks[4], N_HEADS * HEAD_DIM, KV_LRANK), 'Wo': lin(ks[5], D_MODEL, N_HEADS * HEAD_DIM)}
    _L1_attn_all = _L1_attn_setup()
    _L1_attn_in = {k: v for k, v in _L1_attn_all.items() if k in ('Wq', 'Wkv_down', 'Wk_up', 'Wv_up', 'Wo')}
    del _L1_attn_all

    def _L1_ffn_setup():
        import jax, jax.numpy as jnp
        import numpy as np
        B, S, D = (1, 256, 128)
        F = 176
        E = 16
        K = 2
        CAP_FACTOR = 1.25

        def _mlp(h, wg, wu, wd):
            return jax.nn.silu(h @ wg) * (h @ wu) @ wd
        key = jax.random.key(seed)
        ks = jax.random.split(key, 10)
        sd = 0.02
        return {'x': jax.random.normal(ks[0], (B, S, D), jnp.float32), 'router_w': jax.random.normal(ks[1], (D, E), jnp.float32) * sd, 'router_b': jnp.zeros((E,), jnp.float32), 'w_gate': jax.random.normal(ks[2], (E, D, F), jnp.float32) * sd, 'w_up': jax.random.normal(ks[3], (E, D, F), jnp.float32) * sd, 'w_down': jax.random.normal(ks[4], (E, F, D), jnp.float32) * sd, 'sw_gate': jax.random.normal(ks[5], (D, F), jnp.float32) * sd, 'sw_up': jax.random.normal(ks[6], (D, F), jnp.float32) * sd, 'sw_down': jax.random.normal(ks[7], (F, D), jnp.float32) * sd}
    _L1_ffn_all = _L1_ffn_setup()
    _L1_ffn_in = {k: v for k, v in _L1_ffn_all.items() if k in ('router_w', 'router_b', 'w_gate', 'w_up', 'w_down', 'sw_gate', 'sw_up', 'sw_down')}
    del _L1_ffn_all

    def _L2_xattn_setup():
        import jax, jax.numpy as jnp
        import numpy as np
        B, SQ, SKV = (4, 256, 256)
        INPUT_DIM, EMBED_DIM, NUM_HEADS = (128, 128, 16)
        HEAD_DIM = EMBED_DIM // NUM_HEADS
        key = jax.random.key(seed)
        kq, kc, kwkv, kwo = jax.random.split(key, 4)

        def xavier(k, shape):
            fan_in, fan_out = shape
            lim = jnp.sqrt(6.0 / (fan_in + fan_out))
            return jax.random.uniform(k, shape, jnp.float32, -lim, lim)
        return {'q': jax.random.normal(kq, (B, SQ, EMBED_DIM), jnp.float32), 'c': jax.random.normal(kc, (B, SKV, INPUT_DIM), jnp.float32), 'W_kv': xavier(kwkv, (INPUT_DIM, 2 * EMBED_DIM)), 'b_kv': jnp.zeros((2 * EMBED_DIM,), jnp.float32), 'W_o': xavier(kwo, (EMBED_DIM, EMBED_DIM)), 'b_o': jnp.zeros((EMBED_DIM,), jnp.float32)}
    _L2_xattn_all = _L2_xattn_setup()
    _L2_xattn_in = {k: v for k, v in _L2_xattn_all.items() if k in ('W_kv', 'b_kv', 'W_o', 'b_o')}
    del _L2_xattn_all

    def _L2_attn_setup():
        import jax, jax.numpy as jnp
        import numpy as np
        D_MODEL = 128
        N_HEADS = 16
        N_KV = 4
        HEAD_DIM = D_MODEL // N_HEADS
        SEQ = 256
        BATCH = 2
        CAP = 50.0
        EPS = 1e-05
        THETA = 10000.0

        def _rms_norm(x, eps=EPS):
            return x * jax.lax.rsqrt(jnp.mean(jnp.square(x), axis=-1, keepdims=True) + eps)

        def _rope_cos_sin(seq_len, head_dim, theta=THETA):
            inv_freq = 1.0 / theta ** (jnp.arange(0, head_dim, 2, dtype=jnp.float32) / head_dim)
            freqs = jnp.arange(seq_len, dtype=jnp.float32)[:, None] * inv_freq[None, :]
            return (jnp.cos(freqs)[None, :, None, :], jnp.sin(freqs)[None, :, None, :])

        def _apply_rope(x, cos, sin):
            d = x.shape[-1] // 2
            x1, x2 = (x[..., :d], x[..., d:])
            return jnp.concatenate([x1 * cos - x2 * sin, x2 * cos + x1 * sin], axis=-1).astype(x.dtype)
        key = jax.random.key(seed)
        ks = jax.random.split(key, 5)
        s = 0.02
        return {'x': jax.random.normal(ks[0], (BATCH, SEQ, D_MODEL), dtype=jnp.float32), 'w_q': jax.random.normal(ks[1], (D_MODEL, N_HEADS * HEAD_DIM), dtype=jnp.float32) * s, 'w_k': jax.random.normal(ks[2], (D_MODEL, N_KV * HEAD_DIM), dtype=jnp.float32) * s, 'w_v': jax.random.normal(ks[3], (D_MODEL, N_KV * HEAD_DIM), dtype=jnp.float32) * s, 'w_o': jax.random.normal(ks[4], (N_HEADS * HEAD_DIM, D_MODEL), dtype=jnp.float32) * s}
    _L2_attn_all = _L2_attn_setup()
    _L2_attn_in = {k: v for k, v in _L2_attn_all.items() if k in ('w_q', 'w_k', 'w_v', 'w_o')}
    del _L2_attn_all

    def _L2_ffn_setup():
        import jax, jax.numpy as jnp
        import numpy as np
        DIM = 128
        MOE_INTER = 128
        SHARED_INTER = 128
        N_EXPERTS = 6
        TOP_K = 2
        ROUTE_SCALE = 1.0
        B, S = (8, 512)
        STD = 0.02 / np.sqrt(DIM)
        STD_I = 0.02 / np.sqrt(MOE_INTER)
        key = jax.random.key(seed)
        ks = jax.random.split(key, 10)
        inp = {'x': jax.random.normal(ks[0], (B, S, DIM), dtype=jnp.float32), 'gate_w': jax.random.normal(ks[1], (N_EXPERTS, DIM), dtype=jnp.float32) * STD, 'gate_b': jnp.zeros((N_EXPERTS,), dtype=jnp.float32), 'ew1': jax.random.normal(ks[2], (N_EXPERTS, MOE_INTER, DIM), dtype=jnp.float32) * STD, 'ew2': jax.random.normal(ks[3], (N_EXPERTS, DIM, MOE_INTER), dtype=jnp.float32) * STD_I, 'ew3': jax.random.normal(ks[4], (N_EXPERTS, MOE_INTER, DIM), dtype=jnp.float32) * STD, 'fc1': jax.random.normal(ks[5], (SHARED_INTER, DIM), dtype=jnp.float32) * STD, 'fc2': jax.random.normal(ks[6], (SHARED_INTER, DIM), dtype=jnp.float32) * STD, 'fc3': jax.random.normal(ks[7], (DIM, SHARED_INTER), dtype=jnp.float32) * STD_I}
        return inp
    _L2_ffn_all = _L2_ffn_setup()
    _L2_ffn_in = {k: v for k, v in _L2_ffn_all.items() if k in ('gate_w', 'gate_b', 'ew1', 'ew2', 'ew3', 'fc1', 'fc2', 'fc3')}
    del _L2_ffn_all

    def _L3_xattn_setup():
        import jax, jax.numpy as jnp
        import numpy as np
        EMBED = 128
        HEADS = 16
        HIDDEN = 128
        HEAD_DIM = EMBED // HEADS
        key = jax.random.key(seed)
        ks = jax.random.split(key, 9)
        s = 1.0 / np.sqrt(HIDDEN)
        return {'q': jax.random.normal(ks[0], (2, 256, HIDDEN), jnp.float32), 'k': jax.random.normal(ks[1], (2, 256, HIDDEN), jnp.float32), 'v': jax.random.normal(ks[2], (2, 256, HIDDEN), jnp.float32), 'wq': jax.random.normal(ks[3], (HIDDEN, EMBED), jnp.float32) * s, 'bq': jax.random.normal(ks[4], (EMBED,), jnp.float32) * s, 'wk': jax.random.normal(ks[5], (HIDDEN, EMBED), jnp.float32) * s, 'bk': jax.random.normal(ks[6], (EMBED,), jnp.float32) * s, 'wv': jax.random.normal(ks[7], (HIDDEN, EMBED), jnp.float32) * s, 'bv': jax.random.normal(ks[8], (EMBED,), jnp.float32) * s}
    _L3_xattn_all = _L3_xattn_setup()
    _L3_xattn_in = {k: v for k, v in _L3_xattn_all.items() if k in ('wq', 'bq', 'wk', 'bk', 'wv', 'bv')}
    del _L3_xattn_all

    def _L3_attn_setup():
        import jax, jax.numpy as jnp
        import numpy as np
        B, N, DM, H = (1, 256, 128, 16)
        CURV = 1.0
        key = jax.random.key(seed)
        ks = jax.random.split(key, 5)
        s = 1.0 / np.sqrt(DM)
        x = jax.random.normal(ks[0], (B, N, DM), dtype=jnp.float32)
        Wq = jax.random.uniform(ks[1], (DM, DM), jnp.float32, -s, s)
        Wk = jax.random.uniform(ks[2], (DM, DM), jnp.float32, -s, s)
        Wv = jax.random.uniform(ks[3], (DM, DM), jnp.float32, -s, s)
        Wo = jax.random.uniform(ks[4], (DM, DM), jnp.float32, -s, s)
        return {'x': x, 'Wq': Wq, 'Wk': Wk, 'Wv': Wv, 'Wo': Wo}
    _L3_attn_all = _L3_attn_setup()
    _L3_attn_in = {k: v for k, v in _L3_attn_all.items() if k in ('Wq', 'Wk', 'Wv', 'Wo')}
    del _L3_attn_all

    def _L3_ffn_setup():
        import jax, jax.numpy as jnp
        import numpy as np
        TOP_K = 8
        key = jax.random.key(seed)
        ks = jax.random.split(key, 6)
        B, S, D, F, E = (2, 128, 128, 64, 64)
        x = jax.random.normal(ks[0], (B, S, D), dtype=jnp.float32)
        centroids = jax.random.normal(ks[1], (E, D), dtype=jnp.float32) * 0.05
        expert_biases = jnp.zeros((E,), dtype=jnp.float32)
        Ws_up = jax.random.normal(ks[2], (D, F), dtype=jnp.float32) / np.sqrt(D)
        Ws_down = jax.random.normal(ks[3], (F, D), dtype=jnp.float32) / np.sqrt(F)
        W_up = jax.random.normal(ks[4], (E, D, F), dtype=jnp.float32) / np.sqrt(D)
        W_down = jax.random.normal(ks[5], (E, F, D), dtype=jnp.float32) / np.sqrt(F)
        return {'x': x, 'centroids': centroids, 'expert_biases': expert_biases, 'Ws_up': Ws_up, 'Ws_down': Ws_down, 'W_up': W_up, 'W_down': W_down}
    _L3_ffn_all = _L3_ffn_setup()
    _L3_ffn_in = {k: v for k, v in _L3_ffn_all.items() if k in ('centroids', 'expert_biases', 'Ws_up', 'Ws_down', 'W_up', 'W_down')}
    del _L3_ffn_all
    return {'x': x, 'ctx_1024': ctx_1024, 'mask_BxS2_bf1': mask_BxS2_bf1, 'L0_xattn_ln1_s': _L0_xattn_in['ln1_s'], 'L0_xattn_ln1_b': _L0_xattn_in['ln1_b'], 'L0_xattn_lnc_s': _L0_xattn_in['lnc_s'], 'L0_xattn_lnc_b': _L0_xattn_in['lnc_b'], 'L0_xattn_Wq': _L0_xattn_in['Wq'], 'L0_xattn_Wkv': _L0_xattn_in['Wkv'], 'L0_xattn_null_kv': _L0_xattn_in['null_kv'], 'L0_xattn_Wo': _L0_xattn_in['Wo'], 'L0_xattn_lno_s': _L0_xattn_in['lno_s'], 'L0_xattn_lno_b': _L0_xattn_in['lno_b'], 'L0_attn_Wqkv': _L0_attn_in['Wqkv'], 'L0_attn_bqkv': _L0_attn_in['bqkv'], 'L0_attn_Wout': _L0_attn_in['Wout'], 'L0_attn_bout': _L0_attn_in['bout'], 'L0_attn_proj': _L0_attn_in['proj'], 'L0_ffn_w_gate': _L0_ffn_in['w_gate'], 'L0_ffn_w_up': _L0_ffn_in['w_up'], 'L0_ffn_w_down': _L0_ffn_in['w_down'], 'L1_xattn_Wq': _L1_xattn_in['Wq'], 'L1_xattn_bq': _L1_xattn_in['bq'], 'L1_xattn_Wk': _L1_xattn_in['Wk'], 'L1_xattn_bk': _L1_xattn_in['bk'], 'L1_xattn_Wv': _L1_xattn_in['Wv'], 'L1_xattn_bv': _L1_xattn_in['bv'], 'L1_xattn_Wo': _L1_xattn_in['Wo'], 'L1_xattn_bo': _L1_xattn_in['bo'], 'L1_attn_Wq': _L1_attn_in['Wq'], 'L1_attn_Wkv_down': _L1_attn_in['Wkv_down'], 'L1_attn_Wk_up': _L1_attn_in['Wk_up'], 'L1_attn_Wv_up': _L1_attn_in['Wv_up'], 'L1_attn_Wo': _L1_attn_in['Wo'], 'L1_ffn_router_w': _L1_ffn_in['router_w'], 'L1_ffn_router_b': _L1_ffn_in['router_b'], 'L1_ffn_w_gate': _L1_ffn_in['w_gate'], 'L1_ffn_w_up': _L1_ffn_in['w_up'], 'L1_ffn_w_down': _L1_ffn_in['w_down'], 'L1_ffn_sw_gate': _L1_ffn_in['sw_gate'], 'L1_ffn_sw_up': _L1_ffn_in['sw_up'], 'L1_ffn_sw_down': _L1_ffn_in['sw_down'], 'L2_xattn_W_kv': _L2_xattn_in['W_kv'], 'L2_xattn_b_kv': _L2_xattn_in['b_kv'], 'L2_xattn_W_o': _L2_xattn_in['W_o'], 'L2_xattn_b_o': _L2_xattn_in['b_o'], 'L2_attn_w_q': _L2_attn_in['w_q'], 'L2_attn_w_k': _L2_attn_in['w_k'], 'L2_attn_w_v': _L2_attn_in['w_v'], 'L2_attn_w_o': _L2_attn_in['w_o'], 'L2_ffn_gate_w': _L2_ffn_in['gate_w'], 'L2_ffn_gate_b': _L2_ffn_in['gate_b'], 'L2_ffn_ew1': _L2_ffn_in['ew1'], 'L2_ffn_ew2': _L2_ffn_in['ew2'], 'L2_ffn_ew3': _L2_ffn_in['ew3'], 'L2_ffn_fc1': _L2_ffn_in['fc1'], 'L2_ffn_fc2': _L2_ffn_in['fc2'], 'L2_ffn_fc3': _L2_ffn_in['fc3'], 'L3_xattn_wq': _L3_xattn_in['wq'], 'L3_xattn_bq': _L3_xattn_in['bq'], 'L3_xattn_wk': _L3_xattn_in['wk'], 'L3_xattn_bk': _L3_xattn_in['bk'], 'L3_xattn_wv': _L3_xattn_in['wv'], 'L3_xattn_bv': _L3_xattn_in['bv'], 'L3_attn_Wq': _L3_attn_in['Wq'], 'L3_attn_Wk': _L3_attn_in['Wk'], 'L3_attn_Wv': _L3_attn_in['Wv'], 'L3_attn_Wo': _L3_attn_in['Wo'], 'L3_ffn_centroids': _L3_ffn_in['centroids'], 'L3_ffn_expert_biases': _L3_ffn_in['expert_biases'], 'L3_ffn_Ws_up': _L3_ffn_in['Ws_up'], 'L3_ffn_Ws_down': _L3_ffn_in['Ws_down'], 'L3_ffn_W_up': _L3_ffn_in['W_up'], 'L3_ffn_W_down': _L3_ffn_in['W_down']}

def reference(x, ctx_1024, mask_BxS2_bf1, L0_xattn_ln1_s, L0_xattn_ln1_b, L0_xattn_lnc_s, L0_xattn_lnc_b, L0_xattn_Wq, L0_xattn_Wkv, L0_xattn_null_kv, L0_xattn_Wo, L0_xattn_lno_s, L0_xattn_lno_b, L0_attn_Wqkv, L0_attn_bqkv, L0_attn_Wout, L0_attn_bout, L0_attn_proj, L0_ffn_w_gate, L0_ffn_w_up, L0_ffn_w_down, L1_xattn_Wq, L1_xattn_bq, L1_xattn_Wk, L1_xattn_bk, L1_xattn_Wv, L1_xattn_bv, L1_xattn_Wo, L1_xattn_bo, L1_attn_Wq, L1_attn_Wkv_down, L1_attn_Wk_up, L1_attn_Wv_up, L1_attn_Wo, L1_ffn_router_w, L1_ffn_router_b, L1_ffn_w_gate, L1_ffn_w_up, L1_ffn_w_down, L1_ffn_sw_gate, L1_ffn_sw_up, L1_ffn_sw_down, L2_xattn_W_kv, L2_xattn_b_kv, L2_xattn_W_o, L2_xattn_b_o, L2_attn_w_q, L2_attn_w_k, L2_attn_w_v, L2_attn_w_o, L2_ffn_gate_w, L2_ffn_gate_b, L2_ffn_ew1, L2_ffn_ew2, L2_ffn_ew3, L2_ffn_fc1, L2_ffn_fc2, L2_ffn_fc3, L3_xattn_wq, L3_xattn_bq, L3_xattn_wk, L3_xattn_bk, L3_xattn_wv, L3_xattn_bv, L3_attn_Wq, L3_attn_Wk, L3_attn_Wv, L3_attn_Wo, L3_ffn_centroids, L3_ffn_expert_biases, L3_ffn_Ws_up, L3_ffn_Ws_down, L3_ffn_W_up, L3_ffn_W_down):
    import jax
    import jax.numpy as jnp

    def _L0_xattn_ref(x, context, mask, ln1_s, ln1_b, lnc_s, lnc_b, Wq, Wkv, null_kv, Wo, lno_s, lno_b):
        import jax, jax.numpy as jnp
        import numpy as np
        EPS = 1e-06
        NUM_HEADS = 16
        DIM_HEADS = 64

        def _ln(x, scale, bias):
            mu = jnp.mean(x, axis=-1, keepdims=True)
            var = jnp.mean(jnp.square(x - mu), axis=-1, keepdims=True)
            return (x - mu) * jax.lax.rsqrt(var + EPS) * scale + bias
        b, n, _ = x.shape
        h, d = (NUM_HEADS, DIM_HEADS)
        scale = h ** (-0.5)
        xn = _ln(x, ln1_s, ln1_b)
        cn = _ln(context, lnc_s, lnc_b)
        q = xn @ Wq
        kv = cn @ Wkv
        k, v = jnp.split(kv, 2, axis=-1)

        def to_heads(t):
            return t.reshape(t.shape[0], t.shape[1], h, d).transpose(0, 2, 1, 3)
        q, k, v = (to_heads(q), to_heads(k), to_heads(v))
        nk = jnp.broadcast_to(null_kv[0], (b, h, 1, d))
        nv = jnp.broadcast_to(null_kv[1], (b, h, 1, d))
        k = jnp.concatenate((nk, k), axis=2)
        v = jnp.concatenate((nv, v), axis=2)
        sim = jnp.einsum('bhid,bhjd->bhij', q * scale, k)
        mfull = jnp.pad(mask, ((0, 0), (1, 0)), constant_values=True)[:, None, None, :]
        max_neg = -jnp.finfo(sim.dtype).max
        sim = jnp.where(mfull, sim, max_neg)
        attn = jax.nn.softmax(sim, axis=-1)
        out = jnp.einsum('bhij,bhjd->bhid', attn, v)
        out = out.transpose(0, 2, 1, 3).reshape(b, n, h * d)
        out = out @ Wo
        return _ln(out, lno_s, lno_b)

    def _L0_attn_ref(x, Wqkv, bqkv, Wout, bout, proj):
        import jax, jax.numpy as jnp
        import numpy as np
        B, T, C = (2, 256, 128)
        H, M = (16, 64)
        D = C // H
        b, t, c = x.shape
        h, d, m = proj.shape
        qkv = x @ Wqkv.T + bqkv
        q, k, v = jnp.split(qkv, 3, axis=-1)
        to_heads = lambda z: z.reshape(b, t, h, d).transpose(0, 2, 1, 3)
        q, k, v = (to_heads(q), to_heads(k), to_heads(v))
        qf, kf, vf = (q.astype(jnp.float32), k.astype(jnp.float32), v.astype(jnp.float32))
        pf = proj.astype(jnp.float32)
        q_prime = jax.nn.relu(jnp.einsum('bhtd,hdm->bhtm', qf, pf))
        k_prime = jax.nn.relu(jnp.einsum('bhtd,hdm->bhtm', kf, pf))
        k_cumsum = jnp.cumsum(k_prime, axis=2)
        kv_prod = jnp.einsum('bhtm,bhtd->bhtmd', k_prime, vf)
        kv_cumsum = jnp.cumsum(kv_prod, axis=2)
        context = jnp.einsum('bhtm,bhtmd->bhtd', q_prime, kv_cumsum)
        norm = jnp.einsum('bhtm,bhtm->bht', q_prime, k_cumsum)
        out = context / (norm[..., None] + 1e-06)
        out = out.astype(x.dtype).transpose(0, 2, 1, 3).reshape(b, t, c)
        return out @ Wout.T + bout

    def _L0_ffn_ref(x, w_gate, w_up, w_down):
        import jax, jax.numpy as jnp
        import numpy as np
        DIM = 128
        HIDDEN = 384
        SCALE = 1.0 / 127.0

        def _dequant(w_int, dtype):
            return w_int.astype(dtype) * jnp.asarray(SCALE, dtype)
        wg = _dequant(w_gate, x.dtype)
        wu = _dequant(w_up, x.dtype)
        wd = _dequant(w_down, x.dtype)
        gate = jnp.einsum('bsd,hd->bsh', x, wg)
        up = jnp.einsum('bsd,hd->bsh', x, wu)
        h = jax.nn.silu(gate) * up
        return jnp.einsum('bsh,dh->bsd', h, wd)

    def _L1_xattn_ref(queries, keys, values, Wq, bq, Wk, bk, Wv, bv, Wo, bo):
        import jax, jax.numpy as jnp
        import numpy as np
        import math
        D = 128
        H = 16
        B = 4
        S = 256

        def _split_heads(x):
            b, s, d = x.shape
            return x.reshape(b, s, H, d // H).transpose(0, 2, 1, 3)
        q = jax.nn.relu(queries @ Wq + bq)
        k = jax.nn.relu(keys @ Wk + bk)
        v = jax.nn.relu(values @ Wv + bv)
        q, k, v = (_split_heads(q), _split_heads(k), _split_heads(v))
        dk = q.shape[-1]
        scores = jnp.einsum('bhqd,bhkd->bhqk', q, k) / jnp.sqrt(jnp.float32(dk))
        attn = jax.nn.softmax(scores, axis=-1)
        y = jnp.einsum('bhqk,bhkd->bhqd', attn, v)
        y = y.transpose(0, 2, 1, 3).reshape(queries.shape[0], queries.shape[1], -1)
        return jax.nn.relu(y @ Wo + bo)

    def _L1_attn_ref(x, Wq, Wkv_down, Wk_up, Wv_up, Wo):
        import jax, jax.numpy as jnp
        import numpy as np
        B, T = (4, 256)
        D_MODEL = 128
        N_HEADS = 8
        HEAD_DIM = 32
        KV_LRANK = 64

        def _orthogonalize_per_head(w):
            chunks = w.reshape(N_HEADS, HEAD_DIM, D_MODEL)

            def ns(m):
                A = m @ m.T
                Bm = 1.5 * jnp.eye(HEAD_DIM, dtype=m.dtype) - 0.5 * A
                return Bm @ m
            return jax.vmap(ns)(chunks).reshape(w.shape)
        b, t, _ = x.shape
        q = (x @ Wq.T).reshape(b, t, N_HEADS, HEAD_DIM)
        kv_latent = x @ Wkv_down.T
        k = (kv_latent @ Wk_up.T).reshape(b, t, N_HEADS, HEAD_DIM)
        v = (kv_latent @ Wv_up.T).reshape(b, t, N_HEADS, HEAD_DIM)
        scale = HEAD_DIM ** (-0.5)
        scores = jnp.einsum('bqhd,bkhd->bhqk', q, k) * scale
        attn = jax.nn.softmax(scores, axis=-1)
        out = jnp.einsum('bhqk,bkhd->bqhd', attn, v)
        out = out.reshape(b, t, N_HEADS * HEAD_DIM)
        return out @ Wo.T

    def _L1_ffn_ref(x, router_w, router_b, w_gate, w_up, w_down, sw_gate, sw_up, sw_down):
        import jax, jax.numpy as jnp
        import numpy as np
        B, S, D = (1, 256, 128)
        F = 176
        E = 16
        K = 2
        CAP_FACTOR = 1.25

        def _mlp(h, wg, wu, wd):
            return jax.nn.silu(h @ wg) * (h @ wu) @ wd
        b, s, d = x.shape
        N = b * s
        NK = N * K
        C = int(np.ceil(CAP_FACTOR * NK / E))
        x_tokens = x.reshape(N, d)
        logits = x_tokens @ router_w + router_b
        probs = jax.nn.softmax(logits, axis=-1)
        vals, idx = jax.lax.top_k(probs, K)
        vals = vals / (jnp.sum(vals, axis=-1, keepdims=True) + 1e-09)
        idx_flat = idx.reshape(NK)
        vals_flat = vals.reshape(NK)
        oh_e = jax.nn.one_hot(idx_flat, E, dtype=x.dtype)
        pos = (jnp.cumsum(oh_e, axis=0) * oh_e).sum(axis=1) - 1
        within = (pos < C).astype(x.dtype)
        pos_c = jnp.clip(pos, 0, C - 1).astype(jnp.int32)
        token_ids = jnp.arange(NK) // K
        x_pair = x_tokens[token_ids] * within[:, None]
        expert_inputs = jnp.zeros((E, C, d), x.dtype).at[idx_flat, pos_c].add(x_pair)
        expert_outputs = jax.vmap(_mlp)(expert_inputs, w_gate, w_up, w_down)
        gathered = expert_outputs[idx_flat, pos_c] * (vals_flat * within)[:, None]
        output_tokens = gathered.reshape(N, K, d).sum(axis=1)
        return x + _mlp(x, sw_gate, sw_up, sw_down) + output_tokens.reshape(b, s, d)

    def _L2_xattn_ref(q, c, W_kv, b_kv, W_o, b_o):
        import jax, jax.numpy as jnp
        import numpy as np
        B, SQ, SKV = (4, 256, 256)
        INPUT_DIM, EMBED_DIM, NUM_HEADS = (128, 128, 16)
        HEAD_DIM = EMBED_DIM // NUM_HEADS
        Bc, Skv, _ = c.shape
        Bq, Sq, embed_dim = q.shape
        kv = c @ W_kv + b_kv
        kv = kv.reshape(Bc, Skv, NUM_HEADS, 2 * HEAD_DIM).transpose(0, 2, 1, 3)
        k, v = jnp.split(kv, 2, axis=-1)
        qh = q.reshape(Bq, Sq, NUM_HEADS, HEAD_DIM).transpose(0, 2, 1, 3)
        scale = 1.0 / jnp.sqrt(jnp.asarray(HEAD_DIM, q.dtype))
        logits = jnp.einsum('bhqd,bhkd->bhqk', qh, k) * scale
        attn = jax.nn.softmax(logits, axis=-1)
        values = jnp.einsum('bhqk,bhkd->bhqd', attn, v)
        values = values.transpose(0, 2, 1, 3).reshape(Bc, Sq, embed_dim)
        out = values @ W_o + b_o
        return out

    def _L2_attn_ref(x, w_q, w_k, w_v, w_o):
        import jax, jax.numpy as jnp
        import numpy as np
        D_MODEL = 128
        N_HEADS = 16
        N_KV = 4
        HEAD_DIM = D_MODEL // N_HEADS
        SEQ = 256
        BATCH = 2
        CAP = 50.0
        EPS = 1e-05
        THETA = 10000.0

        def _rms_norm(x, eps=EPS):
            return x * jax.lax.rsqrt(jnp.mean(jnp.square(x), axis=-1, keepdims=True) + eps)

        def _rope_cos_sin(seq_len, head_dim, theta=THETA):
            inv_freq = 1.0 / theta ** (jnp.arange(0, head_dim, 2, dtype=jnp.float32) / head_dim)
            freqs = jnp.arange(seq_len, dtype=jnp.float32)[:, None] * inv_freq[None, :]
            return (jnp.cos(freqs)[None, :, None, :], jnp.sin(freqs)[None, :, None, :])

        def _apply_rope(x, cos, sin):
            d = x.shape[-1] // 2
            x1, x2 = (x[..., :d], x[..., d:])
            return jnp.concatenate([x1 * cos - x2 * sin, x2 * cos + x1 * sin], axis=-1).astype(x.dtype)
        B, S, _ = x.shape
        q = (x @ w_q).reshape(B, S, N_HEADS, HEAD_DIM)
        k = (x @ w_k).reshape(B, S, N_KV, HEAD_DIM)
        v = (x @ w_v).reshape(B, S, N_KV, HEAD_DIM)
        q = _rms_norm(q)
        k = _rms_norm(k)
        cos, sin = _rope_cos_sin(S, HEAD_DIM)
        q = _apply_rope(q, cos, sin)
        k = _apply_rope(k, cos, sin)
        rep = N_HEADS // N_KV
        k = jnp.repeat(k, rep, axis=2)
        v = jnp.repeat(v, rep, axis=2)
        scores = jnp.einsum('bqhd,bkhd->bhqk', q, k) / np.sqrt(HEAD_DIM).astype(np.float32)
        scores = jnp.tanh(scores.astype(jnp.float32) / CAP) * CAP
        causal = jnp.tril(jnp.ones((S, S), dtype=bool))
        scores = jnp.where(causal[None, None], scores, -jnp.inf)
        probs = jax.nn.softmax(scores, axis=-1)
        y = jnp.einsum('bhqk,bkhd->bqhd', probs, v).reshape(B, S, N_HEADS * HEAD_DIM)
        return y @ w_o

    def _L2_ffn_ref(x, gate_w, gate_b, ew1, ew2, ew3, fc1, fc2, fc3):
        import jax, jax.numpy as jnp
        import numpy as np
        DIM = 128
        MOE_INTER = 128
        SHARED_INTER = 128
        N_EXPERTS = 6
        TOP_K = 2
        ROUTE_SCALE = 1.0
        B, S = (8, 512)
        STD = 0.02 / np.sqrt(DIM)
        STD_I = 0.02 / np.sqrt(MOE_INTER)
        orig_shape = x.shape
        xt = x.reshape(-1, DIM)
        logits = xt @ gate_w.T + gate_b
        probs = jax.nn.sigmoid(logits)
        w, idx = jax.lax.top_k(probs, TOP_K)
        w = w / (jnp.sum(w, axis=-1, keepdims=True) + 1e-08)
        w = w * ROUTE_SCALE
        ge = jnp.sum(jax.nn.one_hot(idx, N_EXPERTS, dtype=w.dtype) * w[..., None], axis=1)
        y = jnp.zeros_like(xt)
        for e in range(N_EXPERTS):
            h = jax.nn.silu(xt @ ew1[e].T) * (xt @ ew3[e].T)
            y = y + ge[:, e:e + 1] * (h @ ew2[e].T)
        z = jax.nn.silu(xt @ fc1.T) * (xt @ fc2.T) @ fc3.T
        return (y + z).reshape(orig_shape)

    def _L3_xattn_ref(q, k, v, wq, bq, wk, bk, wv, bv):
        import jax, jax.numpy as jnp
        import numpy as np
        EMBED = 128
        HEADS = 16
        HIDDEN = 128
        HEAD_DIM = EMBED // HEADS
        B = q.shape[0]

        def split_heads(x):
            return x.reshape(B, -1, HEADS, HEAD_DIM).transpose(0, 2, 1, 3)
        qh = split_heads(q @ wq + bq)
        kh = split_heads(k @ wk + bk)
        vh = split_heads(v @ wv + bv)
        scale = 1.0 / np.sqrt(HEAD_DIM).astype(np.float32)
        scores = jnp.einsum('bhqd,bhkd->bhqk', qh, kh) * scale
        probs = jax.nn.softmax(scores, axis=-1)
        out = jnp.einsum('bhqk,bhkd->bhqd', probs, vh)
        return out.transpose(0, 2, 1, 3).reshape(B, -1, EMBED)

    def _L3_attn_ref(x, Wq, Wk, Wv, Wo):
        import jax, jax.numpy as jnp
        import numpy as np
        B, N, DM, H = (1, 256, 128, 16)
        CURV = 1.0
        b, n, d = x.shape
        hd = d // H

        def split_heads(t):
            return t.reshape(b, n, H, hd).transpose(0, 2, 1, 3)
        q = split_heads(x @ Wq.T)
        k = split_heads(x @ Wk.T)
        v = split_heads(x @ Wv.T)
        q_norm_sq = jnp.sum(q * q, axis=-1, keepdims=True)
        k_norm_sq = jnp.sum(k * k, axis=-1)[:, :, None, :]
        qk = jnp.einsum('bhnd,bhmd->bhnm', q, k)
        diff_sq = jnp.maximum(q_norm_sq + k_norm_sq - 2.0 * qk, 0.0)
        denom = jnp.maximum((1.0 - CURV * q_norm_sq) * (1.0 - CURV * k_norm_sq), 1e-06)
        cosh_arg = jnp.maximum(1.0 + 2.0 * CURV * diff_sq / denom, 1.0)
        distance = jnp.where(cosh_arg > 1.0, jnp.arccosh(jnp.maximum(cosh_arg, 1.0 + 1e-12)), 0.0)
        attn = jax.nn.softmax(-distance, axis=-1)
        out = jnp.einsum('bhnm,bhmd->bhnd', attn, v)
        out = out.transpose(0, 2, 1, 3).reshape(b, n, d)
        return out @ Wo.T

    def _L3_ffn_ref(x, centroids, expert_biases, Ws_up, Ws_down, W_up, W_down):
        import jax, jax.numpy as jnp
        import numpy as np
        TOP_K = 8
        B, S, D = x.shape
        E = centroids.shape[0]
        T = B * S
        xf = x.reshape(T, D)
        shared = jax.nn.silu(xf @ Ws_up) @ Ws_down
        aff = xf @ centroids.T
        biased = aff + expert_biases
        _, idx = jax.lax.top_k(biased, TOP_K)
        sel = jnp.take_along_axis(aff, idx, axis=1)
        w = jax.nn.sigmoid(sel)
        w = w / (jnp.sum(w, axis=-1, keepdims=True) + 1e-08)
        cw = jnp.zeros((T, E), dtype=x.dtype).at[jnp.arange(T)[:, None], idx].add(w)
        h = jax.nn.silu(jnp.einsum('td,edf->etf', xf, W_up))
        y = jnp.einsum('etf,efd->etd', h, W_down)
        routed = jnp.einsum('etd,te->td', y, cw)
        return (shared + routed).reshape(B, S, D)
    x = x + _L0_xattn_ref(_layernorm(x, axis=-1), ctx_1024, mask_BxS2_bf1, L0_xattn_ln1_s, L0_xattn_ln1_b, L0_xattn_lnc_s, L0_xattn_lnc_b, L0_xattn_Wq, L0_xattn_Wkv, L0_xattn_null_kv, L0_xattn_Wo, L0_xattn_lno_s, L0_xattn_lno_b)
    x = x + _L0_attn_ref(_layernorm(x, axis=-1), L0_attn_Wqkv, L0_attn_bqkv, L0_attn_Wout, L0_attn_bout, L0_attn_proj)
    x = x + _L0_ffn_ref(_layernorm(x, axis=-1), L0_ffn_w_gate, L0_ffn_w_up, L0_ffn_w_down)
    x = x + _L1_xattn_ref(_layernorm(x, axis=-1), ctx_1024, ctx_1024, L1_xattn_Wq, L1_xattn_bq, L1_xattn_Wk, L1_xattn_bk, L1_xattn_Wv, L1_xattn_bv, L1_xattn_Wo, L1_xattn_bo)
    x = x + _L1_attn_ref(_layernorm(x, axis=-1), L1_attn_Wq, L1_attn_Wkv_down, L1_attn_Wk_up, L1_attn_Wv_up, L1_attn_Wo)
    x = x + _L1_ffn_ref(_layernorm(x, axis=-1), L1_ffn_router_w, L1_ffn_router_b, L1_ffn_w_gate, L1_ffn_w_up, L1_ffn_w_down, L1_ffn_sw_gate, L1_ffn_sw_up, L1_ffn_sw_down)
    x = x + _L2_xattn_ref(_layernorm(x, axis=-1), ctx_1024, L2_xattn_W_kv, L2_xattn_b_kv, L2_xattn_W_o, L2_xattn_b_o)
    x = x + _L2_attn_ref(_layernorm(x, axis=-1), L2_attn_w_q, L2_attn_w_k, L2_attn_w_v, L2_attn_w_o)
    x = x + _L2_ffn_ref(_layernorm(x, axis=-1), L2_ffn_gate_w, L2_ffn_gate_b, L2_ffn_ew1, L2_ffn_ew2, L2_ffn_ew3, L2_ffn_fc1, L2_ffn_fc2, L2_ffn_fc3)
    x = x + _L3_xattn_ref(_layernorm(x, axis=-1), ctx_1024, ctx_1024, L3_xattn_wq, L3_xattn_bq, L3_xattn_wk, L3_xattn_bk, L3_xattn_wv, L3_xattn_bv)
    x = x + _L3_attn_ref(_layernorm(x, axis=-1), L3_attn_Wq, L3_attn_Wk, L3_attn_Wv, L3_attn_Wo)
    x = x + _L3_ffn_ref(_layernorm(x, axis=-1), L3_ffn_centroids, L3_ffn_expert_biases, L3_ffn_Ws_up, L3_ffn_Ws_down, L3_ffn_W_up, L3_ffn_W_down)
    return x

_drawn_inputs = setup_inputs


def setup_inputs(seed=0):
    import zlib

    import numpy as np

    out = dict(_drawn_inputs(seed))
    spreads = {'L0_xattn_ln1_s': (1.0, 0.2),
     'L0_xattn_ln1_b': (0.0, 0.1),
     'L0_xattn_lnc_s': (1.0, 0.2),
     'L0_xattn_lnc_b': (0.0, 0.1),
     'L0_xattn_lno_s': (1.0, 0.2),
     'L0_xattn_lno_b': (0.0, 0.1),
     'L1_xattn_bq': (0.0, 0.8),
     'L1_xattn_bk': (0.0, 0.8),
     'L1_xattn_bv': (0.0, 2.0),
     'L1_xattn_bo': (0.0, 2.0),
     'L1_ffn_router_b': (0.0, 2.0),
     'L2_xattn_b_kv': (0.0, 2.0),
     'L2_xattn_b_o': (0.0, 2.0),
     'L2_ffn_gate_b': (0.0, 2.0),
     'L3_ffn_expert_biases': (0.0, 2.0)}
    factors = {'L0_attn_bqkv': 2.704,
     'L0_attn_bout': 2.979,
     'L1_xattn_Wq': 8.0,
     'L1_xattn_Wk': 8.0,
     'L1_xattn_Wv': 8.0,
     'L1_xattn_Wo': 8.0,
     'L1_attn_Wq': 8.0,
     'L1_attn_Wkv_down': 8.0,
     'L1_attn_Wk_up': 8.0,
     'L1_attn_Wv_up': 8.0,
     'L1_attn_Wo': 8.0,
     'L1_ffn_router_w': 46.841,
     'L1_ffn_w_gate': 49.401,
     'L1_ffn_w_up': 44.903,
     'L1_ffn_w_down': 44.569,
     'L1_ffn_sw_gate': 35.404,
     'L1_ffn_sw_up': 31.914,
     'L1_ffn_sw_down': 32.076,
     'L2_xattn_W_kv': 8.0,
     'L2_xattn_W_o': 8.0,
     'L2_attn_w_q': 64.0,
     'L2_attn_w_k': 64.0,
     'L2_attn_w_v': 64.0,
     'L2_attn_w_o': 64.0,
     'L2_ffn_gate_w': 200.0,
     'L2_ffn_ew1': 200.0,
     'L2_ffn_ew2': 200.0,
     'L2_ffn_ew3': 200.0,
     'L2_ffn_fc1': 200.0,
     'L2_ffn_fc2': 200.0,
     'L2_ffn_fc3': 200.0,
     'L3_xattn_wq': 51.494,
     'L3_xattn_bq': 200.0,
     'L3_xattn_wk': 48.36,
     'L3_xattn_bk': 200.0,
     'L3_xattn_wv': 43.644,
     'L3_xattn_bv': 200.0,
     'L3_attn_Wq': 200.0,
     'L3_attn_Wk': 200.0,
     'L3_attn_Wv': 62.347,
     'L3_attn_Wo': 61.218,
     'L3_ffn_centroids': 30.995,
     'L3_ffn_Ws_up': 8.0,
     'L3_ffn_Ws_down': 8.0,
     'L3_ffn_W_up': 33.658,
     'L3_ffn_W_down': 28.257}
    for name, (base, spread) in spreads.items():
        noise = np.random.default_rng([zlib.crc32(name.encode()), seed]).standard_normal(out[name].shape)
        drawn = base * np.exp(spread * noise) if base else spread * noise
        out[name] = jnp.asarray(drawn.astype(out[name].dtype))
    for name, factor in factors.items():
        out[name] = (out[name] * factor).astype(out[name].dtype)
    return out
```

```python
from contextlib import ExitStack

import numpy as np

import concourse.bass as bass
from concourse import mybir

F32 = mybir.dt.float32
BF16 = mybir.dt.bfloat16
U8 = mybir.dt.uint8
U32 = mybir.dt.uint32
I32 = mybir.dt.int32
ALU = mybir.AluOpType
ACT = mybir.ActivationFunctionType
X_AXIS = mybir.AxisListType.X

P = 128
BATCH, SEQ, KEYS = 128, 32, 257
TILES = BATCH * SEQ // P
NB = P // SEQ
CTX_PAD = BATCH + NB
ENGINES = 5


def bc(ap, axis, n):
    u = ap.unsqueeze(axis)
    shape = list(u.shape)
    shape[axis] = n
    return u.to_broadcast(shape)


class Signal:

    PRIMED = 64

    def __init__(self, sem):
        self.sem = sem
        self.count = self.PRIMED

    def stage(self, per, first=0, tiles=TILES):
        return Counted(self, per, first, tiles)


class Counted:

    def __init__(self, signal, per, first, tiles):
        self.sem, self.base, self.per, self.first = signal.sem, signal.count, per, first
        signal.count += first + per * tiles

    def before(self, n):
        return self.base + n

    def at(self, i, n):
        return i * self.per + (self.base + self.first + n)


class Chain:

    def __init__(self, eng, counted):
        self.eng, self.c, self.i, self.n = eng, counted, None, 0

    def round(self, i):
        assert self.i is not None or self.n == self.c.first, self.n
        assert self.i is None or self.n == self.c.per, self.n
        self.i, self.n = i, 0

    def done(self):
        assert self.n == (self.c.first if self.i is None else self.c.per), self.n

    def link(self, ins):
        self.n += 1
        ins.then_inc(self.c.sem, 1)
        self.eng.wait_ge(self.c.sem, self.c.before(self.n) if self.i is None else self.c.at(self.i, self.n))


def constants():
    p = np.arange(P)
    cols = {}
    cols["ident"] = np.eye(P)
    cols["lane"] = (p[:, None] % 32) // 8 == np.arange(4)[None]
    cols["lane_scaled"] = cols["lane"] / np.sqrt(8.0)
    cols["lane_eighth"] = cols["lane"] / 8.0
    cols["quad"] = p[:, None] // 32 == np.arange(4)[None]
    cols["query"] = p[:, None] % 32 == np.arange(32)[None]
    cols["earlier"] = p[:, None] < p[None]
    cols["ones"] = np.ones((P, P))
    win = np.zeros((P, 7, 32))
    win[:, 3] = p[:, None] % 32 == np.arange(32)[None]
    cols["query_window"] = win.reshape(P, -1)
    cols["quad_scaled"] = cols["quad"] / np.sqrt(32.0)
    cols["causal"] = np.arange(32)[None] <= p[:, None] % 32
    cols["causal_T"] = (p[:, None] // 32 == p[None] // 32) & (p[:, None] <= p[None])
    cols["same_head"] = p[:, None] // 8 == p[None] // 8
    cols["head16"] = p[:, None] // 8 == np.arange(16)[None]
    win = np.zeros((P, 248))
    win[:, 120:128] = 1
    cols["head_window"] = win
    inv = np.float32(1.0) / np.float32(10000.0) ** (np.arange(0, 8, 2, dtype=np.float32) / np.float32(8))
    freq = (p % SEQ).astype(np.float32)[:, None] * inv[None]
    cols["cos"], cols["sin"] = np.cos(freq), np.sin(freq)
    cols["row_no"] = p[:, None]
    cols["pair_head"] = (np.arange(16)[None, None] == 2 * np.arange(8)[None, :, None] + p[:, None, None] // 64).reshape(P, -1)
    cols["pair_in_group"] = (np.arange(4)[None, None] == 2 * np.arange(2)[None, :, None] + p[:, None, None] // 64).reshape(P, -1)
    cols["mean_of"] = np.full((P, P), 1.0 / P)
    cols["expert_no"] = np.tile(np.arange(16)[None], (P, 1))
    cols["last_key"] = p[:, None] == np.arange(16)[None]
    out, at, parts = {}, 0, []
    for name, a in cols.items():
        out[name] = (at, a.shape[1])
        at += a.shape[1]
        parts.append(np.asarray(a, np.float32))
    return np.ascontiguousarray(np.concatenate(parts, 1)), out


CONST, CONST_AT = constants()


X0_STEPS, X0_FIRST = 25, 27
SCRATCH = 16100


class Core:

    def __init__(self, nc, ctx, dram):
        self.nc, self.ctx, self.dram = nc, ctx, dram
        self.loads = []
        self.stage_no = 0
        self.X = self.sb("x_tokens", [P, TILES + 1, P])
        self.const = self.sb("consts", [P, CONST.shape[1]])
        self.psum = ctx.enter_context(nc.psum_tensor("psum_banks", [P, 8, 512], F32))
        self.bank = [self.psum[:, b, :] for b in range(8)]
        self.stat = self.sb("ln_stat", [P, 6])
        self.meanvar = self.sb("ln_meanvar", [P, 2])
        self.vareps = self.sb("ln_vareps", [P, 1])
        self.rstd = self.sb("ln_rstd", [P, 1])
        self.rstd_first = self.sb("ln_rstd_first", [P, 1])
        self.rstd_second = self.sb("ln_rstd_second", [P, 1])
        self.ln_eps6 = self.sb("ln_eps6", [P, 1])
        self.minus_half = self.sb("minus_half", [P, 32])
        self.ln_eps = self.sb("ln_eps", [P, 1])
        self.xn = self.sb("x_normed", [P, P])
        self.xnT = self.sb("x_normed_T", [P, P])
        self.carrier = self.sb("wait_carrier", [P, 1])
        self.zero4 = self.sb("zero4", [P, 4])
        self.mask_in = self.sb("mask_in", [P, KEYS], U8)
        self.mask_bias = self.sb("mask_bias", [P, KEYS], BF16)
        self.batch_select = self.sb("batch_select", [P, NB, P], BF16)
        self.out_meanvar = self.sb("out_meanvar", [P, 2])
        self.top_at = self.sb("route_top_at", [P, 8], U32)
        self.area = self.sb("scratch", [P, SCRATCH])
        self.signals = {}

    def sb(self, name, shape, dt=F32):
        return self.ctx.enter_context(self.nc.sbuf_tensor(name, shape, dt))

    def scratch(self, shapes):
        out, at = {}, 0
        for name, shape in shapes.items():
            n = int(np.prod(shape[1:]))
            t = self.area[0:shape[0], at:at + n]
            if len(shape) == 3:
                t = t.rearrange("p (a b) -> p a b", a=shape[1])
            if len(shape) == 4:
                t = t.rearrange("p (a b c) -> p a b c", a=shape[1], b=shape[2])
            out[name] = t
            at += n
        assert at <= SCRATCH, at
        return out

    def sig(self, name):
        if name not in self.signals:
            self.signals[name] = Signal(self.ctx.enter_context(self.nc.semaphore(name)))
        return self.signals[name]

    def c(self, name):
        a, n = CONST_AT[name]
        return self.const[:, a:a + n]

    def load(self, name, shape, src=None, dt=F32):
        t = self.sb("w_" + name, shape, dt)
        self.loads.append((self.stage_no, t, self.dram[name] if src is None else src))
        return t

    def rows(self, name, n):
        t = self.sb("r_" + name, [P, n])
        self.loads.append((self.stage_no, t, self.dram[name].partition_broadcast(P)))
        return t

    def column(self, name):
        t = self.sb("c_" + name, [P, 1])
        self.loads.append((self.stage_no, t, self.dram[name].rearrange("(p a) -> p a", a=1)))
        return t


class Norm:

    def __init__(self, k, twice=False):
        self.k, self.twice = k, twice
        self.var = k.sig("ln_var_ready").stage(1, 1)
        self.rs = k.sig("ln_rstd_ready").stage(1, 1)
        self.xn = k.sig("xn_ready").stage(1, 1)
        self.pool_step = k.sig("pool_ln_step").stage(*((6, 6) if twice else (1, 1)))

    @staticmethod
    def count(c, i):
        return c.before(1) if i is None else c.at(i, 1)

    @staticmethod
    def tile(i):
        return 0 if i is None else i + 1

    def dve_stats(self, dve, chain, i):
        k = self.k
        chain.link(dve.bn_stats(k.stat[:, :], k.X[:, self.tile(i), :]))
        dve.memset(k.carrier[:, :], 0.0)
        dve.bn_aggr(k.meanvar[:, :], k.stat[:, :]).then_inc(self.var.sem, 1)

    def pool(self, pool, i):
        k = self.k
        pool.wait_ge(self.var.sem, self.count(self.var, i))
        pool.tensor_tensor(k.vareps[:, :], k.meanvar[:, 1:2], k.ln_eps[:, :], ALU.add).then_inc(self.pool_step.sem, 1)
        c, n = self.pool_step, 1

        def step(out, a, b, op):
            nonlocal n
            pool.wait_ge(c.sem, c.before(n) if i is None else c.at(i, n))
            n += 1
            return pool.tensor_tensor(out[:, :], a, b, op)

        if self.twice:
            v, r1, r2 = k.vareps, k.rstd_first, k.rstd_second
            step(r1, v[:, :], k.minus_half[:, 0:1], ALU.pow).then_inc(c.sem, 1)
            step(v, r1[:, :], r1[:, :], ALU.mult).then_inc(c.sem, 1)
            step(v, v[:, :], k.meanvar[:, 1:2], ALU.mult).then_inc(c.sem, 1)
            step(v, v[:, :], k.ln_eps6[:, :], ALU.add).then_inc(c.sem, 1)
            step(r2, v[:, :], k.minus_half[:, 0:1], ALU.pow).then_inc(c.sem, 1)
            step(k.rstd, r1[:, :], r2[:, :], ALU.mult).then_inc(self.rs.sem, 1)
        else:
            step(k.rstd, k.vareps[:, :], k.minus_half[:, 0:1], ALU.pow).then_inc(self.rs.sem, 1)

    def dve_apply(self, dve, i):
        k = self.k
        dve.wait_ge(self.rs.sem, self.count(self.rs, i))
        dve.tensor_scalar(k.xn[:, :], k.X[:, self.tile(i), :], k.meanvar[:, 0:1], k.rstd[:, 0:1],
                          ALU.subtract, ALU.mult).then_inc(self.xn.sem, 1)


class Misc:

    def __init__(self, k, per, first, bank):
        self.w = k.sig("misc_written").stage(per, first)
        self.r = k.sig("misc_read").stage(per, first)
        self.bank = k.bank[bank]

    def v(self, c, i, n):
        return c.before(n) if i is None else c.at(i, n)


def cross_attention(k, name, q_w, q_b, k_w, k_b, v_w, v_b, o_w, o_b, relu, shared):
    norm = Norm(k)
    nq = 1 if q_w is None else 2
    last = 2 if o_w is not None else 1
    misc = Misc(k, 2 + last + nq, nq, 7)
    S, T, KB, VB, OB, M = k.bank[0:2], k.bank[2:4], k.bank[4], k.bank[5], k.bank[6], k.bank[7]
    sg = {n: k.sig(n).stage(per, first) for n, (per, first) in {
        **{f"slot{b}_loaded": (16, 16) for b in range(NB)}, "slot_freed": (2 * NB, 0), "last_key_kept": (NB, 0), "k_written": (NB, 1), "k_read": (NB, 1),
        "v_written": (NB, 1), "v_read": (NB, 1), "scores_written": (16, 0), "max_ready": (16, 0),
        "probs_ready": (16, 0), "probs_T_written": (16, 0), "probs_T_read": (16, 0), "pv_done": (16, 0),
        "last_key_added": (1, 0), "heads_ready": (1, 0), "q_ready": (1, 1),
    }.items()}
    chain_c = k.sig("vector_step").stage(5, 2 if q_w is not None else 1)
    wq = k.load(q_w, [P, P]) if q_w else None
    bq = k.column(q_b) if q_b else None
    wk, bk = k.load(k_w, [P, P]), k.column(k_b)
    wv = k.load(v_w, [P, P])
    bv_col, bv_row = k.column(v_b), k.rows(v_b, P)
    wo = k.load(o_w, [P, P]) if o_w else None
    bo = k.rows(o_b, P) if o_w else None
    (slots, last_key, kT, vS, qT, qbd, negm, pbuf, rs, rr, w, pT, pl, vl, vlbd, om, outT, tmp) = (
        shared[n] for n in ("slots", "last_key", "kT", "vS", "qT", "qbd", "negm", "pbuf", "rs", "rr", "w", "pT",
                            "pl", "vl", "vlbd", "om", "outT", "tmp"))
    ctxT = k.dram["ctxT"]

    def sp(sp):
        for b in range(NB):
            sp.dma_start(slots[:, b, :], ctxT[b]).then_inc(sg[f"slot{b}_loaded"].sem, 16)
        with sp.Fori(0, TILES) as i:
            for b in range(NB):
                sp.wait_ge(sg["v_written"].sem, sg["v_written"].at(i, b))
                sp.sem_inc(sg["slot_freed"].sem, 1)
                sp.wait_ge(sg["last_key_kept"].sem, sg["last_key_kept"].at(i, b + 1))
                sp.sem_inc(sg["slot_freed"].sem, 1)
                sp.dma_start(slots[:, b, :], ctxT[i * NB + (NB + b)]).then_inc(sg[f"slot{b}_loaded"].sem, 16)
        for b in range(NB):
            sp.wait_ge(sg[f"slot{b}_loaded"].sem, sg[f"slot{b}_loaded"].at(TILES - 1, 16))

    def pool(pool):
        norm.pool(pool, None)
        with pool.Fori(0, TILES) as i:
            pool.wait_ge(sg["heads_ready"].sem, sg["heads_ready"].at(i, 0))
            for b in range(NB):
                pool.wait_ge(sg[f"slot{b}_loaded"].sem, sg[f"slot{b}_loaded"].at(i, 0))
                pool.tensor_tensor(last_key[:, b, :], bc(slots[:, b, KEYS - 1], 1, 4), k.zero4[:, :], ALU.add
                                   ).then_inc(sg["last_key_kept"].sem, 1)
            norm.pool(pool, i)

    def pe(pe):
        def prep(i):
            m = 0 if i is None else 2 + last
            pe.wait_ge(norm.xn.sem, norm.count(norm.xn, i))
            pe.wait_ge(misc.r.sem, misc.v(misc.r, i, m))
            pe.transpose(M[:, 0:P], k.xn[:, :], k.c("ident")).then_inc(misc.w.sem, 1)
            if wq is not None:
                pe.wait_ge(misc.r.sem, misc.v(misc.r, i, m + 1))
                pe.matmul(M[:, 0:P], wq[:, :], k.xnT[:, :], start=True, stop=True).then_inc(misc.w.sem, 1)

        def kv(i, b):
            s = 0 if i is None else (b + 1) % NB
            loaded = sg[f"slot{s}_loaded"]
            pe.wait_ge(loaded.sem, loaded.before(16) if i is None else loaded.at(i, 16 if s == 0 else 0))
            if i is not None:
                pe.wait_ge(sg["k_read"].sem, sg["k_read"].at(i, b))
            pe.matmul(KB[:, 0:KEYS], wk[:, :], slots[:, s, :], start=True, stop=True
                      ).then_inc(sg["k_written"].sem, 1)
            if i is not None:
                pe.wait_ge(sg["v_read"].sem, sg["v_read"].at(i, b))
            pe.matmul(VB[:, 0:P], slots[:, s, 0:P], wv[:, :], start=True, stop=True)
            pe.matmul(VB[:, P:2 * P], slots[:, s, P:2 * P], wv[:, :], start=True, stop=True
                      ).then_inc(sg["v_written"].sem, 1)

        def scores(i, u):
            b, t = divmod(u, 4)
            if u == 0:
                pe.wait_ge(sg["q_ready"].sem, sg["q_ready"].at(i, 0))
            if t == 0:
                pe.wait_ge(sg["k_read"].sem, sg["k_read"].at(i, b))
            pe.wait_ge(sg["probs_ready"].sem, sg["probs_ready"].at(i, max(u - 1, 0)))
            q = slice(32 * t, 32 * t + 32)
            pe.matmul(S[u % 2][:, 0:KEYS], qbd[q, b, :], kT[q, b % 2, :], start=True, stop=True
                      ).then_inc(sg["scores_written"].sem, 1)

        def turn(i, u):
            pe.wait_ge(sg["probs_ready"].sem, sg["probs_ready"].at(i, u + 1))
            pe.wait_ge(sg["probs_T_read"].sem, sg["probs_T_read"].at(i, max(u - 1, 0)))
            pe.transpose(T[u % 2][:, 0:P], pbuf[:, u, 0:P], k.c("ident"))
            pe.transpose(T[u % 2][:, P:2 * P], pbuf[:, u, P:2 * P], k.c("ident")
                         ).then_inc(sg["probs_T_written"].sem, 1)

        def values(i, u):
            b, t = divmod(u, 4)
            if u == 0:
                pe.wait_ge(sg["heads_ready"].sem, sg["heads_ready"].at(i, 0))
            if t == 0:
                pe.wait_ge(sg["v_read"].sem, sg["v_read"].at(i, b))
            pe.wait_ge(sg["probs_T_read"].sem, sg["probs_T_read"].at(i, u + 1))
            for c in range(2):
                mm = pe.matmul(OB[:, 32 * u:32 * u + 32], pT[:, u % 2, c * P:(c + 1) * P],
                               vS[:, b % 2, c, 32 * t:32 * t + 32], start=(u == 0 and c == 0), stop=False,
                               skip_group_check=True)
            mm.then_inc(sg["pv_done"].sem, 1)

        prep(None)
        kv(None, 0)
        with pe.Fori(0, TILES) as i:
            for u in range(16):
                scores(i, u)
                if u % 4 == 1:
                    kv(i, u // 4)
                if u == 10:
                    pe.wait_ge(sg["last_key_kept"].sem, sg["last_key_kept"].at(i, NB))
                    pe.wait_ge(misc.r.sem, misc.r.at(i, 0))
                    pe.matmul(M[0:16, 0:P], last_key[:, :, :].rearrange("p b t -> p (b t)"), wv[:, :],
                              start=True, stop=True).then_inc(misc.w.sem, 1)
                if u >= 2:
                    turn(i, u - 2)
                if u >= 3:
                    values(i, u - 3)
            turn(i, 14)
            values(i, 13)
            turn(i, 15)
            pe.wait_ge(misc.r.sem, misc.r.at(i, 1))
            pe.transpose(M[0:16, 0:P], pbuf[:, :, KEYS - 1], k.c("ident")).then_inc(misc.w.sem, 1)
            values(i, 14)
            values(i, 15)
            pe.wait_ge(misc.r.sem, misc.r.at(i, 2))
            pe.matmul(OB[:, :], pl[0:16, :], vlbd[0:16, :], start=False, stop=True, skip_group_check=True
                      ).then_inc(sg["last_key_added"].sem, 1)
            pe.wait_ge(sg["heads_ready"].sem, sg["heads_ready"].at(i, 1))
            if wo is not None:
                for b in range(NB):
                    mm = pe.matmul(M[:, 0:P], om[:, b * P:(b + 1) * P], window(k, b), start=(b == 0), stop=(b == NB - 1))
                mm.then_inc(misc.w.sem, 1)
                pe.wait_ge(misc.r.sem, misc.r.at(i, 3))
                pe.matmul(M[:, 0:P], outT[:, :], wo[:, :], start=True, stop=True).then_inc(misc.w.sem, 1)
            else:
                for b in range(NB):
                    mm = pe.matmul(M[32 * b:32 * b + 32, 0:P], k.c("query"), om[:, b * P:(b + 1) * P],
                                   start=True, stop=True, skip_group_check=True)
                mm.then_inc(misc.w.sem, 1)
            prep(i)

    def act(act):
        def k_out(i, b):
            kw = sg["k_written"]
            act.wait_ge(kw.sem, kw.before(1) if i is None else kw.at(i, b + 1))
            if i is not None:
                act.wait_ge(sg["scores_written"].sem, sg["scores_written"].at(i, 4 * b))
            s = 0 if i is None else (b + 1) % 2
            act.activation(kT[:, s, :], KB[:, 0:KEYS], ACT.Relu if relu else ACT.Identity, bias=bk[:, 0:1]
                           ).then_inc(sg["k_read"].sem, 1)

        k_out(None, 0)
        with act.Fori(0, TILES) as i:
            act.wait_ge(sg["heads_ready"].sem, sg["heads_ready"].at(i, 0))
            for u in range(16):
                act.wait_ge(sg["max_ready"].sem, sg["max_ready"].at(i, u + 1))
                act.activation(pbuf[:, u, :], S[u % 2][:, 0:KEYS], ACT.Exp, bias=negm[:, u:u + 1],
                               accum_out=rs[:, u:u + 1]).then_inc(sg["probs_ready"].sem, 1)
                if u % 4 == 1:
                    k_out(i, u // 4)

    def dve(dve):
        chain = Chain(dve, chain_c)

        def prep(i):
            m = 0 if i is None else 2 + last
            norm.dve_apply(dve, i)
            dve.wait_ge(misc.w.sem, misc.v(misc.w, i, m + 1))
            if wq is not None:
                dve.tensor_copy(k.xnT[:, :], M[:, 0:P]).then_inc(misc.r.sem, 1)
                dve.wait_ge(misc.w.sem, misc.v(misc.w, i, m + 2))
                if relu:
                    ins = dve.tensor_scalar(qT[:, :], M[:, 0:P], bq[:, 0:1], 0.0, ALU.add, ALU.max)
                else:
                    ins = dve.tensor_scalar(qT[:, :], M[:, 0:P], bq[:, 0:1], None, ALU.add)
            else:
                ins = dve.tensor_copy(qT[:, :], M[:, 0:P])
            ins.then_inc(misc.r.sem, 1)
            dve.wait_ge(misc.r.sem, misc.v(misc.r, i, m + nq))
            if i is not None:
                dve.wait_ge(sg["scores_written"].sem, sg["scores_written"].at(i, 16))
            dve.tensor_tensor(qbd[:, :, :].rearrange("p b (j q) -> p b j q", j=4),
                              bc(qT[:, :].rearrange("p (b q) -> p b q", b=NB), 2, 4),
                              bc(bc(k.c("lane_scaled"), 1, NB), 3, SEQ), ALU.mult).then_inc(sg["q_ready"].sem, 1)

        def v_out(i, b):
            vw = sg["v_written"]
            dve.wait_ge(vw.sem, vw.before(1) if i is None else vw.at(i, b + 1))
            if i is not None:
                dve.wait_ge(sg["pv_done"].sem, sg["pv_done"].at(i, 4 * b))
            s = 0 if i is None else (b + 1) % 2
            dst, src = vS[:, s, :, :], VB[:, 0:2 * P].rearrange("p (c d) -> p c d", c=2)
            if relu:
                ins = dve.tensor_tensor(dst, src, bc(neg_bv[:, :], 1, 2), ALU.max)
            else:
                ins = dve.tensor_copy(dst, src)
            ins.then_inc(sg["v_read"].sem, 1)

        def turned(i, u):
            dve.wait_ge(sg["probs_T_written"].sem, sg["probs_T_written"].at(i, u + 1))
            dve.wait_ge(sg["pv_done"].sem, sg["pv_done"].at(i, max(u - 1, 0)))
            dve.tensor_copy(pT[:, u % 2, :], T[u % 2][:, 0:2 * P]).then_inc(sg["probs_T_read"].sem, 1)

        neg_bv = shared["neg_bv"]
        norm.dve_stats(dve, chain, None)
        if wq is not None:
            chain.link(dve.tensor_scalar(neg_bv[:, :], bv_row[:, :], -1.0, None, ALU.mult))
        prep(None)
        v_out(None, 0)
        with dve.Fori(0, TILES) as i:
            chain.round(i)
            for u in range(16):
                dve.wait_ge(sg["scores_written"].sem, sg["scores_written"].at(i, u + 1))
                dve.tensor_reduce(negm[:, u:u + 1], S[u % 2][:, 0:KEYS], X_AXIS, ALU.max, negate=True
                                  ).then_inc(sg["max_ready"].sem, 1)
                if u >= 2:
                    turned(i, u - 2)
                if u == 2:
                    norm.dve_stats(dve, chain, i)
                if u % 4 == 2:
                    v_out(i, u // 4)
                if u == 11:
                    dve.wait_ge(misc.w.sem, misc.w.at(i, 1))
                    if relu:
                        ins = dve.tensor_tensor(vl[0:16, :], M[0:16, 0:P], neg_bv[0:16, :], ALU.max)
                    else:
                        ins = dve.tensor_copy(vl[0:16, :], M[0:16, 0:P])
                    ins.then_inc(misc.r.sem, 1)
                    dve.wait_ge(misc.r.sem, misc.r.at(i, 1))
                    dve.wait_ge(sg["last_key_added"].sem, sg["last_key_added"].at(i, 0))
                    chain.link(dve.tensor_tensor(
                        vlbd[0:16, :].rearrange("p (b t d) -> p b t d", b=NB, t=4),
                        bc(vl[0:16, :].rearrange("p (t d) -> p t d", t=4), 1, NB),
                        bc(k.c("last_key")[0:16, :].rearrange("p (b t) -> p b t", b=NB), 3, 32), ALU.mult))
            turned(i, 14)
            turned(i, 15)
            dve.wait_ge(misc.w.sem, misc.w.at(i, 2))
            dve.tensor_copy(pl[0:16, :], M[0:16, 0:P]).then_inc(misc.r.sem, 1)
            dve.wait_ge(sg["probs_ready"].sem, sg["probs_ready"].at(i, 16))
            chain.link(dve.reciprocal(rr[:, :], rs[:, :]))
            chain.link(dve.tensor_tensor(w[:, :, :], bc(rr[:, :], 2, 4), bc(k.c("quad"), 1, 16), ALU.mult))
            dve.wait_ge(sg["last_key_added"].sem, sg["last_key_added"].at(i, 1))
            dve.tensor_tensor(om[:, :].rearrange("p (g d) -> p g d", d=8),
                              OB[:, :].rearrange("p (g d) -> p g d", d=8),
                              bc(w[:, :, :].rearrange("p u j -> p (u j)"), 2, 8), ALU.mult
                              ).then_inc(sg["heads_ready"].sem, 1)
            dve.wait_ge(misc.w.sem, misc.w.at(i, 3))
            if wo is not None:
                dve.tensor_scalar(outT[:, :], M[:, 0:P], bv_col[:, 0:1], None, ALU.add).then_inc(misc.r.sem, 1)
                dve.wait_ge(misc.w.sem, misc.w.at(i, 4))
            row = bo if wo is not None else bv_row
            dve.tensor_tensor(tmp[:, :], M[:, 0:P], row[:, :], ALU.add).then_inc(misc.r.sem, 1)
            dve.wait_ge(misc.r.sem, misc.r.at(i, 2 + last))
            x = k.X[:, i, :]
            if wo is not None and relu:
                chain.link(dve.scalar_tensor_tensor(out=x, in0=tmp[:, :], scalar=0.0, in1=x, op0=ALU.max, op1=ALU.add))
            else:
                chain.link(dve.tensor_tensor(x, x, tmp[:, :], ALU.add))
            prep(i)
        chain.i = i
        chain.done()

    return {"sync": sp, "pool": pool, "tensor": pe, "scalar": act, "vector": dve}


def cross_buffers(k):
    return k.scratch({"slots": [P, NB, KEYS], "last_key": [P, NB, 4], "kT": [P, 2, KEYS], "vS": [P, 2, 2, P],
                     "qT": [P, P], "qbd": [P, NB, P], "negm": [P, 16], "pbuf": [P, 16, KEYS], "rs": [P, 16],
                     "rr": [P, 16], "w": [P, 16, 4], "pT": [P, 2, 2 * P], "pl": [P, P], "vl": [P, P],
                     "vlbd": [P, 512], "om": [P, 512], "outT": [P, P], "tmp": [P, P], "neg_bv": [P, P]})


def window(k, b):
    return k.c("query_window")[:, 32 * (3 - b):32 * (7 - b)]


def self_buffers(k, kind):
    if kind == "L0":
        more = {"feature": [P, 2, 1024], "am": [P, 16, P], "vz": [P, 16 * P], "feature_w": [P, 2, 1024],
                "head_proj": [P, 1024], "feature_bias": [P, 16], "den": [P, P], "proj_rows": [P, 64]}
    else:
        more = {"kT": [P, 2, P], "qbd": [P, 2, 512], "v": [P, 256], "vm": [P, 2, 512],
                "pr": [P, 512], "pT": [P, 512], "nm": [P, 16], "rs": [P, 16], "rr": [P, 16], "w": [P, 16, 4],
                "om": [P, 2, 512], "lat": [64, P], "qkv": [P, 192], "ra": [P, 160], "rb": [P, 160],
                "ms": [P, 20], "r": [P, 20], "kvx": [P, 256], "sq": [P, 2, P], "bd": [P, P], "abd": [P, 512],
                "D": [P, 512], "E": [P, 512], "sD": [P, 512], "sDE": [P, 512], "R": [P, 512]}
    return k.scratch({"qT": [P, 2, P], "outT": [P, 2, P], "tmp": [P, P], **more})


CAP = 50.0


def self_attention(k, kind, s):
    norm = Norm(k)
    first = 3
    misc = Misc(k, 5, first, 7)
    nt = 2 if kind == "L1" else 4
    hd = 32 if kind == "L1" else 8
    M, O = k.bank[7], k.bank[5:7]
    chain_c = k.sig("vector_step").stage(*{"L1": (10, 4), "L2": (14, 10), "L3": (23, 11)}[kind])
    sg = {n: k.sig(n).stage(per, f) for n, (per, f) in {
        "scores_written": (1, 0), "scores_read": (1, 0), "probs_ready": (1, 0), "probs_T_written": (1, 0),
        "probs_T_read": (1, 0), "pv_done": (1, 0), "heads_ready": (1, 0),
        **({} if kind == "L1" else {"q_ready": (1, 1), "weights_ready": (1, 0)}),
        **({"square_ready": (1, 1), "rms_ready": (1, 1)} if kind == "L2" else {}),
    }.items()}
    weights = sg["probs_ready" if kind == "L1" else "weights_ready"]
    if kind == "L1":
        wq, wd, wku, wvu = (k.load(n, sh) for n, sh in (("L1_attn_Wq", [P, 256]), ("L1_attn_Wkv_down", [P, 64]),
                                                        ("L1_attn_Wk_up", [64, 256]), ("L1_attn_Wv_up", [64, 256])))
        wo = k.load("L1_attn_Wo", [P, 2, P])
    elif kind == "L2":
        wqkv, wo = k.load("L2_attn_qkv", [P, 192]), k.load("L2_attn_w_o", [P, P])
    else:
        wq, wk, wv, wo = (k.load(f"L3_attn_W{n}", [P, P]) for n in "qkvo")
    at = norm.count

    def pool(pool):
        def rms(i):
            if kind == "L2":
                pool.wait_ge(sg["square_ready"].sem, at(sg["square_ready"], i))
                pool.tensor_tensor(s["r"][:, :], s["ms"][:, :], k.minus_half[:, 0:20], ALU.pow
                                   ).then_inc(sg["rms_ready"].sem, 1)
        norm.pool(pool, None)
        rms(None)
        with pool.Fori(0, TILES) as i:
            norm.pool(pool, i)
            rms(i)

    def pe(pe):
        def prep(i):
            m = 0 if i is None else 2

            def turn_of(n):
                pe.wait_ge(misc.r.sem, misc.v(misc.r, i, m + n))

            pe.wait_ge(norm.xn.sem, at(norm.xn, i))
            turn_of(0)
            pe.transpose(M[:, 0:P], k.xn[:, :], k.c("ident")).then_inc(misc.w.sem, 1)
            turn_of(1)
            if kind == "L1":
                for t in range(2):
                    pe.matmul(M[:, t * P:(t + 1) * P], wq[:, t * P:(t + 1) * P], k.xnT[:, :], start=True, stop=True,
                              skip_group_check=True)
                pe.matmul(M[0:64, 256:384], wd[:, :], k.xnT[:, :], start=True, stop=True, skip_group_check=True
                          ).then_inc(misc.w.sem, 1)
                turn_of(2)
                for t in range(2):
                    pe.matmul(M[:, t * P:(t + 1) * P], wku[:, t * P:(t + 1) * P], s["lat"][:, :], start=True, stop=True,
                              skip_group_check=True)
                pe.matmul(M[:, 256:512], s["lat"][:, :], wvu[:, :], start=True, stop=True, skip_group_check=True
                          ).then_inc(misc.w.sem, 1)
            elif kind == "L2":
                pe.matmul(M[:, 0:192], k.xnT[:, :], wqkv[:, :], start=True, stop=True).then_inc(misc.w.sem, 1)
                turn_of(2)
                pe.wait_ge(sg["q_ready"].sem, at(sg["q_ready"], i))
                pe.transpose(M[:, 0:P], s["qkv"][:, 0:P], k.c("ident"))
                pe.transpose(M[:, P:2 * P], s["kvx"][:, 0:P], k.c("ident")).then_inc(misc.w.sem, 1)
            else:
                for n, (l, r) in enumerate(((wq, k.xnT), (wk, k.xnT), (k.xnT, wv))):
                    mm = pe.matmul(M[:, n * P:(n + 1) * P], l[:, :], r[:, :], start=True, stop=True,
                                   skip_group_check=True)
                mm.then_inc(misc.w.sem, 1)
                turn_of(2)
                pe.wait_ge(sg["q_ready"].sem, at(sg["q_ready"], i))
                for n in range(2):
                    mm = pe.matmul(M[:, n * P:(n + 1) * P], k.c("same_head"), s["sq"][:, n, :], start=True, stop=True,
                                   skip_group_check=True)
                mm.then_inc(misc.w.sem, 1)

        prep(None)
        with pe.Fori(0, TILES) as i:
            pe.wait_ge(misc.r.sem, misc.r.at(i, 0))
            pe.wait_ge(sg["scores_read"].sem, sg["scores_read"].at(i, 0))
            for t in range(nt):
                q = slice(0, P) if kind == "L1" else slice(32 * t, 32 * t + 32)
                for b in range(NB):
                    kt = t if kind == "L1" else 0
                    rhs = s["kT"][q, kt, 32 * b:32 * b + 32]
                    mm = pe.matmul(k.bank[t][:, 32 * b:32 * b + 32], s["qbd"][q, kt, b * P:(b + 1) * P], rhs,
                                   start=True, stop=(kind != "L3"), skip_group_check=True)
                    if kind == "L3":
                        cols = slice(32 * b, 32 * b + 32)
                        pe.matmul(k.bank[t][:, cols], s["abd"][q, b * P:(b + 1) * P], k.c("ones")[q, 0:32],
                                  start=False, stop=False, skip_group_check=True)
                        pe.matmul(k.bank[t][:, cols], s["qbd"][q, 1, b * P:(b + 1) * P], s["kT"][q, 1, cols],
                                  start=False, stop=True, skip_group_check=True)
                        mm = pe.matmul(k.bank[t][:, P + 32 * b:P + 32 * b + 32], s["om"][q, 1, b * P:(b + 1) * P],
                                       s["bd"][q, cols], start=True, stop=True, skip_group_check=True)
            mm.then_inc(sg["scores_written"].sem, 1)
            pe.wait_ge(weights.sem, weights.at(i, 1))
            for t in range(nt):
                mm = pe.transpose(k.bank[4][:, t * P:(t + 1) * P], s["pr"][:, t * P:(t + 1) * P], k.c("ident"))
            mm.then_inc(sg["probs_T_written"].sem, 1)
            pe.wait_ge(sg["probs_T_read"].sem, sg["probs_T_read"].at(i, 1))
            for t in range(nt):
                if kind == "L1":
                    mm = pe.matmul(O[t][:, :], s["pT"][:, t * P:(t + 1) * P], s["vm"][:, t, :], start=True, stop=True)
                else:
                    mm = pe.matmul(O[0].rearrange("p (b t d) -> p b t d", b=NB, t=4)[:, :, t, :],
                                   s["pT"][:, t * P:(t + 1) * P],
                                   s["vm"][:, 0, :].rearrange("p (b t d) -> p b t d", b=NB, t=4)[:, :, t, :],
                                   start=(t == 0), stop=True, skip_group_check=True)
            mm.then_inc(sg["pv_done"].sem, 1)
            pe.wait_ge(sg["heads_ready"].sem, sg["heads_ready"].at(i, 1))
            pe.wait_ge(misc.r.sem, misc.r.at(i, 0))
            for t in range(2 if kind == "L1" else 1):
                for b in range(NB):
                    mm = pe.matmul(M[:, t * P:(t + 1) * P], s["om"][:, t, b * P:(b + 1) * P], window(k, b),
                                   start=(b == 0 and t == 0), stop=(b == NB - 1), skip_group_check=True)
            mm.then_inc(misc.w.sem, 1)
            pe.wait_ge(misc.r.sem, misc.r.at(i, 1))
            if kind == "L1":
                for t in range(2):
                    mm = pe.matmul(M[:, 0:P], s["outT"][:, t, :], wo[:, t, :], start=(t == 0), stop=(t == 1))
            else:
                mm = pe.matmul(M[:, 0:P], s["outT"][:, 0, :], wo[:, :], start=True, stop=True)
            mm.then_inc(misc.w.sem, 1)
            prep(i)

    def act(act):
        with act.Fori(0, TILES) as i:
            if kind == "L1":
                act.wait_ge(sg["scores_read"].sem, sg["scores_read"].at(i, 1))
                act.activation(s["pr"][:, 0:256], s["pr"][:, 0:256], ACT.Exp).then_inc(sg["probs_ready"].sem, 1)
            elif kind == "L2":
                act.wait_ge(sg["scores_written"].sem, sg["scores_written"].at(i, 1))
                act.wait_ge(sg["weights_ready"].sem, sg["weights_ready"].at(i, 0))
                act.activation(s["D"][:, :].rearrange("p (t c) -> p t c", t=4), k.psum[:, 0:4, 0:P], ACT.Tanh,
                               scale=float(1.0 / (CAP * np.sqrt(8.0)))).then_inc(sg["scores_read"].sem, 1)
                act.wait_ge(sg["scores_read"].sem, sg["scores_read"].at(i, 1))
                act.activation(s["E"][:, :], s["D"][:, :], ACT.Exp, scale=CAP).then_inc(sg["probs_ready"].sem, 1)
            else:
                act.wait_ge(sg["scores_read"].sem, sg["scores_read"].at(i, 1))
                act.activation(s["sD"][:, :], s["D"][:, :], ACT.Sqrt)
                act.activation(s["sDE"][:, :], s["sDE"][:, :], ACT.Sqrt).then_inc(sg["probs_ready"].sem, 1)

    def dve(dve):
        chain = Chain(dve, chain_c)
        link = chain.link

        def rows_by_head(dst, src, mask):
            return dve.tensor_tensor(dst.rearrange("p (b j q) -> p b j q", b=NB, j=4),
                                     bc(src.rearrange("p (b q) -> p b q", b=NB), 2, 4),
                                     bc(bc(mask, 1, NB), 3, SEQ), ALU.mult)

        def by_batch(dst, src):
            return dve.tensor_tensor(dst.rearrange("p (b d) -> p b d", b=NB), bc(src, 1, NB), bc(k.c("quad"), 2, P),
                                     ALU.mult)

        def prep(i):
            m = 0 if i is None else 2

            def written(n):
                dve.wait_ge(misc.w.sem, misc.v(misc.w, i, m + n))

            def read(n):
                dve.wait_ge(misc.r.sem, misc.v(misc.r, i, m + n))

            norm.dve_apply(dve, i)
            written(1)
            dve.tensor_copy(k.xnT[:, :], M[:, 0:P]).then_inc(misc.r.sem, 1)
            written(2)
            if kind == "L1":
                link(dve.tensor_copy(s["qT"][:, :, :], M[:, 0:256].rearrange("p (t c) -> p t c", t=2)))
                dve.tensor_copy(s["lat"][:, :], M[0:64, 256:384]).then_inc(misc.r.sem, 1)
                link(rows_by_head(s["qbd"][:, 0, :], s["qT"][:, 0, :], k.c("quad_scaled")))
                link(rows_by_head(s["qbd"][:, 1, :], s["qT"][:, 1, :], k.c("quad_scaled")))
                written(3)
                dve.tensor_copy(s["v"][:, :], M[:, 256:512])
                dve.tensor_copy(s["kT"][:, :, :], M[:, 0:256].rearrange("p (t c) -> p t c", t=2)
                                ).then_inc(misc.r.sem, 1)
                read(3)
            elif kind == "L2":
                qk = s["qkv"][:, 0:160]
                dve.tensor_copy(s["qkv"][:, :], M[:, 0:192]).then_inc(misc.r.sem, 1)
                read(2)
                link(dve.tensor_tensor(s["ra"][:, :], qk, qk, ALU.mult))
                link(dve.tensor_reduce(s["ms"][:, :], s["ra"][:, :].rearrange("p (h d) -> p h d", d=8), X_AXIS, ALU.add))
                dve.tensor_scalar(s["ms"][:, :], s["ms"][:, :], 0.125, 1e-5, ALU.mult, ALU.add
                                  ).then_inc(sg["square_ready"].sem, 1)
                dve.wait_ge(sg["rms_ready"].sem, at(sg["rms_ready"], i))
                heads = qk.rearrange("p (h d) -> p h d", d=8)
                link(dve.tensor_tensor(heads, heads, bc(s["r"][:, :], 2, 8), ALU.mult))
                halves = qk.rearrange("p (h d) -> p h d", d=4)
                for dst, c in (("ra", "cos"), ("rb", "sin")):
                    link(dve.tensor_tensor(s[dst][:, :].rearrange("p (h d) -> p h d", d=4), halves, bc(k.c(c), 1, 40),
                                           ALU.mult))
                a, b, o = (x.rearrange("p (h e d) -> p h e d", e=2, d=4) for x in (s["ra"][:, :], s["rb"][:, :], qk))
                link(dve.tensor_tensor(o[:, :, 0, :], a[:, :, 0, :], b[:, :, 1, :], ALU.subtract))
                link(dve.tensor_tensor(o[:, :, 1, :], a[:, :, 1, :], b[:, :, 0, :], ALU.add))
                dve.tensor_copy(s["kvx"][:, :].rearrange("p (t j d) -> p t j d", t=8, j=4),
                                bc(s["qkv"][:, P:192].rearrange("p (t d) -> p t d", d=8), 2, 4)
                                ).then_inc(sg["q_ready"].sem, 1)
                dve.wait_ge(sg["q_ready"].sem, at(sg["q_ready"], i))
                written(3)
                link(dve.tensor_copy(s["qT"][:, 0, :], M[:, 0:P]))
                link(rows_by_head(s["qbd"][:, 0, :], s["qT"][:, 0, :], k.c("lane")))
                dve.tensor_copy(s["kT"][:, 0, :], M[:, P:2 * P]).then_inc(misc.r.sem, 1)
                read(3)
            else:
                qkv = s["qkv"]
                link(dve.tensor_copy(s["qT"][:, 0, :], M[:, 0:P]))
                link(dve.tensor_copy(s["kT"][:, 0, :], M[:, P:2 * P]))
                dve.tensor_copy(s["v"][:, 0:P], M[:, 2 * P:3 * P]).then_inc(misc.r.sem, 1)
                link(dve.tensor_tensor(s["sq"][:, 0, :], s["qT"][:, 0, :], s["qT"][:, 0, :], ALU.mult))
                dve.tensor_tensor(s["sq"][:, 1, :], s["kT"][:, 0, :], s["kT"][:, 0, :], ALU.mult
                                  ).then_inc(sg["q_ready"].sem, 1)
                link(dve.tensor_scalar(s["tmp"][:, :], s["qT"][:, 0, :], -2.0, None, ALU.mult))
                link(rows_by_head(s["qbd"][:, 0, :], s["tmp"][:, :], k.c("lane")))
                written(3)
                link(dve.tensor_scalar(s["tmp"][:, :], M[:, 0:P], -1.0, 1.0, ALU.mult, ALU.add))
                link(rows_by_head(s["om"][:, 1, :], s["tmp"][:, :], k.c("lane_eighth")))
                link(rows_by_head(s["abd"][:, :], s["sq"][:, 0, :], k.c("lane")))
                link(dve.tensor_copy(s["kT"][:, 1, :], s["sq"][:, 1, :]))
                dve.tensor_scalar(s["bd"][:, :], M[:, P:2 * P], -1.0, 1.0, ALU.mult, ALU.add).then_inc(misc.r.sem, 1)
                read(3)

        def weights_done(i):
            n = 4 * nt
            link(dve.tensor_reduce(s["rs"][:, 0:n], s["pr"][:, 0:nt * P].rearrange("p (u c) -> p u c", c=32), X_AXIS,
                                   ALU.add))
            link(dve.reciprocal(s["rr"][:, 0:n], s["rs"][:, 0:n]))
            rr = s["rr"][:, 0:n]
            if kind == "L1":
                link(dve.tensor_tensor(s["w"][:, 0:n, :], bc(rr, 2, 4), bc(k.c("quad"), 1, n), ALU.mult))
            else:
                link(dve.tensor_tensor(s["w"][:, :, :].rearrange("p (b t) j -> p b t j", t=4),
                                       bc(rr.rearrange("p (t b) -> p b t", b=NB), 3, 4),
                                       bc(bc(k.c("quad"), 1, 4), 1, NB), ALU.mult))

        norm.dve_stats(dve, chain, None)
        if kind == "L3":
            link(dve.tensor_copy(s["qbd"][:, 1, :].rearrange("p (b j q) -> p b j q", b=NB, j=4),
                                 bc(bc(k.c("lane"), 1, NB), 3, SEQ)))
        prep(None)
        with dve.Fori(0, TILES) as i:
            chain.round(i)
            norm.dve_stats(dve, chain, i)
            vsrc = s["kvx"][:, P:2 * P] if kind == "L2" else s["v"][:, 0:P]
            dve.wait_ge(sg["pv_done"].sem, sg["pv_done"].at(i, 0))
            link(by_batch(s["vm"][:, 0, :], vsrc))
            if kind == "L1":
                link(by_batch(s["vm"][:, 1, :], s["v"][:, P:2 * P]))
            dve.wait_ge(sg["scores_written"].sem, sg["scores_written"].at(i, 1))
            if kind == "L1":
                sc = k.psum[:, 0:2, 0:P].rearrange("p t (b c) -> p t b c", c=32)
                nm = s["nm"][:, 0:8]
                link(dve.tensor_reduce(nm.rearrange("p (t b) -> p t b", t=2), sc, X_AXIS, ALU.max, negate=True))
                pr = s["pr"][:, 0:256]
                dve.tensor_tensor(pr.rearrange("p (t b c) -> p t b c", t=2, c=32), sc,
                                  bc(nm.rearrange("p (t b) -> p t b", t=2), 3, 32), ALU.add
                                  ).then_inc(sg["scores_read"].sem, 1)
                dve.wait_ge(sg["probs_ready"].sem, sg["probs_ready"].at(i, 1))
            elif kind == "L2":
                dve.wait_ge(sg["probs_ready"].sem, sg["probs_ready"].at(i, 1))
                dve.tensor_tensor(s["pr"][:, :].rearrange("p (u c) -> p u c", c=32),
                                  s["E"][:, :].rearrange("p (u c) -> p u c", c=32), bc(k.c("causal"), 1, 16),
                                  ALU.mult).then_inc(weights.sem, 1)
            else:
                def flat(n):
                    return s[n][:, :]

                def grouped(n):
                    return s[n][:, :].rearrange("p (t c) -> p t c", t=4)

                link(dve.tensor_scalar(grouped("D"), k.psum[:, 0:4, 0:P], 0.0, None, ALU.max))
                link(dve.tensor_scalar(grouped("E"), k.psum[:, 0:4, P:2 * P], 1e-6, None, ALU.max))
                dve.tensor_tensor(flat("sDE"), flat("D"), flat("E"), ALU.add).then_inc(sg["scores_read"].sem, 1)
                link(dve.scalar_tensor_tensor(out=flat("R"), in0=flat("D"), scalar=2.0, in1=flat("E"),
                                              op0=ALU.mult, op1=ALU.add))
                dve.wait_ge(sg["probs_ready"].sem, sg["probs_ready"].at(i, 1))
                link(dve.tensor_tensor(flat("sD"), flat("sD"), flat("sDE"), ALU.mult))
                link(dve.scalar_tensor_tensor(out=flat("R"), in0=flat("sD"), scalar=2.0, in1=flat("R"),
                                              op0=ALU.mult, op1=ALU.add))
                link(dve.reciprocal(flat("R"), flat("R")))
                link(dve.tensor_tensor(flat("R"), flat("R"), flat("E"), ALU.mult))
                rows = s["R"][:, :].rearrange("p (u c) -> p u c", c=32)
                link(dve.tensor_reduce(s["nm"][:, :], rows, X_AXIS, ALU.max))
                link(dve.reciprocal(s["nm"][:, :], s["nm"][:, :]))
                dve.tensor_tensor(s["pr"][:, :].rearrange("p (u c) -> p u c", c=32), rows,
                                  bc(s["nm"][:, :], 2, 32), ALU.mult).then_inc(weights.sem, 1)
            dve.wait_ge(weights.sem, weights.at(i, 1))
            weights_done(i)
            dve.wait_ge(sg["probs_T_written"].sem, sg["probs_T_written"].at(i, 1))
            dve.tensor_copy(s["pT"][:, 0:nt * P], k.bank[4][:, 0:nt * P]).then_inc(sg["probs_T_read"].sem, 1)
            dve.wait_ge(sg["pv_done"].sem, sg["pv_done"].at(i, 1))
            w = s["w"][:, 0:4 * nt, :].rearrange("p u j -> p (u j)")
            for t in range(2 if kind == "L1" else 1):
                n = 16 if kind == "L1" else 64
                ins = dve.tensor_tensor(s["om"][:, t, :].rearrange("p (g d) -> p g d", d=hd),
                                        O[t].rearrange("p (g d) -> p g d", d=hd),
                                        bc(w[:, t * n:(t + 1) * n], 2, hd), ALU.mult)
            ins.then_inc(sg["heads_ready"].sem, 1)
            dve.wait_ge(misc.w.sem, misc.w.at(i, 1))
            n = 2 if kind == "L1" else 1
            dve.tensor_copy(s["outT"][:, 0:n, :], M[:, 0:n * P].rearrange("p (t c) -> p t c", t=n)
                            ).then_inc(misc.r.sem, 1)
            dve.wait_ge(misc.w.sem, misc.w.at(i, 2))
            x = k.X[:, i, :]
            dve.tensor_tensor(x, x, M[:, 0:P], ALU.add).then_inc(misc.r.sem, 1)
            dve.wait_ge(misc.r.sem, misc.r.at(i, 2))
            prep(i)
        chain.i = i
        chain.done()

    return {"sync": lambda sp: None, "pool": pool, "tensor": pe, "scalar": act, "vector": dve}


def null_key_attention(k):
    norm = Norm(k, twice=True)
    misc = Misc(k, 3, 2, 7)
    W = KEYS + 1
    a = k.scratch({
        "G": [P, 16, P], "N": [P, 16, P], "wqT": [P, 8, P], "wkT": [P, 8, P], "wvT": [P, 8, P], "wo": [P, 8, P],
        "p": [P, 4, W], "slots": [P, NB, KEYS], "d": [P, KEYS], "sq": [P, KEYS], "ve": [P, KEYS], "zT": [P, 2, KEYS],
        "zk": [P, 2, 2 * P], "zl": [1, 2, P], "pT": [P, 2, 2 * P], "pTl": [1, 2, P], "null_left": [P, 4 * P],
        "null_value": [P, 4, P], "row": [P, P], "U": [P, 16], "rhsU": [P, 8, 16], "kb": [P, 8], "vb": [P, 8],
        "negm": [P, 16], "rs": [P, 16], "rr": [P, 16], "pn": [P, 16], "ns": [P, 16], "nsr": [P, 64], "batch": [P, 1],
        "xs_row": [P, P], "xb_row": [P, P], "cs_row": [P, P], "cb_row": [P, P], "y": [P, P], "y2": [P, P], "cols": [P, 6]})
    qa = k.area[:, 4096:4096 + 2048].rearrange("p (t c) -> p t c", t=4)
    pc = k.area[:, 6144:6144 + 2048].rearrange("p (h c) -> p h c", h=16)
    xrep = a["null_left"]
    setup = a["p"].rearrange("p u c -> p (u c)")[:, 0:1024].rearrange("p (c m) -> p c m", c=8)
    bias, sel, mask = k.mask_bias, k.batch_select, k.mask_in
    for name, dst in (("wqT", a["wqT"]), ("wkT", a["wkT"]), ("wvT", a["wvT"]), ("wo", a["wo"]), ("cols", a["cols"]),
                      ("mask", mask)):
        k.loads.append((k.stage_no, dst, k.dram["L0_xattn_" + name]))
    for name, dst in (("lno_s", a["xs_row"]), ("lno_b", a["xb_row"]), ("lnc_s", a["cs_row"]), ("lnc_b", a["cb_row"])):
        k.loads.append((k.stage_no, dst, k.dram["L0_xattn_" + name].partition_broadcast(P)))
    col = {n: a["cols"][:, c:c + 1] for c, n in enumerate(("x_scale", "x_bias", "c_scale", "null_key", "null_value"))}
    S, T, Z, PC, M = k.bank[0:2], k.bank[2:4], k.bank[4], k.bank[5:7], k.bank[7]
    ctxT = k.dram["ctxT"]
    chain_c = k.sig("vector_step").stage(X0_STEPS, X0_FIRST)
    sg = {n: k.sig(n).stage(per, first) for n, (per, first) in {
        **{f"slot{b}_loaded": (16, 16) for b in range(NB)}, "slot_freed": (NB, 0), "setup_written": (0, 4),
        "setup_read": (0, 5), "mean_written": (NB, 1), "centred": (NB, 1), "squared": (NB, 1), "var_written": (NB, 1),
        "var_read": (NB, 1), "z_rstd": (NB, 1), "zT_ready": (NB, 1), "z_turned": (NB, 1), "z_read": (NB, 1),
        "scores_written": (16, 0), "max_ready": (16, 0), "exp_ready": (16, 0), "probs_ready": (16, 0),
        "probs_T_written": (16, 0), "probs_T_read": (16, 0), "pv_done": (16, 0), "pc_read": (NB, 0),
        "qa_written": (4, 4), "qa_read": (4, 4), "null_ready": (1, 1), "null_left_ready": (1, 0),
        "out_var_ready": (1, 0), "out_rstd_ready": (1, 0), "out_pool_step": (1, 0),
    }.items()}

    def batch(c, i, b):
        return c.before(1) if i is None else c.at(i, b + 1)

    def sp(sp):
        for b in range(NB):
            sp.dma_start(a["slots"][:, b, :], ctxT[b]).then_inc(sg[f"slot{b}_loaded"].sem, 16)
        with sp.Fori(0, TILES) as i:
            for b in range(NB):
                sp.wait_ge(sg["centred"].sem, sg["centred"].at(i, b))
                sp.sem_inc(sg["slot_freed"].sem, 1)
                sp.dma_start(a["slots"][:, b, :], ctxT[i * NB + (NB + b)]).then_inc(sg[f"slot{b}_loaded"].sem, 16)
        for b in range(NB):
            sp.wait_ge(sg[f"slot{b}_loaded"].sem, sg[f"slot{b}_loaded"].at(TILES - 1, 16))

    def pool(pool):
        def squares(i, b):
            pool.wait_ge(sg["centred"].sem, batch(sg["centred"], i, b))
            pool.tensor_tensor(a["sq"], a["d"], a["d"], ALU.mult).then_inc(sg["squared"].sem, 1)

        def rstd(i, b):
            pool.wait_ge(sg["var_read"].sem, batch(sg["var_read"], i, b))
            pool.tensor_tensor(a["ve"], a["ve"], k.minus_half[:, 0:1].to_broadcast([P, KEYS]), ALU.pow
                               ).then_inc(sg["z_rstd"].sem, 1)

        norm.pool(pool, None)
        squares(None, 0)
        rstd(None, 0)
        with pool.Fori(0, TILES) as i:
            for b in range(NB):
                squares(i, b)
                rstd(i, b)
                if b == 1:
                    norm.pool(pool, i)
            ov, os, orr = sg["out_var_ready"], sg["out_pool_step"], sg["out_rstd_ready"]
            pool.wait_ge(ov.sem, ov.at(i, 1))
            pool.tensor_tensor(k.vareps[:, :], k.out_meanvar[:, 1:2], k.ln_eps6[:, :], ALU.add).then_inc(os.sem, 1)
            pool.wait_ge(os.sem, os.at(i, 1))
            pool.tensor_tensor(k.rstd_second[:, :], k.vareps[:, :], k.minus_half[:, 0:1], ALU.pow).then_inc(orr.sem, 1)

    def pe(pe):
        def setup_turn(n):
            pe.wait_ge(sg["setup_read"].sem, sg["setup_read"].before(n))

        def per_head(left, right):
            for odd in range(2):
                rows = slice(64 * odd, 64 * odd + 64)
                for c in range(8):
                    mm = pe.matmul(k.bank[2 * odd + c // 4][:, (c % 4) * P:(c % 4 + 1) * P], left[rows, c, :],
                                   right[rows, c, :], start=True, stop=True, skip_group_check=True)
            mm.then_inc(sg["setup_written"].sem, 1)

        def prep(i):
            m = 0 if i is None else 1
            pe.wait_ge(norm.xn.sem, norm.count(norm.xn, i))
            pe.wait_ge(misc.r.sem, misc.v(misc.r, i, m))
            pe.transpose(M[:, 0:P], k.xn[:, :], k.c("ident")).then_inc(misc.w.sem, 1)
            pe.wait_ge(misc.r.sem, misc.v(misc.r, i, m + 1))
            for b in range(NB):
                mm = pe.matmul(M[:, 16 * b:16 * b + 16], xrep[:, b * P:(b + 1) * P], a["U"][:, :], start=True,
                               stop=True, skip_group_check=True)
            mm.then_inc(misc.w.sem, 1)
            for t in range(4):
                qr = sg["qa_read"]
                pe.wait_ge(qr.sem, (qr.before(max(t - 1, 0)) if i is None else qr.at(i, max(t - 1, 0))))
                if i is not None and t == 0:
                    pe.wait_ge(sg["exp_ready"].sem, sg["exp_ready"].at(i, 16))
                for j in range(4):
                    mm = pe.matmul(S[t % 2][:, j * P:(j + 1) * P], a["G"][:, 4 * t + j, :], k.xnT[:, :],
                                   start=True, stop=True, skip_group_check=True)
                mm.then_inc(sg["qa_written"].sem, 1)

        def slot(b):
            return 0 if b is None else (b + 1) % NB

        def mean(i, b):
            s = slot(b)
            loaded = sg[f"slot{s}_loaded"]
            pe.wait_ge(loaded.sem, loaded.before(16) if i is None else loaded.at(i, 16 if s == 0 else 0))
            if i is not None:
                pe.wait_ge(sg["z_read"].sem, sg["z_read"].at(i, b))
            pe.matmul(Z[:, 0:KEYS], k.c("mean_of"), a["slots"][:, s, :], start=True, stop=True
                      ).then_inc(sg["mean_written"].sem, 1)

        def variance(i, b):
            pe.wait_ge(sg["squared"].sem, batch(sg["squared"], i, b))
            pe.matmul(Z[:, 0:KEYS], k.c("mean_of"), a["sq"], start=True, stop=True).then_inc(sg["var_written"].sem, 1)

        def z_turn(i, b):
            s = 0 if i is None else (b + 1) % 2
            pe.wait_ge(sg["zT_ready"].sem, batch(sg["zT_ready"], i, b))
            pe.transpose(Z[:, 0:P], a["zT"][:, s, 0:P], k.c("ident"))
            pe.transpose(Z[:, P:2 * P], a["zT"][:, s, P:2 * P], k.c("ident"))
            pe.transpose(Z[0:1, 2 * P:3 * P], a["zT"][:, s, 2 * P:KEYS], k.c("ident")).then_inc(sg["z_turned"].sem, 1)

        def scores(i, u):
            b, t = divmod(u, 4)
            if u == 0:
                pe.wait_ge(sg["qa_read"].sem, sg["qa_read"].at(i, 0))
                pe.wait_ge(sg["null_ready"].sem, sg["null_ready"].at(i, 0))
            if t == 0:
                pe.wait_ge(sg["zT_ready"].sem, sg["zT_ready"].at(i, b))
            pe.wait_ge(sg["exp_ready"].sem, sg["exp_ready"].at(i, u - 1))
            pe.matmul(S[u % 2][:, 0:KEYS], qa[:, t, b * P:(b + 1) * P], a["zT"][:, b % 2, :], start=True, stop=False,
                      skip_group_check=True)
            pe.matmul(S[u % 2][:, 0:KEYS], sel[:, b, :], bias[:, :], start=False, stop=True, skip_group_check=True)
            pe.matmul(S[u % 2][:, KEYS:W], k.c("ident"), a["ns"][:, u:u + 1], start=True, stop=True,
                      skip_group_check=True).then_inc(sg["scores_written"].sem, 1)

        def turn(i, u):
            pe.wait_ge(sg["probs_ready"].sem, sg["probs_ready"].at(i, u + 1))
            pe.wait_ge(sg["probs_T_read"].sem, sg["probs_T_read"].at(i, u - 1))
            pe.transpose(T[u % 2][:, 0:P], a["p"][:, u % 4, 0:P], k.c("ident"))
            pe.transpose(T[u % 2][:, P:2 * P], a["p"][:, u % 4, P:2 * P], k.c("ident"))
            pe.transpose(T[u % 2][0:1, 2 * P:3 * P], a["p"][:, u % 4, 2 * P:KEYS], k.c("ident")
                         ).then_inc(sg["probs_T_written"].sem, 1)

        def values(i, u):
            b, t = divmod(u, 4)
            if t == 0:
                pe.wait_ge(sg["z_read"].sem, sg["z_read"].at(i, b))
                pe.wait_ge(sg["pc_read"].sem, sg["pc_read"].at(i, b - 1))
            pe.wait_ge(sg["probs_T_read"].sem, sg["probs_T_read"].at(i, u + 1))
            out = PC[b % 2][:, t * P:(t + 1) * P]
            for c in range(2):
                pe.matmul(out, a["zk"][:, b % 2, c * P:(c + 1) * P], a["pT"][:, u % 2, c * P:(c + 1) * P],
                          start=(c == 0), stop=False, skip_group_check=True)
            pe.matmul(out, a["zl"][:, b % 2, :], a["pTl"][:, u % 2, :], start=False, stop=True, skip_group_check=True
                      ).then_inc(sg["pv_done"].sem, 1)

        per_head(a["wvT"], a["wo"])
        setup_turn(2)
        per_head(a["wqT"], a["wkT"])
        setup_turn(3)
        for c in range(8):
            pe.matmul(k.bank[0][:, 0:16], a["wqT"][:, c, :], a["rhsU"][:, c, :], start=(c == 0), stop=(c == 7))
        for t in range(4):
            for cc in range(2):
                mm = pe.matmul(k.bank[1][:, t * P:(t + 1) * P], setup[:, 2 * t + cc, :], a["wo"][:, 2 * t + cc, :],
                               start=(cc == 0), stop=(cc == 1), skip_group_check=True)
        mm.then_inc(sg["setup_written"].sem, 1)
        setup_turn(4)
        for c in range(8):
            mm = pe.matmul(k.bank[2][:, 0:P], setup[:, c, :], a["wo"][:, c, :], start=(c == 0), stop=(c == 7))
        mm.then_inc(sg["setup_written"].sem, 1)
        setup_turn(5)
        prep(None)
        mean(None, None)
        variance(None, None)
        z_turn(None, None)
        with pe.Fori(0, TILES) as i:
            for u in range(16):
                b, t = divmod(u, 4)
                scores(i, u)
                if t == 0:
                    mean(i, b)
                if t == 1:
                    variance(i, b)
                if t == 3:
                    z_turn(i, b)
                if u >= 2:
                    turn(i, u - 2)
                if u >= 3:
                    values(i, u - 3)
            turn(i, 14)
            values(i, 13)
            turn(i, 15)
            values(i, 14)
            values(i, 15)
            pe.wait_ge(sg["pc_read"].sem, sg["pc_read"].at(i, 4))
            pe.wait_ge(sg["null_left_ready"].sem, sg["null_left_ready"].at(i, 1))
            pe.wait_ge(misc.r.sem, misc.r.at(i, 0))
            for h in range(16):
                pe.matmul(M[:, 0:P], pc[:, h, :], a["N"][:, h, :], start=(h == 0), stop=False)
            for t in range(4):
                mm = pe.matmul(M[:, 0:P], a["null_left"][:, t * P:(t + 1) * P], a["null_value"][:, t, :],
                               start=False, stop=(t == 3))
            mm.then_inc(misc.w.sem, 1)
            prep(i)

    def act(act):
        def queries(i):
            for t in range(4):
                qw = sg["qa_written"]
                act.wait_ge(qw.sem, qw.before(t + 1) if i is None else qw.at(i, t + 1))
                act.activation(qa[:, t, :].rearrange("p (b j q) -> p b j q", b=NB, j=4),
                               S[t % 2].rearrange("p (j b q) -> p b j q", j=4, b=NB), ACT.Copy
                               ).then_inc(sg["qa_read"].sem, 1)

        def z_out(i, b):
            s = 0 if i is None else (b + 1) % 2
            act.wait_ge(sg["z_turned"].sem, batch(sg["z_turned"], i, b))
            if i is not None:
                act.wait_ge(sg["pv_done"].sem, sg["pv_done"].at(i, 4 * b))
            act.activation(a["zk"][:, s, :], Z[:, 0:2 * P], ACT.Copy)
            act.activation(a["zl"][:, s, :], Z[0:1, 2 * P:3 * P], ACT.Copy).then_inc(sg["z_read"].sem, 1)

        def turned(i, u):
            act.wait_ge(sg["probs_T_written"].sem, sg["probs_T_written"].at(i, u + 1))
            act.wait_ge(sg["pv_done"].sem, sg["pv_done"].at(i, u - 1))
            act.activation(a["pT"][:, u % 2, :], T[u % 2][:, 0:2 * P], ACT.Copy)
            act.activation(a["pTl"][:, u % 2, :], T[u % 2][0:1, 2 * P:3 * P], ACT.Copy
                           ).then_inc(sg["probs_T_read"].sem, 1)

        queries(None)
        z_out(None, 0)
        with act.Fori(0, TILES) as i:
            for u in range(16):
                b, t = divmod(u, 4)
                act.wait_ge(sg["max_ready"].sem, sg["max_ready"].at(i, u + 1))
                act.wait_ge(sg["probs_T_written"].sem, sg["probs_T_written"].at(i, u - 3))
                act.activation(a["p"][:, u % 4, :], S[u % 2][:, 0:W], ACT.Exp, bias=a["negm"][:, u:u + 1],
                               accum_out=a["rs"][:, u:u + 1]).then_inc(sg["exp_ready"].sem, 1)
                if t == 3:
                    z_out(i, b)
                if u >= 2:
                    turned(i, u - 2)
            turned(i, 14)
            turned(i, 15)
            queries(i)

    def dve(dve):
        chain = Chain(dve, chain_c)
        link = chain.link

        def centre(i, b):
            s = 0 if i is None else (b + 1) % NB
            dve.wait_ge(sg["mean_written"].sem, batch(sg["mean_written"], i, b))
            dve.tensor_tensor(a["d"], a["slots"][:, s, :], Z[:, 0:KEYS], ALU.subtract).then_inc(sg["centred"].sem, 1)

        def var_out(i, b):
            dve.wait_ge(sg["var_written"].sem, batch(sg["var_written"], i, b))
            dve.tensor_scalar(a["ve"], Z[:, 0:KEYS], 1e-6, None, ALU.add).then_inc(sg["var_read"].sem, 1)

        def z(i, b):
            s = 0 if i is None else (b + 1) % 2
            dve.wait_ge(sg["z_rstd"].sem, batch(sg["z_rstd"], i, b))
            if i is not None:
                dve.wait_ge(sg["scores_written"].sem, sg["scores_written"].at(i, 4 * b))
            dve.tensor_tensor(a["zT"][:, s, :], a["d"], a["ve"], ALU.mult).then_inc(sg["zT_ready"].sem, 1)

        def prep(i):
            m = 0 if i is None else 1
            norm.dve_apply(dve, i)
            dve.wait_ge(misc.w.sem, misc.v(misc.w, i, m + 1))
            link(dve.tensor_scalar(k.xnT[:, :], M[:, 0:P], col["x_scale"], col["x_bias"], ALU.mult, ALU.add))
            dve.tensor_copy(xrep[:, :].rearrange("p (b j q) -> p b j q", b=NB, j=4),
                            bc(k.xnT[:, :].rearrange("p (b q) -> p b q", b=NB), 2, 4)).then_inc(misc.r.sem, 1)
            dve.wait_ge(misc.w.sem, misc.v(misc.w, i, m + 2))
            dve.tensor_tensor(a["nsr"][:, :].rearrange("p (u j) -> p u j", j=4),
                              M[:, 0:64].rearrange("p (u j) -> p u j", j=4), bc(k.c("quad"), 1, 16), ALU.mult
                              ).then_inc(misc.r.sem, 1)
            dve.wait_ge(misc.r.sem, misc.v(misc.r, i, m + 2))
            link(dve.tensor_reduce(a["ns"][:, :], a["nsr"][:, :].rearrange("p (u j) -> p u j", j=4), X_AXIS, ALU.add))
            if i is not None:
                link(dve.tensor_scalar(a["batch"][:, :], a["batch"][:, :], -float(NB), None, ALU.add))
            dve.tensor_tensor(sel[:, :, :], bc(k.c("expert_no")[:, 0:NB], 2, P),
                              bc(a["batch"][:, 0:1].to_broadcast([P, NB]), 2, P), ALU.is_equal
                              ).then_inc(sg["null_ready"].sem, 1)

        def normalise(i, u):
            dve.wait_ge(sg["exp_ready"].sem, sg["exp_ready"].at(i, u + 1))
            link(dve.reciprocal(a["rr"][:, u:u + 1], a["rs"][:, u:u + 1]))
            dve.tensor_tensor(a["pn"][:, u:u + 1], a["p"][:, u % 4, KEYS:W], a["rr"][:, u:u + 1], ALU.mult)
            dve.tensor_scalar(a["p"][:, u % 4, 0:KEYS], a["p"][:, u % 4, 0:KEYS], a["rr"][:, u:u + 1], None, ALU.mult
                              ).then_inc(sg["probs_ready"].sem, 1)

        def gather(i, b):
            dve.wait_ge(sg["pv_done"].sem, sg["pv_done"].at(i, 4 * b + 4))
            dve.tensor_copy(pc[:, :, 32 * b:32 * b + 32], PC[b % 2].rearrange("p (h q) -> p h q", h=16)
                            ).then_inc(sg["pc_read"].sem, 1)

        def heads(n):
            return k.psum[:, 2 * n:2 * n + 2, :].rearrange("p a (c m) -> p a c m", m=P)

        def of_heads(t, n):
            return t.rearrange("p (a c o) m -> p o a c m", o=2, a=2)[:, n]

        norm.dve_stats(dve, chain, None)
        for src, dst in (("wkT", "kb"), ("wvT", "vb")):
            link(dve.tensor_tensor(setup, a[src], bc(a["cb_row"], 1, 8), ALU.mult))
            link(dve.tensor_reduce(a[dst], setup, X_AXIS, ALU.add))
        link(dve.tensor_scalar(a["kb"], a["kb"], col["null_key"], -1.0, ALU.subtract, ALU.mult))
        link(dve.tensor_scalar(a["nsr"][:, 0:8], a["vb"], col["null_value"], -1.0, ALU.subtract, ALU.mult))
        link(dve.tensor_tensor(a["rhsU"], bc(a["kb"], 2, 16), k.c("pair_head").rearrange("p (c h) -> p c h", c=8),
                               ALU.mult))
        for c in range(8):
            link(dve.tensor_tensor(setup[:, c, :].rearrange("p (j q) -> p j q", j=4),
                                   a["nsr"][:, c:c + 1].unsqueeze(2).to_broadcast([P, 4, 32]),
                                   bc(k.c("pair_in_group")[:, 4 * (c % 2):4 * (c % 2) + 4], 2, 32), ALU.mult))
        link(dve.tensor_scalar(bias[:, :], mask[:, :], -1.0, 1e30, ALU.add, ALU.mult))
        dve.tensor_copy(a["batch"][:, :], k.c("row_no")).then_inc(sg["setup_read"].sem, 1)
        dve.wait_ge(sg["setup_written"].sem, sg["setup_written"].before(1))
        for n in range(2):
            link(dve.tensor_scalar(of_heads(a["N"], n), heads(n), col["c_scale"], None, ALU.mult))
        dve.memset(k.carrier[:, :], 0.0).then_inc(sg["setup_read"].sem, 1)
        dve.wait_ge(sg["setup_written"].sem, sg["setup_written"].before(2))
        for n in range(2):
            for h in range(2):
                link(dve.scalar_tensor_tensor(out=of_heads(a["G"], n)[:, h], in0=heads(n)[:, h], scalar=0.25,
                                              in1=bc(a["cs_row"], 1, 4), op0=ALU.mult, op1=ALU.mult))
        dve.memset(k.carrier[:, :], 0.0).then_inc(sg["setup_read"].sem, 1)
        dve.wait_ge(sg["setup_written"].sem, sg["setup_written"].before(3))
        link(dve.tensor_scalar(a["U"], k.bank[0][:, 0:16], 0.25, None, ALU.mult))
        link(dve.tensor_copy(a["null_value"], k.bank[1].rearrange("p (t c) -> p t c", t=4)))
        dve.tensor_copy(setup, bc(a["vb"], 2, P)).then_inc(sg["setup_read"].sem, 1)
        dve.wait_ge(sg["setup_written"].sem, sg["setup_written"].before(4))
        dve.tensor_copy(a["row"], k.bank[2][:, 0:P]).then_inc(sg["setup_read"].sem, 1)
        prep(None)
        centre(None, 0)
        var_out(None, 0)
        z(None, 0)
        with dve.Fori(0, TILES) as i:
            chain.round(i)
            for u in range(16):
                b, t = divmod(u, 4)
                dve.wait_ge(sg["scores_written"].sem, sg["scores_written"].at(i, u + 1))
                dve.tensor_reduce(a["negm"][:, u:u + 1], S[u % 2][:, 0:W], X_AXIS, ALU.max, negate=True
                                  ).then_inc(sg["max_ready"].sem, 1)
                if t == 0:
                    centre(i, b)
                if t == 2:
                    var_out(i, b)
                if t == 3:
                    z(i, b)
                if u >= 1:
                    normalise(i, u - 1)
                if u == 2:
                    norm.dve_stats(dve, chain, i)
                if t == 3 and b >= 1:
                    gather(i, b - 1)
            normalise(i, 15)
            dve.wait_ge(sg["probs_ready"].sem, sg["probs_ready"].at(i, 16))
            for t in range(4):
                ins = dve.tensor_tensor(a["null_left"][:, t * P:(t + 1) * P].rearrange("p (b q) -> p b q", b=NB),
                                        bc(a["pn"][:, :].rearrange("p (b t) -> p b t", t=4)[:, :, t], 2, 32),
                                        bc(k.c("query"), 1, NB), ALU.mult)
            ins.then_inc(sg["null_left_ready"].sem, 1)
            gather(i, 3)
            dve.wait_ge(misc.w.sem, misc.w.at(i, 1))
            dve.tensor_tensor(a["y"], M[:, 0:P], a["row"], ALU.add).then_inc(misc.r.sem, 1)
            dve.wait_ge(misc.r.sem, misc.r.at(i, 1))
            link(dve.bn_stats(k.stat[:, :], a["y"]))
            dve.memset(k.carrier[:, :], 0.0)
            dve.bn_aggr(k.out_meanvar[:, :], k.stat[:, :]).then_inc(sg["out_var_ready"].sem, 1)
            dve.wait_ge(sg["out_rstd_ready"].sem, sg["out_rstd_ready"].at(i, 1))
            link(dve.tensor_scalar(a["y"], a["y"], k.out_meanvar[:, 0:1], k.rstd_second[:, 0:1], ALU.subtract, ALU.mult))
            link(dve.tensor_tensor(a["y"], a["y"], a["xs_row"], ALU.mult))
            link(dve.tensor_tensor(a["y"], a["y"], a["xb_row"], ALU.add))
            x = k.X[:, i, :]
            link(dve.tensor_tensor(x, x, a["y"], ALU.add))
            prep(i)
        chain.i = i
        chain.done()

    return {"sync": sp, "pool": pool, "tensor": pe, "scalar": act, "vector": dve}


def linear_attention(k, s):
    norm = Norm(k)
    misc = Misc(k, 3, 2, 7)
    heads, chunks = 16, 8
    chain_c = k.sig("vector_step").stage(4, 5)
    sg = {n: k.sig(n).stage(per, first) for n, (per, first) in {
        "proj_ready": (0, 1), "feature_w_written": (0, 1), "feature_w_read": (0, 1), "features_written": (1, 0),
        "q_features_ready": (1, 0), "k_features_ready": (1, 0), "products_written": (2, 0), "masked": (2, 0),
        "pv_done": (1, 0), "heads_ready": (1, 0),
    }.items()}
    wqkv = k.load("L0_attn_qkv", [P, 2, P])
    wv, wo = k.load("L0_attn_v", [P, P]), k.load("L0_attn_out", [P, P])
    proj, bqk = k.load("L0_attn_proj", [P, 64]), k.load("L0_attn_bqk", [P, 2])
    bv, bo = k.rows("L0_attn_bv", P), k.rows("L0_attn_bout", P)
    M, O = k.bank[7], k.bank[6]

    def cols(n):
        return slice(n * P, (n + 1) * P)

    def product_bank(h):
        n = h // 2
        return k.bank[(4 if h % 2 == 0 else 0) + n // 4][:, cols(n % 4)]

    def pool(pool):
        norm.pool(pool, None)
        with pool.Fori(0, TILES) as i:
            norm.pool(pool, i)

    def pe(pe):
        def prep(i):
            pe.wait_ge(norm.xn.sem, norm.count(norm.xn, i))
            pe.wait_ge(misc.r.sem, misc.v(misc.r, i, 0))
            pe.transpose(M[:, 0:P], k.xn[:, :], k.c("ident")).then_inc(misc.w.sem, 1)
            pe.wait_ge(misc.r.sem, misc.v(misc.r, i, 1))
            pe.matmul(M[:, 0:P], k.xnT[:, :], wv[:, :], start=True, stop=True).then_inc(misc.w.sem, 1)

        pe.wait_ge(sg["proj_ready"].sem, sg["proj_ready"].before(1))
        for n in range(2):
            for h in range(2):
                pe.matmul(k.bank[2 * n + h][:, :], wqkv[:, n, :], s["head_proj"][:, 512 * h:512 * h + 512],
                          start=True, stop=True)
            for c in range(chunks):
                mm = pe.matmul(k.bank[4][:, 8 * n + c:8 * n + c + 1], s["head_proj"][:, cols(c)], bqk[:, n:n + 1],
                               start=True, stop=True, skip_group_check=True)
        mm.then_inc(sg["feature_w_written"].sem, 1)
        prep(None)
        pe.wait_ge(sg["feature_w_read"].sem, sg["feature_w_read"].before(1))
        with pe.Fori(0, TILES) as i:
            pe.wait_ge(misc.r.sem, misc.r.at(i, 0))
            pe.wait_ge(sg["masked"].sem, sg["masked"].at(i, 0))
            for n in range(2):
                for c in range(chunks):
                    mm = pe.matmul(k.bank[2 * n + c // 4][:, cols(c % 4)], s["feature_w"][:, n, cols(c)], k.xnT[:, :],
                                   start=True, stop=True, skip_group_check=True)
            mm.then_inc(sg["features_written"].sem, 1)
            pe.wait_ge(sg["q_features_ready"].sem, sg["q_features_ready"].at(i, 1))
            pe.wait_ge(sg["k_features_ready"].sem, sg["k_features_ready"].at(i, 1))
            for odd in range(2):
                rows = slice(64 * odd, 64 * odd + 64)
                for c in range(chunks):
                    mm = pe.matmul(product_bank(2 * c + odd), s["feature"][rows, 1, cols(c)], s["feature"][rows, 0, cols(c)],
                                   start=True, stop=True, skip_group_check=True)
                mm.then_inc(sg["products_written"].sem, 1)
            pe.wait_ge(sg["masked"].sem, sg["masked"].at(i, 2))
            for n in range(2):
                for h in range(heads):
                    if n == 0:
                        left = s["vz"][:, 120 * h + 120:120 * h + 120 + P]
                    else:
                        left = k.c("head_window")[:, 120 - 8 * h:120 - 8 * h + P]
                    mm = pe.matmul(O[:, cols(n)], left, s["am"][:, 8 * (h % 2) + h // 2, :],
                                   start=(h == 0), stop=(h == heads - 1), skip_group_check=True)
            mm.then_inc(sg["pv_done"].sem, 1)
            prep(i)
            pe.wait_ge(sg["heads_ready"].sem, sg["heads_ready"].at(i, 1))
            pe.wait_ge(misc.r.sem, misc.r.at(i, 2))
            pe.matmul(M[:, 0:P], s["outT"][:, 0, :], wo[:, :], start=True, stop=True).then_inc(misc.w.sem, 1)

    def act(act):
        with act.Fori(0, TILES) as i:
            act.wait_ge(sg["features_written"].sem, sg["features_written"].at(i, 1))
            for c in range(chunks):
                ins = act.activation(s["feature"][:, 0, cols(c)], k.bank[c // 4][:, cols(c % 4)], ACT.Relu,
                                     bias=s["feature_bias"][:, c:c + 1])
            ins.then_inc(sg["q_features_ready"].sem, 1)

    def dve(dve):
        chain = Chain(dve, chain_c)
        link = chain.link

        def prep_x(i):
            norm.dve_apply(dve, i)
            dve.wait_ge(misc.w.sem, misc.v(misc.w, i, 1))
            dve.tensor_copy(k.xnT[:, :], M[:, 0:P]).then_inc(misc.r.sem, 1)

        def prep_v(i):
            dve.wait_ge(misc.w.sem, misc.v(misc.w, i, 2))
            dve.tensor_tensor(s["vz"][:, :].rearrange("p (h c) -> p h c", h=heads)[:, :, 120:128],
                              M[:, 0:P].rearrange("p (h d) -> p h d", h=heads),
                              bv[:, :].rearrange("p (h d) -> p h d", h=heads), ALU.add).then_inc(misc.r.sem, 1)

        norm.dve_stats(dve, chain, None)
        dve.tensor_tensor(s["head_proj"][:, :].rearrange("p (h m) -> p h m", h=heads), bc(proj[:, :], 1, heads),
                          bc(k.c("head16"), 2, 64), ALU.mult).then_inc(sg["proj_ready"].sem, 1)
        link(dve.memset(s["vz"][:, :], 0.0))
        dve.wait_ge(sg["feature_w_written"].sem, sg["feature_w_written"].before(1))
        for n in range(2):
            link(dve.tensor_copy(s["feature_w"][:, n, :].rearrange("p (a b) -> p a b", a=2),
                                 k.psum[:, 2 * n:2 * n + 2, :]))
        link(dve.tensor_copy(s["feature_bias"][:, :], k.bank[4][:, 0:16]))
        dve.memset(k.carrier[:, :], 0.0).then_inc(sg["feature_w_read"].sem, 1)
        prep_x(None)
        prep_v(None)
        with dve.Fori(0, TILES) as i:
            chain.round(i)
            norm.dve_stats(dve, chain, i)
            dve.wait_ge(sg["features_written"].sem, sg["features_written"].at(i, 1))
            for c in range(chunks):
                ins = dve.tensor_scalar(s["feature"][:, 1, cols(c)], k.bank[2 + c // 4][:, cols(c % 4)],
                                        s["feature_bias"][:, 8 + c:9 + c], 0.0, ALU.add, ALU.max)
            ins.then_inc(sg["k_features_ready"].sem, 1)
            for odd in range(2):
                dve.wait_ge(sg["products_written"].sem, sg["products_written"].at(i, odd + 1))
                b = 4 if odd == 0 else 0
                dve.tensor_tensor(s["am"][:, 8 * odd:8 * odd + 8, :].rearrange("p (a n) q -> p a n q", a=2),
                                  k.psum[:, b:b + 2, :].rearrange("p a (n q) -> p a n q", q=P),
                                  bc(bc(k.c("causal_T"), 1, 4), 1, 2), ALU.mult).then_inc(sg["masked"].sem, 1)
            prep_x(i)
            dve.wait_ge(sg["pv_done"].sem, sg["pv_done"].at(i, 1))
            prep_v(i)
            link(dve.tensor_scalar(s["den"][:, :], O[:, P:2 * P], 1e-6, None, ALU.add))
            link(dve.reciprocal(s["den"][:, :], s["den"][:, :]))
            dve.tensor_tensor(s["outT"][:, 0, :], O[:, 0:P], s["den"][:, :], ALU.mult).then_inc(sg["heads_ready"].sem, 1)
            dve.wait_ge(misc.w.sem, misc.w.at(i, 3))
            dve.tensor_tensor(s["tmp"][:, :], M[:, 0:P], bo[:, :], ALU.add).then_inc(misc.r.sem, 1)
            dve.wait_ge(misc.r.sem, misc.r.at(i, 3))
            x = k.X[:, i, :]
            link(dve.tensor_tensor(x, x, s["tmp"][:, :], ALU.add))
        chain.i = i
        chain.done()

    return {"sync": lambda sp: None, "pool": pool, "tensor": pe, "scalar": act, "vector": dve}


MOE1_EXPERTS, MOE1_WIDTH, MOE1_TOP = 16, 176, 2
CAPACITY = -(-5 * BATCH * SEQ * MOE1_TOP // (4 * MOE1_EXPERTS))
MOE2_EXPERTS, MOE3_EXPERTS, MOE3_WIDTH = 6, 64, 64


def ffn_buffers(k):
    return {"ix": k.top_at, **k.scratch({
        "H": [P, 4224], "G": [P, 2, 512], "HT": [P, 2, 512], "cw": [P, 64], "lg": [P, 64], "pr": [P, 64],
        "ex": [P, 64], "m8": [P, 8], "ixf": [P, 8], "oh": [P, 2, 16], "sel": [P, P], "acc": [P, P],
        "t": [P, 2, 64], "s1": [P, 1], "s2": [P, 1], "wr": [P, P], "nm": [P, 1]})}


def feed_forward(k, kind, up_w, down_w, fb, router=None, router_b=None):
    norm = Norm(k)
    if kind == "L0":
        groups = [(192, g * 384, g * 192, None) for g in range(2)]
    elif kind == "L1":
        groups = [(176, g * 352, g * 176, g if g < MOE1_EXPERTS else None) for g in range(MOE1_EXPERTS + 1)]
    elif kind == "L2":
        groups = [(128, g * 256, g * 128, g if g < MOE2_EXPERTS else None) for g in range(MOE2_EXPERTS + 1)]
    else:
        groups = [(512, g * 512, g * 512, 8 * g) for g in range(8)] + [(64, 4096, 4096, None)]
    halves = 1 if kind == "L3" else 2
    E = {"L0": 0, "L1": MOE1_EXPERTS, "L2": MOE2_EXPERTS, "L3": MOE3_EXPERTS}[kind]
    hidden = groups[-1][2] + groups[-1][0]
    chunks = -(-hidden // P)
    quads = [list(range(q, min(q + 4, chunks))) for q in range(0, chunks, 4)]
    G, NQ = len(groups), len(quads)

    def group_of(h):
        return max(g for g, x in enumerate(groups) if x[2] <= h)

    last_group = [group_of(min(q[-1] * P + P, hidden) - 1) for q in quads]
    plan, turned, done = [], 0, 0
    for g in range(G + NQ + 1):
        step = []
        if g < G:
            while turned < NQ and last_group[turned] <= g - 2:
                step.append(("turn", turned))
                turned += 1
                if turned - done >= 2:
                    step.append(("down", done))
                    done += 1
        elif turned < NQ:
            step.append(("turn", turned))
            turned += 1
            if turned - done >= 2:
                step.append(("down", done))
                done += 1
        elif done < NQ:
            step.append(("down", done))
            done += 1
        plan.append(step)
    assert turned == NQ and done == NQ

    routed = router is not None
    nmisc = 1 + {"L0": 0, "L1": 2, "L2": 1, "L3": 1}[kind]
    misc = Misc(k, nmisc, nmisc, 7)
    U, T, Y, M = k.bank[0:3], k.bank[3:5], k.bank[5], k.bank[7]
    sg = {n: k.sig(n).stage(per, first) for n, (per, first) in {
        "up_written": (G, 0), "gate_ready": (G, 0), "hidden_ready": (G, 0), "hidden_T_written": (NQ, 0),
        "hidden_T_read": (NQ, 0), "down_used": (NQ, 0), "y_read": (1, 0),
        **({"route_exp": (1, 1)} if routed else {}),
        **({"logits_ready": (1, 1), "selected": (1, 1)} if kind == "L1" else {}),
    }.items()}
    steps = {"L0": 0, "L1": 13, "L2": 11, "L3": 11}[kind]
    chain_c = k.sig("vector_step").stage(steps + 1 + (kind == "L1"),
                                         steps + 1 + {"L0": 2, "L1": 5, "L2": 3, "L3": 3}[kind])
    wdt = I32 if kind == "L0" else F32
    up_n = halves * hidden
    up = k.load(up_w, [P, up_n], dt=wdt)
    down = k.load(down_w, [P, chunks, P], dt=wdt)
    if kind == "L0":
        up_i, down_i = up, down
        up, down = k.sb("up_dequantized", [P, up_n]), k.sb("down_dequantized", [P, chunks, P])
    H, Gt, HT, cw = fb["H"], fb["G"], fb["HT"], fb["cw"]
    if routed:
        rw = k.load(router, [P, E])
        rb = k.rows(router_b, E)

    def pool(pool):
        norm.pool(pool, None)
        with pool.Fori(0, TILES) as i:
            norm.pool(pool, i)

    def pe(pe):
        def prep(i):
            pe.wait_ge(norm.xn.sem, norm.count(norm.xn, i))
            pe.wait_ge(misc.r.sem, misc.v(misc.r, i, 0))
            pe.transpose(M[:, 0:P], k.xn[:, :], k.c("ident")).then_inc(misc.w.sem, 1)
            if routed:
                pe.wait_ge(misc.r.sem, misc.v(misc.r, i, 1))
                pe.matmul(M[:, 0:P], k.xnT[:, :], fb["wr"][:, :], start=True, stop=True).then_inc(misc.w.sem, 1)
            if kind == "L1":
                pe.wait_ge(misc.r.sem, misc.v(misc.r, i, 2))
                pe.wait_ge(sg["selected"].sem, norm.count(sg["selected"], i))
                pe.matmul(M[:, 0:P], k.c("earlier"), fb["sel"][:, :], start=True, stop=False)
                pe.matmul(M[:, 0:P], k.c("ones"), fb["acc"][:, :], start=False, stop=True).then_inc(misc.w.sem, 1)

        def turn(i, q):
            pe.wait_ge(sg["hidden_ready"].sem, sg["hidden_ready"].at(i, last_group[q] + 1))
            pe.wait_ge(sg["hidden_T_read"].sem, sg["hidden_T_read"].at(i, q - 1))
            for j, c in enumerate(quads[q]):
                mm = pe.transpose(T[q % 2][:, j * P:(j + 1) * P], H[:, c * P:(c + 1) * P], k.c("ident"))
            mm.then_inc(sg["hidden_T_written"].sem, 1)

        def downs(i, q):
            pe.wait_ge(sg["hidden_T_read"].sem, sg["hidden_T_read"].at(i, q + 1))
            if q == 0:
                pe.wait_ge(sg["y_read"].sem, sg["y_read"].at(i, 0))
            for j, c in enumerate(quads[q]):
                mm = pe.matmul(Y[:, 0:P], HT[:, q % 2, j * P:(j + 1) * P], down[:, c, :],
                               start=(c == 0), stop=(c == chunks - 1))
            mm.then_inc(sg["down_used"].sem, 1)

        prep(None)
        with pe.Fori(0, TILES) as i:
            pe.wait_ge(misc.r.sem, misc.r.at(i, 0))
            for g, step in enumerate(plan):
                if g < G:
                    fw, c0, _, _ = groups[g]
                    free = sg["hidden_ready"]
                    pe.wait_ge(free.sem, free.at(i, g - 2))
                    pe.matmul(U[g % 3][:, 0:fw * halves], k.xnT[:, :], up[:, c0:c0 + fw * halves],
                              start=True, stop=True).then_inc(sg["up_written"].sem, 1)
                for what, q in step:
                    (turn if what == "turn" else downs)(i, q)
            prep(i)

    def act(act):
        def prep(i):
            if not routed:
                return
            if kind == "L1":
                act.wait_ge(sg["logits_ready"].sem, norm.count(sg["logits_ready"], i))
                ins = act.activation(fb["ex"][:, 0:E], fb["lg"][:, 0:E], ACT.Exp, bias=fb["nm"][:, 0:1],
                                     accum_out=fb["s1"][:, :])
            else:
                act.wait_ge(misc.r.sem, misc.v(misc.r, i, 2))
                src = fb["lg"] if kind == "L2" else fb["pr"]
                ins = act.activation(fb["ex"][:, 0:E], src[:, 0:E], ACT.Exp, scale=-1.0)
            ins.then_inc(sg["route_exp"].sem, 1)

        def out(i, q):
            act.wait_ge(sg["hidden_T_written"].sem, sg["hidden_T_written"].at(i, q + 1))
            act.wait_ge(sg["down_used"].sem, sg["down_used"].at(i, q - 1))
            m = len(quads[q]) * P
            act.activation(HT[:, q % 2, 0:m], T[q % 2][:, 0:m], ACT.Copy).then_inc(sg["hidden_T_read"].sem, 1)

        prep(None)
        with act.Fori(0, TILES) as i:
            for g, step in enumerate(plan):
                if g < G:
                    fw = groups[g][0]
                    act.wait_ge(sg["up_written"].sem, sg["up_written"].at(i, g + 1))
                    act.wait_ge(sg["hidden_ready"].sem, sg["hidden_ready"].at(i, g - 1))
                    act.activation(Gt[:, g % 2, 0:fw], U[g % 3][:, 0:fw], ACT.Silu).then_inc(sg["gate_ready"].sem, 1)
                for what, q in step:
                    if what == "turn":
                        out(i, q)
            prep(i)

    def dve(dve):
        chain = Chain(dve, chain_c)
        lg, pr, ex, m8, ix, ixf, oh = (fb[n] for n in ("lg", "pr", "ex", "m8", "ix", "ixf", "oh"))
        sel, acc, t, s1, s2, nm = (fb[n] for n in ("sel", "acc", "t", "s1", "s2", "nm"))

        def top2(src):
            dve.memset(k.carrier[:, :], 0.0)
            chain.link(dve.max(m8[:, :], src))
            dve.memset(k.carrier[:, :], 0.0)
            chain.link(dve.max_index(ix[:, :], m8[:, :], src))
            chain.link(dve.tensor_copy(ixf[:, :], ix[:, :]))
            chain.link(dve.tensor_tensor(oh[:, :, :], bc(k.c("expert_no"), 1, 2), bc(ixf[:, 0:2], 2, 16), ALU.is_equal))

        def weigh(eps):
            chain.link(dve.tensor_scalar(s2[:, :], m8[:, 0:1], m8[:, 1:2], eps, ALU.add, ALU.add))
            chain.link(dve.reciprocal(s2[:, :], s2[:, :]))
            for j in range(2):
                chain.link(dve.tensor_scalar(t[:, j, 0:E], oh[:, j, 0:E], m8[:, j:j + 1], s2[:, 0:1],
                                             ALU.mult, ALU.mult))

        def route_l1(i):
            misc_r = misc.r
            dve.tensor_tensor(lg[:, 0:E], M[:, 0:E], rb[:, :], ALU.add).then_inc(misc_r.sem, 1)
            dve.wait_ge(misc_r.sem, misc.v(misc_r, i, 2))
            dve.tensor_reduce(nm[:, :], lg[:, 0:E], X_AXIS, ALU.max, negate=True).then_inc(sg["logits_ready"].sem, 1)
            dve.wait_ge(sg["route_exp"].sem, norm.count(sg["route_exp"], i))
            chain.link(dve.reciprocal(s2[:, :], s1[:, :]))
            chain.link(dve.tensor_scalar(pr[:, 0:E], ex[:, 0:E], s2[:, 0:1], None, ALU.mult))
            top2(pr[:, 0:E])
            dve.tensor_tensor(sel[:, 0:E], oh[:, 0, :], oh[:, 1, :], ALU.add).then_inc(sg["selected"].sem, 1)
            weigh(1e-9)
            chain.link(dve.tensor_tensor(lg[:, 0:E], t[:, 0, 0:E], t[:, 1, 0:E], ALU.add))
            dve.wait_ge(misc.w.sem, misc.v(misc.w, i, 3))
            chain.link(dve.tensor_scalar(pr[:, 0:E], M[:, 0:E], float(CAPACITY), None, ALU.is_lt))
            chain.link(dve.tensor_tensor(cw[:, 0:E], lg[:, 0:E], pr[:, 0:E], ALU.mult))
            dve.tensor_tensor(acc[:, 0:E], acc[:, 0:E], sel[:, 0:E], ALU.add).then_inc(misc_r.sem, 1)
            dve.wait_ge(misc_r.sem, misc.v(misc_r, i, 3))

        def route_l2(i):
            dve.tensor_tensor(lg[:, 0:E], M[:, 0:E], rb[:, :], ALU.add).then_inc(misc.r.sem, 1)
            dve.wait_ge(sg["route_exp"].sem, norm.count(sg["route_exp"], i))
            chain.link(dve.tensor_scalar(ex[:, 0:E], ex[:, 0:E], 1.0, None, ALU.add))
            chain.link(dve.reciprocal(pr[:, 0:E], ex[:, 0:E]))
            top2(pr[:, 0:8])
            weigh(1e-8)
            chain.link(dve.tensor_tensor(cw[:, 0:E], t[:, 0, 0:E], t[:, 1, 0:E], ALU.add))

        def route_l3(i):
            dve.tensor_copy(pr[:, 0:E], M[:, 0:E]).then_inc(misc.r.sem, 1)
            dve.wait_ge(misc.r.sem, misc.v(misc.r, i, 2))
            chain.link(dve.tensor_tensor(lg[:, 0:E], pr[:, 0:E], rb[:, :], ALU.add))
            dve.memset(k.carrier[:, :], 0.0)
            chain.link(dve.max(m8[:, :], lg[:, 0:E]))
            dve.memset(k.carrier[:, :], 0.0)
            chain.link(dve.match_replace(t[:, 0, :], m8[:, :], lg[:, 0:E], NEG_BIG))
            chain.link(dve.tensor_tensor(t[:, 1, :], t[:, 0, :], lg[:, 0:E], ALU.not_equal))
            dve.wait_ge(sg["route_exp"].sem, norm.count(sg["route_exp"], i))
            chain.link(dve.tensor_scalar(ex[:, 0:E], ex[:, 0:E], 1.0, None, ALU.add))
            chain.link(dve.reciprocal(lg[:, 0:E], ex[:, 0:E]))
            chain.link(dve.tensor_tensor(t[:, 0, :], lg[:, 0:E], t[:, 1, :], ALU.mult))
            chain.link(dve.tensor_reduce(s1[:, :], t[:, 0, :], X_AXIS, ALU.add))
            chain.link(dve.tensor_scalar(s2[:, :], s1[:, :], 1e-8, None, ALU.add))
            chain.link(dve.reciprocal(s2[:, :], s2[:, :]))
            chain.link(dve.tensor_scalar(cw[:, 0:E], t[:, 0, :], s2[:, 0:1], None, ALU.mult))

        def prep(i):
            norm.dve_apply(dve, i)
            dve.wait_ge(misc.w.sem, misc.v(misc.w, i, 1))
            dve.tensor_copy(k.xnT[:, :], M[:, 0:P]).then_inc(misc.r.sem, 1)
            if routed:
                dve.wait_ge(misc.w.sem, misc.v(misc.w, i, 2))
                {"L1": route_l1, "L2": route_l2, "L3": route_l3}[kind](i)

        norm.dve_stats(dve, chain, None)
        if kind == "L0":
            for dst, src in ((up, up_i), (down, down_i)):
                full = (slice(None),) * len(dst.shape)
                chain.link(dve.tensor_scalar(dst[full], src[full], float(np.float32(1.0 / 127.0)), None, ALU.mult))
        else:
            chain.link(dve.memset(fb["wr"][:, :], 0.0))
            chain.link(dve.tensor_copy(fb["wr"][:, 0:E], rw[:, :]))
        if kind == "L1":
            chain.link(dve.memset(sel[:, :], 0.0))
            chain.link(dve.memset(acc[:, :], 0.0))
        if kind == "L2":
            chain.link(dve.memset(pr[:, 0:8], -1.0))
        if hidden < chunks * P:
            chain.link(dve.memset(H[:, hidden:chunks * P], 0.0))
        prep(None)
        with dve.Fori(0, TILES) as i:
            chain.round(i)
            x = k.X[:, i, :]
            if kind == "L1":
                chain.link(dve.tensor_tensor(x, x, k.xn[:, :], ALU.add))
            dve.wait_ge(sg["hidden_T_written"].sem, sg["hidden_T_written"].at(i, 0))
            for g, (fw, c0, h0, e) in enumerate(groups):
                if kind != "L3":
                    dve.wait_ge(sg["up_written"].sem, sg["up_written"].at(i, g + 1))
                dve.wait_ge(sg["gate_ready"].sem, sg["gate_ready"].at(i, g + 1))
                h, gate = H[:, h0:h0 + fw], Gt[:, g % 2, 0:fw]
                if kind != "L3":
                    ins = dve.scalar_tensor_tensor(out=h, in0=gate, scalar=1.0 if e is None else cw[:, e:e + 1],
                                                   in1=U[g % 3][:, fw:2 * fw], op0=ALU.mult, op1=ALU.mult)
                elif e is not None:
                    ins = dve.tensor_tensor(h.rearrange("p (e f) -> p e f", f=MOE3_WIDTH),
                                            gate.rearrange("p (e f) -> p e f", f=MOE3_WIDTH),
                                            bc(cw[:, e:e + 8], 2, MOE3_WIDTH), ALU.mult)
                else:
                    ins = dve.tensor_copy(h, gate)
                ins.then_inc(sg["hidden_ready"].sem, 1)
                if g == 1:
                    norm.dve_stats(dve, chain, i)
            dve.wait_ge(sg["down_used"].sem, sg["down_used"].at(i, NQ))
            dve.tensor_tensor(x, x, Y[:, 0:P], ALU.add).then_inc(sg["y_read"].sem, 1)
            prep(i)
        chain.i = i
        chain.done()

    return {"sync": lambda sp: None, "pool": pool, "tensor": pe, "scalar": act, "vector": dve}


NEG_BIG = -3.0e38


STAGES = ["L0_xattn", "L0_attn", "L0_ffn", "L1_xattn", "L1_attn", "L1_ffn", "L2_xattn", "L2_attn", "L2_ffn", "L3_xattn", "L3_attn", "L3_ffn"]


def perceiver(nc, dram, out):
    with ExitStack() as ctx:
        k = Core(nc, ctx, dram)
        shared = cross_buffers(k)
        fb = ffn_buffers(k)
        stages = []
        for n, name in enumerate(STAGES):
            k.stage_no = n
            if name == "L1_xattn":
                stages.append(cross_attention(k, "L1x", "L1_xattn_Wq", "L1_xattn_bq", "L1_xattn_Wk", "L1_xattn_bk",
                                              "L1_xattn_Wv", "L1_xattn_bv", "L1_xattn_Wo", "L1_xattn_bo", True, shared))
            if name == "L0_xattn":
                stages.append(null_key_attention(k))
            if name == "L0_attn":
                stages.append(linear_attention(k, self_buffers(k, "L0")))
            if name in ("L1_attn", "L2_attn", "L3_attn"):
                stages.append(self_attention(k, name[:2], self_buffers(k, name[:2])))
            if name == "L0_ffn":
                stages.append(feed_forward(k, "L0", "L0_ffn_up", "L0_ffn_down", fb))
            if name == "L1_ffn":
                stages.append(feed_forward(k, "L1", "L1_ffn_up", "L1_ffn_down", fb, "L1_ffn_router_w", "L1_ffn_router_b"))
            if name == "L2_ffn":
                stages.append(feed_forward(k, "L2", "L2_ffn_up", "L2_ffn_down", fb, "L2_ffn_gate_w", "L2_ffn_gate_b"))
            if name == "L3_ffn":
                stages.append(feed_forward(k, "L3", "L3_ffn_up", "L3_ffn_down", fb, "L3_ffn_centroids", "L3_ffn_expert_biases"))
            if name == "L2_xattn":
                stages.append(cross_attention(k, "L2x", None, None, "L2_xattn_Wk", "L2_xattn_bk",
                                              "L2_xattn_Wv", "L2_xattn_bv", "L2_xattn_W_o", "L2_xattn_b_o", False, shared))
            if name == "L3_xattn":
                stages.append(cross_attention(k, "L3x", "L3_xattn_wq", "L3_xattn_bq", "L3_xattn_wk", "L3_xattn_bk",
                                              "L3_xattn_wv", "L3_xattn_bv", None, None, False, shared))
        weights = [ctx.enter_context(nc.semaphore(f"weights_in_{n}")) for n in range(len(stages))]
        x_in = ctx.enter_context(nc.semaphore("x_in"))
        primed = ctx.enter_context(nc.semaphore("primed"))
        stage_done = ctx.enter_context(nc.semaphore("stage_done"))
        stored = ctx.enter_context(nc.semaphore("stored"))
        counts = [16 * sum(1 for l in k.loads if l[0] == n) for n in range(len(stages))]
        block = ctx.enter_context(nc.Block())

        def start(eng):
            eng.wait_ge(x_in, 32)
            eng.wait_ge(primed, 1)

        def run(eng, which):
            for n, st in enumerate(stages):
                if counts[n]:
                    eng.wait_ge(weights[n], counts[n])
                st[which](eng)
                eng.drain().then_inc(stage_done, 1)
                eng.wait_ge(stage_done, ENGINES * (n + 1))

        @block.sync
        def _(sp):
            sp.dma_start(k.X[:, 0:TILES, :], dram["x"]).then_inc(x_in, 16)
            sp.dma_start(k.const[:, :], dram["const"]).then_inc(x_in, 16)
            for n, dst, src in k.loads:
                shape = dst.shape
                sp.dma_start(dst[(slice(None),) * len(shape)], src).then_inc(weights[n], 16)
            start(sp)
            run(sp, "sync")
            sp.dma_start(out, k.X[:, 0:TILES, :]).then_inc(stored, 16)
            sp.wait_ge(stored, 16)

        @block.gpsimd
        def _(pool):
            pool.memset(k.minus_half[:, :], -0.5)
            pool.memset(k.ln_eps[:, :], 1e-5)
            pool.memset(k.ln_eps6[:, :], 1e-6)
            pool.memset(k.zero4[:, :], 0.0)
            pool.memset(k.X[:, TILES, :], 0.0)
            for s in k.signals.values():
                pool.sem_inc(s.sem, s.PRIMED)
            pool.drain().then_inc(primed, 1)
            start(pool)
            run(pool, "pool")

        @block.scalar
        def _(act):
            start(act)
            run(act, "scalar")

        @block.tensor
        def _(pe):
            start(pe)
            run(pe, "tensor")

        @block.vector
        def _(dve):
            start(dve)
            run(dve, "vector")


def lay_out(inputs):
    a = {n: np.asarray(v) for n, v in inputs.items()}
    d = {"const": CONST}
    d["x"] = a["x"].reshape(TILES, P, P).transpose(1, 0, 2)
    ctxT = np.zeros((CTX_PAD, P, KEYS), np.float32)
    ctxT[:BATCH] = a["ctx_1024"].transpose(0, 2, 1)
    d["ctxT"] = ctxT
    for n in ("L1_xattn_Wq", "L1_xattn_bq", "L1_xattn_Wk", "L1_xattn_bk", "L1_xattn_Wv", "L1_xattn_bv", "L1_xattn_Wo",
              "L1_xattn_bo", "L3_xattn_wq", "L3_xattn_bq", "L3_xattn_wk", "L3_xattn_bk", "L3_xattn_wv", "L3_xattn_bv",
              "L2_xattn_W_o", "L2_xattn_b_o"):
        d[n] = a[n]
    kvw = a["L2_xattn_W_kv"].reshape(P, 16, 2, 8)
    kvb = a["L2_xattn_b_kv"].reshape(16, 2, 8)
    d["L2_xattn_Wk"], d["L2_xattn_Wv"] = kvw[:, :, 0].reshape(P, P), kvw[:, :, 1].reshape(P, P)
    d["L2_xattn_bk"], d["L2_xattn_bv"] = kvb[:, 0].reshape(P), kvb[:, 1].reshape(P)
    for n, w in (("Wq", "Wq"), ("Wkv_down", "Wkv_down"), ("Wk_up", "Wk_up"), ("Wv_up", "Wv_up")):
        d["L1_attn_" + n] = a["L1_attn_" + w].T
    d["L1_attn_Wo"] = a["L1_attn_Wo"].T.reshape(2, P, P).transpose(1, 0, 2)
    d["L2_attn_qkv"] = np.concatenate([a["L2_attn_w_q"], a["L2_attn_w_k"], a["L2_attn_w_v"]], 1)
    d["L2_attn_w_o"] = a["L2_attn_w_o"]
    wkv = a["L0_xattn_Wkv"]
    for n, w in (("wqT", a["L0_xattn_Wq"].T), ("wkT", wkv[:, :1024].T), ("wvT", wkv[:, 1024:].T), ("wo", a["L0_xattn_Wo"])):
        d["L0_xattn_" + n] = w.reshape(8, P, P).transpose(1, 0, 2)
    null = [np.concatenate([v, v]) for v in a["L0_xattn_null_kv"]]
    d["L0_xattn_cols"] = np.stack([a["L0_xattn_ln1_s"], a["L0_xattn_ln1_b"], a["L0_xattn_lnc_s"], *null, null[0]], 1)
    d["L0_xattn_mask"] = a["mask_BxS2_bf1"].view(np.uint8)
    for n in ("lno_s", "lno_b", "lnc_s", "lnc_b"):
        d["L0_xattn_" + n] = a["L0_xattn_" + n]
    d["L0_attn_qkv"] = a["L0_attn_Wqkv"][:2 * P].reshape(2, P, P).transpose(1, 0, 2)
    d["L0_attn_v"], d["L0_attn_out"] = a["L0_attn_Wqkv"][2 * P:].T, a["L0_attn_Wout"].T
    d["L0_attn_proj"] = a["L0_attn_proj"].reshape(P, 64)
    d["L0_attn_bqk"] = a["L0_attn_bqkv"][:2 * P].reshape(2, P).T
    d["L0_attn_bv"], d["L0_attn_bout"] = a["L0_attn_bqkv"][2 * P:], a["L0_attn_bout"]
    for n in "qkvo":
        d["L3_attn_W" + n] = a["L3_attn_W" + n].T

    def by_chunk(w):
        n = -(-w.shape[0] // P)
        out = np.zeros((n * P, P), w.dtype)
        out[:w.shape[0]] = w
        return out.reshape(n, P, P).transpose(1, 0, 2)

    g, u = (a[f"L0_ffn_w_{n}"].T.reshape(P, 2, 1, 192) for n in ("gate", "up"))
    d["L0_ffn_up"] = np.concatenate([g, u], 2).reshape(P, -1)
    d["L0_ffn_down"] = by_chunk(a["L0_ffn_w_down"].T)
    g = np.concatenate([a["L1_ffn_w_gate"], a["L1_ffn_sw_gate"][None]])
    u = np.concatenate([a["L1_ffn_w_up"], a["L1_ffn_sw_up"][None]])
    d["L1_ffn_up"] = np.stack([g, u], 2).transpose(1, 0, 2, 3).reshape(P, -1)
    d["L1_ffn_down"] = by_chunk(np.concatenate([a["L1_ffn_w_down"], a["L1_ffn_sw_down"][None]]).reshape(-1, P))
    d["L1_ffn_router_w"], d["L1_ffn_router_b"] = a["L1_ffn_router_w"], a["L1_ffn_router_b"]
    g = np.concatenate([a["L2_ffn_ew1"], a["L2_ffn_fc1"][None]]).transpose(2, 0, 1)
    u = np.concatenate([a["L2_ffn_ew3"], a["L2_ffn_fc2"][None]]).transpose(2, 0, 1)
    d["L2_ffn_up"] = np.stack([g, u], 2).reshape(P, -1)
    d["L2_ffn_down"] = by_chunk(np.concatenate([a["L2_ffn_ew2"], a["L2_ffn_fc3"][None]]).transpose(0, 2, 1).reshape(-1, P))
    d["L2_ffn_gate_w"], d["L2_ffn_gate_b"] = a["L2_ffn_gate_w"].T, a["L2_ffn_gate_b"]
    d["L3_ffn_up"] = np.concatenate([a["L3_ffn_W_up"].transpose(1, 0, 2).reshape(P, -1), a["L3_ffn_Ws_up"]], 1)
    d["L3_ffn_down"] = by_chunk(np.concatenate([a["L3_ffn_W_down"].reshape(-1, P), a["L3_ffn_Ws_down"]]))
    d["L3_ffn_centroids"], d["L3_ffn_expert_biases"] = a["L3_ffn_centroids"].T, a["L3_ffn_expert_biases"]
    return {n: np.ascontiguousarray(v) for n, v in d.items()}


def kernel(**inputs):
    import concourse.bacc as _bacc
    from concourse import mybir as _mybir
    from concourse.bass_utils import run_bass_kernel_spmd as _run

    nc = _bacc.Bacc("TRN2", target_bir_lowering=False, num_devices=1)
    arrays, dram = {}, {}
    for name, v in lay_out(inputs).items():
        arrays[f"in_{name}"] = v
        dram[name] = nc.dram_tensor(f"in_{name}", v.shape, _mybir.dt.from_np(v.dtype), kind="ExternalInput").ap()
    out = nc.dram_tensor("out_0", (P, TILES, P), F32, kind="ExternalOutput").ap()
    perceiver(nc, dram, out)
    r = _run(nc, [arrays], core_ids=[0])
    return np.ascontiguousarray(r.results[0]["out_0"].transpose(1, 0, 2)).reshape(BATCH, SEQ, P)
```

```python
from contextlib import ExitStack

import numpy as np

import concourse.bass as bass
from concourse import mybir

F32 = mybir.dt.float32
BF16 = mybir.dt.bfloat16
U8 = mybir.dt.uint8
U32 = mybir.dt.uint32
I32 = mybir.dt.int32
ALU = mybir.AluOpType
ACT = mybir.ActivationFunctionType
X_AXIS = mybir.AxisListType.X

P = 128
BATCH, SEQ, KEYS = 128, 32, 257
TILES = BATCH * SEQ // P
NB = P // SEQ
CTX_PAD = BATCH + NB
ENGINES = 5


def bc(ap, axis, n):
    u = ap.unsqueeze(axis)
    shape = list(u.shape)
    shape[axis] = n
    return u.to_broadcast(shape)


class Signal:

    PRIMED = 64

    def __init__(self, sem):
        self.sem = sem
        self.count = self.PRIMED

    def stage(self, per, first=0, last=0):
        return Counted(self, per, first, last)


class Counted:

    def __init__(self, signal, per, first, last):
        self.sem, self.base, self.per, self.first, self.last = signal.sem, signal.count, per, first, last
        signal.count += first + per * TILES + last

    def before(self, n):
        return self.base + n

    def at(self, i, n):
        return i * self.per + (self.base + self.first + n)


class Chain:

    def __init__(self, eng, counted):
        self.eng, self.c, self.i, self.n = eng, counted, None, 0

    def round(self, i):
        assert self.i is not None or self.n == self.c.first, self.n
        assert self.i is None or self.n == self.c.per, self.n
        self.i, self.n = i, 0

    def done(self):
        last = self.i is not None and self.i is TILES
        assert self.n == (self.c.last if last else self.c.first if self.i is None else self.c.per), self.n

    def link(self, ins):
        self.n += 1
        ins.then_inc(self.c.sem, 1)
        self.eng.wait_ge(self.c.sem, self.c.before(self.n) if self.i is None else self.c.at(self.i, self.n))


def constants():
    p = np.arange(P)
    cols = {}
    cols["ident"] = np.eye(P)
    cols["lane"] = (p[:, None] % 32) // 8 == np.arange(4)[None]
    cols["lane_scaled"] = cols["lane"] / np.sqrt(8.0)
    cols["lane_eighth"] = cols["lane"] / 8.0
    cols["quad"] = p[:, None] // 32 == np.arange(4)[None]
    cols["query"] = p[:, None] % 32 == np.arange(32)[None]
    cols["earlier"] = p[:, None] < p[None]
    cols["ones"] = np.ones((P, P))
    win = np.zeros((P, 7, 32))
    win[:, 3] = p[:, None] % 32 == np.arange(32)[None]
    cols["query_window"] = win.reshape(P, -1)
    cols["quad_scaled"] = cols["quad"] / np.sqrt(32.0)
    cols["causal"] = np.arange(32)[None] <= p[:, None] % 32
    cols["causal_T"] = (p[:, None] // 32 == p[None] // 32) & (p[:, None] <= p[None])
    cols["same_head"] = p[:, None] // 8 == p[None] // 8
    cols["head16"] = p[:, None] // 8 == np.arange(16)[None]
    win = np.zeros((P, 248))
    win[:, 120:128] = 1
    cols["head_window"] = win
    inv = np.float32(1.0) / np.float32(10000.0) ** (np.arange(0, 8, 2, dtype=np.float32) / np.float32(8))
    freq = (p % SEQ).astype(np.float32)[:, None] * inv[None]
    cols["cos"], cols["sin"] = np.cos(freq), np.sin(freq)
    cols["row_no"] = p[:, None]
    cols["pair_head"] = (np.arange(16)[None, None] == 2 * np.arange(8)[None, :, None] + p[:, None, None] // 64).reshape(P, -1)
    cols["pair_in_group"] = (np.arange(4)[None, None] == 2 * np.arange(2)[None, :, None] + p[:, None, None] // 64).reshape(P, -1)
    cols["mean_of"] = np.full((P, P), 1.0 / P)
    cols["expert_no"] = np.tile(np.arange(16)[None], (P, 1))
    cols["last_key"] = p[:, None] == np.arange(16)[None]
    out, at, parts = {}, 0, []
    for name, a in cols.items():
        out[name] = (at, a.shape[1])
        at += a.shape[1]
        parts.append(np.asarray(a, np.float32))
    return np.ascontiguousarray(np.concatenate(parts, 1)), out


CONST, CONST_AT = constants()


X0_STEPS, X0_FIRST = 25, 27
SCRATCH = 16100


class Core:

    def __init__(self, nc, ctx, dram):
        self.nc, self.ctx, self.dram = nc, ctx, dram
        self.loads = []
        self.stage_no = 0
        self.X_spare = self.sb("x_tokens", [P, TILES + 2, P])
        self.X = self.X_spare[:, 1:TILES + 2, :]
        self.const = self.sb("consts", [P, CONST.shape[1]])
        self.psum = ctx.enter_context(nc.psum_tensor("psum_banks", [P, 8, 512], F32))
        self.bank = [self.psum[:, b, :] for b in range(8)]
        self.stat = self.sb("ln_stat", [P, 6])
        self.meanvar = self.sb("ln_meanvar", [P, 2])
        self.vareps = self.sb("ln_vareps", [P, 1])
        self.rstd = self.sb("ln_rstd", [P, 1])
        self.rstd_first = self.sb("ln_rstd_first", [P, 1])
        self.rstd_second = self.sb("ln_rstd_second", [P, 1])
        self.ln_eps6 = self.sb("ln_eps6", [P, 1])
        self.minus_half = self.sb("minus_half", [P, 32])
        self.ln_eps = self.sb("ln_eps", [P, 1])
        self.xn = self.sb("x_normed", [P, P])
        self.xnT = self.sb("x_normed_T", [P, P])
        self.carrier = self.sb("wait_carrier", [P, 1])
        self.zero4 = self.sb("zero4", [P, 4])
        self.mask_in = self.sb("mask_in", [P, KEYS], U8)
        self.mask_bias = self.sb("mask_bias", [P, KEYS], BF16)
        self.batch_select = self.sb("batch_select", [P, NB, P], BF16)
        self.out_meanvar = self.sb("out_meanvar", [P, 2])
        self.top_at = self.sb("route_top_at", [P, 8], U32)
        self.area = self.sb("scratch", [P, SCRATCH])
        self.signals = {}

    def sb(self, name, shape, dt=F32):
        return self.ctx.enter_context(self.nc.sbuf_tensor(name, shape, dt))

    def scratch(self, shapes):
        out, at = {}, 0
        for name, shape in shapes.items():
            n = int(np.prod(shape[1:]))
            t = self.area[0:shape[0], at:at + n]
            if len(shape) == 3:
                t = t.rearrange("p (a b) -> p a b", a=shape[1])
            if len(shape) == 4:
                t = t.rearrange("p (a b c) -> p a b c", a=shape[1], b=shape[2])
            out[name] = t
            at += n
        assert at <= SCRATCH, at
        return out

    def sig(self, name):
        if name not in self.signals:
            self.signals[name] = Signal(self.ctx.enter_context(self.nc.semaphore(name)))
        return self.signals[name]

    def c(self, name):
        a, n = CONST_AT[name]
        return self.const[:, a:a + n]

    def load(self, name, shape, src=None, dt=F32):
        t = self.sb("w_" + name, shape, dt)
        self.loads.append((self.stage_no, t, self.dram[name] if src is None else src))
        return t

    def rows(self, name, n):
        t = self.sb("r_" + name, [P, n])
        self.loads.append((self.stage_no, t, self.dram[name].partition_broadcast(P)))
        return t

    def column(self, name):
        t = self.sb("c_" + name, [P, 1])
        self.loads.append((self.stage_no, t, self.dram[name].rearrange("(p a) -> p a", a=1)))
        return t


class Norm:

    def __init__(self, k, twice=False):
        self.k, self.twice = k, twice
        self.var = k.sig("ln_var_ready").stage(1, 1)
        self.rs = k.sig("ln_rstd_ready").stage(1, 1)
        self.xn = k.sig("xn_ready").stage(1, 1)
        self.pool_step = k.sig("pool_ln_step").stage(*((6, 6) if twice else (1, 1)))

    @staticmethod
    def count(c, i):
        return c.before(1) if i is None else c.at(i, 1)

    @staticmethod
    def tile(i):
        return 0 if i is None else i + 1

    def dve_stats(self, dve, chain, i):
        k = self.k
        chain.link(dve.bn_stats(k.stat[:, :], k.X[:, self.tile(i), :]))
        dve.memset(k.carrier[:, :], 0.0)
        dve.bn_aggr(k.meanvar[:, :], k.stat[:, :]).then_inc(self.var.sem, 1)

    def pool(self, pool, i):
        k = self.k
        pool.wait_ge(self.var.sem, self.count(self.var, i))
        pool.tensor_tensor(k.vareps[:, :], k.meanvar[:, 1:2], k.ln_eps[:, :], ALU.add).then_inc(self.pool_step.sem, 1)
        c, n = self.pool_step, 1

        def step(out, a, b, op):
            nonlocal n
            pool.wait_ge(c.sem, c.before(n) if i is None else c.at(i, n))
            n += 1
            return pool.tensor_tensor(out[:, :], a, b, op)

        if self.twice:
            v, r1, r2 = k.vareps, k.rstd_first, k.rstd_second
            step(r1, v[:, :], k.minus_half[:, 0:1], ALU.pow).then_inc(c.sem, 1)
            step(v, r1[:, :], r1[:, :], ALU.mult).then_inc(c.sem, 1)
            step(v, v[:, :], k.meanvar[:, 1:2], ALU.mult).then_inc(c.sem, 1)
            step(v, v[:, :], k.ln_eps6[:, :], ALU.add).then_inc(c.sem, 1)
            step(r2, v[:, :], k.minus_half[:, 0:1], ALU.pow).then_inc(c.sem, 1)
            step(k.rstd, r1[:, :], r2[:, :], ALU.mult).then_inc(self.rs.sem, 1)
        else:
            step(k.rstd, k.vareps[:, :], k.minus_half[:, 0:1], ALU.pow).then_inc(self.rs.sem, 1)

    def dve_apply(self, dve, i):
        k = self.k
        dve.wait_ge(self.rs.sem, self.count(self.rs, i))
        dve.tensor_scalar(k.xn[:, :], k.X[:, self.tile(i), :], k.meanvar[:, 0:1], k.rstd[:, 0:1],
                          ALU.subtract, ALU.mult).then_inc(self.xn.sem, 1)


class Misc:

    def __init__(self, k, per, first, bank, last=0):
        self.w = k.sig("misc_written").stage(per, first, last)
        self.r = k.sig("misc_read").stage(per, first, last)
        self.bank = k.bank[bank]

    def v(self, c, i, n):
        return c.before(n) if i is None else c.at(i, n)


def cross_attention(k, name, q_w, q_b, k_w, k_b, v_w, v_b, o_w, o_b, relu, a):
    norm = Norm(k)
    has_q, has_o = q_w is not None, o_w is not None
    finish = 3 + has_o
    misc = Misc(k, finish + 1 + has_q, 1 + has_q, 7, finish)
    S, T, KB, OB, VB, M = k.bank[0:2], k.bank[2:4], k.bank[4], k.bank[5], k.bank[6], k.bank[7]
    sg = {n: k.sig(n).stage(*v) for n, v in {
        **{f"slot{b}_loaded": (16, 16) for b in range(NB)}, "slot_freed": (2 * NB, 0), "last_key_kept": (NB, 0),
        "k_written": (NB, 1), "k_read": (NB, 1), "v_written": (NB, 1), "v_read": (NB, 1), "scores_written": (16, 0),
        "max_ready": (16, 0), "probs_ready": (16, 0), "probs_T_written": (16, 0, 2), "probs_T_read_even": (8, 0, 1), "probs_T_read_odd": (8, 0, 1),
        "pv_done": (16, 0, 3), "heads_read": (NB, 0, 1), "q_ready": (2, 2), "cleared": (0, 1),
    }.items()}
    chain_c = k.sig("vector_step").stage(1 + 3 * NB + 2, 1 + has_q, 4)
    wq = k.load(q_w, [P, P]) if has_q else None
    bq = k.column(q_b) if has_q else None
    wk, bk = k.load(k_w, [P, P]), k.column(k_b)
    wv = k.load(v_w, [P, P])
    bv_col, bv_row = k.column(v_b), k.rows(v_b, P)
    wo = k.load(o_w, [P, P]) if has_o else None
    bo = k.rows(o_b, P) if has_o else None
    slots, last_key, kT, vS, qT, qbd = (a[n] for n in ("slots", "last_key", "kT", "vS", "qT", "qbd"))
    negm, pbuf, rs, rr, w, pT = (a[n] for n in ("negm", "pbuf", "rs", "rr", "w", "pT"))
    last_w, pl, vl, vlbd, om, heads, outT, tmp, neg_bv = (
        a[n] for n in ("last_w", "pl", "vl", "vlbd", "om", "heads", "outT", "tmp", "neg_bv"))
    ctxT = k.dram["ctxT"]
    LAST_WEIGHTS, LAST_KEY, HEADS, OUT, NEXT_X, NEXT_Q = 0, 1, 2, 3, finish, finish + 1

    def at_step(s, back):
        return (s - back) % 16

    def wait_turned(eng, i, s):
        c = sg["probs_T_read_odd" if s % 2 else "probs_T_read_even"]
        eng.wait_ge(c.sem, c.at(i, s // 2 + 1))

    def sp(sp):
        for b in range(NB):
            sp.dma_start(slots[:, b, :], ctxT[b]).then_inc(sg[f"slot{b}_loaded"].sem, 16)
        with sp.Fori(0, TILES) as i:
            for b in range(NB):
                sp.wait_ge(sg["v_written"].sem, sg["v_written"].at(i, b))
                sp.sem_inc(sg["slot_freed"].sem, 1)
                sp.wait_ge(sg["last_key_kept"].sem, sg["last_key_kept"].at(i, b + 1))
                sp.sem_inc(sg["slot_freed"].sem, 1)
                sp.dma_start(slots[:, b, :], ctxT[i * NB + (NB + b)]).then_inc(sg[f"slot{b}_loaded"].sem, 16)
        for b in range(NB):
            sp.wait_ge(sg[f"slot{b}_loaded"].sem, sg[f"slot{b}_loaded"].at(TILES - 1, 16))

    def pool(pool):
        norm.pool(pool, None)
        with pool.Fori(0, TILES) as i:
            pool.wait_ge(misc.w.sem, misc.w.at(i, 0))
            for b in range(NB):
                pool.wait_ge(sg[f"slot{b}_loaded"].sem, sg[f"slot{b}_loaded"].at(i, 0))
                pool.tensor_tensor(last_key[:, b, :], bc(slots[:, b, KEYS - 1], 1, 4), k.zero4[:, :], ALU.add
                                   ).then_inc(sg["last_key_kept"].sem, 1)
            norm.pool(pool, i)

    def pe(pe):
        def my_turn(i, n):
            pe.wait_ge(misc.r.sem, misc.v(misc.r, i, n))

        def kv(i, b):
            s = 0 if i is None else (b + 1) % NB
            loaded = sg[f"slot{s}_loaded"]
            pe.wait_ge(loaded.sem, loaded.before(16) if i is None else loaded.at(i, 16 if s == 0 else 0))
            if i is not None:
                pe.wait_ge(sg["k_read"].sem, sg["k_read"].at(i, b))
            pe.matmul(KB[:, 0:KEYS], wk[:, :], slots[:, s, :], start=True, stop=True
                      ).then_inc(sg["k_written"].sem, 1)
            if i is not None:
                pe.wait_ge(sg["v_read"].sem, sg["v_read"].at(i, b))
            pe.matmul(VB[:, 0:P], slots[:, s, 0:P], wv[:, :], start=True, stop=True)
            pe.matmul(VB[:, P:2 * P], slots[:, s, P:2 * P], wv[:, :], start=True, stop=True
                      ).then_inc(sg["v_written"].sem, 1)

        def scores(i, u):
            b, t = divmod(u, 4)
            if u == 0 or u == 12:
                pe.wait_ge(sg["q_ready"].sem, sg["q_ready"].at(i, -1 if u == 0 else 0))
            if t == 0:
                pe.wait_ge(sg["k_read"].sem, sg["k_read"].at(i, b))
            pe.wait_ge(sg["probs_ready"].sem, sg["probs_ready"].at(i, u - 1))
            q = slice(32 * t, 32 * t + 32)
            pe.matmul(S[u % 2][:, 0:KEYS], qbd[q, b, :], kT[q, b % 2, :], start=True, stop=True
                      ).then_inc(sg["scores_written"].sem, 1)

        def turn(i, s):
            u = at_step(s, 2)
            pe.wait_ge(sg["probs_ready"].sem, sg["probs_ready"].at(i, s - 1))
            wait_turned(pe, i, s - 2)
            pe.transpose(T[u % 2][:, 0:P], pbuf[:, u % 8, 0:P], k.c("ident"))
            pe.transpose(T[u % 2][:, P:2 * P], pbuf[:, u % 8, P:2 * P], k.c("ident")
                         ).then_inc(sg["probs_T_written"].sem, 1)

        def values(i, s):
            u = at_step(s, 3)
            b, t = divmod(u, 4)
            if t == 0:
                pe.wait_ge(sg["v_read"].sem, sg["v_read"].at(i, b))
                pe.wait_ge(sg["heads_read"].sem, sg["heads_read"].at(i, b + 1))
            wait_turned(pe, i, s - 1)
            for c in range(2):
                mm = pe.matmul(OB[:, t * P:(t + 1) * P], pT[:, u % 2, c * P:(c + 1) * P], vS[:, b % 2, c, :],
                               start=(c == 0), stop=(c == 1), skip_group_check=True)
            mm.then_inc(sg["pv_done"].sem, 1)

        def finish_tile(i, s):
            if s == 3:
                my_turn(i, LAST_WEIGHTS)
                pe.wait_ge(sg["heads_read"].sem, sg["heads_read"].at(i, 1))
                pe.transpose(M[0:16, 0:P], last_w[:, :], k.c("ident")).then_inc(misc.w.sem, 1)
            if s == 5:
                my_turn(i, LAST_KEY)
                pe.matmul(M[:, :], pl[0:16, :], vlbd[0:16, :], start=True, stop=True).then_inc(misc.w.sem, 1)
            if s == 7:
                my_turn(i, HEADS)
                if has_o:
                    for b in range(NB):
                        mm = pe.matmul(M[:, 0:P], heads[:, b * P:(b + 1) * P], window(k, b), start=(b == 0),
                                       stop=(b == NB - 1))
                else:
                    for b in range(NB):
                        mm = pe.matmul(M[:, 0:P], window(k, b), heads[:, b * P:(b + 1) * P], start=(b == 0),
                                       stop=(b == NB - 1))
                mm.then_inc(misc.w.sem, 1)
            if s == 9 and has_o:
                my_turn(i, OUT)
                pe.matmul(M[:, 0:P], outT[:, :], wo[:, :], start=True, stop=True).then_inc(misc.w.sem, 1)

        def next_x(i):
            m = 0 if i is None else NEXT_X
            pe.wait_ge(norm.xn.sem, norm.count(norm.xn, i))
            my_turn(i, m)
            if i is not None:
                pe.wait_ge(sg["last_key_kept"].sem, sg["last_key_kept"].at(i, NB))
                pe.matmul(M[0:16, P:2 * P], last_key.rearrange("p b t -> p (b t)"), wv[:, :],
                          start=True, stop=True, skip_group_check=True)
            pe.transpose(M[:, 0:P], k.xn[:, :], k.c("ident")).then_inc(misc.w.sem, 1)

        def next_q(i):
            my_turn(i, 1 if i is None else NEXT_Q)
            pe.matmul(M[:, 0:P], wq[:, :], k.xnT[:, :], start=True, stop=True).then_inc(misc.w.sem, 1)

        pe.wait_ge(sg["cleared"].sem, sg["cleared"].before(1))
        next_x(None)
        if has_q:
            next_q(None)
        kv(None, 0)
        with pe.Fori(0, TILES) as i:
            for s in range(16):
                scores(i, s)
                if s % 4 == 1:
                    kv(i, s // 4)
                turn(i, s)
                values(i, s)
                finish_tile(i, s)
                if s == 11:
                    next_x(i)
                if s == 13 and has_q:
                    next_q(i)
        for s in range(10):
            if s < 2:
                turn(TILES, s)
            if s < 3:
                values(TILES, s)
            finish_tile(TILES, s)

    def act(act):
        def k_out(i, b):
            kw = sg["k_written"]
            act.wait_ge(kw.sem, kw.before(1) if i is None else kw.at(i, b + 1))
            if i is not None:
                act.wait_ge(sg["scores_written"].sem, sg["scores_written"].at(i, 4 * b))
            s = 0 if i is None else (b + 1) % 2
            act.activation(kT[:, s, :], KB[:, 0:KEYS], ACT.Relu if relu else ACT.Identity, bias=bk[:, 0:1]
                           ).then_inc(sg["k_read"].sem, 1)

        def turned(i, s):
            u = at_step(s, 2)
            act.wait_ge(sg["probs_T_written"].sem, sg["probs_T_written"].at(i, s + 1))
            act.wait_ge(sg["pv_done"].sem, sg["pv_done"].at(i, s))
            act.activation(pT[:, u % 2, :], T[u % 2][:, 0:2 * P], ACT.Copy).then_inc(sg["probs_T_read_odd"].sem, 1)

        k_out(None, 0)
        act.wait_ge(sg["cleared"].sem, sg["cleared"].before(1))
        with act.Fori(0, TILES) as i:
            for u in range(16):
                act.wait_ge(sg["max_ready"].sem, sg["max_ready"].at(i, u + 1))
                act.wait_ge(sg["probs_T_written"].sem, sg["probs_T_written"].at(i, u - 5))
                if u % 4 == 0:
                    act.wait_ge(sg["heads_read"].sem, sg["heads_read"].at(i, u // 4))
                act.activation(pbuf[:, u % 8, :], S[u % 2][:, 0:KEYS], ACT.Exp, bias=negm[:, u:u + 1],
                               accum_out=rs[:, u:u + 1]).then_inc(sg["probs_ready"].sem, 1)
                if u % 4 == 1:
                    k_out(i, u // 4)
                if u % 2 == 1:
                    turned(i, u)
        turned(TILES, 1)

    def dve(dve):
        chain = Chain(dve, chain_c)
        link = chain.link

        def written(i, n):
            dve.wait_ge(misc.w.sem, misc.v(misc.w, i, n + 1))

        def spread(i, b0, b1):
            if i is not None:
                dve.wait_ge(sg["scores_written"].sem, sg["scores_written"].at(i, 4 * b1))
            dve.tensor_tensor(qbd[:, b0:b1, :].rearrange("p b (j q) -> p b j q", j=4),
                              bc(qT[:, 32 * b0:32 * b1].rearrange("p (b q) -> p b q", b=b1 - b0), 2, 4),
                              bc(bc(k.c("lane_scaled"), 1, b1 - b0), 3, SEQ), ALU.mult).then_inc(sg["q_ready"].sem, 1)

        def take_x(i):
            m = 0 if i is None else NEXT_X
            written(i, m)
            if i is not None:
                if relu:
                    link(dve.tensor_tensor(vl[0:16, :], M[0:16, P:2 * P], neg_bv[0:16, :], ALU.max))
                else:
                    link(dve.tensor_copy(vl[0:16, :], M[0:16, P:2 * P]))
                dve.tensor_tensor(vlbd[0:16, :].rearrange("p (b t d) -> p b t d", b=NB, t=4),
                                  bc(vl[0:16, :].rearrange("p (t d) -> p t d", t=4), 1, NB),
                                  bc(k.c("last_key")[0:16, :].rearrange("p (b t) -> p b t", b=NB), 3, 32), ALU.mult)
            dve.tensor_copy((k.xnT if has_q else qT)[:, :], M[:, 0:P]).then_inc(misc.r.sem, 1)

        def take_q(i):
            m = 0 if i is None else NEXT_X
            if has_q:
                m += 1
                written(i, m)
                if relu:
                    ins = dve.tensor_scalar(qT[:, :], M[:, 0:P], bq[:, 0:1], 0.0, ALU.add, ALU.max)
                else:
                    ins = dve.tensor_scalar(qT[:, :], M[:, 0:P], bq[:, 0:1], None, ALU.add)
                ins.then_inc(misc.r.sem, 1)
            dve.wait_ge(misc.r.sem, misc.v(misc.r, i, m + 1))
            spread(i, 0, NB - 1)

        def v_out(i, b):
            vw = sg["v_written"]
            dve.wait_ge(vw.sem, vw.before(1) if i is None else vw.at(i, b + 1))
            if i is not None:
                dve.wait_ge(sg["pv_done"].sem, sg["pv_done"].at(i, 4 * b + 3))
            s = 0 if i is None else (b + 1) % 2
            dst, src = vS[:, s, :, :], VB[:, 0:2 * P].rearrange("p (c d) -> p c d", c=2)
            if relu:
                ins = dve.tensor_tensor(dst, src, bc(neg_bv[:, :], 1, 2), ALU.max)
            else:
                ins = dve.tensor_copy(dst, src)
            ins.then_inc(sg["v_read"].sem, 1)

        def turned(i, s):
            u = at_step(s, 2)
            dve.wait_ge(sg["probs_T_written"].sem, sg["probs_T_written"].at(i, s + 1))
            dve.wait_ge(sg["pv_done"].sem, sg["pv_done"].at(i, s))
            dve.tensor_copy(pT[:, u % 2, :], T[u % 2][:, 0:2 * P]).then_inc(sg["probs_T_read_even"].sem, 1)

        def sums_out(i, s):
            b = at_step(s, 6) // 4
            us = slice(4 * b, 4 * b + 4)
            dve.wait_ge(sg["probs_ready"].sem, sg["probs_ready"].at(i, s - 2))
            link(dve.reciprocal(rr[:, us], rs[:, us]))
            link(dve.tensor_tensor(w[:, us, :], bc(rr[:, us], 2, 4), bc(k.c("quad"), 1, 4), ALU.mult))
            link(dve.tensor_tensor(last_w[:, us], pbuf[:, 4 * (b % 2):4 * (b % 2) + 4, KEYS - 1], rr[:, us], ALU.mult))

        def heads_out(i, s):
            b = at_step(s, 7) // 4
            us = slice(4 * b, 4 * b + 4)
            if s == 7:
                dve.wait_ge(misc.r.sem, misc.v(misc.r, i, LAST_KEY + 1))
            dve.wait_ge(sg["pv_done"].sem, sg["pv_done"].at(i, s))
            own = k.psum[:, 5:7, :].rearrange("p b c -> p (b c)")[:, 0:640].rearrange("p (t c) -> p t c", c=160)
            dve.tensor_tensor(om[:, b * P:(b + 1) * P].rearrange("p (t j d) -> p t j d", t=4, j=4),
                              own[:, :, 0:32].rearrange("p t (j d) -> p t j d", j=4), bc(w[:, us, :], 3, 8), ALU.mult
                              ).then_inc(sg["heads_read"].sem, 1)

        def finish_tile(i, s):
            if s == 4:
                written(i, LAST_WEIGHTS)
                dve.tensor_copy(pl[0:16, :], M[0:16, 0:P]).then_inc(misc.r.sem, 1)
            if s == 6:
                written(i, LAST_KEY)
                link(dve.tensor_tensor(heads[:, :].rearrange("p (u j d) -> p u j d", u=16, j=4),
                                       M.rearrange("p (u j d) -> p u j d", u=16, j=4),
                                       bc(bc(k.c("quad"), 1, 16), 3, 8), ALU.mult))
                dve.tensor_tensor(heads[:, :], heads[:, :], om[:, :], ALU.add).then_inc(misc.r.sem, 1)
            if s == 8:
                written(i, HEADS)
                if has_o:
                    dve.tensor_scalar(outT[:, :], M[:, 0:P], bv_col[:, 0:1], None, ALU.add).then_inc(misc.r.sem, 1)
            if s == (10 if has_o else 8):
                last = OUT if has_o else HEADS
                if has_o:
                    written(i, OUT)
                row = bo if has_o else bv_row
                dve.tensor_tensor(tmp[:, :], M[:, 0:P], row[:, :], ALU.add).then_inc(misc.r.sem, 1)
                dve.wait_ge(misc.r.sem, misc.v(misc.r, i, last + 1))
                x = k.X_spare[:, i, :]
                if has_o and relu:
                    dve.scalar_tensor_tensor(out=x, in0=tmp[:, :], scalar=0.0, in1=x, op0=ALU.max, op1=ALU.add)
                else:
                    dve.tensor_tensor(x, x, tmp[:, :], ALU.add)

        norm.dve_stats(dve, chain, None)
        if has_q:
            link(dve.tensor_scalar(neg_bv[:, :], bv_row[:, :], -1.0, None, ALU.mult))
        for t in (pbuf, pT, vS, om, last_w, vlbd[0:16, :]):
            dve.memset(t[(slice(None),) * len(t.shape)], 0.0)
        dve.memset(OB[:, 0:P], 0.0)
        dve.memset(rs[:, :], 1.0).then_inc(sg["cleared"].sem, 1)
        norm.dve_apply(dve, None)
        take_x(None)
        take_q(None)
        spread(None, NB - 1, NB)
        v_out(None, 0)
        with dve.Fori(0, TILES) as i:
            chain.round(i)
            for s in range(16):
                dve.wait_ge(sg["scores_written"].sem, sg["scores_written"].at(i, s + 1))
                dve.tensor_reduce(negm[:, s:s + 1], S[s % 2][:, 0:KEYS], X_AXIS, ALU.max, negate=True
                                  ).then_inc(sg["max_ready"].sem, 1)
                if s % 4 == 3:
                    heads_out(i, s)
                    v_out(i, s // 4)
                if s % 2 == 0:
                    turned(i, s)
                if s % 4 == 2:
                    sums_out(i, s)
                if s == 5:
                    norm.dve_stats(dve, chain, i)
                if s == 9:
                    norm.dve_apply(dve, i)
                finish_tile(i, s)
                if s == 12:
                    take_x(i)
                if s == 14:
                    take_q(i)
            spread(i, NB - 1, NB)
        chain.round(TILES)
        for s in range(11):
            if s == 0:
                turned(TILES, s)
            if s == 2:
                sums_out(TILES, s)
            if s == 3:
                heads_out(TILES, s)
            finish_tile(TILES, s)
        chain.done()

    return {"sync": sp, "pool": pool, "tensor": pe, "scalar": act, "vector": dve}


def cross_buffers(k):
    return k.scratch({"slots": [P, NB, KEYS], "last_key": [P, NB, 4], "kT": [P, 2, KEYS], "vS": [P, 2, 2, P],
                      "qT": [P, P], "qbd": [P, NB, P], "negm": [P, 16], "pbuf": [P, 8, KEYS], "rs": [P, 16],
                      "rr": [P, 16], "w": [P, 16, 4], "pT": [P, 2, 2 * P], "last_w": [P, 16], "pl": [P, P],
                      "vl": [P, P], "vlbd": [P, 512], "om": [P, 512], "heads": [P, 512], "outT": [P, P], "tmp": [P, P],
                      "neg_bv": [P, P]})


def window(k, b):
    return k.c("query_window")[:, 32 * (3 - b):32 * (7 - b)]


def self_buffers(k, kind):
    if kind == "L0":
        more = {"feature": [P, 2, 1024], "am": [P, 16, P], "vz": [P, 16 * P], "feature_w": [P, 2, 1024],
                "head_proj": [P, 1024], "feature_bias": [P, 16], "den": [P, P], "proj_rows": [P, 64]}
    else:
        more = {"kT": [P, 2, P], "qbd": [P, 2, 512], "kbd": [P, 3, 512], "group": [P, P], "v": [P, 256], "vm": [P, 2, 512],
                "pr": [P, 512], "pT": [P, 512], "nm": [P, 16], "rs": [P, 16], "rr": [P, 16], "w": [P, 16, 4],
                "om": [P, 2, 512], "lat": [64, P], "qkv": [P, 192], "ra": [P, 160], "rb": [P, 160],
                "ms": [P, 20], "r": [P, 20], "kvx": [P, 256], "sq": [P, 2, P], "bd": [P, P], "abd": [P, 512],
                "D": [P, 512], "E": [P, 512], "sD": [P, 512], "sDE": [P, 512], "R": [P, 512]}
    return k.scratch({"qT": [P, 2, P], "outT": [P, 2, P], "tmp": [P, P], **more})


CAP = 50.0


def self_attention(k, kind, s):
    norm = Norm(k)
    first = 3
    misc = Misc(k, 5, first, 7)
    nt = 2 if kind == "L1" else 4
    hd = 32 if kind == "L1" else 8
    M, O = k.bank[7], k.bank[5:7]
    chain_c = k.sig("vector_step").stage(*{"L1": (11, 5), "L2": (14, 10), "L3": (23, 12)}[kind])
    sg = {n: k.sig(n).stage(per, f) for n, (per, f) in {
        "scores_written": (1, 0), "scores_read": (1, 0), "probs_ready": (1, 0), "probs_T_written": (1, 0),
        "probs_T_read": (1, 0), "pv_done": (1, 0), "heads_ready": (1, 0),
        "operands_ready": (1, 1), **({} if kind == "L1" else {"q_ready": (1, 1), "weights_ready": (1, 0)}),
        **({"square_ready": (1, 1), "rms_ready": (1, 1)} if kind == "L2" else {}),
    }.items()}
    weights = sg["probs_ready" if kind == "L1" else "weights_ready"]
    if kind == "L1":
        wq, wd, wku, wvu = (k.load(n, sh) for n, sh in (("L1_attn_Wq", [P, 256]), ("L1_attn_Wkv_down", [P, 64]),
                                                        ("L1_attn_Wk_up", [64, 256]), ("L1_attn_Wv_up", [64, 256])))
        wo = k.load("L1_attn_Wo", [P, 2, P])
    elif kind == "L2":
        wqkv, wo = k.load("L2_attn_qkv", [P, 192]), k.load("L2_attn_w_o", [P, P])
    else:
        wq, wk, wv, wo = (k.load(f"L3_attn_W{n}", [P, P]) for n in "qkvo")
    at = norm.count

    def scores(n):
        return k.psum[:, 0:4, n * P:(n + 1) * P].rearrange("p b (t k) -> p b t k", k=32)

    def by_group(t):
        return t[:, :].rearrange("p (t b k) -> p b t k", b=NB, k=32)

    def pool(pool):
        def rms(i):
            if kind == "L2":
                pool.wait_ge(sg["square_ready"].sem, at(sg["square_ready"], i))
                pool.tensor_tensor(s["r"][:, :], s["ms"][:, :], k.minus_half[:, 0:20], ALU.pow
                                   ).then_inc(sg["rms_ready"].sem, 1)
        norm.pool(pool, None)
        rms(None)
        with pool.Fori(0, TILES) as i:
            norm.pool(pool, i)
            rms(i)

    def pe(pe):
        def turn_of(i, n):
            pe.wait_ge(misc.r.sem, misc.v(misc.r, i, n))

        def prep_x(i):
            pe.wait_ge(norm.xn.sem, at(norm.xn, i))
            turn_of(i, 0)
            pe.transpose(M[:, 0:P], k.xn[:, :], k.c("ident")).then_inc(misc.w.sem, 1)

        def prep_qkv(i):
            turn_of(i, 1)
            if kind == "L1":
                for t in range(2):
                    pe.matmul(M[:, t * P:(t + 1) * P], wq[:, t * P:(t + 1) * P], k.xnT[:, :], start=True, stop=True,
                              skip_group_check=True)
                pe.matmul(M[0:64, 256:384], wd[:, :], k.xnT[:, :], start=True, stop=True, skip_group_check=True
                          ).then_inc(misc.w.sem, 1)
            elif kind == "L2":
                pe.matmul(M[:, 0:192], k.xnT[:, :], wqkv[:, :], start=True, stop=True).then_inc(misc.w.sem, 1)
            else:
                for n, (l, r) in enumerate(((wq, k.xnT), (wk, k.xnT), (k.xnT, wv))):
                    mm = pe.matmul(M[:, n * P:(n + 1) * P], l[:, :], r[:, :], start=True, stop=True,
                                   skip_group_check=True)
                mm.then_inc(misc.w.sem, 1)

        def prep_last(i):
            turn_of(i, 2 if i is None else 4)
            if kind == "L1":
                for t in range(2):
                    pe.matmul(M[:, t * P:(t + 1) * P], wku[:, t * P:(t + 1) * P], s["lat"][:, :], start=True, stop=True,
                              skip_group_check=True)
                pe.matmul(M[:, 256:512], s["lat"][:, :], wvu[:, :], start=True, stop=True, skip_group_check=True
                          ).then_inc(misc.w.sem, 1)
            elif kind == "L2":
                pe.wait_ge(sg["q_ready"].sem, at(sg["q_ready"], i))
                pe.transpose(M[:, 0:P], s["qkv"][:, 0:P], k.c("ident"))
                pe.transpose(M[:, P:2 * P], s["kvx"][:, 0:P], k.c("ident")).then_inc(misc.w.sem, 1)
            else:
                pe.wait_ge(sg["q_ready"].sem, at(sg["q_ready"], i))
                for n in range(2):
                    mm = pe.matmul(M[:, n * P:(n + 1) * P], k.c("same_head"), s["sq"][:, n, :], start=True, stop=True,
                                   skip_group_check=True)
                mm.then_inc(misc.w.sem, 1)

        prep_x(None)
        prep_qkv(None)
        prep_last(None)
        with pe.Fori(0, TILES) as i:
            pe.wait_ge(sg["operands_ready"].sem, sg["operands_ready"].at(i, 0))
            pe.wait_ge(sg["scores_read"].sem, sg["scores_read"].at(i, 0))
            if kind == "L1":
                for t in range(nt):
                    for b in range(NB):
                        mm = pe.matmul(k.bank[t][:, 32 * b:32 * b + 32], s["qbd"][:, t, b * P:(b + 1) * P],
                                       s["kT"][:, t, 32 * b:32 * b + 32], start=True, stop=True, skip_group_check=True)
            else:
                for b in range(NB):
                    cols = slice(b * P, (b + 1) * P)
                    mm = pe.matmul(k.bank[b][:, 0:P], s["qbd"][:, 0, cols], s["kbd"][:, 0, cols], start=True,
                                   stop=(kind != "L3"), skip_group_check=True)
                    if kind == "L3":
                        pe.matmul(k.bank[b][:, 0:P], s["abd"][:, cols], s["group"][:, :], start=False, stop=False,
                                  skip_group_check=True)
                        pe.matmul(k.bank[b][:, 0:P], s["qbd"][:, 1, cols], s["kbd"][:, 1, cols], start=False, stop=True,
                                  skip_group_check=True)
                        mm = pe.matmul(k.bank[b][:, P:2 * P], s["om"][:, 1, cols], s["kbd"][:, 2, cols], start=True,
                                       stop=True, skip_group_check=True)
            mm.then_inc(sg["scores_written"].sem, 1)
            prep_x(i)
            pe.wait_ge(weights.sem, weights.at(i, 1))
            for t in range(nt):
                mm = pe.transpose(k.bank[4][:, t * P:(t + 1) * P], s["pr"][:, t * P:(t + 1) * P], k.c("ident"))
            mm.then_inc(sg["probs_T_written"].sem, 1)
            prep_qkv(i)
            pe.wait_ge(sg["probs_T_read"].sem, sg["probs_T_read"].at(i, 1))
            for t in range(nt):
                if kind == "L1":
                    mm = pe.matmul(O[t][:, :], s["pT"][:, t * P:(t + 1) * P], s["vm"][:, t, :], start=True, stop=True)
                else:
                    mm = pe.matmul(O[0].rearrange("p (b t d) -> p b t d", b=NB, t=4)[:, :, t, :],
                                   s["pT"][:, t * P:(t + 1) * P],
                                   s["vm"][:, 0, :].rearrange("p (b t d) -> p b t d", b=NB, t=4)[:, :, t, :],
                                   start=(t == 0), stop=True, skip_group_check=True)
            mm.then_inc(sg["pv_done"].sem, 1)
            pe.wait_ge(sg["heads_ready"].sem, sg["heads_ready"].at(i, 1))
            turn_of(i, 2)
            for t in range(2 if kind == "L1" else 1):
                for b in range(NB):
                    mm = pe.matmul(M[:, t * P:(t + 1) * P], s["om"][:, t, b * P:(b + 1) * P], window(k, b),
                                   start=(b == 0 and t == 0), stop=(b == NB - 1), skip_group_check=True)
            mm.then_inc(misc.w.sem, 1)
            turn_of(i, 3)
            if kind == "L1":
                for t in range(2):
                    mm = pe.matmul(M[:, 0:P], s["outT"][:, t, :], wo[:, t, :], start=(t == 0), stop=(t == 1))
            else:
                mm = pe.matmul(M[:, 0:P], s["outT"][:, 0, :], wo[:, :], start=True, stop=True)
            mm.then_inc(misc.w.sem, 1)
            prep_last(i)

    def act(act):
        with act.Fori(0, TILES) as i:
            if kind == "L1":
                act.wait_ge(sg["scores_read"].sem, sg["scores_read"].at(i, 1))
                act.activation(s["pr"][:, 0:256], s["pr"][:, 0:256], ACT.Exp).then_inc(sg["probs_ready"].sem, 1)
            elif kind == "L2":
                act.wait_ge(sg["scores_written"].sem, sg["scores_written"].at(i, 1))
                act.wait_ge(sg["weights_ready"].sem, sg["weights_ready"].at(i, 0))
                act.activation(by_group(s["D"]), scores(0), ACT.Tanh,
                               scale=float(1.0 / (CAP * np.sqrt(8.0)))).then_inc(sg["scores_read"].sem, 1)
                act.wait_ge(sg["scores_read"].sem, sg["scores_read"].at(i, 1))
                act.activation(s["E"][:, :], s["D"][:, :], ACT.Exp, scale=CAP).then_inc(sg["probs_ready"].sem, 1)
            else:
                act.wait_ge(sg["scores_read"].sem, sg["scores_read"].at(i, 1))
                act.activation(s["sD"][:, :], s["D"][:, :], ACT.Sqrt)
                act.activation(s["sDE"][:, :], s["sDE"][:, :], ACT.Sqrt).then_inc(sg["probs_ready"].sem, 1)

    def dve(dve):
        chain = Chain(dve, chain_c)
        link = chain.link

        def rows_by_head(dst, src, mask):
            return dve.tensor_tensor(dst.rearrange("p (b j q) -> p b j q", b=NB, j=4),
                                     bc(src.rearrange("p (b q) -> p b q", b=NB), 2, 4),
                                     bc(bc(mask, 1, NB), 3, SEQ), ALU.mult)

        def by_batch(dst, src):
            return dve.tensor_tensor(dst.rearrange("p (b d) -> p b d", b=NB), bc(src, 1, NB), bc(k.c("quad"), 2, P),
                                     ALU.mult)

        def written(i, n):
            dve.wait_ge(misc.w.sem, misc.v(misc.w, i, n))

        def read(i, n):
            dve.wait_ge(misc.r.sem, misc.v(misc.r, i, n))

        def prep_x(i):
            written(i, 1)
            dve.tensor_copy(k.xnT[:, :], M[:, 0:P]).then_inc(misc.r.sem, 1)

        def prep_qkv(i):
            written(i, 2)
            if kind == "L1":
                link(dve.tensor_copy(s["qT"][:, :, :], M[:, 0:256].rearrange("p (t c) -> p t c", t=2)))
                dve.tensor_copy(s["lat"][:, :], M[0:64, 256:384]).then_inc(misc.r.sem, 1)
                link(rows_by_head(s["qbd"][:, 0, :], s["qT"][:, 0, :], k.c("quad_scaled")))
                link(rows_by_head(s["qbd"][:, 1, :], s["qT"][:, 1, :], k.c("quad_scaled")))
            elif kind == "L2":
                qk = s["qkv"][:, 0:160]
                dve.tensor_copy(s["qkv"][:, :], M[:, 0:192]).then_inc(misc.r.sem, 1)
                read(i, 2)
                link(dve.tensor_tensor(s["ra"][:, :], qk, qk, ALU.mult))
                link(dve.tensor_reduce(s["ms"][:, :], s["ra"][:, :].rearrange("p (h d) -> p h d", d=8), X_AXIS, ALU.add))
                dve.tensor_scalar(s["ms"][:, :], s["ms"][:, :], 0.125, 1e-5, ALU.mult, ALU.add
                                  ).then_inc(sg["square_ready"].sem, 1)
            else:
                link(dve.tensor_copy(s["qT"][:, 0, :], M[:, 0:P]))
                link(dve.tensor_copy(s["kT"][:, 0, :], M[:, P:2 * P]))
                dve.tensor_copy(s["v"][:, 0:P], M[:, 2 * P:3 * P]).then_inc(misc.r.sem, 1)
                link(dve.tensor_tensor(s["sq"][:, 0, :], s["qT"][:, 0, :], s["qT"][:, 0, :], ALU.mult))
                dve.tensor_tensor(s["sq"][:, 1, :], s["kT"][:, 0, :], s["kT"][:, 0, :], ALU.mult
                                  ).then_inc(sg["q_ready"].sem, 1)
                link(dve.tensor_scalar(s["tmp"][:, :], s["qT"][:, 0, :], -2.0, None, ALU.mult))
                link(rows_by_head(s["qbd"][:, 0, :], s["tmp"][:, :], k.c("lane")))

        def rotate(i):
            if kind != "L2":
                return
            dve.wait_ge(sg["rms_ready"].sem, at(sg["rms_ready"], i))
            qk = s["qkv"][:, 0:160]
            heads = qk.rearrange("p (h d) -> p h d", d=8)
            link(dve.tensor_tensor(heads, heads, bc(s["r"][:, :], 2, 8), ALU.mult))
            halves = qk.rearrange("p (h d) -> p h d", d=4)
            for dst, c in (("ra", "cos"), ("rb", "sin")):
                link(dve.tensor_tensor(s[dst][:, :].rearrange("p (h d) -> p h d", d=4), halves, bc(k.c(c), 1, 40),
                                       ALU.mult))
            a, b, o = (x.rearrange("p (h e d) -> p h e d", e=2, d=4) for x in (s["ra"][:, :], s["rb"][:, :], qk))
            link(dve.tensor_tensor(o[:, :, 0, :], a[:, :, 0, :], b[:, :, 1, :], ALU.subtract))
            link(dve.tensor_tensor(o[:, :, 1, :], a[:, :, 1, :], b[:, :, 0, :], ALU.add))
            dve.tensor_copy(s["kvx"][:, :].rearrange("p (t j d) -> p t j d", t=8, j=4),
                            bc(s["qkv"][:, P:192].rearrange("p (t d) -> p t d", d=8), 2, 4)
                            ).then_inc(sg["q_ready"].sem, 1)

        def prep_last(i):
            last = 3 if i is None else 5
            written(i, last)
            if kind == "L1":
                link(dve.tensor_copy(s["v"][:, :], M[:, 256:512]))
                dve.tensor_copy(s["kT"][:, :, :], M[:, 0:256].rearrange("p (t c) -> p t c", t=2)
                                ).then_inc(misc.r.sem, 1)
                read(i, last)
                dve.memset(k.carrier[:, :], 0.0).then_inc(sg["operands_ready"].sem, 1)
            elif kind == "L2":
                dve.wait_ge(sg["q_ready"].sem, at(sg["q_ready"], i))
                link(dve.tensor_copy(s["qT"][:, 0, :], M[:, 0:P]))
                dve.tensor_copy(s["kT"][:, 0, :], M[:, P:2 * P]).then_inc(misc.r.sem, 1)
                link(rows_by_head(s["qbd"][:, 0, :], s["qT"][:, 0, :], k.c("lane")))
                read(i, last)
                rows_by_head(s["kbd"][:, 0, :], s["kT"][:, 0, :], k.c("quad")).then_inc(sg["operands_ready"].sem, 1)
            else:
                link(dve.tensor_scalar(s["tmp"][:, :], M[:, 0:P], -1.0, 1.0, ALU.mult, ALU.add))
                link(rows_by_head(s["om"][:, 1, :], s["tmp"][:, :], k.c("lane_eighth")))
                link(dve.tensor_scalar(s["bd"][:, :], M[:, P:2 * P], -1.0, 1.0, ALU.mult, ALU.add))
                dve.memset(k.carrier[:, :], 0.0).then_inc(misc.r.sem, 1)
                read(i, last)
                rows_by_head(s["abd"][:, :], s["sq"][:, 0, :], k.c("lane"))
                rows_by_head(s["kbd"][:, 0, :], s["kT"][:, 0, :], k.c("quad"))
                rows_by_head(s["kbd"][:, 1, :], s["sq"][:, 1, :], k.c("quad"))
                link(rows_by_head(s["kbd"][:, 2, :], s["bd"][:, :], k.c("quad")))
                dve.memset(k.carrier[:, :], 0.0).then_inc(sg["operands_ready"].sem, 1)

        def weights_done(i):
            n = 4 * nt
            link(dve.tensor_reduce(s["rs"][:, 0:n], s["pr"][:, 0:nt * P].rearrange("p (u c) -> p u c", c=32), X_AXIS,
                                   ALU.add))
            link(dve.reciprocal(s["rr"][:, 0:n], s["rs"][:, 0:n]))
            rr = s["rr"][:, 0:n]
            if kind == "L1":
                link(dve.tensor_tensor(s["w"][:, 0:n, :], bc(rr, 2, 4), bc(k.c("quad"), 1, n), ALU.mult))
            else:
                link(dve.tensor_tensor(s["w"][:, :, :].rearrange("p (b t) j -> p b t j", t=4),
                                       bc(rr.rearrange("p (t b) -> p b t", b=NB), 3, 4),
                                       bc(bc(k.c("quad"), 1, 4), 1, NB), ALU.mult))

        norm.dve_stats(dve, chain, None)
        if kind == "L3":
            link(dve.tensor_copy(s["qbd"][:, 1, :].rearrange("p (b j q) -> p b j q", b=NB, j=4),
                                 bc(bc(k.c("lane"), 1, NB), 3, SEQ)))
            link(dve.tensor_copy(s["group"][:, :].rearrange("p (t k) -> p t k", t=4), bc(k.c("quad"), 2, SEQ)))
        norm.dve_apply(dve, None)
        prep_x(None)
        prep_qkv(None)
        rotate(None)
        prep_last(None)
        with dve.Fori(0, TILES) as i:
            chain.round(i)
            norm.dve_stats(dve, chain, i)
            vsrc = s["kvx"][:, P:2 * P] if kind == "L2" else s["v"][:, 0:P]
            dve.wait_ge(sg["pv_done"].sem, sg["pv_done"].at(i, 0))
            link(by_batch(s["vm"][:, 0, :], vsrc))
            if kind == "L1":
                link(by_batch(s["vm"][:, 1, :], s["v"][:, P:2 * P]))
            norm.dve_apply(dve, i)
            dve.wait_ge(sg["scores_written"].sem, sg["scores_written"].at(i, 1))
            if kind == "L1":
                sc = k.psum[:, 0:2, 0:P].rearrange("p t (b c) -> p t b c", c=32)
                nm = s["nm"][:, 0:8]
                link(dve.tensor_reduce(nm.rearrange("p (t b) -> p t b", t=2), sc, X_AXIS, ALU.max, negate=True))
                pr = s["pr"][:, 0:256]
                dve.tensor_tensor(pr.rearrange("p (t b c) -> p t b c", t=2, c=32), sc,
                                  bc(nm.rearrange("p (t b) -> p t b", t=2), 3, 32), ALU.add
                                  ).then_inc(sg["scores_read"].sem, 1)
                dve.wait_ge(sg["probs_ready"].sem, sg["probs_ready"].at(i, 1))
            elif kind == "L2":
                dve.wait_ge(sg["probs_ready"].sem, sg["probs_ready"].at(i, 1))
                dve.tensor_tensor(s["pr"][:, :].rearrange("p (u c) -> p u c", c=32),
                                  s["E"][:, :].rearrange("p (u c) -> p u c", c=32), bc(k.c("causal"), 1, 16),
                                  ALU.mult).then_inc(weights.sem, 1)
            else:
                def flat(n):
                    return s[n][:, :]

                link(dve.tensor_scalar(by_group(s["D"]), scores(0), 0.0, None, ALU.max))
                link(dve.tensor_scalar(by_group(s["E"]), scores(1), 1e-6, None, ALU.max))
                dve.tensor_tensor(flat("sDE"), flat("D"), flat("E"), ALU.add).then_inc(sg["scores_read"].sem, 1)
                link(dve.scalar_tensor_tensor(out=flat("R"), in0=flat("D"), scalar=2.0, in1=flat("E"),
                                              op0=ALU.mult, op1=ALU.add))
                dve.wait_ge(sg["probs_ready"].sem, sg["probs_ready"].at(i, 1))
                link(dve.tensor_tensor(flat("sD"), flat("sD"), flat("sDE"), ALU.mult))
                link(dve.scalar_tensor_tensor(out=flat("R"), in0=flat("sD"), scalar=2.0, in1=flat("R"),
                                              op0=ALU.mult, op1=ALU.add))
                link(dve.reciprocal(flat("R"), flat("R")))
                link(dve.tensor_tensor(flat("R"), flat("R"), flat("E"), ALU.mult))
                rows = s["R"][:, :].rearrange("p (u c) -> p u c", c=32)
                link(dve.tensor_reduce(s["nm"][:, :], rows, X_AXIS, ALU.max))
                link(dve.reciprocal(s["nm"][:, :], s["nm"][:, :]))
                dve.tensor_tensor(s["pr"][:, :].rearrange("p (u c) -> p u c", c=32), rows,
                                  bc(s["nm"][:, :], 2, 32), ALU.mult).then_inc(weights.sem, 1)
            prep_x(i)
            dve.wait_ge(weights.sem, weights.at(i, 1))
            weights_done(i)
            dve.wait_ge(sg["probs_T_written"].sem, sg["probs_T_written"].at(i, 1))
            dve.tensor_copy(s["pT"][:, 0:nt * P], k.bank[4][:, 0:nt * P]).then_inc(sg["probs_T_read"].sem, 1)
            prep_qkv(i)
            dve.wait_ge(sg["pv_done"].sem, sg["pv_done"].at(i, 1))
            w = s["w"][:, 0:4 * nt, :].rearrange("p u j -> p (u j)")
            for t in range(2 if kind == "L1" else 1):
                n = 16 if kind == "L1" else 64
                ins = dve.tensor_tensor(s["om"][:, t, :].rearrange("p (g d) -> p g d", d=hd),
                                        O[t].rearrange("p (g d) -> p g d", d=hd),
                                        bc(w[:, t * n:(t + 1) * n], 2, hd), ALU.mult)
            ins.then_inc(sg["heads_ready"].sem, 1)
            rotate(i)
            written(i, 3)
            n = 2 if kind == "L1" else 1
            dve.tensor_copy(s["outT"][:, 0:n, :], M[:, 0:n * P].rearrange("p (t c) -> p t c", t=n)
                            ).then_inc(misc.r.sem, 1)
            written(i, 4)
            x = k.X[:, i, :]
            dve.tensor_tensor(x, x, M[:, 0:P], ALU.add).then_inc(misc.r.sem, 1)
            read(i, 4)
            prep_last(i)
        chain.i = i
        chain.done()

    return {"sync": lambda sp: None, "pool": pool, "tensor": pe, "scalar": act, "vector": dve}


def null_key_attention(k):
    norm = Norm(k, twice=True)
    misc = Misc(k, 3, 2, 7)
    W = KEYS + 1
    a = k.scratch({
        "G": [P, 16, P], "N": [P, 16, P], "wqT": [P, 8, P], "wkT": [P, 8, P], "wvT": [P, 8, P], "wo": [P, 8, P],
        "p": [P, 4, W], "slots": [P, NB, KEYS], "d": [P, KEYS], "sq": [P, KEYS], "ve": [P, 3], "zT": [P, 2, KEYS],
        "zk": [P, 2, 2 * P], "zl": [1, 2, P], "pT": [P, 2, 2 * P], "pTl": [1, 2, P], "null_left": [P, 4 * P],
        "null_value": [P, 4, P], "row": [P, P], "U": [P, 16], "rhsU": [P, 8, 16], "kb": [P, 8], "vb": [P, 8],
        "negm": [P, 16], "rs": [P, 16], "rr": [P, 16], "pn": [P, 16], "ns": [P, 16], "nsr": [P, 64], "batch": [P, 1],
        "xs_row": [P, P], "xb_row": [P, P], "cs_row": [P, P], "cb_row": [P, P], "y": [P, P], "y2": [P, P], "cols": [P, 6]})
    qa = k.area[:, 4096:4096 + 2048].rearrange("p (t c) -> p t c", t=4)
    pc = k.area[:, 6144:6144 + 2048].rearrange("p (h c) -> p h c", h=16)
    xrep = a["null_left"]
    setup = a["p"].rearrange("p u c -> p (u c)")[:, 0:1024].rearrange("p (c m) -> p c m", c=8)
    bias, sel, mask = k.mask_bias, k.batch_select, k.mask_in
    for name, dst in (("wqT", a["wqT"]), ("wkT", a["wkT"]), ("wvT", a["wvT"]), ("wo", a["wo"]), ("cols", a["cols"]),
                      ("mask", mask)):
        k.loads.append((k.stage_no, dst, k.dram["L0_xattn_" + name]))
    for name, dst in (("lno_s", a["xs_row"]), ("lno_b", a["xb_row"]), ("lnc_s", a["cs_row"]), ("lnc_b", a["cb_row"])):
        k.loads.append((k.stage_no, dst, k.dram["L0_xattn_" + name].partition_broadcast(P)))
    col = {n: a["cols"][:, c:c + 1] for c, n in enumerate(("x_scale", "x_bias", "c_scale", "null_key", "null_value"))}
    S, T, Z, PC, M = k.bank[0:2], k.bank[2:4], k.bank[4], k.bank[5:7], k.bank[7]
    ctxT = k.dram["ctxT"]
    chain_c = k.sig("vector_step").stage(X0_STEPS, X0_FIRST)
    sg = {n: k.sig(n).stage(per, first) for n, (per, first) in {
        **{f"slot{b}_loaded": (16, 16) for b in range(NB)}, "slot_freed": (NB, 0), "setup_written": (0, 4),
        "setup_read": (0, 5), "mean_written": (NB, 1), "centred": (NB, 1), "squared": (NB, 1), "var_written": (NB, 1),
        "var_read": (NB, 1), "z_rstd": (NB, 1), "z_read": (NB, 1), "z_turned": (NB, 1), "zT_ready": (NB, 1),
        "scores_written": (16, 0), "max_ready": (16, 0), "exp_ready": (16, 0), "probs_ready": (16, 0),
        "probs_T_written": (16, 0), "probs_T_read": (16, 0), "pv_done": (16, 0), "pc_read": (NB, 0),
        "qa_written": (4, 4), "qa_read": (4, 4), "null_ready": (1, 1), "null_left_ready": (1, 0),
        "out_var_ready": (1, 0), "out_rstd_ready": (1, 0), "out_pool_step": (1, 0),
    }.items()}

    def batch(c, i, b):
        return c.before(1) if i is None else c.at(i, b + 1)

    def sp(sp):
        for b in range(NB):
            sp.dma_start(a["slots"][:, b, :], ctxT[b]).then_inc(sg[f"slot{b}_loaded"].sem, 16)
        with sp.Fori(0, TILES) as i:
            for b in range(NB):
                sp.wait_ge(sg["centred"].sem, sg["centred"].at(i, b))
                sp.sem_inc(sg["slot_freed"].sem, 1)
                sp.dma_start(a["slots"][:, b, :], ctxT[i * NB + (NB + b)]).then_inc(sg[f"slot{b}_loaded"].sem, 16)
        for b in range(NB):
            sp.wait_ge(sg[f"slot{b}_loaded"].sem, sg[f"slot{b}_loaded"].at(TILES - 1, 16))

    def pool(pool):
        def squares(i, b):
            pool.wait_ge(sg["centred"].sem, batch(sg["centred"], i, b))
            pool.tensor_tensor(a["sq"], a["d"], a["d"], ALU.mult).then_inc(sg["squared"].sem, 1)

        def rstd(i, b):
            pool.wait_ge(sg["var_read"].sem, batch(sg["var_read"], i, b))
            pool.tensor_tensor(a["ve"], a["ve"], k.minus_half[:, 0:3], ALU.pow).then_inc(sg["z_rstd"].sem, 1)

        norm.pool(pool, None)
        squares(None, 0)
        rstd(None, 0)
        with pool.Fori(0, TILES) as i:
            for b in range(NB):
                squares(i, b)
                rstd(i, b)
                if b == 1:
                    norm.pool(pool, i)
            ov, os, orr = sg["out_var_ready"], sg["out_pool_step"], sg["out_rstd_ready"]
            pool.wait_ge(ov.sem, ov.at(i, 1))
            pool.tensor_tensor(k.vareps[:, :], k.out_meanvar[:, 1:2], k.ln_eps6[:, :], ALU.add).then_inc(os.sem, 1)
            pool.wait_ge(os.sem, os.at(i, 1))
            pool.tensor_tensor(k.rstd_second[:, :], k.vareps[:, :], k.minus_half[:, 0:1], ALU.pow).then_inc(orr.sem, 1)

    def pe(pe):
        def setup_turn(n):
            pe.wait_ge(sg["setup_read"].sem, sg["setup_read"].before(n))

        def per_head(left, right):
            for odd in range(2):
                rows = slice(64 * odd, 64 * odd + 64)
                for c in range(8):
                    mm = pe.matmul(k.bank[2 * odd + c // 4][:, (c % 4) * P:(c % 4 + 1) * P], left[rows, c, :],
                                   right[rows, c, :], start=True, stop=True, skip_group_check=True)
            mm.then_inc(sg["setup_written"].sem, 1)

        def prep(i):
            m = 0 if i is None else 1
            pe.wait_ge(norm.xn.sem, norm.count(norm.xn, i))
            pe.wait_ge(misc.r.sem, misc.v(misc.r, i, m))
            pe.transpose(M[:, 0:P], k.xn[:, :], k.c("ident")).then_inc(misc.w.sem, 1)
            pe.wait_ge(misc.r.sem, misc.v(misc.r, i, m + 1))
            for b in range(NB):
                mm = pe.matmul(M[:, 16 * b:16 * b + 16], xrep[:, b * P:(b + 1) * P], a["U"][:, :], start=True,
                               stop=True, skip_group_check=True)
            mm.then_inc(misc.w.sem, 1)
            for t in range(4):
                qr = sg["qa_read"]
                pe.wait_ge(qr.sem, (qr.before(max(t - 1, 0)) if i is None else qr.at(i, max(t - 1, 0))))
                if i is not None and t == 0:
                    pe.wait_ge(sg["exp_ready"].sem, sg["exp_ready"].at(i, 16))
                for j in range(4):
                    mm = pe.matmul(S[t % 2][:, j * P:(j + 1) * P], a["G"][:, 4 * t + j, :], k.xnT[:, :],
                                   start=True, stop=True, skip_group_check=True)
                mm.then_inc(sg["qa_written"].sem, 1)

        def slot(b):
            return 0 if b is None else (b + 1) % NB

        def mean(i, b):
            s = slot(b)
            loaded = sg[f"slot{s}_loaded"]
            pe.wait_ge(loaded.sem, loaded.before(16) if i is None else loaded.at(i, 16 if s == 0 else 0))
            if i is not None:
                pe.wait_ge(sg["zT_ready"].sem, sg["zT_ready"].at(i, b))
            pe.matmul(Z[:, 0:KEYS], k.c("mean_of"), a["slots"][:, s, :], start=True, stop=True
                      ).then_inc(sg["mean_written"].sem, 1)

        def variance(i, b):
            pe.wait_ge(sg["centred"].sem, batch(sg["centred"], i, b))
            pe.transpose(Z[:, 0:P], a["d"][:, 0:P], k.c("ident"))
            pe.transpose(Z[:, P:2 * P], a["d"][:, P:2 * P], k.c("ident"))
            pe.transpose(Z[0:1, 2 * P:3 * P], a["d"][:, 2 * P:KEYS], k.c("ident"))
            pe.wait_ge(sg["squared"].sem, batch(sg["squared"], i, b))
            for n, left in enumerate((a["sq"][:, 0:P], a["sq"][:, P:2 * P], a["sq"][:, 2 * P:KEYS].to_broadcast([P, P]))):
                mm = pe.matmul(Z[:, 384 + n:385 + n], left, k.c("mean_of")[:, 0:1], start=True, stop=True,
                               skip_group_check=True)
            mm.then_inc(sg["var_written"].sem, 1)

        def z_turn(i, b):
            s = 0 if i is None else (b + 1) % 2
            pe.wait_ge(sg["z_read"].sem, batch(sg["z_read"], i, b))
            pe.transpose(Z[:, 0:P], a["zk"][:, s, 0:P], k.c("ident"))
            pe.transpose(Z[:, P:2 * P], a["zk"][:, s, P:2 * P], k.c("ident"))
            pe.transpose(Z[:, 2 * P:KEYS], a["zl"][:, s, :], k.c("ident")[0:1, 0:1]).then_inc(sg["z_turned"].sem, 1)

        def scores(i, u):
            b, t = divmod(u, 4)
            if u == 0:
                pe.wait_ge(sg["qa_read"].sem, sg["qa_read"].at(i, 0))
                pe.wait_ge(sg["null_ready"].sem, sg["null_ready"].at(i, 0))
            if t == 0:
                pe.wait_ge(sg["zT_ready"].sem, sg["zT_ready"].at(i, b))
            pe.wait_ge(sg["exp_ready"].sem, sg["exp_ready"].at(i, u - 1))
            pe.matmul(S[u % 2][:, 0:KEYS], qa[:, t, b * P:(b + 1) * P], a["zT"][:, b % 2, :], start=True, stop=False,
                      skip_group_check=True)
            pe.matmul(S[u % 2][:, 0:KEYS], sel[:, b, :], bias[:, :], start=False, stop=True, skip_group_check=True)
            pe.matmul(S[u % 2][:, KEYS:W], k.c("ident"), a["ns"][:, u:u + 1], start=True, stop=True,
                      skip_group_check=True).then_inc(sg["scores_written"].sem, 1)

        def turn(i, u):
            pe.wait_ge(sg["probs_ready"].sem, sg["probs_ready"].at(i, u + 1))
            pe.wait_ge(sg["probs_T_read"].sem, sg["probs_T_read"].at(i, u - 1))
            pe.transpose(T[u % 2][:, 0:P], a["p"][:, u % 4, 0:P], k.c("ident"))
            pe.transpose(T[u % 2][:, P:2 * P], a["p"][:, u % 4, P:2 * P], k.c("ident"))
            pe.transpose(T[u % 2][0:1, 2 * P:3 * P], a["p"][:, u % 4, 2 * P:KEYS], k.c("ident")
                         ).then_inc(sg["probs_T_written"].sem, 1)

        def values(i, u):
            b, t = divmod(u, 4)
            if t == 0:
                pe.wait_ge(sg["z_read"].sem, sg["z_read"].at(i, b))
                pe.wait_ge(sg["pc_read"].sem, sg["pc_read"].at(i, b - 1))
            pe.wait_ge(sg["probs_T_read"].sem, sg["probs_T_read"].at(i, u + 1))
            out = PC[b % 2][:, t * P:(t + 1) * P]
            for c in range(2):
                pe.matmul(out, a["zk"][:, b % 2, c * P:(c + 1) * P], a["pT"][:, u % 2, c * P:(c + 1) * P],
                          start=(c == 0), stop=False, skip_group_check=True)
            pe.matmul(out, a["zl"][:, b % 2, :], a["pTl"][:, u % 2, :], start=False, stop=True, skip_group_check=True
                      ).then_inc(sg["pv_done"].sem, 1)

        per_head(a["wvT"], a["wo"])
        setup_turn(2)
        per_head(a["wqT"], a["wkT"])
        setup_turn(3)
        for c in range(8):
            pe.matmul(k.bank[0][:, 0:16], a["wqT"][:, c, :], a["rhsU"][:, c, :], start=(c == 0), stop=(c == 7))
        for t in range(4):
            for cc in range(2):
                mm = pe.matmul(k.bank[1][:, t * P:(t + 1) * P], setup[:, 2 * t + cc, :], a["wo"][:, 2 * t + cc, :],
                               start=(cc == 0), stop=(cc == 1), skip_group_check=True)
        mm.then_inc(sg["setup_written"].sem, 1)
        setup_turn(4)
        for c in range(8):
            mm = pe.matmul(k.bank[2][:, 0:P], setup[:, c, :], a["wo"][:, c, :], start=(c == 0), stop=(c == 7))
        mm.then_inc(sg["setup_written"].sem, 1)
        setup_turn(5)
        prep(None)
        mean(None, None)
        variance(None, None)
        z_turn(None, None)
        with pe.Fori(0, TILES) as i:
            for u in range(16):
                b, t = divmod(u, 4)
                scores(i, u)
                if t == 0:
                    mean(i, b)
                if t == 1:
                    variance(i, b)
                if t == 3:
                    z_turn(i, b)
                if u >= 2:
                    turn(i, u - 2)
                if u >= 3:
                    values(i, u - 3)
            turn(i, 14)
            values(i, 13)
            turn(i, 15)
            values(i, 14)
            values(i, 15)
            pe.wait_ge(sg["pc_read"].sem, sg["pc_read"].at(i, 4))
            pe.wait_ge(sg["null_left_ready"].sem, sg["null_left_ready"].at(i, 1))
            pe.wait_ge(misc.r.sem, misc.r.at(i, 0))
            for h in range(16):
                pe.matmul(M[:, 0:P], pc[:, h, :], a["N"][:, h, :], start=(h == 0), stop=False)
            for t in range(4):
                mm = pe.matmul(M[:, 0:P], a["null_left"][:, t * P:(t + 1) * P], a["null_value"][:, t, :],
                               start=False, stop=(t == 3))
            mm.then_inc(misc.w.sem, 1)
            prep(i)

    def act(act):
        def queries(i):
            for t in range(4):
                qw = sg["qa_written"]
                act.wait_ge(qw.sem, qw.before(t + 1) if i is None else qw.at(i, t + 1))
                act.activation(qa[:, t, :].rearrange("p (b j q) -> p b j q", b=NB, j=4),
                               S[t % 2].rearrange("p (j b q) -> p b j q", j=4, b=NB), ACT.Copy
                               ).then_inc(sg["qa_read"].sem, 1)

        def z_out(i, b):
            s = 0 if i is None else (b + 1) % 2
            act.wait_ge(sg["z_rstd"].sem, batch(sg["z_rstd"], i, b))
            if i is not None:
                act.wait_ge(sg["pv_done"].sem, sg["pv_done"].at(i, 4 * b))
            for c in range(2):
                act.activation(a["zk"][:, s, c * P:(c + 1) * P], Z[:, c * P:(c + 1) * P], ACT.Copy, scale=a["ve"][:, c:c + 1])
            act.activation(a["zl"][:, s, :], Z[0:1, 2 * P:3 * P], ACT.Copy, scale=a["ve"][0:1, 2:3]
                           ).then_inc(sg["z_read"].sem, 1)

        def turned(i, u):
            act.wait_ge(sg["probs_T_written"].sem, sg["probs_T_written"].at(i, u + 1))
            act.wait_ge(sg["pv_done"].sem, sg["pv_done"].at(i, u - 1))
            act.activation(a["pT"][:, u % 2, :], T[u % 2][:, 0:2 * P], ACT.Copy)
            act.activation(a["pTl"][:, u % 2, :], T[u % 2][0:1, 2 * P:3 * P], ACT.Copy
                           ).then_inc(sg["probs_T_read"].sem, 1)

        queries(None)
        z_out(None, 0)
        with act.Fori(0, TILES) as i:
            for u in range(16):
                b, t = divmod(u, 4)
                act.wait_ge(sg["max_ready"].sem, sg["max_ready"].at(i, u + 1))
                act.wait_ge(sg["probs_T_written"].sem, sg["probs_T_written"].at(i, u - 3))
                act.activation(a["p"][:, u % 4, :], S[u % 2][:, 0:W], ACT.Exp, bias=a["negm"][:, u:u + 1],
                               accum_out=a["rs"][:, u:u + 1]).then_inc(sg["exp_ready"].sem, 1)
                if u >= 2:
                    turned(i, u - 2)
                if t == 2:
                    z_out(i, b)
            turned(i, 14)
            turned(i, 15)
            queries(i)

    def dve(dve):
        chain = Chain(dve, chain_c)
        link = chain.link

        def centre(i, b):
            s = 0 if i is None else (b + 1) % NB
            dve.wait_ge(sg["mean_written"].sem, batch(sg["mean_written"], i, b))
            dve.tensor_tensor(a["d"], a["slots"][:, s, :], Z[:, 0:KEYS], ALU.subtract).then_inc(sg["centred"].sem, 1)

        def var_out(i, b):
            dve.wait_ge(sg["var_written"].sem, batch(sg["var_written"], i, b))
            dve.tensor_scalar(a["ve"], Z[:, 384:387], 1e-6, None, ALU.add).then_inc(sg["var_read"].sem, 1)

        def z(i, b):
            s = 0 if i is None else (b + 1) % 2
            dve.wait_ge(sg["z_turned"].sem, batch(sg["z_turned"], i, b))
            dve.tensor_copy(a["zT"][:, s, :], Z[:, 0:KEYS]).then_inc(sg["zT_ready"].sem, 1)

        def prep(i):
            m = 0 if i is None else 1
            norm.dve_apply(dve, i)
            dve.wait_ge(misc.w.sem, misc.v(misc.w, i, m + 1))
            link(dve.tensor_scalar(k.xnT[:, :], M[:, 0:P], col["x_scale"], col["x_bias"], ALU.mult, ALU.add))
            dve.tensor_copy(xrep[:, :].rearrange("p (b j q) -> p b j q", b=NB, j=4),
                            bc(k.xnT[:, :].rearrange("p (b q) -> p b q", b=NB), 2, 4)).then_inc(misc.r.sem, 1)
            dve.wait_ge(misc.w.sem, misc.v(misc.w, i, m + 2))
            dve.tensor_tensor(a["nsr"][:, :].rearrange("p (u j) -> p u j", j=4),
                              M[:, 0:64].rearrange("p (u j) -> p u j", j=4), bc(k.c("quad"), 1, 16), ALU.mult
                              ).then_inc(misc.r.sem, 1)
            dve.wait_ge(misc.r.sem, misc.v(misc.r, i, m + 2))
            link(dve.tensor_reduce(a["ns"][:, :], a["nsr"][:, :].rearrange("p (u j) -> p u j", j=4), X_AXIS, ALU.add))
            if i is not None:
                link(dve.tensor_scalar(a["batch"][:, :], a["batch"][:, :], -float(NB), None, ALU.add))
            dve.tensor_tensor(sel[:, :, :], bc(k.c("expert_no")[:, 0:NB], 2, P),
                              bc(a["batch"][:, 0:1].to_broadcast([P, NB]), 2, P), ALU.is_equal
                              ).then_inc(sg["null_ready"].sem, 1)

        def normalise(i, u):
            dve.wait_ge(sg["exp_ready"].sem, sg["exp_ready"].at(i, u + 1))
            link(dve.reciprocal(a["rr"][:, u:u + 1], a["rs"][:, u:u + 1]))
            dve.tensor_tensor(a["pn"][:, u:u + 1], a["p"][:, u % 4, KEYS:W], a["rr"][:, u:u + 1], ALU.mult)
            dve.tensor_scalar(a["p"][:, u % 4, 0:KEYS], a["p"][:, u % 4, 0:KEYS], a["rr"][:, u:u + 1], None, ALU.mult
                              ).then_inc(sg["probs_ready"].sem, 1)

        def gather(i, b):
            dve.wait_ge(sg["pv_done"].sem, sg["pv_done"].at(i, 4 * b + 4))
            dve.tensor_copy(pc[:, :, 32 * b:32 * b + 32], PC[b % 2].rearrange("p (h q) -> p h q", h=16)
                            ).then_inc(sg["pc_read"].sem, 1)

        def heads(n):
            return k.psum[:, 2 * n:2 * n + 2, :].rearrange("p a (c m) -> p a c m", m=P)

        def of_heads(t, n):
            return t.rearrange("p (a c o) m -> p o a c m", o=2, a=2)[:, n]

        norm.dve_stats(dve, chain, None)
        for src, dst in (("wkT", "kb"), ("wvT", "vb")):
            link(dve.tensor_tensor(setup, a[src], bc(a["cb_row"], 1, 8), ALU.mult))
            link(dve.tensor_reduce(a[dst], setup, X_AXIS, ALU.add))
        link(dve.tensor_scalar(a["kb"], a["kb"], col["null_key"], -1.0, ALU.subtract, ALU.mult))
        link(dve.tensor_scalar(a["nsr"][:, 0:8], a["vb"], col["null_value"], -1.0, ALU.subtract, ALU.mult))
        link(dve.tensor_tensor(a["rhsU"], bc(a["kb"], 2, 16), k.c("pair_head").rearrange("p (c h) -> p c h", c=8),
                               ALU.mult))
        for c in range(8):
            link(dve.tensor_tensor(setup[:, c, :].rearrange("p (j q) -> p j q", j=4),
                                   a["nsr"][:, c:c + 1].unsqueeze(2).to_broadcast([P, 4, 32]),
                                   bc(k.c("pair_in_group")[:, 4 * (c % 2):4 * (c % 2) + 4], 2, 32), ALU.mult))
        link(dve.tensor_scalar(bias[:, :], mask[:, :], -1.0, 1e30, ALU.add, ALU.mult))
        dve.tensor_copy(a["batch"][:, :], k.c("row_no")).then_inc(sg["setup_read"].sem, 1)
        dve.wait_ge(sg["setup_written"].sem, sg["setup_written"].before(1))
        for n in range(2):
            link(dve.tensor_scalar(of_heads(a["N"], n), heads(n), col["c_scale"], None, ALU.mult))
        dve.memset(k.carrier[:, :], 0.0).then_inc(sg["setup_read"].sem, 1)
        dve.wait_ge(sg["setup_written"].sem, sg["setup_written"].before(2))
        for n in range(2):
            for h in range(2):
                link(dve.scalar_tensor_tensor(out=of_heads(a["G"], n)[:, h], in0=heads(n)[:, h], scalar=0.25,
                                              in1=bc(a["cs_row"], 1, 4), op0=ALU.mult, op1=ALU.mult))
        dve.memset(k.carrier[:, :], 0.0).then_inc(sg["setup_read"].sem, 1)
        dve.wait_ge(sg["setup_written"].sem, sg["setup_written"].before(3))
        link(dve.tensor_scalar(a["U"], k.bank[0][:, 0:16], 0.25, None, ALU.mult))
        link(dve.tensor_copy(a["null_value"], k.bank[1].rearrange("p (t c) -> p t c", t=4)))
        dve.tensor_copy(setup, bc(a["vb"], 2, P)).then_inc(sg["setup_read"].sem, 1)
        dve.wait_ge(sg["setup_written"].sem, sg["setup_written"].before(4))
        dve.tensor_copy(a["row"], k.bank[2][:, 0:P]).then_inc(sg["setup_read"].sem, 1)
        prep(None)
        centre(None, 0)
        var_out(None, 0)
        z(None, 0)
        with dve.Fori(0, TILES) as i:
            chain.round(i)
            for u in range(16):
                b, t = divmod(u, 4)
                dve.wait_ge(sg["scores_written"].sem, sg["scores_written"].at(i, u + 1))
                dve.tensor_reduce(a["negm"][:, u:u + 1], S[u % 2][:, 0:W], X_AXIS, ALU.max, negate=True
                                  ).then_inc(sg["max_ready"].sem, 1)
                if t == 0:
                    centre(i, b)
                if u >= 1:
                    normalise(i, u - 1)
                if t == 1:
                    var_out(i, b)
                if u == 2:
                    norm.dve_stats(dve, chain, i)
                if t == 3 and b >= 1:
                    gather(i, b - 1)
                if t == 3:
                    z(i, b)
            normalise(i, 15)
            dve.wait_ge(sg["probs_ready"].sem, sg["probs_ready"].at(i, 16))
            for t in range(4):
                ins = dve.tensor_tensor(a["null_left"][:, t * P:(t + 1) * P].rearrange("p (b q) -> p b q", b=NB),
                                        bc(a["pn"][:, :].rearrange("p (b t) -> p b t", t=4)[:, :, t], 2, 32),
                                        bc(k.c("query"), 1, NB), ALU.mult)
            ins.then_inc(sg["null_left_ready"].sem, 1)
            gather(i, 3)
            dve.wait_ge(misc.w.sem, misc.w.at(i, 1))
            dve.tensor_tensor(a["y"], M[:, 0:P], a["row"], ALU.add).then_inc(misc.r.sem, 1)
            dve.wait_ge(misc.r.sem, misc.r.at(i, 1))
            link(dve.bn_stats(k.stat[:, :], a["y"]))
            dve.memset(k.carrier[:, :], 0.0)
            dve.bn_aggr(k.out_meanvar[:, :], k.stat[:, :]).then_inc(sg["out_var_ready"].sem, 1)
            dve.wait_ge(sg["out_rstd_ready"].sem, sg["out_rstd_ready"].at(i, 1))
            link(dve.tensor_scalar(a["y"], a["y"], k.out_meanvar[:, 0:1], k.rstd_second[:, 0:1], ALU.subtract, ALU.mult))
            link(dve.tensor_tensor(a["y"], a["y"], a["xs_row"], ALU.mult))
            link(dve.tensor_tensor(a["y"], a["y"], a["xb_row"], ALU.add))
            x = k.X[:, i, :]
            link(dve.tensor_tensor(x, x, a["y"], ALU.add))
            prep(i)
        chain.i = i
        chain.done()

    return {"sync": sp, "pool": pool, "tensor": pe, "scalar": act, "vector": dve}


def linear_attention(k, s):
    norm = Norm(k)
    misc = Misc(k, 3, 2, 7)
    heads, chunks = 16, 8
    chain_c = k.sig("vector_step").stage(4, 5)
    sg = {n: k.sig(n).stage(per, first) for n, (per, first) in {
        "proj_ready": (0, 1), "feature_w_written": (0, 1), "feature_w_read": (0, 1), "features_written": (1, 0),
        "q_features_ready": (1, 0), "k_features_ready": (1, 0), "products_written": (2, 0), "masked": (2, 0),
        "pv_done": (1, 0), "heads_ready": (1, 0),
    }.items()}
    wqkv = k.load("L0_attn_qkv", [P, 2, P])
    wv, wo = k.load("L0_attn_v", [P, P]), k.load("L0_attn_out", [P, P])
    proj, bqk = k.load("L0_attn_proj", [P, 64]), k.load("L0_attn_bqk", [P, 2])
    bv, bo = k.rows("L0_attn_bv", P), k.rows("L0_attn_bout", P)
    M, O = k.bank[7], k.bank[6]

    def cols(n):
        return slice(n * P, (n + 1) * P)

    def product_bank(h):
        n = h // 2
        return k.bank[(4 if h % 2 == 0 else 0) + n // 4][:, cols(n % 4)]

    def pool(pool):
        norm.pool(pool, None)
        with pool.Fori(0, TILES) as i:
            norm.pool(pool, i)

    def pe(pe):
        def prep(i):
            pe.wait_ge(norm.xn.sem, norm.count(norm.xn, i))
            pe.wait_ge(misc.r.sem, misc.v(misc.r, i, 0))
            pe.transpose(M[:, 0:P], k.xn[:, :], k.c("ident")).then_inc(misc.w.sem, 1)
            pe.wait_ge(misc.r.sem, misc.v(misc.r, i, 1))
            pe.matmul(M[:, 0:P], k.xnT[:, :], wv[:, :], start=True, stop=True).then_inc(misc.w.sem, 1)

        pe.wait_ge(sg["proj_ready"].sem, sg["proj_ready"].before(1))
        for n in range(2):
            for h in range(2):
                pe.matmul(k.bank[2 * n + h][:, :], wqkv[:, n, :], s["head_proj"][:, 512 * h:512 * h + 512],
                          start=True, stop=True)
            for c in range(chunks):
                mm = pe.matmul(k.bank[4][:, 8 * n + c:8 * n + c + 1], s["head_proj"][:, cols(c)], bqk[:, n:n + 1],
                               start=True, stop=True, skip_group_check=True)
        mm.then_inc(sg["feature_w_written"].sem, 1)
        prep(None)
        pe.wait_ge(sg["feature_w_read"].sem, sg["feature_w_read"].before(1))
        with pe.Fori(0, TILES) as i:
            pe.wait_ge(misc.r.sem, misc.r.at(i, 0))
            pe.wait_ge(sg["masked"].sem, sg["masked"].at(i, 0))
            for n in range(2):
                for c in range(chunks):
                    mm = pe.matmul(k.bank[2 * n + c // 4][:, cols(c % 4)], s["feature_w"][:, n, cols(c)], k.xnT[:, :],
                                   start=True, stop=True, skip_group_check=True)
            mm.then_inc(sg["features_written"].sem, 1)
            pe.wait_ge(sg["q_features_ready"].sem, sg["q_features_ready"].at(i, 1))
            pe.wait_ge(sg["k_features_ready"].sem, sg["k_features_ready"].at(i, 1))
            for odd in range(2):
                rows = slice(64 * odd, 64 * odd + 64)
                for c in range(chunks):
                    mm = pe.matmul(product_bank(2 * c + odd), s["feature"][rows, 1, cols(c)], s["feature"][rows, 0, cols(c)],
                                   start=True, stop=True, skip_group_check=True)
                mm.then_inc(sg["products_written"].sem, 1)
            pe.wait_ge(sg["masked"].sem, sg["masked"].at(i, 2))
            for n in range(2):
                for h in range(heads):
                    if n == 0:
                        left = s["vz"][:, 120 * h + 120:120 * h + 120 + P]
                    else:
                        left = k.c("head_window")[:, 120 - 8 * h:120 - 8 * h + P]
                    mm = pe.matmul(O[:, cols(n)], left, s["am"][:, 8 * (h % 2) + h // 2, :],
                                   start=(h == 0), stop=(h == heads - 1), skip_group_check=True)
            mm.then_inc(sg["pv_done"].sem, 1)
            prep(i)
            pe.wait_ge(sg["heads_ready"].sem, sg["heads_ready"].at(i, 1))
            pe.wait_ge(misc.r.sem, misc.r.at(i, 2))
            pe.matmul(M[:, 0:P], s["outT"][:, 0, :], wo[:, :], start=True, stop=True).then_inc(misc.w.sem, 1)

    def act(act):
        with act.Fori(0, TILES) as i:
            act.wait_ge(sg["features_written"].sem, sg["features_written"].at(i, 1))
            for c in range(chunks):
                ins = act.activation(s["feature"][:, 0, cols(c)], k.bank[c // 4][:, cols(c % 4)], ACT.Relu,
                                     bias=s["feature_bias"][:, c:c + 1])
            ins.then_inc(sg["q_features_ready"].sem, 1)

    def dve(dve):
        chain = Chain(dve, chain_c)
        link = chain.link

        def prep_x(i):
            norm.dve_apply(dve, i)
            dve.wait_ge(misc.w.sem, misc.v(misc.w, i, 1))
            dve.tensor_copy(k.xnT[:, :], M[:, 0:P]).then_inc(misc.r.sem, 1)

        def prep_v(i):
            dve.wait_ge(misc.w.sem, misc.v(misc.w, i, 2))
            dve.tensor_tensor(s["vz"][:, :].rearrange("p (h c) -> p h c", h=heads)[:, :, 120:128],
                              M[:, 0:P].rearrange("p (h d) -> p h d", h=heads),
                              bv[:, :].rearrange("p (h d) -> p h d", h=heads), ALU.add).then_inc(misc.r.sem, 1)

        norm.dve_stats(dve, chain, None)
        dve.tensor_tensor(s["head_proj"][:, :].rearrange("p (h m) -> p h m", h=heads), bc(proj[:, :], 1, heads),
                          bc(k.c("head16"), 2, 64), ALU.mult).then_inc(sg["proj_ready"].sem, 1)
        link(dve.memset(s["vz"][:, :], 0.0))
        dve.wait_ge(sg["feature_w_written"].sem, sg["feature_w_written"].before(1))
        for n in range(2):
            link(dve.tensor_copy(s["feature_w"][:, n, :].rearrange("p (a b) -> p a b", a=2),
                                 k.psum[:, 2 * n:2 * n + 2, :]))
        link(dve.tensor_copy(s["feature_bias"][:, :], k.bank[4][:, 0:16]))
        dve.memset(k.carrier[:, :], 0.0).then_inc(sg["feature_w_read"].sem, 1)
        prep_x(None)
        prep_v(None)
        with dve.Fori(0, TILES) as i:
            chain.round(i)
            norm.dve_stats(dve, chain, i)
            dve.wait_ge(sg["features_written"].sem, sg["features_written"].at(i, 1))
            for c in range(chunks):
                ins = dve.tensor_scalar(s["feature"][:, 1, cols(c)], k.bank[2 + c // 4][:, cols(c % 4)],
                                        s["feature_bias"][:, 8 + c:9 + c], 0.0, ALU.add, ALU.max)
            ins.then_inc(sg["k_features_ready"].sem, 1)
            for odd in range(2):
                dve.wait_ge(sg["products_written"].sem, sg["products_written"].at(i, odd + 1))
                b = 4 if odd == 0 else 0
                dve.tensor_tensor(s["am"][:, 8 * odd:8 * odd + 8, :].rearrange("p (a n) q -> p a n q", a=2),
                                  k.psum[:, b:b + 2, :].rearrange("p a (n q) -> p a n q", q=P),
                                  bc(bc(k.c("causal_T"), 1, 4), 1, 2), ALU.mult).then_inc(sg["masked"].sem, 1)
            prep_x(i)
            dve.wait_ge(sg["pv_done"].sem, sg["pv_done"].at(i, 1))
            prep_v(i)
            link(dve.tensor_scalar(s["den"][:, :], O[:, P:2 * P], 1e-6, None, ALU.add))
            link(dve.reciprocal(s["den"][:, :], s["den"][:, :]))
            dve.tensor_tensor(s["outT"][:, 0, :], O[:, 0:P], s["den"][:, :], ALU.mult).then_inc(sg["heads_ready"].sem, 1)
            dve.wait_ge(misc.w.sem, misc.w.at(i, 3))
            dve.tensor_tensor(s["tmp"][:, :], M[:, 0:P], bo[:, :], ALU.add).then_inc(misc.r.sem, 1)
            dve.wait_ge(misc.r.sem, misc.r.at(i, 3))
            x = k.X[:, i, :]
            link(dve.tensor_tensor(x, x, s["tmp"][:, :], ALU.add))
        chain.i = i
        chain.done()

    return {"sync": lambda sp: None, "pool": pool, "tensor": pe, "scalar": act, "vector": dve}


MOE1_EXPERTS, MOE1_WIDTH, MOE1_TOP = 16, 176, 2
CAPACITY = -(-5 * BATCH * SEQ * MOE1_TOP // (4 * MOE1_EXPERTS))
MOE2_EXPERTS, MOE3_EXPERTS, MOE3_WIDTH = 6, 64, 64


def ffn_buffers(k):
    return {"ix": k.top_at, **k.scratch({
        "H": [P, 4224], "G": [P, 2, 512], "HT": [P, 2, 512], "cw": [P, 64], "lg": [P, 64], "pr": [P, 64],
        "ex": [P, 64], "m8": [P, 8], "ixf": [P, 8], "oh": [P, 2, 16], "sel": [P, P], "acc": [P, P],
        "t": [P, 2, 64], "s1": [P, 1], "s2": [P, 1], "wr": [P, P], "nm": [P, 1]})}


def feed_forward(k, kind, up_w, down_w, fb, router=None, router_b=None):
    norm = Norm(k)
    if kind == "L0":
        groups = [(192, g * 384, g * 192, None) for g in range(2)]
    elif kind == "L1":
        groups = [(176, g * 352, g * 176, g if g < MOE1_EXPERTS else None) for g in range(MOE1_EXPERTS + 1)]
    elif kind == "L2":
        groups = [(128, g * 256, g * 128, g if g < MOE2_EXPERTS else None) for g in range(MOE2_EXPERTS + 1)]
    else:
        groups = [(512, g * 512, g * 512, 8 * g) for g in range(8)] + [(64, 4096, 4096, None)]
    halves = 1 if kind == "L3" else 2
    E = {"L0": 0, "L1": MOE1_EXPERTS, "L2": MOE2_EXPERTS, "L3": MOE3_EXPERTS}[kind]
    hidden = groups[-1][2] + groups[-1][0]
    chunks = -(-hidden // P)
    quads = [list(range(q, min(q + 4, chunks))) for q in range(0, chunks, 4)]
    G, NQ = len(groups), len(quads)

    def group_of(h):
        return max(g for g, x in enumerate(groups) if x[2] <= h)

    last_group = [group_of(min(q[-1] * P + P, hidden) - 1) for q in quads]
    plan, turned, done = [], 0, 0
    for g in range(G + NQ + 1):
        step = []
        if g < G:
            while turned < NQ and last_group[turned] <= g - 2:
                step.append(("turn", turned))
                turned += 1
                if turned - done >= 2:
                    step.append(("down", done))
                    done += 1
        elif turned < NQ:
            step.append(("turn", turned))
            turned += 1
            if turned - done >= 2:
                step.append(("down", done))
                done += 1
        elif done < NQ:
            step.append(("down", done))
            done += 1
        plan.append(step)
    assert turned == NQ and done == NQ

    routed = router is not None
    nmisc = 1 + {"L0": 0, "L1": 2, "L2": 1, "L3": 1}[kind]
    misc = Misc(k, nmisc, nmisc, 7)
    U, T, Y, M = k.bank[0:3], k.bank[3:5], k.bank[5], k.bank[7]
    sg = {n: k.sig(n).stage(per, first) for n, (per, first) in {
        "up_written": (G, 0), "gate_ready": (G, 0), "hidden_ready": (G, 0), "hidden_T_written": (NQ, 0),
        "hidden_T_read": (NQ, 0), "down_used": (NQ, 0), "y_read": (1, 0),
        **({"route_exp": (1, 1)} if routed else {}),
        **({"logits_ready": (1, 1), "selected": (1, 1)} if kind == "L1" else {}),
    }.items()}
    steps = {"L0": 0, "L1": 13, "L2": 11, "L3": 11}[kind]
    chain_c = k.sig("vector_step").stage(steps + 1 + (kind == "L1"),
                                         steps + 1 + {"L0": 2, "L1": 5, "L2": 3, "L3": 3}[kind])
    wdt = I32 if kind == "L0" else F32
    up_n = halves * hidden
    up = k.load(up_w, [P, up_n], dt=wdt)
    down = k.load(down_w, [P, chunks, P], dt=wdt)
    if kind == "L0":
        up_i, down_i = up, down
        up, down = k.sb("up_dequantized", [P, up_n]), k.sb("down_dequantized", [P, chunks, P])
    H, Gt, HT, cw = fb["H"], fb["G"], fb["HT"], fb["cw"]
    if routed:
        rw = k.load(router, [P, E])
        rb = k.rows(router_b, E)

    def pool(pool):
        norm.pool(pool, None)
        with pool.Fori(0, TILES) as i:
            norm.pool(pool, i)

    def pe(pe):
        def prep(i):
            pe.wait_ge(norm.xn.sem, norm.count(norm.xn, i))
            pe.wait_ge(misc.r.sem, misc.v(misc.r, i, 0))
            pe.transpose(M[:, 0:P], k.xn[:, :], k.c("ident")).then_inc(misc.w.sem, 1)
            if routed:
                pe.wait_ge(misc.r.sem, misc.v(misc.r, i, 1))
                pe.matmul(M[:, 0:P], k.xnT[:, :], fb["wr"][:, :], start=True, stop=True).then_inc(misc.w.sem, 1)
            if kind == "L1":
                pe.wait_ge(misc.r.sem, misc.v(misc.r, i, 2))
                pe.wait_ge(sg["selected"].sem, norm.count(sg["selected"], i))
                pe.matmul(M[:, 0:P], k.c("earlier"), fb["sel"][:, :], start=True, stop=False)
                pe.matmul(M[:, 0:P], k.c("ones"), fb["acc"][:, :], start=False, stop=True).then_inc(misc.w.sem, 1)

        def turn(i, q):
            pe.wait_ge(sg["hidden_ready"].sem, sg["hidden_ready"].at(i, last_group[q] + 1))
            pe.wait_ge(sg["hidden_T_read"].sem, sg["hidden_T_read"].at(i, q - 1))
            for j, c in enumerate(quads[q]):
                mm = pe.transpose(T[q % 2][:, j * P:(j + 1) * P], H[:, c * P:(c + 1) * P], k.c("ident"))
            mm.then_inc(sg["hidden_T_written"].sem, 1)

        def downs(i, q):
            pe.wait_ge(sg["hidden_T_read"].sem, sg["hidden_T_read"].at(i, q + 1))
            if q == 0:
                pe.wait_ge(sg["y_read"].sem, sg["y_read"].at(i, 0))
            for j, c in enumerate(quads[q]):
                mm = pe.matmul(Y[:, 0:P], HT[:, q % 2, j * P:(j + 1) * P], down[:, c, :],
                               start=(c == 0), stop=(c == chunks - 1))
            mm.then_inc(sg["down_used"].sem, 1)

        prep(None)
        with pe.Fori(0, TILES) as i:
            pe.wait_ge(misc.r.sem, misc.r.at(i, 0))
            for g, step in enumerate(plan):
                if g < G:
                    fw, c0, _, _ = groups[g]
                    free = sg["hidden_ready"]
                    pe.wait_ge(free.sem, free.at(i, g - 2))
                    pe.matmul(U[g % 3][:, 0:fw * halves], k.xnT[:, :], up[:, c0:c0 + fw * halves],
                              start=True, stop=True).then_inc(sg["up_written"].sem, 1)
                for what, q in step:
                    (turn if what == "turn" else downs)(i, q)
            prep(i)

    def act(act):
        def prep(i):
            if not routed:
                return
            if kind == "L1":
                act.wait_ge(sg["logits_ready"].sem, norm.count(sg["logits_ready"], i))
                ins = act.activation(fb["ex"][:, 0:E], fb["lg"][:, 0:E], ACT.Exp, bias=fb["nm"][:, 0:1],
                                     accum_out=fb["s1"][:, :])
            else:
                act.wait_ge(misc.r.sem, misc.v(misc.r, i, 2))
                src = fb["lg"] if kind == "L2" else fb["pr"]
                ins = act.activation(fb["ex"][:, 0:E], src[:, 0:E], ACT.Exp, scale=-1.0)
            ins.then_inc(sg["route_exp"].sem, 1)

        def out(i, q):
            act.wait_ge(sg["hidden_T_written"].sem, sg["hidden_T_written"].at(i, q + 1))
            act.wait_ge(sg["down_used"].sem, sg["down_used"].at(i, q - 1))
            m = len(quads[q]) * P
            act.activation(HT[:, q % 2, 0:m], T[q % 2][:, 0:m], ACT.Copy).then_inc(sg["hidden_T_read"].sem, 1)

        prep(None)
        with act.Fori(0, TILES) as i:
            for g, step in enumerate(plan):
                if g < G:
                    fw = groups[g][0]
                    act.wait_ge(sg["up_written"].sem, sg["up_written"].at(i, g + 1))
                    act.wait_ge(sg["hidden_ready"].sem, sg["hidden_ready"].at(i, g - 1))
                    act.activation(Gt[:, g % 2, 0:fw], U[g % 3][:, 0:fw], ACT.Silu).then_inc(sg["gate_ready"].sem, 1)
                for what, q in step:
                    if what == "turn":
                        out(i, q)
            prep(i)

    def dve(dve):
        chain = Chain(dve, chain_c)
        lg, pr, ex, m8, ix, ixf, oh = (fb[n] for n in ("lg", "pr", "ex", "m8", "ix", "ixf", "oh"))
        sel, acc, t, s1, s2, nm = (fb[n] for n in ("sel", "acc", "t", "s1", "s2", "nm"))

        def top2(src):
            dve.memset(k.carrier[:, :], 0.0)
            chain.link(dve.max(m8[:, :], src))
            dve.memset(k.carrier[:, :], 0.0)
            chain.link(dve.max_index(ix[:, :], m8[:, :], src))
            chain.link(dve.tensor_copy(ixf[:, :], ix[:, :]))
            chain.link(dve.tensor_tensor(oh[:, :, :], bc(k.c("expert_no"), 1, 2), bc(ixf[:, 0:2], 2, 16), ALU.is_equal))

        def weigh(eps):
            chain.link(dve.tensor_scalar(s2[:, :], m8[:, 0:1], m8[:, 1:2], eps, ALU.add, ALU.add))
            chain.link(dve.reciprocal(s2[:, :], s2[:, :]))
            for j in range(2):
                chain.link(dve.tensor_scalar(t[:, j, 0:E], oh[:, j, 0:E], m8[:, j:j + 1], s2[:, 0:1],
                                             ALU.mult, ALU.mult))

        def route_l1(i):
            misc_r = misc.r
            dve.tensor_tensor(lg[:, 0:E], M[:, 0:E], rb[:, :], ALU.add).then_inc(misc_r.sem, 1)
            dve.wait_ge(misc_r.sem, misc.v(misc_r, i, 2))
            dve.tensor_reduce(nm[:, :], lg[:, 0:E], X_AXIS, ALU.max, negate=True).then_inc(sg["logits_ready"].sem, 1)
            dve.wait_ge(sg["route_exp"].sem, norm.count(sg["route_exp"], i))
            chain.link(dve.reciprocal(s2[:, :], s1[:, :]))
            chain.link(dve.tensor_scalar(pr[:, 0:E], ex[:, 0:E], s2[:, 0:1], None, ALU.mult))
            top2(pr[:, 0:E])
            dve.tensor_tensor(sel[:, 0:E], oh[:, 0, :], oh[:, 1, :], ALU.add).then_inc(sg["selected"].sem, 1)
            weigh(1e-9)
            chain.link(dve.tensor_tensor(lg[:, 0:E], t[:, 0, 0:E], t[:, 1, 0:E], ALU.add))
            dve.wait_ge(misc.w.sem, misc.v(misc.w, i, 3))
            chain.link(dve.tensor_scalar(pr[:, 0:E], M[:, 0:E], float(CAPACITY), None, ALU.is_lt))
            chain.link(dve.tensor_tensor(cw[:, 0:E], lg[:, 0:E], pr[:, 0:E], ALU.mult))
            dve.tensor_tensor(acc[:, 0:E], acc[:, 0:E], sel[:, 0:E], ALU.add).then_inc(misc_r.sem, 1)
            dve.wait_ge(misc_r.sem, misc.v(misc_r, i, 3))

        def route_l2(i):
            dve.tensor_tensor(lg[:, 0:E], M[:, 0:E], rb[:, :], ALU.add).then_inc(misc.r.sem, 1)
            dve.wait_ge(sg["route_exp"].sem, norm.count(sg["route_exp"], i))
            chain.link(dve.tensor_scalar(ex[:, 0:E], ex[:, 0:E], 1.0, None, ALU.add))
            chain.link(dve.reciprocal(pr[:, 0:E], ex[:, 0:E]))
            top2(pr[:, 0:8])
            weigh(1e-8)
            chain.link(dve.tensor_tensor(cw[:, 0:E], t[:, 0, 0:E], t[:, 1, 0:E], ALU.add))

        def route_l3(i):
            dve.tensor_copy(pr[:, 0:E], M[:, 0:E]).then_inc(misc.r.sem, 1)
            dve.wait_ge(misc.r.sem, misc.v(misc.r, i, 2))
            chain.link(dve.tensor_tensor(lg[:, 0:E], pr[:, 0:E], rb[:, :], ALU.add))
            dve.memset(k.carrier[:, :], 0.0)
            chain.link(dve.max(m8[:, :], lg[:, 0:E]))
            dve.memset(k.carrier[:, :], 0.0)
            chain.link(dve.match_replace(t[:, 0, :], m8[:, :], lg[:, 0:E], NEG_BIG))
            chain.link(dve.tensor_tensor(t[:, 1, :], t[:, 0, :], lg[:, 0:E], ALU.not_equal))
            dve.wait_ge(sg["route_exp"].sem, norm.count(sg["route_exp"], i))
            chain.link(dve.tensor_scalar(ex[:, 0:E], ex[:, 0:E], 1.0, None, ALU.add))
            chain.link(dve.reciprocal(lg[:, 0:E], ex[:, 0:E]))
            chain.link(dve.tensor_tensor(t[:, 0, :], lg[:, 0:E], t[:, 1, :], ALU.mult))
            chain.link(dve.tensor_reduce(s1[:, :], t[:, 0, :], X_AXIS, ALU.add))
            chain.link(dve.tensor_scalar(s2[:, :], s1[:, :], 1e-8, None, ALU.add))
            chain.link(dve.reciprocal(s2[:, :], s2[:, :]))
            chain.link(dve.tensor_scalar(cw[:, 0:E], t[:, 0, :], s2[:, 0:1], None, ALU.mult))

        def prep(i):
            norm.dve_apply(dve, i)
            dve.wait_ge(misc.w.sem, misc.v(misc.w, i, 1))
            dve.tensor_copy(k.xnT[:, :], M[:, 0:P]).then_inc(misc.r.sem, 1)
            if routed:
                dve.wait_ge(misc.w.sem, misc.v(misc.w, i, 2))
                {"L1": route_l1, "L2": route_l2, "L3": route_l3}[kind](i)

        norm.dve_stats(dve, chain, None)
        if kind == "L0":
            for dst, src in ((up, up_i), (down, down_i)):
                full = (slice(None),) * len(dst.shape)
                chain.link(dve.tensor_scalar(dst[full], src[full], float(np.float32(1.0 / 127.0)), None, ALU.mult))
        else:
            chain.link(dve.memset(fb["wr"][:, :], 0.0))
            chain.link(dve.tensor_copy(fb["wr"][:, 0:E], rw[:, :]))
        if kind == "L1":
            chain.link(dve.memset(sel[:, :], 0.0))
            chain.link(dve.memset(acc[:, :], 0.0))
        if kind == "L2":
            chain.link(dve.memset(pr[:, 0:8], -1.0))
        if hidden < chunks * P:
            chain.link(dve.memset(H[:, hidden:chunks * P], 0.0))
        prep(None)
        with dve.Fori(0, TILES) as i:
            chain.round(i)
            x = k.X[:, i, :]
            if kind == "L1":
                chain.link(dve.tensor_tensor(x, x, k.xn[:, :], ALU.add))
            dve.wait_ge(sg["hidden_T_written"].sem, sg["hidden_T_written"].at(i, 0))
            for g, (fw, c0, h0, e) in enumerate(groups):
                if kind != "L3":
                    dve.wait_ge(sg["up_written"].sem, sg["up_written"].at(i, g + 1))
                dve.wait_ge(sg["gate_ready"].sem, sg["gate_ready"].at(i, g + 1))
                h, gate = H[:, h0:h0 + fw], Gt[:, g % 2, 0:fw]
                if kind != "L3":
                    ins = dve.scalar_tensor_tensor(out=h, in0=gate, scalar=1.0 if e is None else cw[:, e:e + 1],
                                                   in1=U[g % 3][:, fw:2 * fw], op0=ALU.mult, op1=ALU.mult)
                elif e is not None:
                    ins = dve.tensor_tensor(h.rearrange("p (e f) -> p e f", f=MOE3_WIDTH),
                                            gate.rearrange("p (e f) -> p e f", f=MOE3_WIDTH),
                                            bc(cw[:, e:e + 8], 2, MOE3_WIDTH), ALU.mult)
                else:
                    ins = dve.tensor_copy(h, gate)
                ins.then_inc(sg["hidden_ready"].sem, 1)
                if g == 1:
                    norm.dve_stats(dve, chain, i)
            dve.wait_ge(sg["down_used"].sem, sg["down_used"].at(i, NQ))
            dve.tensor_tensor(x, x, Y[:, 0:P], ALU.add).then_inc(sg["y_read"].sem, 1)
            prep(i)
        chain.i = i
        chain.done()

    return {"sync": lambda sp: None, "pool": pool, "tensor": pe, "scalar": act, "vector": dve}


NEG_BIG = -3.0e38


STAGES = ["L0_xattn", "L0_attn", "L0_ffn", "L1_xattn", "L1_attn", "L1_ffn", "L2_xattn", "L2_attn", "L2_ffn", "L3_xattn", "L3_attn", "L3_ffn"]


def perceiver(nc, dram, out):
    with ExitStack() as ctx:
        k = Core(nc, ctx, dram)
        shared = cross_buffers(k)
        fb = ffn_buffers(k)
        stages = []
        for n, name in enumerate(STAGES):
            k.stage_no = n
            if name == "L1_xattn":
                stages.append(cross_attention(k, "L1x", "L1_xattn_Wq", "L1_xattn_bq", "L1_xattn_Wk", "L1_xattn_bk",
                                              "L1_xattn_Wv", "L1_xattn_bv", "L1_xattn_Wo", "L1_xattn_bo", True, shared))
            if name == "L0_xattn":
                stages.append(null_key_attention(k))
            if name == "L0_attn":
                stages.append(linear_attention(k, self_buffers(k, "L0")))
            if name in ("L1_attn", "L2_attn", "L3_attn"):
                stages.append(self_attention(k, name[:2], self_buffers(k, name[:2])))
            if name == "L0_ffn":
                stages.append(feed_forward(k, "L0", "L0_ffn_up", "L0_ffn_down", fb))
            if name == "L1_ffn":
                stages.append(feed_forward(k, "L1", "L1_ffn_up", "L1_ffn_down", fb, "L1_ffn_router_w", "L1_ffn_router_b"))
            if name == "L2_ffn":
                stages.append(feed_forward(k, "L2", "L2_ffn_up", "L2_ffn_down", fb, "L2_ffn_gate_w", "L2_ffn_gate_b"))
            if name == "L3_ffn":
                stages.append(feed_forward(k, "L3", "L3_ffn_up", "L3_ffn_down", fb, "L3_ffn_centroids", "L3_ffn_expert_biases"))
            if name == "L2_xattn":
                stages.append(cross_attention(k, "L2x", None, None, "L2_xattn_Wk", "L2_xattn_bk",
                                              "L2_xattn_Wv", "L2_xattn_bv", "L2_xattn_W_o", "L2_xattn_b_o", False, shared))
            if name == "L3_xattn":
                stages.append(cross_attention(k, "L3x", "L3_xattn_wq", "L3_xattn_bq", "L3_xattn_wk", "L3_xattn_bk",
                                              "L3_xattn_wv", "L3_xattn_bv", None, None, False, shared))
        weights = [ctx.enter_context(nc.semaphore(f"weights_in_{n}")) for n in range(len(stages))]
        x_in = ctx.enter_context(nc.semaphore("x_in"))
        primed = ctx.enter_context(nc.semaphore("primed"))
        stage_done = ctx.enter_context(nc.semaphore("stage_done"))
        stored = ctx.enter_context(nc.semaphore("stored"))
        counts = [16 * sum(1 for l in k.loads if l[0] == n) for n in range(len(stages))]
        block = ctx.enter_context(nc.Block())

        def start(eng):
            eng.wait_ge(x_in, 32)
            eng.wait_ge(primed, 1)

        def run(eng, which):
            for n, st in enumerate(stages):
                if counts[n]:
                    eng.wait_ge(weights[n], counts[n])
                st[which](eng)
                eng.drain().then_inc(stage_done, 1)
                eng.wait_ge(stage_done, ENGINES * (n + 1))

        @block.sync
        def _(sp):
            sp.dma_start(k.X[:, 0:TILES, :], dram["x"]).then_inc(x_in, 16)
            sp.dma_start(k.const[:, :], dram["const"]).then_inc(x_in, 16)
            for n, dst, src in k.loads:
                shape = dst.shape
                sp.dma_start(dst[(slice(None),) * len(shape)], src).then_inc(weights[n], 16)
            start(sp)
            run(sp, "sync")
            sp.dma_start(out, k.X[:, 0:TILES, :]).then_inc(stored, 16)
            sp.wait_ge(stored, 16)

        @block.gpsimd
        def _(pool):
            pool.memset(k.minus_half[:, :], -0.5)
            pool.memset(k.ln_eps[:, :], 1e-5)
            pool.memset(k.ln_eps6[:, :], 1e-6)
            pool.memset(k.zero4[:, :], 0.0)
            pool.memset(k.X[:, TILES, :], 0.0)
            pool.memset(k.X_spare[:, 0, :], 0.0)
            for s in k.signals.values():
                pool.sem_inc(s.sem, s.PRIMED)
            pool.drain().then_inc(primed, 1)
            start(pool)
            run(pool, "pool")

        @block.scalar
        def _(act):
            start(act)
            run(act, "scalar")

        @block.tensor
        def _(pe):
            start(pe)
            run(pe, "tensor")

        @block.vector
        def _(dve):
            start(dve)
            run(dve, "vector")


def lay_out(inputs):
    a = {n: np.asarray(v) for n, v in inputs.items()}
    d = {"const": CONST}
    d["x"] = a["x"].reshape(TILES, P, P).transpose(1, 0, 2)
    ctxT = np.zeros((CTX_PAD, P, KEYS), np.float32)
    ctxT[:BATCH] = a["ctx_1024"].transpose(0, 2, 1)
    d["ctxT"] = ctxT
    for n in ("L1_xattn_Wq", "L1_xattn_bq", "L1_xattn_Wk", "L1_xattn_bk", "L1_xattn_Wv", "L1_xattn_bv", "L1_xattn_Wo",
              "L1_xattn_bo", "L3_xattn_wq", "L3_xattn_bq", "L3_xattn_wk", "L3_xattn_bk", "L3_xattn_wv", "L3_xattn_bv",
              "L2_xattn_W_o", "L2_xattn_b_o"):
        d[n] = a[n]
    kvw = a["L2_xattn_W_kv"].reshape(P, 16, 2, 8)
    kvb = a["L2_xattn_b_kv"].reshape(16, 2, 8)
    d["L2_xattn_Wk"], d["L2_xattn_Wv"] = kvw[:, :, 0].reshape(P, P), kvw[:, :, 1].reshape(P, P)
    d["L2_xattn_bk"], d["L2_xattn_bv"] = kvb[:, 0].reshape(P), kvb[:, 1].reshape(P)
    for n, w in (("Wq", "Wq"), ("Wkv_down", "Wkv_down"), ("Wk_up", "Wk_up"), ("Wv_up", "Wv_up")):
        d["L1_attn_" + n] = a["L1_attn_" + w].T
    d["L1_attn_Wo"] = a["L1_attn_Wo"].T.reshape(2, P, P).transpose(1, 0, 2)
    d["L2_attn_qkv"] = np.concatenate([a["L2_attn_w_q"], a["L2_attn_w_k"], a["L2_attn_w_v"]], 1)
    d["L2_attn_w_o"] = a["L2_attn_w_o"]
    wkv = a["L0_xattn_Wkv"]
    for n, w in (("wqT", a["L0_xattn_Wq"].T), ("wkT", wkv[:, :1024].T), ("wvT", wkv[:, 1024:].T), ("wo", a["L0_xattn_Wo"])):
        d["L0_xattn_" + n] = w.reshape(8, P, P).transpose(1, 0, 2)
    null = [np.concatenate([v, v]) for v in a["L0_xattn_null_kv"]]
    d["L0_xattn_cols"] = np.stack([a["L0_xattn_ln1_s"], a["L0_xattn_ln1_b"], a["L0_xattn_lnc_s"], *null, null[0]], 1)
    d["L0_xattn_mask"] = a["mask_BxS2_bf1"].view(np.uint8)
    for n in ("lno_s", "lno_b", "lnc_s", "lnc_b"):
        d["L0_xattn_" + n] = a["L0_xattn_" + n]
    d["L0_attn_qkv"] = a["L0_attn_Wqkv"][:2 * P].reshape(2, P, P).transpose(1, 0, 2)
    d["L0_attn_v"], d["L0_attn_out"] = a["L0_attn_Wqkv"][2 * P:].T, a["L0_attn_Wout"].T
    d["L0_attn_proj"] = a["L0_attn_proj"].reshape(P, 64)
    d["L0_attn_bqk"] = a["L0_attn_bqkv"][:2 * P].reshape(2, P).T
    d["L0_attn_bv"], d["L0_attn_bout"] = a["L0_attn_bqkv"][2 * P:], a["L0_attn_bout"]
    for n in "qkvo":
        d["L3_attn_W" + n] = a["L3_attn_W" + n].T

    def by_chunk(w):
        n = -(-w.shape[0] // P)
        out = np.zeros((n * P, P), w.dtype)
        out[:w.shape[0]] = w
        return out.reshape(n, P, P).transpose(1, 0, 2)

    g, u = (a[f"L0_ffn_w_{n}"].T.reshape(P, 2, 1, 192) for n in ("gate", "up"))
    d["L0_ffn_up"] = np.concatenate([g, u], 2).reshape(P, -1)
    d["L0_ffn_down"] = by_chunk(a["L0_ffn_w_down"].T)
    g = np.concatenate([a["L1_ffn_w_gate"], a["L1_ffn_sw_gate"][None]])
    u = np.concatenate([a["L1_ffn_w_up"], a["L1_ffn_sw_up"][None]])
    d["L1_ffn_up"] = np.stack([g, u], 2).transpose(1, 0, 2, 3).reshape(P, -1)
    d["L1_ffn_down"] = by_chunk(np.concatenate([a["L1_ffn_w_down"], a["L1_ffn_sw_down"][None]]).reshape(-1, P))
    d["L1_ffn_router_w"], d["L1_ffn_router_b"] = a["L1_ffn_router_w"], a["L1_ffn_router_b"]
    g = np.concatenate([a["L2_ffn_ew1"], a["L2_ffn_fc1"][None]]).transpose(2, 0, 1)
    u = np.concatenate([a["L2_ffn_ew3"], a["L2_ffn_fc2"][None]]).transpose(2, 0, 1)
    d["L2_ffn_up"] = np.stack([g, u], 2).reshape(P, -1)
    d["L2_ffn_down"] = by_chunk(np.concatenate([a["L2_ffn_ew2"], a["L2_ffn_fc3"][None]]).transpose(0, 2, 1).reshape(-1, P))
    d["L2_ffn_gate_w"], d["L2_ffn_gate_b"] = a["L2_ffn_gate_w"].T, a["L2_ffn_gate_b"]
    d["L3_ffn_up"] = np.concatenate([a["L3_ffn_W_up"].transpose(1, 0, 2).reshape(P, -1), a["L3_ffn_Ws_up"]], 1)
    d["L3_ffn_down"] = by_chunk(np.concatenate([a["L3_ffn_W_down"].reshape(-1, P), a["L3_ffn_Ws_down"]]))
    d["L3_ffn_centroids"], d["L3_ffn_expert_biases"] = a["L3_ffn_centroids"].T, a["L3_ffn_expert_biases"]
    return {n: np.ascontiguousarray(v) for n, v in d.items()}


def kernel(**inputs):
    import concourse.bacc as _bacc
    from concourse import mybir as _mybir
    from concourse.bass_utils import run_bass_kernel_spmd as _run

    nc = _bacc.Bacc("TRN2", target_bir_lowering=False, num_devices=1)
    arrays, dram = {}, {}
    for name, v in lay_out(inputs).items():
        arrays[f"in_{name}"] = v
        dram[name] = nc.dram_tensor(f"in_{name}", v.shape, _mybir.dt.from_np(v.dtype), kind="ExternalInput").ap()
    out = nc.dram_tensor("out_0", (P, TILES, P), F32, kind="ExternalOutput").ap()
    perceiver(nc, dram, out)
    r = _run(nc, [arrays], core_ids=[0])
    return np.ascontiguousarray(r.results[0]["out_0"].transpose(1, 0, 2)).reshape(BATCH, SEQ, P)
```

```python
from contextlib import ExitStack

import numpy as np

import concourse.bass as bass
from concourse import mybir

F32 = mybir.dt.float32
BF16 = mybir.dt.bfloat16
U8 = mybir.dt.uint8
U32 = mybir.dt.uint32
I32 = mybir.dt.int32
ALU = mybir.AluOpType
ACT = mybir.ActivationFunctionType
X_AXIS = mybir.AxisListType.X

P = 128
BATCH, SEQ, KEYS = 128, 32, 257
TILES = BATCH * SEQ // P
NB = P // SEQ
CTX_PAD = BATCH + NB
ENGINES = 5


def bc(ap, axis, n):
    u = ap.unsqueeze(axis)
    shape = list(u.shape)
    shape[axis] = n
    return u.to_broadcast(shape)


class Signal:

    PRIMED = 64

    def __init__(self, sem):
        self.sem = sem
        self.count = self.PRIMED

    def stage(self, per, first=0, last=0):
        return Counted(self, per, first, last)


class Counted:

    def __init__(self, signal, per, first, last):
        self.sem, self.base, self.per, self.first, self.last = signal.sem, signal.count, per, first, last
        signal.count += first + per * TILES + last

    def before(self, n):
        return self.base + n

    def at(self, i, n):
        return i * self.per + (self.base + self.first + n)


class Chain:

    def __init__(self, eng, counted):
        self.eng, self.c, self.i, self.n = eng, counted, None, 0

    def round(self, i):
        assert self.i is not None or self.n == self.c.first, self.n
        assert self.i is None or self.n == self.c.per, self.n
        self.i, self.n = i, 0

    def done(self):
        last = self.i is not None and self.i is TILES
        assert self.n == (self.c.last if last else self.c.first if self.i is None else self.c.per), self.n

    def link(self, ins):
        self.n += 1
        ins.then_inc(self.c.sem, 1)
        self.eng.wait_ge(self.c.sem, self.c.before(self.n) if self.i is None else self.c.at(self.i, self.n))


def constants():
    p = np.arange(P)
    cols = {}
    cols["ident"] = np.eye(P)
    cols["lane"] = (p[:, None] % 32) // 8 == np.arange(4)[None]
    cols["lane_scaled"] = cols["lane"] / np.sqrt(8.0)
    cols["lane_eighth"] = cols["lane"] / 8.0
    cols["quad"] = p[:, None] // 32 == np.arange(4)[None]
    cols["query"] = p[:, None] % 32 == np.arange(32)[None]
    cols["earlier"] = p[:, None] < p[None]
    cols["ones"] = np.ones((P, P))
    win = np.zeros((P, 7, 32))
    win[:, 3] = p[:, None] % 32 == np.arange(32)[None]
    cols["query_window"] = win.reshape(P, -1)
    cols["quad_scaled"] = cols["quad"] / np.sqrt(32.0)
    cols["causal"] = np.arange(32)[None] <= p[:, None] % 32
    cols["causal_T"] = (p[:, None] // 32 == p[None] // 32) & (p[:, None] <= p[None])
    cols["same_head"] = p[:, None] // 8 == p[None] // 8
    cols["head16"] = p[:, None] // 8 == np.arange(16)[None]
    win = np.zeros((P, 248))
    win[:, 120:128] = 1
    cols["head_window"] = win
    inv = np.float32(1.0) / np.float32(10000.0) ** (np.arange(0, 8, 2, dtype=np.float32) / np.float32(8))
    freq = (p % SEQ).astype(np.float32)[:, None] * inv[None]
    cols["cos"], cols["sin"] = np.cos(freq), np.sin(freq)
    cols["row_no"] = p[:, None]
    cols["pair_head"] = (np.arange(16)[None, None] == 2 * np.arange(8)[None, :, None] + p[:, None, None] // 64).reshape(P, -1)
    cols["pair_in_group"] = (np.arange(4)[None, None] == 2 * np.arange(2)[None, :, None] + p[:, None, None] // 64).reshape(P, -1)
    cols["mean_of"] = np.full((P, P), 1.0 / P)
    c = np.arange(P)[None, None]
    cols["own_lane"] = ((c // 32 == p[:, None, None] % 4) & ((c % 32) // 8 == np.arange(4)[None, :, None])).reshape(P, -1)
    cols["row_batch"] = p[:, None] // 4 == np.arange(4)[None]
    cols["minus_one"] = np.full((P, 4), -1.0)
    cols["expert_no"] = np.tile(np.arange(16)[None], (P, 1))
    cols["last_key"] = p[:, None] == np.arange(16)[None]
    out, at, parts = {}, 0, []
    for name, a in cols.items():
        out[name] = (at, a.shape[1])
        at += a.shape[1]
        parts.append(np.asarray(a, np.float32))
    return np.ascontiguousarray(np.concatenate(parts, 1)), out


CONST, CONST_AT = constants()


X0_STEPS = 24, 27, 6
SCRATCH = 16100


class Core:

    def __init__(self, nc, ctx, dram):
        self.nc, self.ctx, self.dram = nc, ctx, dram
        self.loads = []
        self.stage_no = 0
        self.X_spare = self.sb("x_tokens", [P, TILES + 2, P])
        self.X = self.X_spare[:, 1:TILES + 2, :]
        self.const = self.sb("consts", [P, CONST.shape[1]])
        self.psum = ctx.enter_context(nc.psum_tensor("psum_banks", [P, 8, 512], F32))
        self.bank = [self.psum[:, b, :] for b in range(8)]
        self.stat = self.sb("ln_stat", [P, 6])
        self.meanvar = self.sb("ln_meanvar", [P, 2])
        self.vareps = self.sb("ln_vareps", [P, 1])
        self.rstd = self.sb("ln_rstd", [P, 1])
        self.rstd_first = self.sb("ln_rstd_first", [P, 1])
        self.rstd_second = self.sb("ln_rstd_second", [P, 1])
        self.ln_eps6 = self.sb("ln_eps6", [P, 1])
        self.minus_half = self.sb("minus_half", [P, 32])
        self.ln_eps = self.sb("ln_eps", [P, 1])
        self.xn = self.sb("x_normed", [P, P])
        self.xnT = self.sb("x_normed_T", [P, P])
        self.carrier = self.sb("wait_carrier", [P, 1])
        self.zero4 = self.sb("zero4", [P, 4])
        self.mask_in = self.sb("mask_in", [P, KEYS], U8)
        self.mask_bias = self.sb("mask_bias", [P, KEYS], BF16)
        self.batch_select = self.sb("batch_select", [P, NB, P], BF16)
        self.out_meanvar = self.sb("out_meanvar", [P, 2])
        self.out_vareps = self.sb("out_vareps", [P, 1])
        self.out_stat = self.sb("out_stat", [P, 6])
        self.out_rstd = self.sb("out_rstd", [P, 1])
        self.top_at = self.sb("route_top_at", [P, 8], U32)
        self.area = self.sb("scratch", [P, SCRATCH])
        self.signals = {}

    def sb(self, name, shape, dt=F32):
        return self.ctx.enter_context(self.nc.sbuf_tensor(name, shape, dt))

    def scratch(self, shapes):
        out, at = {}, 0
        for name, shape in shapes.items():
            n = int(np.prod(shape[1:]))
            t = self.area[0:shape[0], at:at + n]
            if len(shape) == 3:
                t = t.rearrange("p (a b) -> p a b", a=shape[1])
            if len(shape) == 4:
                t = t.rearrange("p (a b c) -> p a b c", a=shape[1], b=shape[2])
            out[name] = t
            at += n
        assert at <= SCRATCH, at
        return out

    def sig(self, name):
        if name not in self.signals:
            self.signals[name] = Signal(self.ctx.enter_context(self.nc.semaphore(name)))
        return self.signals[name]

    def c(self, name):
        a, n = CONST_AT[name]
        return self.const[:, a:a + n]

    def load(self, name, shape, src=None, dt=F32):
        t = self.sb("w_" + name, shape, dt)
        self.loads.append((self.stage_no, t, self.dram[name] if src is None else src))
        return t

    def rows(self, name, n):
        t = self.sb("r_" + name, [P, n])
        self.loads.append((self.stage_no, t, self.dram[name].partition_broadcast(P)))
        return t

    def column(self, name):
        t = self.sb("c_" + name, [P, 1])
        self.loads.append((self.stage_no, t, self.dram[name].rearrange("(p a) -> p a", a=1)))
        return t


class Norm:

    def __init__(self, k, twice=False):
        self.k, self.twice = k, twice
        self.var = k.sig("ln_var_ready").stage(1, 1)
        self.rs = k.sig("ln_rstd_ready").stage(1, 1)
        self.xn = k.sig("xn_ready").stage(1, 1)
        self.pool_step = k.sig("pool_ln_step").stage(*((6, 6) if twice else (1, 1)))

    @staticmethod
    def count(c, i):
        return c.before(1) if i is None else c.at(i, 1)

    @staticmethod
    def tile(i):
        return 0 if i is None else i + 1

    def dve_stats(self, dve, chain, i):
        k = self.k
        chain.link(dve.bn_stats(k.stat[:, :], k.X[:, self.tile(i), :]))
        dve.memset(k.carrier[:, :], 0.0)
        dve.bn_aggr(k.meanvar[:, :], k.stat[:, :]).then_inc(self.var.sem, 1)

    def pool(self, pool, i):
        k = self.k
        pool.wait_ge(self.var.sem, self.count(self.var, i))
        pool.tensor_tensor(k.vareps[:, :], k.meanvar[:, 1:2], k.ln_eps[:, :], ALU.add).then_inc(self.pool_step.sem, 1)
        c, n = self.pool_step, 1

        def step(out, a, b, op):
            nonlocal n
            pool.wait_ge(c.sem, c.before(n) if i is None else c.at(i, n))
            n += 1
            return pool.tensor_tensor(out[:, :], a, b, op)

        if self.twice:
            v, r1, r2 = k.vareps, k.rstd_first, k.rstd_second
            step(r1, v[:, :], k.minus_half[:, 0:1], ALU.pow).then_inc(c.sem, 1)
            step(v, r1[:, :], r1[:, :], ALU.mult).then_inc(c.sem, 1)
            step(v, v[:, :], k.meanvar[:, 1:2], ALU.mult).then_inc(c.sem, 1)
            step(v, v[:, :], k.ln_eps6[:, :], ALU.add).then_inc(c.sem, 1)
            step(r2, v[:, :], k.minus_half[:, 0:1], ALU.pow).then_inc(c.sem, 1)
            step(k.rstd, r1[:, :], r2[:, :], ALU.mult).then_inc(self.rs.sem, 1)
        else:
            step(k.rstd, k.vareps[:, :], k.minus_half[:, 0:1], ALU.pow).then_inc(self.rs.sem, 1)

    def dve_apply(self, dve, i):
        k = self.k
        dve.wait_ge(self.rs.sem, self.count(self.rs, i))
        dve.tensor_scalar(k.xn[:, :], k.X[:, self.tile(i), :], k.meanvar[:, 0:1], k.rstd[:, 0:1],
                          ALU.subtract, ALU.mult).then_inc(self.xn.sem, 1)


class Misc:

    def __init__(self, k, per, first, bank, last=0):
        self.w = k.sig("misc_written").stage(per, first, last)
        self.r = k.sig("misc_read").stage(per, first, last)
        self.bank = k.bank[bank]

    def v(self, c, i, n):
        return c.before(n) if i is None else c.at(i, n)


def cross_attention(k, name, q_w, q_b, k_w, k_b, v_w, v_b, o_w, o_b, relu, a):
    norm = Norm(k)
    has_q, has_o = q_w is not None, o_w is not None
    finish = 2 + has_o
    misc = Misc(k, finish + 1 + has_q, 1 + has_q, 7, finish)
    S, T, KB, OB, VB, M = k.bank[0:2], k.bank[2:4], k.bank[4], k.bank[5], k.bank[6], k.bank[7]
    sg = {n: k.sig(n).stage(*v) for n, v in {
        **{f"slot{b}_loaded": (16, 16) for b in range(NB)}, "slot_freed": (2 * NB, 0), "last_key_kept": (NB, 0),
        "k_written": (NB, 1), "k_read": (NB, 1), "v_written": (NB, 1), "v_read": (NB, 1), "scores_written": (16, 0),
        "max_ready": (16, 0), "probs_ready": (16, 0), "probs_T_written": (16, 0, 2), "probs_T_read_even": (8, 0, 1), "probs_T_read_odd": (8, 0, 1),
        "pv_done": (16, 0, 3), "heads_read": (NB, 0, 1), "q_ready": (2, 2), "cleared": (0, 1),
        "sum_step": (NB, 0, 1), "sums_ready": (NB, 0, 1),
    }.items()}
    chain_c = k.sig("vector_step").stage(2, 1 + has_q, 0)
    wq = k.load(q_w, [P, P]) if has_q else None
    bq = k.column(q_b) if has_q else None
    wk, bk = k.load(k_w, [P, P]), k.column(k_b)
    wv = k.load(v_w, [P, P])
    bv_col, bv_row = k.column(v_b), k.rows(v_b, P)
    wo = k.load(o_w, [P, P]) if has_o else None
    bo = k.rows(o_b, P) if has_o else None
    slots, last_key, kT, vS, qT, qbd = (a[n] for n in ("slots", "last_key", "kT", "vS", "qT", "qbd"))
    negm, pbuf, rs, rr, w, pT = (a[n] for n in ("negm", "pbuf", "rs", "rr", "w", "pT"))
    last_w, pl, vl, vlane, om, outT, tmp, neg_bv = (
        a[n] for n in ("last_w", "pl", "vl", "vlane", "om", "outT", "tmp", "neg_bv"))
    ctxT = k.dram["ctxT"]
    LAST_WEIGHTS, HEADS, OUT, NEXT_X, NEXT_Q = 0, 1, 2, finish, finish + 1

    def at_step(s, back):
        return (s - back) % 16

    def wait_turned(eng, i, s):
        c = sg["probs_T_read_odd" if s % 2 else "probs_T_read_even"]
        eng.wait_ge(c.sem, c.at(i, s // 2 + 1))

    def sp(sp):
        for b in range(NB):
            sp.dma_start(slots[:, b, :], ctxT[b]).then_inc(sg[f"slot{b}_loaded"].sem, 16)
        with sp.Fori(0, TILES) as i:
            for b in range(NB):
                sp.wait_ge(sg["v_written"].sem, sg["v_written"].at(i, b))
                sp.sem_inc(sg["slot_freed"].sem, 1)
                sp.wait_ge(sg["last_key_kept"].sem, sg["last_key_kept"].at(i, b + 1))
                sp.sem_inc(sg["slot_freed"].sem, 1)
                sp.dma_start(slots[:, b, :], ctxT[i * NB + (NB + b)]).then_inc(sg[f"slot{b}_loaded"].sem, 16)
        for b in range(NB):
            sp.wait_ge(sg[f"slot{b}_loaded"].sem, sg[f"slot{b}_loaded"].at(TILES - 1, 16))

    def pool(pool):
        def sums(i, s):
            b = at_step(s, 6) // 4
            us = slice(4 * b, 4 * b + 4)
            st = sg["sum_step"]
            pool.wait_ge(sg["probs_ready"].sem, sg["probs_ready"].at(i, s - 2))
            pool.wait_ge(sg["heads_read"].sem, sg["heads_read"].at(i, s // 4))
            if s == 6:
                pool.wait_ge(misc.w.sem, misc.w.at(i, LAST_WEIGHTS + 1))
            pool.tensor_tensor(rr[:, us], rs[:, us], k.c("minus_one"), ALU.pow).then_inc(st.sem, 1)
            pool.wait_ge(st.sem, st.at(i, s // 4 + 1))
            pool.tensor_tensor(w[:, us, :], bc(rr[:, us], 2, 4), bc(k.c("quad"), 1, 4), ALU.mult)
            pool.tensor_tensor(last_w[:, us], pbuf[:, 4 * (b % 2):4 * (b % 2) + 4, KEYS - 1], rr[:, us], ALU.mult
                               ).then_inc(sg["sums_ready"].sem, 1)

        norm.pool(pool, None)
        pool.wait_ge(sg["cleared"].sem, sg["cleared"].before(1))
        with pool.Fori(0, TILES) as i:
            sums(i, 2)
            pool.wait_ge(misc.w.sem, misc.w.at(i, 0))
            for b in range(NB):
                pool.wait_ge(sg[f"slot{b}_loaded"].sem, sg[f"slot{b}_loaded"].at(i, 0))
                pool.tensor_tensor(last_key[:, b, :], bc(slots[:, b, KEYS - 1], 1, 4), k.zero4[:, :], ALU.add
                                   ).then_inc(sg["last_key_kept"].sem, 1)
            for s in (6, 10, 14):
                sums(i, s)
                if s == 6:
                    norm.pool(pool, i)
        sums(TILES, 2)

    def pe(pe):
        def my_turn(i, n):
            pe.wait_ge(misc.r.sem, misc.v(misc.r, i, n))

        def kv(i, b):
            s = 0 if i is None else (b + 1) % NB
            loaded = sg[f"slot{s}_loaded"]
            pe.wait_ge(loaded.sem, loaded.before(16) if i is None else loaded.at(i, 16 if s == 0 else 0))
            if i is not None:
                pe.wait_ge(sg["k_read"].sem, sg["k_read"].at(i, b))
            pe.matmul(KB[:, 0:KEYS], wk[:, :], slots[:, s, :], start=True, stop=True
                      ).then_inc(sg["k_written"].sem, 1)
            if i is not None:
                pe.wait_ge(sg["v_read"].sem, sg["v_read"].at(i, b))
            pe.matmul(VB[:, 0:P], slots[:, s, 0:P], wv[:, :], start=True, stop=True)
            pe.matmul(VB[:, P:2 * P], slots[:, s, P:2 * P], wv[:, :], start=True, stop=True
                      ).then_inc(sg["v_written"].sem, 1)

        def scores(i, u):
            b, t = divmod(u, 4)
            if u == 0 or u == 12:
                pe.wait_ge(sg["q_ready"].sem, sg["q_ready"].at(i, -1 if u == 0 else 0))
            if t == 0:
                pe.wait_ge(sg["k_read"].sem, sg["k_read"].at(i, b))
            pe.wait_ge(sg["probs_ready"].sem, sg["probs_ready"].at(i, u - 1))
            q = slice(32 * t, 32 * t + 32)
            pe.matmul(S[u % 2][:, 0:KEYS], qbd[q, b, :], kT[q, b % 2, :], start=True, stop=True
                      ).then_inc(sg["scores_written"].sem, 1)

        def turn(i, s):
            u = at_step(s, 2)
            pe.wait_ge(sg["probs_ready"].sem, sg["probs_ready"].at(i, s - 1))
            wait_turned(pe, i, s - 2)
            pe.transpose(T[u % 2][:, 0:P], pbuf[:, u % 8, 0:P], k.c("ident"))
            pe.transpose(T[u % 2][:, P:2 * P], pbuf[:, u % 8, P:2 * P], k.c("ident")
                         ).then_inc(sg["probs_T_written"].sem, 1)

        def values(i, s):
            u = at_step(s, 3)
            b, t = divmod(u, 4)
            if t == 0:
                pe.wait_ge(sg["v_read"].sem, sg["v_read"].at(i, b))
                pe.wait_ge(sg["heads_read"].sem, sg["heads_read"].at(i, b + 1))
            wait_turned(pe, i, s - 1)
            for c in range(2):
                mm = pe.matmul(OB[:, t * P:(t + 1) * P], pT[:, u % 2, c * P:(c + 1) * P], vS[:, b % 2, c, :],
                               start=(c == 0), stop=(c == 1), skip_group_check=True)
            mm.then_inc(sg["pv_done"].sem, 1)

        def finish_tile(i, s):
            if s == 3:
                my_turn(i, LAST_WEIGHTS)
                pe.wait_ge(sg["heads_read"].sem, sg["heads_read"].at(i, 1))
                pe.transpose(M[0:16, 0:P], last_w[:, :], k.c("ident")).then_inc(misc.w.sem, 1)
            if s == 5:
                my_turn(i, HEADS)
                for b in range(NB):
                    left, right = om[:, b * P:(b + 1) * P], window(k, b)
                    if not has_o:
                        left, right = right, left
                    pe.matmul(M[:, 0:P], left, right, start=(b == 0), stop=False)
                for j in range(4):
                    left, right = vlane[0:16, j, :], pl[0:16, j * P:(j + 1) * P]
                    if not has_o:
                        left, right = right, left
                    mm = pe.matmul(M[:, 0:P], left, right, start=False, stop=(j == 3))
                mm.then_inc(misc.w.sem, 1)
            if s == 7 and has_o:
                my_turn(i, OUT)
                pe.matmul(M[:, 0:P], outT[:, :], wo[:, :], start=True, stop=True).then_inc(misc.w.sem, 1)

        def next_x(i):
            m = 0 if i is None else NEXT_X
            pe.wait_ge(norm.xn.sem, norm.count(norm.xn, i))
            my_turn(i, m)
            if i is not None:
                pe.wait_ge(sg["last_key_kept"].sem, sg["last_key_kept"].at(i, NB))
                pe.matmul(M[0:16, P:2 * P], last_key.rearrange("p b t -> p (b t)"), wv[:, :],
                          start=True, stop=True, skip_group_check=True)
            pe.transpose(M[:, 0:P], k.xn[:, :], k.c("ident")).then_inc(misc.w.sem, 1)

        def next_q(i):
            my_turn(i, 1 if i is None else NEXT_Q)
            pe.matmul(M[:, 0:P], wq[:, :], k.xnT[:, :], start=True, stop=True).then_inc(misc.w.sem, 1)

        pe.wait_ge(sg["cleared"].sem, sg["cleared"].before(1))
        next_x(None)
        if has_q:
            next_q(None)
        kv(None, 0)
        with pe.Fori(0, TILES) as i:
            for s in range(16):
                scores(i, s)
                if s % 4 == 1:
                    kv(i, s // 4)
                turn(i, s)
                values(i, s)
                finish_tile(i, s)
                if s == 10:
                    next_x(i)
                if s == 12 and has_q:
                    next_q(i)
        for s in range(8):
            if s < 2:
                turn(TILES, s)
            if s < 3:
                values(TILES, s)
            finish_tile(TILES, s)

    def act(act):
        def k_out(i, b):
            kw = sg["k_written"]
            act.wait_ge(kw.sem, kw.before(1) if i is None else kw.at(i, b + 1))
            if i is not None:
                act.wait_ge(sg["scores_written"].sem, sg["scores_written"].at(i, 4 * b))
            s = 0 if i is None else (b + 1) % 2
            act.activation(kT[:, s, :], KB[:, 0:KEYS], ACT.Relu if relu else ACT.Identity, bias=bk[:, 0:1]
                           ).then_inc(sg["k_read"].sem, 1)

        def turned(i, s):
            u = at_step(s, 2)
            act.wait_ge(sg["probs_T_written"].sem, sg["probs_T_written"].at(i, s + 1))
            act.wait_ge(sg["pv_done"].sem, sg["pv_done"].at(i, s))
            act.activation(pT[:, u % 2, :], T[u % 2][:, 0:2 * P], ACT.Copy).then_inc(sg["probs_T_read_odd"].sem, 1)

        k_out(None, 0)
        act.wait_ge(sg["cleared"].sem, sg["cleared"].before(1))
        with act.Fori(0, TILES) as i:
            for u in range(16):
                act.wait_ge(sg["max_ready"].sem, sg["max_ready"].at(i, u + 1))
                act.wait_ge(sg["probs_T_written"].sem, sg["probs_T_written"].at(i, u - 5))
                if u % 4 == 0:
                    act.wait_ge(sg["heads_read"].sem, sg["heads_read"].at(i, u // 4))
                act.activation(pbuf[:, u % 8, :], S[u % 2][:, 0:KEYS], ACT.Exp, bias=negm[:, u:u + 1],
                               accum_out=rs[:, u:u + 1]).then_inc(sg["probs_ready"].sem, 1)
                if u % 4 == 1:
                    k_out(i, u // 4)
                if u % 2 == 1:
                    turned(i, u)
        turned(TILES, 1)

    def dve(dve):
        chain = Chain(dve, chain_c)
        link = chain.link

        def written(i, n):
            dve.wait_ge(misc.w.sem, misc.v(misc.w, i, n + 1))

        def spread(i, b0, b1):
            if i is not None:
                dve.wait_ge(sg["scores_written"].sem, sg["scores_written"].at(i, 4 * b1))
            dve.tensor_tensor(qbd[:, b0:b1, :].rearrange("p b (j q) -> p b j q", j=4),
                              bc(qT[:, 32 * b0:32 * b1].rearrange("p (b q) -> p b q", b=b1 - b0), 2, 4),
                              bc(bc(k.c("lane_scaled"), 1, b1 - b0), 3, SEQ), ALU.mult).then_inc(sg["q_ready"].sem, 1)

        def take_x(i):
            m = 0 if i is None else NEXT_X
            written(i, m)
            if i is not None:
                if relu:
                    link(dve.tensor_tensor(vl[0:16, :], M[0:16, P:2 * P], neg_bv[0:16, :], ALU.max))
                else:
                    link(dve.tensor_copy(vl[0:16, :], M[0:16, P:2 * P]))
                dve.tensor_tensor(vlane[0:16, :, :], bc(vl[0:16, :], 1, 4),
                                  k.c("own_lane")[0:16, :].rearrange("p (j c) -> p j c", j=4), ALU.mult)
            dve.tensor_copy((k.xnT if has_q else qT)[:, :], M[:, 0:P]).then_inc(misc.r.sem, 1)

        def take_q(i):
            m = 0 if i is None else NEXT_X
            if has_q:
                m += 1
                written(i, m)
                if relu:
                    ins = dve.tensor_scalar(qT[:, :], M[:, 0:P], bq[:, 0:1], 0.0, ALU.add, ALU.max)
                else:
                    ins = dve.tensor_scalar(qT[:, :], M[:, 0:P], bq[:, 0:1], None, ALU.add)
                ins.then_inc(misc.r.sem, 1)
            dve.wait_ge(misc.r.sem, misc.v(misc.r, i, m + 1))
            spread(i, 0, NB - 1)

        def v_out(i, b):
            vw = sg["v_written"]
            dve.wait_ge(vw.sem, vw.before(1) if i is None else vw.at(i, b + 1))
            if i is not None:
                dve.wait_ge(sg["pv_done"].sem, sg["pv_done"].at(i, 4 * b + 3))
            s = 0 if i is None else (b + 1) % 2
            dst, src = vS[:, s, :, :], VB[:, 0:2 * P].rearrange("p (c d) -> p c d", c=2)
            if relu:
                ins = dve.tensor_tensor(dst, src, bc(neg_bv[:, :], 1, 2), ALU.max)
            else:
                ins = dve.tensor_copy(dst, src)
            ins.then_inc(sg["v_read"].sem, 1)

        def turned(i, s):
            u = at_step(s, 2)
            dve.wait_ge(sg["probs_T_written"].sem, sg["probs_T_written"].at(i, s + 1))
            dve.wait_ge(sg["pv_done"].sem, sg["pv_done"].at(i, s))
            dve.tensor_copy(pT[:, u % 2, :], T[u % 2][:, 0:2 * P]).then_inc(sg["probs_T_read_even"].sem, 1)

        def heads_out(i, s):
            b = at_step(s, 7) // 4
            us = slice(4 * b, 4 * b + 4)
            dve.wait_ge(sg["sums_ready"].sem, sg["sums_ready"].at(i, (s + 1) // 4))
            dve.wait_ge(sg["pv_done"].sem, sg["pv_done"].at(i, s))
            own = k.psum[:, 5:7, :].rearrange("p b c -> p (b c)")[:, 0:640].rearrange("p (t c) -> p t c", c=160)
            dve.tensor_tensor(om[:, b * P:(b + 1) * P].rearrange("p (t j d) -> p t j d", t=4, j=4),
                              own[:, :, 0:32].rearrange("p t (j d) -> p t j d", j=4), bc(w[:, us, :], 3, 8), ALU.mult
                              ).then_inc(sg["heads_read"].sem, 1)

        def finish_tile(i, s):
            if s == 4:
                written(i, LAST_WEIGHTS)
                dve.tensor_tensor(pl[0:16, :].rearrange("p (j b q) -> p j b q", j=4, b=NB),
                                  bc(M[0:16, 0:P].rearrange("p (j q) -> p j q", j=4), 2, NB),
                                  bc(bc(k.c("row_batch")[0:16, :], 1, 4), 3, SEQ), ALU.mult).then_inc(misc.r.sem, 1)
            if s == 6:
                written(i, HEADS)
                if has_o:
                    dve.tensor_scalar(outT[:, :], M[:, 0:P], bv_col[:, 0:1], None, ALU.add).then_inc(misc.r.sem, 1)
            if s == (8 if has_o else 6):
                last = OUT if has_o else HEADS
                if has_o:
                    written(i, OUT)
                row = bo if has_o else bv_row
                dve.tensor_tensor(tmp[:, :], M[:, 0:P], row[:, :], ALU.add).then_inc(misc.r.sem, 1)
                dve.wait_ge(misc.r.sem, misc.v(misc.r, i, last + 1))
                x = k.X_spare[:, i, :]
                if has_o and relu:
                    dve.scalar_tensor_tensor(out=x, in0=tmp[:, :], scalar=0.0, in1=x, op0=ALU.max, op1=ALU.add)
                else:
                    dve.tensor_tensor(x, x, tmp[:, :], ALU.add)

        norm.dve_stats(dve, chain, None)
        if has_q:
            link(dve.tensor_scalar(neg_bv[:, :], bv_row[:, :], -1.0, None, ALU.mult))
        for t in (pbuf, pT, vS, om, last_w, vlane[0:16, :, :]):
            dve.memset(t[(slice(None),) * len(t.shape)], 0.0)
        dve.memset(OB[:, 0:P], 0.0)
        dve.memset(rs[:, :], 1.0).then_inc(sg["cleared"].sem, 1)
        norm.dve_apply(dve, None)
        take_x(None)
        take_q(None)
        spread(None, NB - 1, NB)
        v_out(None, 0)
        with dve.Fori(0, TILES) as i:
            chain.round(i)
            for s in range(16):
                dve.wait_ge(sg["scores_written"].sem, sg["scores_written"].at(i, s + 1))
                dve.tensor_reduce(negm[:, s:s + 1], S[s % 2][:, 0:KEYS], X_AXIS, ALU.max, negate=True
                                  ).then_inc(sg["max_ready"].sem, 1)
                if s % 4 == 3:
                    heads_out(i, s)
                    v_out(i, s // 4)
                if s % 2 == 0:
                    turned(i, s)
                if s == 5:
                    norm.dve_stats(dve, chain, i)
                if s == 9:
                    norm.dve_apply(dve, i)
                finish_tile(i, s)
                if s == 11:
                    take_x(i)
                if s == 13:
                    take_q(i)
            spread(i, NB - 1, NB)
        chain.round(TILES)
        for s in range(9):
            if s == 0:
                turned(TILES, s)
            if s == 3:
                heads_out(TILES, s)
            finish_tile(TILES, s)
        chain.done()

    return {"sync": sp, "pool": pool, "tensor": pe, "scalar": act, "vector": dve}


def cross_buffers(k):
    return k.scratch({"slots": [P, NB, KEYS], "last_key": [P, NB, 4], "kT": [P, 2, KEYS], "vS": [P, 2, 2, P],
                      "qT": [P, P], "qbd": [P, NB, P], "negm": [P, 16], "pbuf": [P, 8, KEYS], "rs": [P, 16],
                      "rr": [P, 16], "w": [P, 16, 4], "pT": [P, 2, 2 * P], "last_w": [P, 16], "pl": [P, 512],
                      "vl": [P, P], "vlane": [P, 4, P], "om": [P, 512], "outT": [P, P], "tmp": [P, P],
                      "neg_bv": [P, P]})


def window(k, b):
    return k.c("query_window")[:, 32 * (3 - b):32 * (7 - b)]


def self_buffers(k, kind):
    if kind == "L0":
        more = {"feature": [P, 2, 1024], "am": [P, 16, P], "vz": [P, 16 * P], "feature_w": [P, 2, 1024],
                "head_proj": [P, 1024], "feature_bias": [P, 16], "den": [P, P]}
    else:
        more = {"kT": [P, 2, P], "qbd": [P, 2, 512], "kbd": [P, 3, 512], "group": [P, P], "v": [P, 256], "vm": [P, 2, 512],
                "pr": [P, 512], "pT": [P, 512], "nm": [P, 16], "rs": [P, 16], "rr": [P, 16], "w": [P, 16, 4],
                "om": [P, 2, 512], "lat": [64, P], "qkv": [P, 192], "ra": [P, 160], "rb": [P, 160],
                "ms": [P, 20], "r": [P, 20], "kvx": [P, 256], "sq": [P, 2, P], "bd": [P, P], "abd": [P, 512],
                "D": [P, 512], "E": [P, 512], "sD": [P, 512], "sDE": [P, 512], "R": [P, 512]}
    return k.scratch({"qT": [P, 2, P], "outT": [P, 2, P], "tmp": [P, P], **more})


CAP = 50.0


def self_attention(k, kind, s):
    norm = Norm(k)
    first = 3
    misc = Misc(k, 5, first, 7)
    nt = 2 if kind == "L1" else 4
    hd = 32 if kind == "L1" else 8
    M, O = k.bank[7], k.bank[5:7]
    chain_c = k.sig("vector_step").stage(*{"L1": (11, 5), "L2": (14, 10), "L3": (22, 11)}[kind])
    sg = {n: k.sig(n).stage(per, f) for n, (per, f) in {
        "scores_written": (1, 0), "scores_read": (1, 0), "probs_ready": (1, 0), "probs_T_written": (1, 0),
        "probs_T_read": (1, 0), "pv_done": (1, 0), "heads_ready": (1, 0),
        "operands_ready": (1, 1), **({} if kind == "L1" else {"q_ready": (1, 1), "weights_ready": (1, 0)}),
        **({"square_ready": (1, 1), "rms_ready": (1, 1)} if kind == "L2" else {}),
        **({"squares_spread": (1, 1)} if kind == "L3" else {}),
    }.items()}
    weights = sg["probs_ready" if kind == "L1" else "weights_ready"]
    if kind == "L1":
        wq, wd, wku, wvu = (k.load(n, sh) for n, sh in (("L1_attn_Wq", [P, 256]), ("L1_attn_Wkv_down", [P, 64]),
                                                        ("L1_attn_Wk_up", [64, 256]), ("L1_attn_Wv_up", [64, 256])))
        wo = k.load("L1_attn_Wo", [P, 2, P])
    elif kind == "L2":
        wqkv, wo = k.load("L2_attn_qkv", [P, 192]), k.load("L2_attn_w_o", [P, P])
    else:
        wq, wk, wv, wo = (k.load(f"L3_attn_W{n}", [P, P]) for n in "qkvo")
    at = norm.count

    def rows_by_head(eng, dst, src, mask):
        return eng.tensor_tensor(dst.rearrange("p (b j q) -> p b j q", b=NB, j=4),
                                 bc(src.rearrange("p (b q) -> p b q", b=NB), 2, 4),
                                 bc(bc(mask, 1, NB), 3, SEQ), ALU.mult)

    def scores(n):
        return k.psum[:, 0:4, n * P:(n + 1) * P].rearrange("p b (t k) -> p b t k", k=32)

    def by_group(t):
        return t[:, :].rearrange("p (t b k) -> p b t k", b=NB, k=32)

    def pool(pool):
        def rms(i):
            if kind == "L2":
                pool.wait_ge(sg["square_ready"].sem, at(sg["square_ready"], i))
                pool.tensor_tensor(s["r"][:, :], s["ms"][:, :], k.minus_half[:, 0:20], ALU.pow
                                   ).then_inc(sg["rms_ready"].sem, 1)
        def spread_squares(i):
            if kind == "L3":
                if i is not None:
                    pool.wait_ge(sg["scores_written"].sem, sg["scores_written"].at(i, 1))
                pool.wait_ge(sg["q_ready"].sem, at(sg["q_ready"], i))
                rows_by_head(pool, s["abd"][:, :], s["sq"][:, 0, :], k.c("lane"))
                rows_by_head(pool, s["kbd"][:, 0, :], s["kT"][:, 0, :], k.c("quad"))
                rows_by_head(pool, s["kbd"][:, 1, :], s["sq"][:, 1, :], k.c("quad")
                             ).then_inc(sg["squares_spread"].sem, 1)

        norm.pool(pool, None)
        rms(None)
        spread_squares(None)
        with pool.Fori(0, TILES) as i:
            norm.pool(pool, i)
            rms(i)
            spread_squares(i)

    def pe(pe):
        def turn_of(i, n):
            pe.wait_ge(misc.r.sem, misc.v(misc.r, i, n))

        def prep_x(i):
            pe.wait_ge(norm.xn.sem, at(norm.xn, i))
            turn_of(i, 0)
            pe.transpose(M[:, 0:P], k.xn[:, :], k.c("ident")).then_inc(misc.w.sem, 1)

        def prep_qkv(i):
            turn_of(i, 1)
            if kind == "L1":
                for t in range(2):
                    pe.matmul(M[:, t * P:(t + 1) * P], wq[:, t * P:(t + 1) * P], k.xnT[:, :], start=True, stop=True,
                              skip_group_check=True)
                pe.matmul(M[0:64, 256:384], wd[:, :], k.xnT[:, :], start=True, stop=True, skip_group_check=True
                          ).then_inc(misc.w.sem, 1)
            elif kind == "L2":
                pe.matmul(M[:, 0:192], k.xnT[:, :], wqkv[:, :], start=True, stop=True).then_inc(misc.w.sem, 1)
            else:
                for n, (l, r) in enumerate(((wq, k.xnT), (wk, k.xnT), (k.xnT, wv))):
                    mm = pe.matmul(M[:, n * P:(n + 1) * P], l[:, :], r[:, :], start=True, stop=True,
                                   skip_group_check=True)
                mm.then_inc(misc.w.sem, 1)

        def prep_last(i):
            turn_of(i, 2 if i is None else 4)
            if kind == "L1":
                for t in range(2):
                    pe.matmul(M[:, t * P:(t + 1) * P], wku[:, t * P:(t + 1) * P], s["lat"][:, :], start=True, stop=True,
                              skip_group_check=True)
                pe.matmul(M[:, 256:512], s["lat"][:, :], wvu[:, :], start=True, stop=True, skip_group_check=True
                          ).then_inc(misc.w.sem, 1)
            elif kind == "L2":
                pe.wait_ge(sg["q_ready"].sem, at(sg["q_ready"], i))
                pe.transpose(M[:, 0:P], s["qkv"][:, 0:P], k.c("ident"))
                pe.transpose(M[:, P:2 * P], s["kvx"][:, 0:P], k.c("ident")).then_inc(misc.w.sem, 1)
            else:
                pe.wait_ge(sg["q_ready"].sem, at(sg["q_ready"], i))
                for n in range(2):
                    mm = pe.matmul(M[:, n * P:(n + 1) * P], k.c("same_head"), s["sq"][:, n, :], start=True, stop=True,
                                   skip_group_check=True)
                mm.then_inc(misc.w.sem, 1)

        prep_x(None)
        prep_qkv(None)
        prep_last(None)
        with pe.Fori(0, TILES) as i:
            pe.wait_ge(sg["operands_ready"].sem, sg["operands_ready"].at(i, 0))
            if kind == "L3":
                pe.wait_ge(sg["squares_spread"].sem, sg["squares_spread"].at(i, 0))
            pe.wait_ge(sg["scores_read"].sem, sg["scores_read"].at(i, 0))
            if kind == "L1":
                for t in range(nt):
                    for b in range(NB):
                        mm = pe.matmul(k.bank[t][:, 32 * b:32 * b + 32], s["qbd"][:, t, b * P:(b + 1) * P],
                                       s["kT"][:, t, 32 * b:32 * b + 32], start=True, stop=True, skip_group_check=True)
            else:
                for b in range(NB):
                    cols = slice(b * P, (b + 1) * P)
                    mm = pe.matmul(k.bank[b][:, 0:P], s["qbd"][:, 0, cols], s["kbd"][:, 0, cols], start=True,
                                   stop=(kind != "L3"), skip_group_check=True)
                    if kind == "L3":
                        pe.matmul(k.bank[b][:, 0:P], s["abd"][:, cols], s["group"][:, :], start=False, stop=False,
                                  skip_group_check=True)
                        pe.matmul(k.bank[b][:, 0:P], s["qbd"][:, 1, cols], s["kbd"][:, 1, cols], start=False, stop=True,
                                  skip_group_check=True)
                        mm = pe.matmul(k.bank[b][:, P:2 * P], s["om"][:, 1, cols], s["kbd"][:, 2, cols], start=True,
                                       stop=True, skip_group_check=True)
            mm.then_inc(sg["scores_written"].sem, 1)
            prep_x(i)
            pe.wait_ge(weights.sem, weights.at(i, 1))
            for t in range(nt):
                mm = pe.transpose(k.bank[4][:, t * P:(t + 1) * P], s["pr"][:, t * P:(t + 1) * P], k.c("ident"))
            mm.then_inc(sg["probs_T_written"].sem, 1)
            prep_qkv(i)
            pe.wait_ge(sg["probs_T_read"].sem, sg["probs_T_read"].at(i, 1))
            for t in range(nt):
                if kind == "L1":
                    mm = pe.matmul(O[t][:, :], s["pT"][:, t * P:(t + 1) * P], s["vm"][:, t, :], start=True, stop=True)
                else:
                    mm = pe.matmul(O[0].rearrange("p (b t d) -> p b t d", b=NB, t=4)[:, :, t, :],
                                   s["pT"][:, t * P:(t + 1) * P],
                                   s["vm"][:, 0, :].rearrange("p (b t d) -> p b t d", b=NB, t=4)[:, :, t, :],
                                   start=(t == 0), stop=True, skip_group_check=True)
            mm.then_inc(sg["pv_done"].sem, 1)
            pe.wait_ge(sg["heads_ready"].sem, sg["heads_ready"].at(i, 1))
            turn_of(i, 2)
            for t in range(2 if kind == "L1" else 1):
                for b in range(NB):
                    mm = pe.matmul(M[:, t * P:(t + 1) * P], s["om"][:, t, b * P:(b + 1) * P], window(k, b),
                                   start=(b == 0 and t == 0), stop=(b == NB - 1), skip_group_check=True)
            mm.then_inc(misc.w.sem, 1)
            turn_of(i, 3)
            if kind == "L1":
                for t in range(2):
                    mm = pe.matmul(M[:, 0:P], s["outT"][:, t, :], wo[:, t, :], start=(t == 0), stop=(t == 1))
            else:
                mm = pe.matmul(M[:, 0:P], s["outT"][:, 0, :], wo[:, :], start=True, stop=True)
            mm.then_inc(misc.w.sem, 1)
            prep_last(i)

    def act(act):
        with act.Fori(0, TILES) as i:
            if kind == "L1":
                act.wait_ge(sg["scores_read"].sem, sg["scores_read"].at(i, 1))
                act.activation(s["pr"][:, 0:256], s["pr"][:, 0:256], ACT.Exp).then_inc(sg["probs_ready"].sem, 1)
            elif kind == "L2":
                act.wait_ge(sg["scores_written"].sem, sg["scores_written"].at(i, 1))
                act.wait_ge(sg["weights_ready"].sem, sg["weights_ready"].at(i, 0))
                act.activation(by_group(s["D"]), scores(0), ACT.Tanh,
                               scale=float(1.0 / (CAP * np.sqrt(8.0)))).then_inc(sg["scores_read"].sem, 1)
                act.wait_ge(sg["scores_read"].sem, sg["scores_read"].at(i, 1))
                act.activation(s["E"][:, :], s["D"][:, :], ACT.Exp, scale=CAP).then_inc(sg["probs_ready"].sem, 1)
            else:
                act.wait_ge(sg["scores_read"].sem, sg["scores_read"].at(i, 1))
                act.activation(s["sD"][:, :], s["D"][:, :], ACT.Sqrt)
                act.activation(s["sDE"][:, :], s["sDE"][:, :], ACT.Sqrt).then_inc(sg["probs_ready"].sem, 1)

    def dve(dve):
        chain = Chain(dve, chain_c)
        link = chain.link

        def by_batch(dst, src):
            return dve.tensor_tensor(dst.rearrange("p (b d) -> p b d", b=NB), bc(src, 1, NB), bc(k.c("quad"), 2, P),
                                     ALU.mult)

        def written(i, n):
            dve.wait_ge(misc.w.sem, misc.v(misc.w, i, n))

        def read(i, n):
            dve.wait_ge(misc.r.sem, misc.v(misc.r, i, n))

        def prep_x(i):
            written(i, 1)
            dve.tensor_copy(k.xnT[:, :], M[:, 0:P]).then_inc(misc.r.sem, 1)

        def prep_qkv(i):
            written(i, 2)
            if kind == "L1":
                link(dve.tensor_copy(s["qT"][:, :, :], M[:, 0:256].rearrange("p (t c) -> p t c", t=2)))
                dve.tensor_copy(s["lat"][:, :], M[0:64, 256:384]).then_inc(misc.r.sem, 1)
                link(rows_by_head(dve, s["qbd"][:, 0, :], s["qT"][:, 0, :], k.c("quad_scaled")))
                link(rows_by_head(dve, s["qbd"][:, 1, :], s["qT"][:, 1, :], k.c("quad_scaled")))
            elif kind == "L2":
                qk = s["qkv"][:, 0:160]
                dve.tensor_copy(s["qkv"][:, :], M[:, 0:192]).then_inc(misc.r.sem, 1)
                read(i, 2)
                link(dve.tensor_tensor(s["ra"][:, :], qk, qk, ALU.mult))
                link(dve.tensor_reduce(s["ms"][:, :], s["ra"][:, :].rearrange("p (h d) -> p h d", d=8), X_AXIS, ALU.add))
                dve.tensor_scalar(s["ms"][:, :], s["ms"][:, :], 0.125, 1e-5, ALU.mult, ALU.add
                                  ).then_inc(sg["square_ready"].sem, 1)
            else:
                link(dve.tensor_copy(s["qT"][:, 0, :], M[:, 0:P]))
                link(dve.tensor_copy(s["kT"][:, 0, :], M[:, P:2 * P]))
                dve.tensor_copy(s["v"][:, 0:P], M[:, 2 * P:3 * P]).then_inc(misc.r.sem, 1)
                link(dve.tensor_tensor(s["sq"][:, 0, :], s["qT"][:, 0, :], s["qT"][:, 0, :], ALU.mult))
                dve.tensor_tensor(s["sq"][:, 1, :], s["kT"][:, 0, :], s["kT"][:, 0, :], ALU.mult
                                  ).then_inc(sg["q_ready"].sem, 1)
                link(dve.tensor_scalar(s["tmp"][:, :], s["qT"][:, 0, :], -2.0, None, ALU.mult))
                link(rows_by_head(dve, s["qbd"][:, 0, :], s["tmp"][:, :], k.c("lane")))

        def rotate(i):
            if kind != "L2":
                return
            dve.wait_ge(sg["rms_ready"].sem, at(sg["rms_ready"], i))
            qk = s["qkv"][:, 0:160]
            heads = qk.rearrange("p (h d) -> p h d", d=8)
            link(dve.tensor_tensor(heads, heads, bc(s["r"][:, :], 2, 8), ALU.mult))
            halves = qk.rearrange("p (h d) -> p h d", d=4)
            for dst, c in (("ra", "cos"), ("rb", "sin")):
                link(dve.tensor_tensor(s[dst][:, :].rearrange("p (h d) -> p h d", d=4), halves, bc(k.c(c), 1, 40),
                                       ALU.mult))
            a, b, o = (x.rearrange("p (h e d) -> p h e d", e=2, d=4) for x in (s["ra"][:, :], s["rb"][:, :], qk))
            link(dve.tensor_tensor(o[:, :, 0, :], a[:, :, 0, :], b[:, :, 1, :], ALU.subtract))
            link(dve.tensor_tensor(o[:, :, 1, :], a[:, :, 1, :], b[:, :, 0, :], ALU.add))
            dve.tensor_copy(s["kvx"][:, :].rearrange("p (t j d) -> p t j d", t=8, j=4),
                            bc(s["qkv"][:, P:192].rearrange("p (t d) -> p t d", d=8), 2, 4)
                            ).then_inc(sg["q_ready"].sem, 1)

        def prep_last(i):
            last = 3 if i is None else 5
            written(i, last)
            if kind == "L1":
                link(dve.tensor_copy(s["v"][:, :], M[:, 256:512]))
                dve.tensor_copy(s["kT"][:, :, :], M[:, 0:256].rearrange("p (t c) -> p t c", t=2)
                                ).then_inc(misc.r.sem, 1)
                read(i, last)
                dve.memset(k.carrier[:, :], 0.0).then_inc(sg["operands_ready"].sem, 1)
            elif kind == "L2":
                dve.wait_ge(sg["q_ready"].sem, at(sg["q_ready"], i))
                link(dve.tensor_copy(s["qT"][:, 0, :], M[:, 0:P]))
                dve.tensor_copy(s["kT"][:, 0, :], M[:, P:2 * P]).then_inc(misc.r.sem, 1)
                link(rows_by_head(dve, s["qbd"][:, 0, :], s["qT"][:, 0, :], k.c("lane")))
                read(i, last)
                rows_by_head(dve, s["kbd"][:, 0, :], s["kT"][:, 0, :], k.c("quad")).then_inc(sg["operands_ready"].sem, 1)
            else:
                link(dve.tensor_scalar(s["tmp"][:, :], M[:, 0:P], -1.0, 1.0, ALU.mult, ALU.add))
                link(rows_by_head(dve, s["om"][:, 1, :], s["tmp"][:, :], k.c("lane_eighth")))
                link(dve.tensor_scalar(s["bd"][:, :], M[:, P:2 * P], -1.0, 1.0, ALU.mult, ALU.add))
                dve.memset(k.carrier[:, :], 0.0).then_inc(misc.r.sem, 1)
                read(i, last)
                rows_by_head(dve, s["kbd"][:, 2, :], s["bd"][:, :], k.c("quad")).then_inc(sg["operands_ready"].sem, 1)

        def weights_done(i):
            n = 4 * nt
            link(dve.tensor_reduce(s["rs"][:, 0:n], s["pr"][:, 0:nt * P].rearrange("p (u c) -> p u c", c=32), X_AXIS,
                                   ALU.add))
            link(dve.reciprocal(s["rr"][:, 0:n], s["rs"][:, 0:n]))
            rr = s["rr"][:, 0:n]
            if kind == "L1":
                link(dve.tensor_tensor(s["w"][:, 0:n, :], bc(rr, 2, 4), bc(k.c("quad"), 1, n), ALU.mult))
            else:
                link(dve.tensor_tensor(s["w"][:, :, :].rearrange("p (b t) j -> p b t j", t=4),
                                       bc(rr.rearrange("p (t b) -> p b t", b=NB), 3, 4),
                                       bc(bc(k.c("quad"), 1, 4), 1, NB), ALU.mult))

        norm.dve_stats(dve, chain, None)
        if kind == "L3":
            link(dve.tensor_copy(s["qbd"][:, 1, :].rearrange("p (b j q) -> p b j q", b=NB, j=4),
                                 bc(bc(k.c("lane"), 1, NB), 3, SEQ)))
            link(dve.tensor_copy(s["group"][:, :].rearrange("p (t k) -> p t k", t=4), bc(k.c("quad"), 2, SEQ)))
        norm.dve_apply(dve, None)
        prep_x(None)
        prep_qkv(None)
        rotate(None)
        prep_last(None)
        with dve.Fori(0, TILES) as i:
            chain.round(i)
            norm.dve_stats(dve, chain, i)
            vsrc = s["kvx"][:, P:2 * P] if kind == "L2" else s["v"][:, 0:P]
            dve.wait_ge(sg["pv_done"].sem, sg["pv_done"].at(i, 0))
            link(by_batch(s["vm"][:, 0, :], vsrc))
            if kind == "L1":
                link(by_batch(s["vm"][:, 1, :], s["v"][:, P:2 * P]))
            norm.dve_apply(dve, i)
            dve.wait_ge(sg["scores_written"].sem, sg["scores_written"].at(i, 1))
            if kind == "L1":
                sc = k.psum[:, 0:2, 0:P].rearrange("p t (b c) -> p t b c", c=32)
                nm = s["nm"][:, 0:8]
                link(dve.tensor_reduce(nm.rearrange("p (t b) -> p t b", t=2), sc, X_AXIS, ALU.max, negate=True))
                pr = s["pr"][:, 0:256]
                dve.tensor_tensor(pr.rearrange("p (t b c) -> p t b c", t=2, c=32), sc,
                                  bc(nm.rearrange("p (t b) -> p t b", t=2), 3, 32), ALU.add
                                  ).then_inc(sg["scores_read"].sem, 1)
                dve.wait_ge(sg["probs_ready"].sem, sg["probs_ready"].at(i, 1))
            elif kind == "L2":
                dve.wait_ge(sg["probs_ready"].sem, sg["probs_ready"].at(i, 1))
                dve.tensor_tensor(s["pr"][:, :].rearrange("p (u c) -> p u c", c=32),
                                  s["E"][:, :].rearrange("p (u c) -> p u c", c=32), bc(k.c("causal"), 1, 16),
                                  ALU.mult).then_inc(weights.sem, 1)
            else:
                def flat(n):
                    return s[n][:, :]

                link(dve.tensor_scalar(by_group(s["D"]), scores(0), 0.0, None, ALU.max))
                link(dve.tensor_scalar(by_group(s["E"]), scores(1), 1e-6, None, ALU.max))
                dve.tensor_tensor(flat("sDE"), flat("D"), flat("E"), ALU.add).then_inc(sg["scores_read"].sem, 1)
                link(dve.scalar_tensor_tensor(out=flat("R"), in0=flat("D"), scalar=2.0, in1=flat("E"),
                                              op0=ALU.mult, op1=ALU.add))
                dve.wait_ge(sg["probs_ready"].sem, sg["probs_ready"].at(i, 1))
                link(dve.tensor_tensor(flat("sD"), flat("sD"), flat("sDE"), ALU.mult))
                link(dve.scalar_tensor_tensor(out=flat("R"), in0=flat("sD"), scalar=2.0, in1=flat("R"),
                                              op0=ALU.mult, op1=ALU.add))
                link(dve.reciprocal(flat("R"), flat("R")))
                link(dve.tensor_tensor(flat("R"), flat("R"), flat("E"), ALU.mult))
                rows = s["R"][:, :].rearrange("p (u c) -> p u c", c=32)
                link(dve.tensor_reduce(s["nm"][:, :], rows, X_AXIS, ALU.max))
                link(dve.reciprocal(s["nm"][:, :], s["nm"][:, :]))
                dve.tensor_tensor(s["pr"][:, :].rearrange("p (u c) -> p u c", c=32), rows,
                                  bc(s["nm"][:, :], 2, 32), ALU.mult).then_inc(weights.sem, 1)
            prep_x(i)
            dve.wait_ge(weights.sem, weights.at(i, 1))
            weights_done(i)
            dve.wait_ge(sg["probs_T_written"].sem, sg["probs_T_written"].at(i, 1))
            dve.tensor_copy(s["pT"][:, 0:nt * P], k.bank[4][:, 0:nt * P]).then_inc(sg["probs_T_read"].sem, 1)
            prep_qkv(i)
            dve.wait_ge(sg["pv_done"].sem, sg["pv_done"].at(i, 1))
            w = s["w"][:, 0:4 * nt, :].rearrange("p u j -> p (u j)")
            for t in range(2 if kind == "L1" else 1):
                n = 16 if kind == "L1" else 64
                ins = dve.tensor_tensor(s["om"][:, t, :].rearrange("p (g d) -> p g d", d=hd),
                                        O[t].rearrange("p (g d) -> p g d", d=hd),
                                        bc(w[:, t * n:(t + 1) * n], 2, hd), ALU.mult)
            ins.then_inc(sg["heads_ready"].sem, 1)
            rotate(i)
            written(i, 3)
            n = 2 if kind == "L1" else 1
            dve.tensor_copy(s["outT"][:, 0:n, :], M[:, 0:n * P].rearrange("p (t c) -> p t c", t=n)
                            ).then_inc(misc.r.sem, 1)
            written(i, 4)
            x = k.X[:, i, :]
            dve.tensor_tensor(x, x, M[:, 0:P], ALU.add).then_inc(misc.r.sem, 1)
            read(i, 4)
            prep_last(i)
        chain.i = i
        chain.done()

    return {"sync": lambda sp: None, "pool": pool, "tensor": pe, "scalar": act, "vector": dve}


def null_key_attention(k):
    norm = Norm(k, twice=True)
    misc = Misc(k, 3, 2, 7, 1)
    W = KEYS + 1
    a = k.scratch({
        "G": [P, 16, P], "N": [P, 16, P], "wqT": [P, 8, P], "wkT": [P, 8, P], "wvT": [P, 8, P], "wo": [P, 8, P],
        "p": [P, 4, W], "slots": [P, NB, KEYS], "d": [P, KEYS], "sq": [P, KEYS], "ve": [P, 3], "zT": [P, 2, KEYS],
        "zk": [P, 2, 2 * P], "zl": [1, 2, P], "pT": [P, 2, 2 * P], "pTl": [1, 2, P], "null_left": [P, 4 * P],
        "null_value": [P, 4, P], "row": [P, P], "U": [P, 16], "rhsU": [P, 8, 16], "kb": [P, 8], "vb": [P, 8],
        "negm": [P, 16], "rs": [P, 16], "rr": [P, 16], "pn": [P, 16], "ns": [P, 16], "nsr": [P, 64], "batch": [P, 1],
        "xs_row": [P, P], "xb_row": [P, P], "cs_row": [P, P], "cb_row": [P, P], "y": [P, P], "y2": [P, P], "cols": [P, 6]})
    qa = k.area[:, 4096:4096 + 2048].rearrange("p (t c) -> p t c", t=4)
    pc = k.area[:, 6144:6144 + 2048].rearrange("p (h c) -> p h c", h=16)
    xrep = a["null_left"]
    setup = a["p"].rearrange("p u c -> p (u c)")[:, 0:1024].rearrange("p (c m) -> p c m", c=8)
    bias, sel, mask = k.mask_bias, k.batch_select, k.mask_in
    for name, dst in (("wqT", a["wqT"]), ("wkT", a["wkT"]), ("wvT", a["wvT"]), ("wo", a["wo"]), ("cols", a["cols"]),
                      ("mask", mask)):
        k.loads.append((k.stage_no, dst, k.dram["L0_xattn_" + name]))
    for name, dst in (("lno_s", a["xs_row"]), ("lno_b", a["xb_row"]), ("lnc_s", a["cs_row"]), ("lnc_b", a["cb_row"])):
        k.loads.append((k.stage_no, dst, k.dram["L0_xattn_" + name].partition_broadcast(P)))
    col = {n: a["cols"][:, c:c + 1] for c, n in enumerate(("x_scale", "x_bias", "c_scale", "null_key", "null_value"))}
    S, T, Z, PC, M = k.bank[0:2], k.bank[2:4], k.bank[4], k.bank[5:7], k.bank[7]
    ctxT = k.dram["ctxT"]
    chain_c = k.sig("vector_step").stage(*X0_STEPS)
    sg = {n: k.sig(n).stage(*v) for n, v in {
        **{f"slot{b}_loaded": (16, 16) for b in range(NB)}, "slot_freed": (NB, 0), "setup_written": (0, 4),
        "setup_read": (0, 5), "mean_written": (NB, 1), "centred": (NB, 1), "squared": (NB, 1), "var_written": (NB, 1),
        "var_read": (NB, 1), "z_rstd": (NB, 1), "z_read": (NB, 1), "z_turned": (NB, 1), "zT_ready": (NB, 1),
        "scores_written": (16, 0), "max_ready": (16, 0), "exp_ready": (16, 0), "probs_ready": (16, 0, 1),
        "probs_T_written": (16, 0, 2), "probs_T_read": (16, 0, 2), "pv_done": (16, 0, 3), "pc_read": (NB, 0, 1),
        "qa_written": (4, 3), "qa_read": (4, 3), "null_ready": (2, 2), "null_left_ready": (1, 0, 1),
        "out_var_ready": (1, 0, 1), "out_rstd_ready": (1, 0, 1), "out_pool_step": (1, 0, 1),
    }.items()}

    OUT, NEXT_X, NEXT_NULL = 0, 1, 2

    def at_step(s, back):
        return (s - back) % 16

    def batch(c, i, b):
        return c.before(1) if i is None else c.at(i, b + 1)

    def sp(sp):
        for b in range(NB):
            sp.dma_start(a["slots"][:, b, :], ctxT[b]).then_inc(sg[f"slot{b}_loaded"].sem, 16)
        with sp.Fori(0, TILES) as i:
            for b in range(NB):
                sp.wait_ge(sg["centred"].sem, sg["centred"].at(i, b))
                sp.sem_inc(sg["slot_freed"].sem, 1)
                sp.dma_start(a["slots"][:, b, :], ctxT[i * NB + (NB + b)]).then_inc(sg[f"slot{b}_loaded"].sem, 16)
        for b in range(NB):
            sp.wait_ge(sg[f"slot{b}_loaded"].sem, sg[f"slot{b}_loaded"].at(TILES - 1, 16))

    def pool(pool):
        def squares(i, b):
            pool.wait_ge(sg["centred"].sem, batch(sg["centred"], i, b))
            pool.tensor_tensor(a["sq"], a["d"], a["d"], ALU.mult).then_inc(sg["squared"].sem, 1)

        def rstd(i, b):
            pool.wait_ge(sg["var_read"].sem, batch(sg["var_read"], i, b))
            pool.tensor_tensor(a["ve"], a["ve"], k.minus_half[:, 0:3], ALU.pow).then_inc(sg["z_rstd"].sem, 1)

        norm.pool(pool, None)
        squares(None, 0)
        rstd(None, 0)
        def out_rstd(i):
            ov, os, orr = sg["out_var_ready"], sg["out_pool_step"], sg["out_rstd_ready"]
            pool.wait_ge(ov.sem, ov.at(i, 1))
            pool.tensor_tensor(k.out_vareps[:, :], k.out_meanvar[:, 1:2], k.ln_eps6[:, :], ALU.add).then_inc(os.sem, 1)
            pool.wait_ge(os.sem, os.at(i, 1))
            pool.tensor_tensor(k.out_rstd[:, :], k.out_vareps[:, :], k.minus_half[:, 0:1], ALU.pow).then_inc(orr.sem, 1)

        with pool.Fori(0, TILES) as i:
            for b in range(NB):
                squares(i, b)
                if b == 2:
                    norm.pool(pool, i)
                rstd(i, b)
                if b == 1:
                    out_rstd(i)
        out_rstd(TILES)

    def pe(pe):
        def setup_turn(n):
            pe.wait_ge(sg["setup_read"].sem, sg["setup_read"].before(n))

        def per_head(left, right):
            for odd in range(2):
                rows = slice(64 * odd, 64 * odd + 64)
                for c in range(8):
                    mm = pe.matmul(k.bank[2 * odd + c // 4][:, (c % 4) * P:(c % 4 + 1) * P], left[rows, c, :],
                                   right[rows, c, :], start=True, stop=True, skip_group_check=True)
            mm.then_inc(sg["setup_written"].sem, 1)

        def next_x(i):
            pe.wait_ge(norm.xn.sem, norm.count(norm.xn, i))
            pe.wait_ge(misc.r.sem, misc.v(misc.r, i, 0 if i is None else NEXT_X))
            pe.transpose(M[:, 0:P], k.xn[:, :], k.c("ident")).then_inc(misc.w.sem, 1)

        def next_null(i):
            pe.wait_ge(misc.r.sem, misc.v(misc.r, i, 1 if i is None else NEXT_NULL))
            for b in range(NB):
                mm = pe.matmul(M[:, 16 * b:16 * b + 16], xrep[:, b * P:(b + 1) * P], a["U"][:, :], start=True,
                               stop=True, skip_group_check=True)
            mm.then_inc(misc.w.sem, 1)

        def queries(i, t, n):
            if t == 0:
                pe.wait_ge(misc.r.sem, misc.v(misc.r, i, 2 if i is None else NEXT_NULL + 1))
            else:
                qr = sg["qa_read"]
                pe.wait_ge(qr.sem, qr.before(n) if i is None else qr.at(i, n))
            for j in range(4):
                mm = pe.matmul(M[:, j * P:(j + 1) * P], a["G"][:, 4 * t + j, :], k.xnT[:, :],
                               start=True, stop=True, skip_group_check=True)
            mm.then_inc(sg["qa_written"].sem, 1)

        def slot(b):
            return 0 if b is None else (b + 1) % NB

        def mean(i, b):
            s = slot(b)
            loaded = sg[f"slot{s}_loaded"]
            pe.wait_ge(loaded.sem, loaded.before(16) if i is None else loaded.at(i, 16 if s == 0 else 0))
            if i is not None:
                pe.wait_ge(sg["zT_ready"].sem, sg["zT_ready"].at(i, b))
            pe.matmul(Z[:, 0:KEYS], k.c("mean_of"), a["slots"][:, s, :], start=True, stop=True
                      ).then_inc(sg["mean_written"].sem, 1)

        def variance(i, b):
            pe.wait_ge(sg["centred"].sem, batch(sg["centred"], i, b))
            pe.transpose(Z[:, 0:P], a["d"][:, 0:P], k.c("ident"))
            pe.transpose(Z[:, P:2 * P], a["d"][:, P:2 * P], k.c("ident"))
            pe.transpose(Z[0:1, 2 * P:3 * P], a["d"][:, 2 * P:KEYS], k.c("ident"))
            pe.wait_ge(sg["squared"].sem, batch(sg["squared"], i, b))
            for n, left in enumerate((a["sq"][:, 0:P], a["sq"][:, P:2 * P], a["sq"][:, 2 * P:KEYS].to_broadcast([P, P]))):
                mm = pe.matmul(Z[:, 384 + n:385 + n], left, k.c("mean_of")[:, 0:1], start=True, stop=True,
                               skip_group_check=True)
            mm.then_inc(sg["var_written"].sem, 1)

        def z_turn(i, b):
            s = 0 if i is None else (b + 1) % 2
            pe.wait_ge(sg["z_read"].sem, batch(sg["z_read"], i, b))
            pe.transpose(Z[:, 0:P], a["zk"][:, s, 0:P], k.c("ident"))
            pe.transpose(Z[:, P:2 * P], a["zk"][:, s, P:2 * P], k.c("ident"))
            pe.transpose(Z[:, 2 * P:KEYS], a["zl"][:, s, :], k.c("ident")[0:1, 0:1]).then_inc(sg["z_turned"].sem, 1)

        def scores(i, u):
            b, t = divmod(u, 4)
            if u == 0 or u == 3:
                pe.wait_ge(sg["qa_read"].sem, sg["qa_read"].at(i, u // 3))
            if u == 0 or u == 12:
                pe.wait_ge(sg["null_ready"].sem, sg["null_ready"].at(i, -1 if u == 0 else 0))
            if t == 0:
                pe.wait_ge(sg["zT_ready"].sem, sg["zT_ready"].at(i, b))
            pe.wait_ge(sg["exp_ready"].sem, sg["exp_ready"].at(i, u - 1))
            pe.matmul(S[u % 2][:, 0:KEYS], qa[:, t, b * P:(b + 1) * P], a["zT"][:, b % 2, :], start=True, stop=False,
                      skip_group_check=True)
            pe.matmul(S[u % 2][:, 0:KEYS], sel[:, b, :], bias[:, :], start=False, stop=True, skip_group_check=True)
            pe.matmul(S[u % 2][:, KEYS:W], k.c("ident"), a["ns"][:, u:u + 1], start=True, stop=True,
                      skip_group_check=True).then_inc(sg["scores_written"].sem, 1)

        def turn(i, s):
            u = at_step(s, 2)
            pe.wait_ge(sg["probs_ready"].sem, sg["probs_ready"].at(i, s))
            pe.wait_ge(sg["probs_T_read"].sem, sg["probs_T_read"].at(i, s - 1))
            pe.transpose(T[u % 2][:, 0:P], a["p"][:, u % 4, 0:P], k.c("ident"))
            pe.transpose(T[u % 2][:, P:2 * P], a["p"][:, u % 4, P:2 * P], k.c("ident"))
            pe.transpose(T[u % 2][0:1, 2 * P:3 * P], a["p"][:, u % 4, 2 * P:KEYS], k.c("ident")
                         ).then_inc(sg["probs_T_written"].sem, 1)

        def values(i, s):
            u = at_step(s, 3)
            b, t = divmod(u, 4)
            if t == 0:
                pe.wait_ge(sg["z_read"].sem, sg["z_read"].at(i, b))
                pe.wait_ge(sg["pc_read"].sem, sg["pc_read"].at(i, b))
            pe.wait_ge(sg["probs_T_read"].sem, sg["probs_T_read"].at(i, s))
            out = PC[b % 2][:, t * P:(t + 1) * P]
            for c in range(2):
                pe.matmul(out, a["zk"][:, b % 2, c * P:(c + 1) * P], a["pT"][:, u % 2, c * P:(c + 1) * P],
                          start=(c == 0), stop=False, skip_group_check=True)
            pe.matmul(out, a["zl"][:, b % 2, :], a["pTl"][:, u % 2, :], start=False, stop=True, skip_group_check=True
                      ).then_inc(sg["pv_done"].sem, 1)

        def finish_tile(i, s):
            if s not in (3, 4, 5, 6):
                return
            t = s - 3
            if s == 3:
                pe.wait_ge(sg["pc_read"].sem, sg["pc_read"].at(i, 1))
                pe.wait_ge(sg["null_left_ready"].sem, sg["null_left_ready"].at(i, 1))
                pe.wait_ge(sg["qa_read"].sem, sg["qa_read"].at(i, 0 if i is TILES else 1))
            for h in range(4 * t, 4 * t + 4):
                pe.matmul(M[:, 0:P], pc[:, h, :], a["N"][:, h, :], start=(h == 0), stop=False)
            mm = pe.matmul(M[:, 0:P], a["null_left"][:, t * P:(t + 1) * P], a["null_value"][:, t, :],
                           start=False, stop=(t == 3))
            if t == 3:
                mm.then_inc(misc.w.sem, 1)

        per_head(a["wvT"], a["wo"])
        setup_turn(2)
        per_head(a["wqT"], a["wkT"])
        setup_turn(3)
        for c in range(8):
            pe.matmul(k.bank[0][:, 0:16], a["wqT"][:, c, :], a["rhsU"][:, c, :], start=(c == 0), stop=(c == 7))
        for t in range(4):
            for cc in range(2):
                mm = pe.matmul(k.bank[1][:, t * P:(t + 1) * P], setup[:, 2 * t + cc, :], a["wo"][:, 2 * t + cc, :],
                               start=(cc == 0), stop=(cc == 1), skip_group_check=True)
        mm.then_inc(sg["setup_written"].sem, 1)
        setup_turn(4)
        for c in range(8):
            mm = pe.matmul(k.bank[2][:, 0:P], setup[:, c, :], a["wo"][:, c, :], start=(c == 0), stop=(c == 7))
        mm.then_inc(sg["setup_written"].sem, 1)
        setup_turn(5)
        next_x(None)
        next_null(None)
        for t in range(3):
            queries(None, t, t)
        mean(None, None)
        variance(None, None)
        z_turn(None, None)
        with pe.Fori(0, TILES) as i:
            for s in range(16):
                b, t = divmod(s, 4)
                scores(i, s)
                if t == 0:
                    mean(i, b)
                if t == 1:
                    variance(i, b)
                if t == 3:
                    z_turn(i, b)
                turn(i, s)
                values(i, s)
                finish_tile(i, s)
                if s == 0:
                    queries(i, 3, 0)
                if s == 10:
                    next_x(i)
                if s == 12:
                    next_null(i)
                if s >= 13:
                    queries(i, s - 13, s - 12)
        for s in range(7):
            if s < 2:
                turn(TILES, s)
            if s < 3:
                values(TILES, s)
            finish_tile(TILES, s)

    def act(act):
        def queries(i, t, n):
            qw = sg["qa_written"]
            act.wait_ge(qw.sem, qw.before(n + 1) if i is None else qw.at(i, n + 1))
            act.activation(qa[:, t, :].rearrange("p (b j q) -> p b j q", b=NB, j=4),
                           M.rearrange("p (j b q) -> p b j q", j=4, b=NB), ACT.Copy).then_inc(sg["qa_read"].sem, 1)

        def z_out(i, b):
            s = 0 if i is None else (b + 1) % 2
            act.wait_ge(sg["z_rstd"].sem, batch(sg["z_rstd"], i, b))
            if i is not None:
                act.wait_ge(sg["pv_done"].sem, sg["pv_done"].at(i, 4 * b + 3))
            for c in range(2):
                act.activation(a["zk"][:, s, c * P:(c + 1) * P], Z[:, c * P:(c + 1) * P], ACT.Copy, scale=a["ve"][:, c:c + 1])
            act.activation(a["zl"][:, s, :], Z[0:1, 2 * P:3 * P], ACT.Copy, scale=a["ve"][0:1, 2:3]
                           ).then_inc(sg["z_read"].sem, 1)

        def turned(i, s):
            u = at_step(s, 2)
            act.wait_ge(sg["probs_T_written"].sem, sg["probs_T_written"].at(i, s + 1))
            act.wait_ge(sg["pv_done"].sem, sg["pv_done"].at(i, s))
            act.activation(a["pT"][:, u % 2, :], T[u % 2][:, 0:2 * P], ACT.Copy)
            act.activation(a["pTl"][:, u % 2, :], T[u % 2][0:1, 2 * P:3 * P], ACT.Copy
                           ).then_inc(sg["probs_T_read"].sem, 1)

        for t in range(3):
            queries(None, t, t)
        z_out(None, 0)
        with act.Fori(0, TILES) as i:
            for s in range(16):
                act.wait_ge(sg["max_ready"].sem, sg["max_ready"].at(i, s + 1))
                act.wait_ge(sg["probs_T_written"].sem, sg["probs_T_written"].at(i, s - 1))
                act.activation(a["p"][:, s % 4, :], S[s % 2][:, 0:W], ACT.Exp, bias=a["negm"][:, s:s + 1],
                               accum_out=a["rs"][:, s:s + 1]).then_inc(sg["exp_ready"].sem, 1)
                turned(i, s)
                if s % 4 == 2:
                    z_out(i, s // 4)
                if s == 0:
                    queries(i, 3, 0)
                if s >= 13:
                    queries(i, s - 13, s - 12)
        for s in range(2):
            turned(TILES, s)

    def dve(dve):
        chain = Chain(dve, chain_c)
        link = chain.link

        def centre(i, b):
            s = 0 if i is None else (b + 1) % NB
            dve.wait_ge(sg["mean_written"].sem, batch(sg["mean_written"], i, b))
            dve.tensor_tensor(a["d"], a["slots"][:, s, :], Z[:, 0:KEYS], ALU.subtract).then_inc(sg["centred"].sem, 1)

        def var_out(i, b):
            dve.wait_ge(sg["var_written"].sem, batch(sg["var_written"], i, b))
            dve.tensor_scalar(a["ve"], Z[:, 384:387], 1e-6, None, ALU.add).then_inc(sg["var_read"].sem, 1)

        def z(i, b):
            s = 0 if i is None else (b + 1) % 2
            dve.wait_ge(sg["z_turned"].sem, batch(sg["z_turned"], i, b))
            dve.tensor_copy(a["zT"][:, s, :], Z[:, 0:KEYS]).then_inc(sg["zT_ready"].sem, 1)

        def take_x(i):
            dve.wait_ge(misc.w.sem, misc.v(misc.w, i, 1 if i is None else NEXT_X + 1))
            if i is not None:
                dve.wait_ge(sg["qa_written"].sem, sg["qa_written"].at(i, 1))
            link(dve.tensor_scalar(k.xnT[:, :], M[:, 0:P], col["x_scale"], col["x_bias"], ALU.mult, ALU.add))
            dve.tensor_copy(xrep[:, :].rearrange("p (b j q) -> p b j q", b=NB, j=4),
                            bc(k.xnT[:, :].rearrange("p (b q) -> p b q", b=NB), 2, 4)).then_inc(misc.r.sem, 1)

        def null_scores(i, b0, b1):
            if i is not None:
                dve.wait_ge(sg["scores_written"].sem, sg["scores_written"].at(i, 4 * b1))
            dve.tensor_reduce(a["ns"][:, 4 * b0:4 * b1],
                              a["nsr"][:, 16 * b0:16 * b1].rearrange("p (u j) -> p u j", j=4), X_AXIS, ALU.add)
            dve.tensor_tensor(sel[:, b0:b1, :], bc(k.c("expert_no")[:, b0:b1], 2, P),
                              bc(a["batch"][:, 0:1].to_broadcast([P, b1 - b0]), 2, P), ALU.is_equal
                              ).then_inc(sg["null_ready"].sem, 1)

        def take_null(i):
            n = 2 if i is None else NEXT_NULL + 1
            dve.wait_ge(misc.w.sem, misc.v(misc.w, i, n))
            dve.tensor_tensor(a["nsr"][:, :].rearrange("p (u j) -> p u j", j=4),
                              M[:, 0:64].rearrange("p (u j) -> p u j", j=4), bc(k.c("quad"), 1, 16), ALU.mult
                              ).then_inc(misc.r.sem, 1)
            dve.wait_ge(misc.r.sem, misc.v(misc.r, i, n))
            if i is not None:
                link(dve.tensor_scalar(a["batch"][:, :], a["batch"][:, :], -float(NB), None, ALU.add))
            null_scores(i, 0, NB - 1)

        def normalise(i, s):
            u = at_step(s, 1)
            dve.wait_ge(sg["exp_ready"].sem, sg["exp_ready"].at(i, s))
            link(dve.reciprocal(a["rr"][:, u:u + 1], a["rs"][:, u:u + 1]))
            dve.tensor_tensor(a["pn"][:, u:u + 1], a["p"][:, u % 4, KEYS:W], a["rr"][:, u:u + 1], ALU.mult)
            dve.tensor_scalar(a["p"][:, u % 4, 0:KEYS], a["p"][:, u % 4, 0:KEYS], a["rr"][:, u:u + 1], None, ALU.mult
                              ).then_inc(sg["probs_ready"].sem, 1)

        def spread_null(i):
            dve.wait_ge(sg["probs_ready"].sem, sg["probs_ready"].at(i, 1))
            for t in range(4):
                ins = dve.tensor_tensor(a["null_left"][:, t * P:(t + 1) * P].rearrange("p (b q) -> p b q", b=NB),
                                        bc(a["pn"][:, :].rearrange("p (b t) -> p b t", t=4)[:, :, t], 2, 32),
                                        bc(k.c("query"), 1, NB), ALU.mult)
            ins.then_inc(sg["null_left_ready"].sem, 1)
            dve.wait_ge(sg["null_left_ready"].sem, sg["null_left_ready"].at(i, 1))

        def gather(i, s):
            b = at_step(s, 7) // 4
            if s == 7:
                dve.wait_ge(misc.w.sem, misc.w.at(i, OUT + 1))
            dve.wait_ge(sg["pv_done"].sem, sg["pv_done"].at(i, s))
            dve.tensor_copy(pc[:, :, 32 * b:32 * b + 32], PC[b % 2].rearrange("p (h q) -> p h q", h=16)
                            ).then_inc(sg["pc_read"].sem, 1)

        def finish_tile(i, s):
            if s == 7:
                dve.wait_ge(misc.w.sem, misc.w.at(i, OUT + 1))
                dve.tensor_tensor(a["y"], M[:, 0:P], a["row"], ALU.add).then_inc(misc.r.sem, 1)
                dve.wait_ge(misc.r.sem, misc.r.at(i, OUT + 1))
                link(dve.bn_stats(k.out_stat[:, :], a["y"]))
                dve.memset(k.carrier[:, :], 0.0)
                dve.bn_aggr(k.out_meanvar[:, :], k.out_stat[:, :]).then_inc(sg["out_var_ready"].sem, 1)
            if s == 9:
                dve.wait_ge(sg["out_rstd_ready"].sem, sg["out_rstd_ready"].at(i, 1))
                link(dve.tensor_scalar(a["y"], a["y"], k.out_meanvar[:, 0:1], k.out_rstd[:, 0:1], ALU.subtract, ALU.mult))
                link(dve.tensor_tensor(a["y"], a["y"], a["xs_row"], ALU.mult))
                link(dve.tensor_tensor(a["y"], a["y"], a["xb_row"], ALU.add))
                x = k.X_spare[:, i, :]
                link(dve.tensor_tensor(x, x, a["y"], ALU.add))

        def heads(n):
            return k.psum[:, 2 * n:2 * n + 2, :].rearrange("p a (c m) -> p a c m", m=P)

        def of_heads(t, n):
            return t.rearrange("p (a c o) m -> p o a c m", o=2, a=2)[:, n]

        norm.dve_stats(dve, chain, None)
        for src, dst in (("wkT", "kb"), ("wvT", "vb")):
            link(dve.tensor_tensor(setup, a[src], bc(a["cb_row"], 1, 8), ALU.mult))
            link(dve.tensor_reduce(a[dst], setup, X_AXIS, ALU.add))
        link(dve.tensor_scalar(a["kb"], a["kb"], col["null_key"], -1.0, ALU.subtract, ALU.mult))
        link(dve.tensor_scalar(a["nsr"][:, 0:8], a["vb"], col["null_value"], -1.0, ALU.subtract, ALU.mult))
        link(dve.tensor_tensor(a["rhsU"], bc(a["kb"], 2, 16), k.c("pair_head").rearrange("p (c h) -> p c h", c=8),
                               ALU.mult))
        for c in range(8):
            link(dve.tensor_tensor(setup[:, c, :].rearrange("p (j q) -> p j q", j=4),
                                   a["nsr"][:, c:c + 1].unsqueeze(2).to_broadcast([P, 4, 32]),
                                   bc(k.c("pair_in_group")[:, 4 * (c % 2):4 * (c % 2) + 4], 2, 32), ALU.mult))
        link(dve.tensor_scalar(bias[:, :], mask[:, :], -1.0, 1e30, ALU.add, ALU.mult))
        dve.tensor_copy(a["batch"][:, :], k.c("row_no")).then_inc(sg["setup_read"].sem, 1)
        dve.wait_ge(sg["setup_written"].sem, sg["setup_written"].before(1))
        for n in range(2):
            link(dve.tensor_scalar(of_heads(a["N"], n), heads(n), col["c_scale"], None, ALU.mult))
        dve.memset(k.carrier[:, :], 0.0).then_inc(sg["setup_read"].sem, 1)
        dve.wait_ge(sg["setup_written"].sem, sg["setup_written"].before(2))
        for n in range(2):
            for h in range(2):
                link(dve.scalar_tensor_tensor(out=of_heads(a["G"], n)[:, h], in0=heads(n)[:, h], scalar=0.25,
                                              in1=bc(a["cs_row"], 1, 4), op0=ALU.mult, op1=ALU.mult))
        dve.memset(k.carrier[:, :], 0.0).then_inc(sg["setup_read"].sem, 1)
        dve.wait_ge(sg["setup_written"].sem, sg["setup_written"].before(3))
        link(dve.tensor_scalar(a["U"], k.bank[0][:, 0:16], 0.25, None, ALU.mult))
        link(dve.tensor_copy(a["null_value"], k.bank[1].rearrange("p (t c) -> p t c", t=4)))
        dve.tensor_copy(setup, bc(a["vb"], 2, P)).then_inc(sg["setup_read"].sem, 1)
        dve.wait_ge(sg["setup_written"].sem, sg["setup_written"].before(4))
        for x in (a["p"], a["pT"], a["pTl"], a["zk"], a["zl"], a["pn"]):
            dve.memset(x, 0.0)
        dve.memset(PC[1][:, 0:P], 0.0)
        link(dve.memset(a["rs"], 1.0))
        dve.tensor_copy(a["row"], k.bank[2][:, 0:P]).then_inc(sg["setup_read"].sem, 1)
        norm.dve_apply(dve, None)
        take_x(None)
        take_null(None)
        null_scores(None, NB - 1, NB)
        centre(None, 0)
        var_out(None, 0)
        z(None, 0)
        with dve.Fori(0, TILES) as i:
            chain.round(i)
            for s in range(16):
                b, t = divmod(s, 4)
                dve.wait_ge(sg["scores_written"].sem, sg["scores_written"].at(i, s + 1))
                dve.tensor_reduce(a["negm"][:, s:s + 1], S[s % 2][:, 0:W], X_AXIS, ALU.max, negate=True
                                  ).then_inc(sg["max_ready"].sem, 1)
                if t == 0:
                    centre(i, b)
                normalise(i, s)
                if s == 0:
                    spread_null(i)
                if t == 1:
                    var_out(i, b)
                if t == 3:
                    gather(i, s)
                    z(i, b)
                finish_tile(i, s)
                if s == 8:
                    norm.dve_stats(dve, chain, i)
                if s == 10:
                    norm.dve_apply(dve, i)
                if s == 11:
                    take_x(i)
                if s == 13:
                    take_null(i)
            null_scores(i, NB - 1, NB)
        chain.round(TILES)
        normalise(TILES, 0)
        spread_null(TILES)
        gather(TILES, 3)
        finish_tile(TILES, 7)
        finish_tile(TILES, 9)
        chain.done()

    return {"sync": sp, "pool": pool, "tensor": pe, "scalar": act, "vector": dve}


def linear_attention(k, s):
    norm = Norm(k)
    misc = Misc(k, 3, 2, 7)
    heads, chunks = 16, 8
    chain_c = k.sig("vector_step").stage(4, 5)
    sg = {n: k.sig(n).stage(per, first) for n, (per, first) in {
        "proj_ready": (0, 1), "feature_w_written": (0, 1), "feature_w_read": (0, 1), "k_features_written": (1, 1),
        "q_features_written": (1, 1), "q_features_ready": (1, 1), "k_features_ready": (1, 1), "products_written": (2, 0), "masked": (2, 0),
        "pv_done": (1, 0), "heads_ready": (1, 0),
    }.items()}
    wqkv = k.load("L0_attn_qkv", [P, 2, P])
    wv, wo = k.load("L0_attn_v", [P, P]), k.load("L0_attn_out", [P, P])
    proj, bqk = k.load("L0_attn_proj", [P, 64]), k.load("L0_attn_bqk", [P, 2])
    bv, bo = k.rows("L0_attn_bv", P), k.rows("L0_attn_bout", P)
    M, O = k.bank[7], k.bank[6]

    def cols(n):
        return slice(n * P, (n + 1) * P)

    def product_bank(h):
        n = h // 2
        return k.bank[(4 if h % 2 == 0 else 0) + n // 4][:, cols(n % 4)]

    def pool(pool):
        norm.pool(pool, None)
        with pool.Fori(0, TILES) as i:
            norm.pool(pool, i)

    def pe(pe):
        def next_x(i):
            pe.wait_ge(norm.xn.sem, norm.count(norm.xn, i))
            pe.wait_ge(misc.r.sem, misc.v(misc.r, i, 0))
            pe.transpose(M[:, 0:P], k.xn[:, :], k.c("ident")).then_inc(misc.w.sem, 1)
            pe.wait_ge(misc.r.sem, misc.v(misc.r, i, 1))

        def next_v():
            pe.matmul(M[:, 0:P], k.xnT[:, :], wv[:, :], start=True, stop=True).then_inc(misc.w.sem, 1)

        def features(n):
            for c in range(chunks):
                mm = pe.matmul(k.bank[2 * n + c // 4][:, cols(c % 4)], s["feature_w"][:, n, cols(c)], k.xnT[:, :],
                               start=True, stop=True, skip_group_check=True)
            mm.then_inc(sg["q_features_written" if n == 0 else "k_features_written"].sem, 1)

        pe.wait_ge(sg["proj_ready"].sem, sg["proj_ready"].before(1))
        for n in range(2):
            for h in range(2):
                pe.matmul(k.bank[2 * n + h][:, :], wqkv[:, n, :], s["head_proj"][:, 512 * h:512 * h + 512],
                          start=True, stop=True)
            for c in range(chunks):
                mm = pe.matmul(k.bank[4][:, 8 * n + c:8 * n + c + 1], s["head_proj"][:, cols(c)], bqk[:, n:n + 1],
                               start=True, stop=True, skip_group_check=True)
        mm.then_inc(sg["feature_w_written"].sem, 1)
        next_x(None)
        pe.wait_ge(sg["feature_w_read"].sem, sg["feature_w_read"].before(1))
        features(1)
        features(0)
        next_v()
        with pe.Fori(0, TILES) as i:
            pe.wait_ge(sg["q_features_ready"].sem, sg["q_features_ready"].at(i, 0))
            pe.wait_ge(sg["k_features_ready"].sem, sg["k_features_ready"].at(i, 0))
            for odd in range(2):
                rows = slice(64 * odd, 64 * odd + 64)
                for c in range(chunks):
                    mm = pe.matmul(product_bank(2 * c + odd), s["feature"][rows, 1, cols(c)], s["feature"][rows, 0, cols(c)],
                                   start=True, stop=True, skip_group_check=True)
                mm.then_inc(sg["products_written"].sem, 1)
            next_x(i)
            features(1)
            pe.wait_ge(sg["masked"].sem, sg["masked"].at(i, 2))
            features(0)
            pe.wait_ge(misc.r.sem, misc.r.at(i, 0))
            for n in range(2):
                for h in range(heads):
                    if n == 0:
                        left = s["vz"][:, 120 * h + 120:120 * h + 120 + P]
                    else:
                        left = k.c("head_window")[:, 120 - 8 * h:120 - 8 * h + P]
                    mm = pe.matmul(O[:, cols(n)], left, s["am"][:, 8 * (h % 2) + h // 2, :],
                                   start=(h == 0), stop=(h == heads - 1), skip_group_check=True)
            mm.then_inc(sg["pv_done"].sem, 1)
            next_v()
            pe.wait_ge(sg["heads_ready"].sem, sg["heads_ready"].at(i, 1))
            pe.wait_ge(misc.r.sem, misc.r.at(i, 2))
            pe.matmul(M[:, 0:P], s["outT"][:, 0, :], wo[:, :], start=True, stop=True).then_inc(misc.w.sem, 1)

    def act(act):
        def q_features(i):
            act.wait_ge(sg["q_features_written"].sem, norm.count(sg["q_features_written"], i))
            for c in range(chunks):
                ins = act.activation(s["feature"][:, 0, cols(c)], k.bank[c // 4][:, cols(c % 4)], ACT.Relu,
                                     bias=s["feature_bias"][:, c:c + 1])
            ins.then_inc(sg["q_features_ready"].sem, 1)

        q_features(None)
        with act.Fori(0, TILES) as i:
            q_features(i)

    def dve(dve):
        chain = Chain(dve, chain_c)
        link = chain.link

        def k_features(i):
            dve.wait_ge(sg["k_features_written"].sem, norm.count(sg["k_features_written"], i))
            for c in range(chunks):
                ins = dve.tensor_scalar(s["feature"][:, 1, cols(c)], k.bank[2 + c // 4][:, cols(c % 4)],
                                        s["feature_bias"][:, 8 + c:9 + c], 0.0, ALU.add, ALU.max)
            ins.then_inc(sg["k_features_ready"].sem, 1)

        def prep_x(i):
            dve.wait_ge(misc.w.sem, misc.v(misc.w, i, 1))
            dve.tensor_copy(k.xnT[:, :], M[:, 0:P]).then_inc(misc.r.sem, 1)

        def prep_v(i):
            dve.wait_ge(misc.w.sem, misc.v(misc.w, i, 2))
            dve.tensor_tensor(s["vz"][:, :].rearrange("p (h c) -> p h c", h=heads)[:, :, 120:128],
                              M[:, 0:P].rearrange("p (h d) -> p h d", h=heads),
                              bv[:, :].rearrange("p (h d) -> p h d", h=heads), ALU.add).then_inc(misc.r.sem, 1)

        norm.dve_stats(dve, chain, None)
        dve.tensor_tensor(s["head_proj"][:, :].rearrange("p (h m) -> p h m", h=heads), bc(proj[:, :], 1, heads),
                          bc(k.c("head16"), 2, 64), ALU.mult).then_inc(sg["proj_ready"].sem, 1)
        link(dve.memset(s["vz"][:, :], 0.0))
        dve.wait_ge(sg["feature_w_written"].sem, sg["feature_w_written"].before(1))
        for n in range(2):
            link(dve.tensor_copy(s["feature_w"][:, n, :].rearrange("p (a b) -> p a b", a=2),
                                 k.psum[:, 2 * n:2 * n + 2, :]))
        link(dve.tensor_copy(s["feature_bias"][:, :], k.bank[4][:, 0:16]))
        dve.memset(k.carrier[:, :], 0.0).then_inc(sg["feature_w_read"].sem, 1)
        norm.dve_apply(dve, None)
        prep_x(None)
        k_features(None)
        prep_v(None)
        with dve.Fori(0, TILES) as i:
            chain.round(i)
            norm.dve_stats(dve, chain, i)
            norm.dve_apply(dve, i)
            for odd in range(2):
                dve.wait_ge(sg["products_written"].sem, sg["products_written"].at(i, odd + 1))
                b = 4 if odd == 0 else 0
                dve.tensor_tensor(s["am"][:, 8 * odd:8 * odd + 8, :].rearrange("p (a n) q -> p a n q", a=2),
                                  k.psum[:, b:b + 2, :].rearrange("p a (n q) -> p a n q", q=P),
                                  bc(bc(k.c("causal_T"), 1, 4), 1, 2), ALU.mult).then_inc(sg["masked"].sem, 1)
                if odd == 0:
                    prep_x(i)
            k_features(i)
            dve.wait_ge(sg["pv_done"].sem, sg["pv_done"].at(i, 1))
            prep_v(i)
            link(dve.tensor_scalar(s["den"][:, :], O[:, P:2 * P], 1e-6, None, ALU.add))
            link(dve.reciprocal(s["den"][:, :], s["den"][:, :]))
            dve.tensor_tensor(s["outT"][:, 0, :], O[:, 0:P], s["den"][:, :], ALU.mult).then_inc(sg["heads_ready"].sem, 1)
            dve.wait_ge(misc.w.sem, misc.w.at(i, 3))
            dve.tensor_tensor(s["tmp"][:, :], M[:, 0:P], bo[:, :], ALU.add).then_inc(misc.r.sem, 1)
            dve.wait_ge(misc.r.sem, misc.r.at(i, 3))
            x = k.X[:, i, :]
            link(dve.tensor_tensor(x, x, s["tmp"][:, :], ALU.add))
        chain.i = i
        chain.done()

    return {"sync": lambda sp: None, "pool": pool, "tensor": pe, "scalar": act, "vector": dve}


MOE1_EXPERTS, MOE1_WIDTH, MOE1_TOP = 16, 176, 2
CAPACITY = -(-5 * BATCH * SEQ * MOE1_TOP // (4 * MOE1_EXPERTS))
MOE2_EXPERTS, MOE3_EXPERTS, MOE3_WIDTH = 6, 64, 64


def ffn_buffers(k):
    return {"ix": k.top_at, **k.scratch({
        "H": [P, 4224], "G": [P, 2, 512], "HT": [P, 2, 512], "cw": [P, 64], "lg": [P, 64], "pr": [P, 64],
        "ex": [P, 64], "m8": [P, 8], "ixf": [P, 8], "oh": [P, 2, 16], "sel": [P, P], "acc": [P, P],
        "t": [P, 2, 64], "s1": [P, 1], "s2": [P, 1], "wr": [P, P], "xnT_next": [P, P], "cw_next": [P, 64], "xn_now": [P, P], "nm": [P, 1]})}


def feed_forward(k, kind, up_w, down_w, fb, router=None, router_b=None):
    norm = Norm(k)
    if kind == "L0":
        groups = [(192, g * 384, g * 192, None) for g in range(2)]
    elif kind == "L1":
        groups = [(176, g * 352, g * 176, g if g < MOE1_EXPERTS else None) for g in range(MOE1_EXPERTS + 1)]
    elif kind == "L2":
        groups = [(128, g * 256, g * 128, g if g < MOE2_EXPERTS else None) for g in range(MOE2_EXPERTS + 1)]
    else:
        groups = [(512, g * 512, g * 512, 8 * g) for g in range(8)] + [(64, 4096, 4096, None)]
    halves = 1 if kind == "L3" else 2
    E = {"L0": 0, "L1": MOE1_EXPERTS, "L2": MOE2_EXPERTS, "L3": MOE3_EXPERTS}[kind]
    hidden = groups[-1][2] + groups[-1][0]
    chunks = -(-hidden // P)
    quads = [list(range(q, min(q + 4, chunks))) for q in range(0, chunks, 4)]
    G, NQ = len(groups), len(quads)

    def group_of(h):
        return max(g for g, x in enumerate(groups) if x[2] <= h)

    last_group = [group_of(min(q[-1] * P + P, hidden) - 1) for q in quads]
    plan, turned, done = [], 0, 0
    for g in range(G + NQ + 1):
        step = []
        if g < G:
            while turned < NQ and last_group[turned] <= g - 2:
                step.append(("turn", turned))
                turned += 1
                if turned - done >= 2:
                    step.append(("down", done))
                    done += 1
        elif turned < NQ:
            step.append(("turn", turned))
            turned += 1
            if turned - done >= 2:
                step.append(("down", done))
                done += 1
        elif done < NQ:
            step.append(("down", done))
            done += 1
        plan.append(step)
    assert turned == NQ and done == NQ

    routed = router is not None
    nmisc = 1 + {"L0": 0, "L1": 2, "L2": 1, "L3": 1}[kind]
    misc = Misc(k, nmisc, nmisc, 7)
    U, T, Y, M = k.bank[0:3], k.bank[3:5], k.bank[5], k.bank[7]
    sg = {n: k.sig(n).stage(per, first) for n, (per, first) in {
        "up_written": (G, 0), "gate_ready": (G, 0), "hidden_ready": (G, 0), "hidden_T_written": (NQ, 0),
        "hidden_T_read": (NQ, 0), "down_used": (NQ, 0), "y_read": (1, 0),
        "x_moved": (1, 1), **({"route_exp": (1, 1)} if routed else {}),
        **({"logits_ready": (1, 1), "selected": (1, 1)} if kind == "L1" else {}),
    }.items()}
    steps = {"L0": 0, "L1": 13, "L2": 11, "L3": 11}[kind]
    chain_c = k.sig("vector_step").stage(steps + 1 + (kind == "L1"),
                                         steps + 1 + {"L0": 2, "L1": 5, "L2": 3, "L3": 3}[kind])
    wdt = I32 if kind == "L0" else F32
    up_n = halves * hidden
    up = k.load(up_w, [P, up_n], dt=wdt)
    down = k.load(down_w, [P, chunks, P], dt=wdt)
    if kind == "L0":
        up_i, down_i = up, down
        up, down = k.sb("up_dequantized", [P, up_n]), k.sb("down_dequantized", [P, chunks, P])
    H, Gt, HT, cw = fb["H"], fb["G"], fb["HT"], fb["cw"]
    if routed:
        rw = k.load(router, [P, E])
        rb = k.rows(router_b, E)

    X_AT, LOGITS_AT, COUNTS_AT = {"L0": (2, 2, 2), "L1": (3, 6, 11), "L2": (2, 5, 7), "L3": (2, 4, 9)}[kind]
    xnT, cw_next = fb["xnT_next"], fb["cw_next"]

    def pool(pool):
        norm.pool(pool, None)
        with pool.Fori(0, TILES) as i:
            norm.pool(pool, i)

    def pe(pe):
        def next_x(i):
            pe.wait_ge(norm.xn.sem, norm.count(norm.xn, i))
            pe.wait_ge(misc.r.sem, misc.v(misc.r, i, 0))
            pe.transpose(M[:, 0:P], k.xn[:, :], k.c("ident")).then_inc(misc.w.sem, 1)

        def next_logits(i):
            if routed:
                pe.wait_ge(misc.r.sem, misc.v(misc.r, i, 1))
                pe.matmul(M[:, 0:P], xnT[:, :], fb["wr"][:, :], start=True, stop=True).then_inc(misc.w.sem, 1)

        def next_counts(i):
            if kind == "L1":
                pe.wait_ge(misc.r.sem, misc.v(misc.r, i, 2))
                pe.wait_ge(sg["selected"].sem, norm.count(sg["selected"], i))
                pe.matmul(M[:, 0:P], k.c("earlier"), fb["sel"][:, :], start=True, stop=False)
                pe.matmul(M[:, 0:P], k.c("ones"), fb["acc"][:, :], start=False, stop=True).then_inc(misc.w.sem, 1)

        def turn(i, q):
            pe.wait_ge(sg["hidden_ready"].sem, sg["hidden_ready"].at(i, last_group[q] + 1))
            pe.wait_ge(sg["hidden_T_read"].sem, sg["hidden_T_read"].at(i, q - 1))
            for j, c in enumerate(quads[q]):
                mm = pe.transpose(T[q % 2][:, j * P:(j + 1) * P], H[:, c * P:(c + 1) * P], k.c("ident"))
            mm.then_inc(sg["hidden_T_written"].sem, 1)

        def downs(i, q):
            pe.wait_ge(sg["hidden_T_read"].sem, sg["hidden_T_read"].at(i, q + 1))
            if q == 0:
                pe.wait_ge(sg["y_read"].sem, sg["y_read"].at(i, 0))
            for j, c in enumerate(quads[q]):
                mm = pe.matmul(Y[:, 0:P], HT[:, q % 2, j * P:(j + 1) * P], down[:, c, :],
                               start=(c == 0), stop=(c == chunks - 1))
            mm.then_inc(sg["down_used"].sem, 1)

        next_x(None)
        next_logits(None)
        next_counts(None)
        with pe.Fori(0, TILES) as i:
            pe.wait_ge(sg["x_moved"].sem, sg["x_moved"].at(i, 0))
            for g, step in enumerate(plan):
                if g < G:
                    fw, c0, _, _ = groups[g]
                    free = sg["hidden_ready"]
                    pe.wait_ge(free.sem, free.at(i, g - 2))
                    pe.matmul(U[g % 3][:, 0:fw * halves], k.xnT[:, :], up[:, c0:c0 + fw * halves],
                              start=True, stop=True).then_inc(sg["up_written"].sem, 1)
                for what, q in step:
                    (turn if what == "turn" else downs)(i, q)
                if g == X_AT:
                    next_x(i)
                if g == LOGITS_AT:
                    next_logits(i)
                if g == COUNTS_AT:
                    next_counts(i)

    def act(act):
        def next_exp(i):
            if not routed:
                return
            if kind == "L1":
                act.wait_ge(sg["logits_ready"].sem, norm.count(sg["logits_ready"], i))
                ins = act.activation(fb["ex"][:, 0:E], fb["lg"][:, 0:E], ACT.Exp, bias=fb["nm"][:, 0:1],
                                     accum_out=fb["s1"][:, :])
            else:
                act.wait_ge(misc.r.sem, misc.v(misc.r, i, 2))
                src = fb["lg"] if kind == "L2" else fb["pr"]
                ins = act.activation(fb["ex"][:, 0:E], src[:, 0:E], ACT.Exp, scale=-1.0)
            ins.then_inc(sg["route_exp"].sem, 1)

        def out(i, q):
            act.wait_ge(sg["hidden_T_written"].sem, sg["hidden_T_written"].at(i, q + 1))
            act.wait_ge(sg["down_used"].sem, sg["down_used"].at(i, q - 1))
            m = len(quads[q]) * P
            act.activation(HT[:, q % 2, 0:m], T[q % 2][:, 0:m], ACT.Copy).then_inc(sg["hidden_T_read"].sem, 1)

        next_exp(None)
        with act.Fori(0, TILES) as i:
            for g, step in enumerate(plan):
                if g < G:
                    fw = groups[g][0]
                    act.wait_ge(sg["up_written"].sem, sg["up_written"].at(i, g + 1))
                    act.wait_ge(sg["hidden_ready"].sem, sg["hidden_ready"].at(i, g - 1))
                    act.activation(Gt[:, g % 2, 0:fw], U[g % 3][:, 0:fw], ACT.Silu).then_inc(sg["gate_ready"].sem, 1)
                for what, q in step:
                    if what == "turn":
                        out(i, q)
                if g == LOGITS_AT + 1:
                    next_exp(i)

    def dve(dve):
        chain = Chain(dve, chain_c)
        lg, pr, ex, m8, ix, ixf, oh = (fb[n] for n in ("lg", "pr", "ex", "m8", "ix", "ixf", "oh"))
        sel, acc, t, s1, s2, nm = (fb[n] for n in ("sel", "acc", "t", "s1", "s2", "nm"))

        def top2(src):
            dve.memset(k.carrier[:, :], 0.0)
            chain.link(dve.max(m8[:, :], src))
            dve.memset(k.carrier[:, :], 0.0)
            chain.link(dve.max_index(ix[:, :], m8[:, :], src))
            chain.link(dve.tensor_copy(ixf[:, :], ix[:, :]))
            chain.link(dve.tensor_tensor(oh[:, :, :], bc(k.c("expert_no"), 1, 2), bc(ixf[:, 0:2], 2, 16), ALU.is_equal))

        def weigh(eps):
            chain.link(dve.tensor_scalar(s2[:, :], m8[:, 0:1], m8[:, 1:2], eps, ALU.add, ALU.add))
            chain.link(dve.reciprocal(s2[:, :], s2[:, :]))
            for j in range(2):
                chain.link(dve.tensor_scalar(t[:, j, 0:E], oh[:, j, 0:E], m8[:, j:j + 1], s2[:, 0:1],
                                             ALU.mult, ALU.mult))

        def logits(i):
            if not routed:
                return
            dve.wait_ge(misc.w.sem, misc.v(misc.w, i, 2))
            if kind == "L3":
                dve.tensor_copy(pr[:, 0:E], M[:, 0:E]).then_inc(misc.r.sem, 1)
            else:
                dve.tensor_tensor(lg[:, 0:E], M[:, 0:E], rb[:, :], ALU.add).then_inc(misc.r.sem, 1)
            dve.wait_ge(misc.r.sem, misc.v(misc.r, i, 2))
            if kind == "L1":
                dve.tensor_reduce(nm[:, :], lg[:, 0:E], X_AXIS, ALU.max, negate=True
                                  ).then_inc(sg["logits_ready"].sem, 1)
            if kind == "L3":
                chain.link(dve.tensor_tensor(lg[:, 0:E], pr[:, 0:E], rb[:, :], ALU.add))
                dve.memset(k.carrier[:, :], 0.0)
                chain.link(dve.max(m8[:, :], lg[:, 0:E]))
                dve.memset(k.carrier[:, :], 0.0)
                chain.link(dve.match_replace(t[:, 0, :], m8[:, :], lg[:, 0:E], NEG_BIG))
                chain.link(dve.tensor_tensor(t[:, 1, :], t[:, 0, :], lg[:, 0:E], ALU.not_equal))

        def choose(i):
            if routed:
                dve.wait_ge(sg["route_exp"].sem, norm.count(sg["route_exp"], i))
                {"L1": choose_l1, "L2": choose_l2, "L3": choose_l3}[kind]()
                if kind == "L1":
                    dve.tensor_tensor(sel[:, 0:E], oh[:, 0, :], oh[:, 1, :], ALU.add).then_inc(sg["selected"].sem, 1)

        def choose_l1():
            chain.link(dve.reciprocal(s2[:, :], s1[:, :]))
            chain.link(dve.tensor_scalar(pr[:, 0:E], ex[:, 0:E], s2[:, 0:1], None, ALU.mult))
            top2(pr[:, 0:E])
            weigh(1e-9)
            chain.link(dve.tensor_tensor(lg[:, 0:E], t[:, 0, 0:E], t[:, 1, 0:E], ALU.add))

        def counts(i):
            if kind != "L1":
                return
            dve.wait_ge(misc.w.sem, misc.v(misc.w, i, 3))
            chain.link(dve.tensor_scalar(pr[:, 0:E], M[:, 0:E], float(CAPACITY), None, ALU.is_lt))
            chain.link(dve.tensor_tensor(cw_next[:, 0:E], lg[:, 0:E], pr[:, 0:E], ALU.mult))
            dve.tensor_tensor(acc[:, 0:E], acc[:, 0:E], sel[:, 0:E], ALU.add).then_inc(misc.r.sem, 1)
            dve.wait_ge(misc.r.sem, misc.v(misc.r, i, 3))

        def choose_l2():
            chain.link(dve.tensor_scalar(ex[:, 0:E], ex[:, 0:E], 1.0, None, ALU.add))
            chain.link(dve.reciprocal(pr[:, 0:E], ex[:, 0:E]))
            top2(pr[:, 0:8])
            weigh(1e-8)
            chain.link(dve.tensor_tensor(cw_next[:, 0:E], t[:, 0, 0:E], t[:, 1, 0:E], ALU.add))

        def choose_l3():
            chain.link(dve.tensor_scalar(ex[:, 0:E], ex[:, 0:E], 1.0, None, ALU.add))
            chain.link(dve.reciprocal(lg[:, 0:E], ex[:, 0:E]))
            chain.link(dve.tensor_tensor(t[:, 0, :], lg[:, 0:E], t[:, 1, :], ALU.mult))
            chain.link(dve.tensor_reduce(s1[:, :], t[:, 0, :], X_AXIS, ALU.add))
            chain.link(dve.tensor_scalar(s2[:, :], s1[:, :], 1e-8, None, ALU.add))
            chain.link(dve.reciprocal(s2[:, :], s2[:, :]))
            chain.link(dve.tensor_scalar(cw_next[:, 0:E], t[:, 0, :], s2[:, 0:1], None, ALU.mult))

        def take_x(i):
            dve.wait_ge(misc.w.sem, misc.v(misc.w, i, 1))
            dve.tensor_copy(xnT[:, :], M[:, 0:P]).then_inc(misc.r.sem, 1)

        def move(i):
            dve.wait_ge(misc.r.sem, misc.v(misc.r, i, 1))
            if i is not None:
                dve.wait_ge(sg["hidden_ready"].sem, sg["hidden_ready"].at(i, G))
            if routed:
                dve.tensor_copy(cw[:, 0:E], cw_next[:, 0:E])
            if kind == "L1":
                dve.tensor_copy(xn_now[:, :], k.xn[:, :])
            dve.tensor_copy(k.xnT[:, :], xnT[:, :]).then_inc(sg["x_moved"].sem, 1)
            dve.wait_ge(sg["x_moved"].sem, norm.count(sg["x_moved"], i))

        xn_now = fb["xn_now"]
        norm.dve_stats(dve, chain, None)
        if kind == "L0":
            for dst, src in ((up, up_i), (down, down_i)):
                full = (slice(None),) * len(dst.shape)
                chain.link(dve.tensor_scalar(dst[full], src[full], float(np.float32(1.0 / 127.0)), None, ALU.mult))
        else:
            chain.link(dve.memset(fb["wr"][:, :], 0.0))
            chain.link(dve.tensor_copy(fb["wr"][:, 0:E], rw[:, :]))
        if kind == "L1":
            chain.link(dve.memset(sel[:, :], 0.0))
            chain.link(dve.memset(acc[:, :], 0.0))
        if kind == "L2":
            chain.link(dve.memset(pr[:, 0:8], -1.0))
        if hidden < chunks * P:
            chain.link(dve.memset(H[:, hidden:chunks * P], 0.0))
        norm.dve_apply(dve, None)
        take_x(None)
        logits(None)
        choose(None)
        counts(None)
        move(None)
        with dve.Fori(0, TILES) as i:
            chain.round(i)
            x = k.X[:, i, :]
            if kind == "L1":
                chain.link(dve.tensor_tensor(x, x, xn_now[:, :], ALU.add))
            dve.wait_ge(sg["hidden_T_written"].sem, sg["hidden_T_written"].at(i, 0))
            for g in range(COUNTS_AT + 2):
                if g < G:
                    fw, c0, h0, e = groups[g]
                    if kind != "L3":
                        dve.wait_ge(sg["up_written"].sem, sg["up_written"].at(i, g + 1))
                    dve.wait_ge(sg["gate_ready"].sem, sg["gate_ready"].at(i, g + 1))
                    h, gate = H[:, h0:h0 + fw], Gt[:, g % 2, 0:fw]
                    if kind != "L3":
                        ins = dve.scalar_tensor_tensor(out=h, in0=gate, scalar=1.0 if e is None else cw[:, e:e + 1],
                                                       in1=U[g % 3][:, fw:2 * fw], op0=ALU.mult, op1=ALU.mult)
                    elif e is not None:
                        ins = dve.tensor_tensor(h.rearrange("p (e f) -> p e f", f=MOE3_WIDTH),
                                                gate.rearrange("p (e f) -> p e f", f=MOE3_WIDTH),
                                                bc(cw[:, e:e + 8], 2, MOE3_WIDTH), ALU.mult)
                    else:
                        ins = dve.tensor_copy(h, gate)
                    ins.then_inc(sg["hidden_ready"].sem, 1)
                if g == 0:
                    norm.dve_stats(dve, chain, i)
                if g == 1:
                    norm.dve_apply(dve, i)
                if g == X_AT:
                    take_x(i)
                if g == LOGITS_AT:
                    logits(i)
                if g == LOGITS_AT + 2:
                    choose(i)
                if g == COUNTS_AT + 1:
                    counts(i)
            for g in range(COUNTS_AT + 2, G):
                fw, c0, h0, e = groups[g]
                dve.wait_ge(sg["up_written"].sem, sg["up_written"].at(i, g + 1))
                dve.wait_ge(sg["gate_ready"].sem, sg["gate_ready"].at(i, g + 1))
                dve.scalar_tensor_tensor(out=H[:, h0:h0 + fw], in0=Gt[:, g % 2, 0:fw],
                                         scalar=1.0 if e is None else cw[:, e:e + 1], in1=U[g % 3][:, fw:2 * fw],
                                         op0=ALU.mult, op1=ALU.mult).then_inc(sg["hidden_ready"].sem, 1)
            move(i)
            dve.wait_ge(sg["down_used"].sem, sg["down_used"].at(i, NQ))
            dve.tensor_tensor(x, x, Y[:, 0:P], ALU.add).then_inc(sg["y_read"].sem, 1)
        chain.i = i
        chain.done()

    return {"sync": lambda sp: None, "pool": pool, "tensor": pe, "scalar": act, "vector": dve}


NEG_BIG = -3.0e38


STAGES = ["L0_xattn", "L0_attn", "L0_ffn", "L1_xattn", "L1_attn", "L1_ffn", "L2_xattn", "L2_attn", "L2_ffn", "L3_xattn", "L3_attn", "L3_ffn"]


def perceiver(nc, dram, out):
    with ExitStack() as ctx:
        k = Core(nc, ctx, dram)
        shared = cross_buffers(k)
        fb = ffn_buffers(k)
        stages = []
        for n, name in enumerate(STAGES):
            k.stage_no = n
            if name == "L1_xattn":
                stages.append(cross_attention(k, "L1x", "L1_xattn_Wq", "L1_xattn_bq", "L1_xattn_Wk", "L1_xattn_bk",
                                              "L1_xattn_Wv", "L1_xattn_bv", "L1_xattn_Wo", "L1_xattn_bo", True, shared))
            if name == "L0_xattn":
                stages.append(null_key_attention(k))
            if name == "L0_attn":
                stages.append(linear_attention(k, self_buffers(k, "L0")))
            if name in ("L1_attn", "L2_attn", "L3_attn"):
                stages.append(self_attention(k, name[:2], self_buffers(k, name[:2])))
            if name == "L0_ffn":
                stages.append(feed_forward(k, "L0", "L0_ffn_up", "L0_ffn_down", fb))
            if name == "L1_ffn":
                stages.append(feed_forward(k, "L1", "L1_ffn_up", "L1_ffn_down", fb, "L1_ffn_router_w", "L1_ffn_router_b"))
            if name == "L2_ffn":
                stages.append(feed_forward(k, "L2", "L2_ffn_up", "L2_ffn_down", fb, "L2_ffn_gate_w", "L2_ffn_gate_b"))
            if name == "L3_ffn":
                stages.append(feed_forward(k, "L3", "L3_ffn_up", "L3_ffn_down", fb, "L3_ffn_centroids", "L3_ffn_expert_biases"))
            if name == "L2_xattn":
                stages.append(cross_attention(k, "L2x", None, None, "L2_xattn_Wk", "L2_xattn_bk",
                                              "L2_xattn_Wv", "L2_xattn_bv", "L2_xattn_W_o", "L2_xattn_b_o", False, shared))
            if name == "L3_xattn":
                stages.append(cross_attention(k, "L3x", "L3_xattn_wq", "L3_xattn_bq", "L3_xattn_wk", "L3_xattn_bk",
                                              "L3_xattn_wv", "L3_xattn_bv", None, None, False, shared))
        weights = [ctx.enter_context(nc.semaphore(f"weights_in_{n}")) for n in range(len(stages))]
        x_in = ctx.enter_context(nc.semaphore("x_in"))
        primed = ctx.enter_context(nc.semaphore("primed"))
        stage_done = ctx.enter_context(nc.semaphore("stage_done"))
        stored = ctx.enter_context(nc.semaphore("stored"))
        counts = [16 * sum(1 for l in k.loads if l[0] == n) for n in range(len(stages))]
        block = ctx.enter_context(nc.Block())

        def start(eng):
            eng.wait_ge(x_in, 32)
            eng.wait_ge(primed, 1)

        def run(eng, which):
            for n, st in enumerate(stages):
                if counts[n]:
                    eng.wait_ge(weights[n], counts[n])
                st[which](eng)
                eng.drain().then_inc(stage_done, 1)
                eng.wait_ge(stage_done, ENGINES * (n + 1))

        @block.sync
        def _(sp):
            sp.dma_start(k.X[:, 0:TILES, :], dram["x"]).then_inc(x_in, 16)
            sp.dma_start(k.const[:, :], dram["const"]).then_inc(x_in, 16)
            for n, dst, src in k.loads:
                shape = dst.shape
                sp.dma_start(dst[(slice(None),) * len(shape)], src).then_inc(weights[n], 16)
            start(sp)
            run(sp, "sync")
            sp.dma_start(out, k.X[:, 0:TILES, :]).then_inc(stored, 16)
            sp.wait_ge(stored, 16)

        @block.gpsimd
        def _(pool):
            pool.memset(k.minus_half[:, :], -0.5)
            pool.memset(k.ln_eps[:, :], 1e-5)
            pool.memset(k.ln_eps6[:, :], 1e-6)
            pool.memset(k.zero4[:, :], 0.0)
            pool.memset(k.X[:, TILES, :], 0.0)
            pool.memset(k.X_spare[:, 0, :], 0.0)
            for s in k.signals.values():
                pool.sem_inc(s.sem, s.PRIMED)
            pool.drain().then_inc(primed, 1)
            start(pool)
            run(pool, "pool")

        @block.scalar
        def _(act):
            start(act)
            run(act, "scalar")

        @block.tensor
        def _(pe):
            start(pe)
            run(pe, "tensor")

        @block.vector
        def _(dve):
            start(dve)
            run(dve, "vector")


def lay_out(inputs):
    a = {n: np.asarray(v) for n, v in inputs.items()}
    d = {"const": CONST}
    d["x"] = a["x"].reshape(TILES, P, P).transpose(1, 0, 2)
    ctxT = np.zeros((CTX_PAD, P, KEYS), np.float32)
    ctxT[:BATCH] = a["ctx_1024"].transpose(0, 2, 1)
    d["ctxT"] = ctxT
    for n in ("L1_xattn_Wq", "L1_xattn_bq", "L1_xattn_Wk", "L1_xattn_bk", "L1_xattn_Wv", "L1_xattn_bv", "L1_xattn_Wo",
              "L1_xattn_bo", "L3_xattn_wq", "L3_xattn_bq", "L3_xattn_wk", "L3_xattn_bk", "L3_xattn_wv", "L3_xattn_bv",
              "L2_xattn_W_o", "L2_xattn_b_o"):
        d[n] = a[n]
    kvw = a["L2_xattn_W_kv"].reshape(P, 16, 2, 8)
    kvb = a["L2_xattn_b_kv"].reshape(16, 2, 8)
    d["L2_xattn_Wk"], d["L2_xattn_Wv"] = kvw[:, :, 0].reshape(P, P), kvw[:, :, 1].reshape(P, P)
    d["L2_xattn_bk"], d["L2_xattn_bv"] = kvb[:, 0].reshape(P), kvb[:, 1].reshape(P)
    for n, w in (("Wq", "Wq"), ("Wkv_down", "Wkv_down"), ("Wk_up", "Wk_up"), ("Wv_up", "Wv_up")):
        d["L1_attn_" + n] = a["L1_attn_" + w].T
    d["L1_attn_Wo"] = a["L1_attn_Wo"].T.reshape(2, P, P).transpose(1, 0, 2)
    d["L2_attn_qkv"] = np.concatenate([a["L2_attn_w_q"], a["L2_attn_w_k"], a["L2_attn_w_v"]], 1)
    d["L2_attn_w_o"] = a["L2_attn_w_o"]
    wkv = a["L0_xattn_Wkv"]
    for n, w in (("wqT", a["L0_xattn_Wq"].T), ("wkT", wkv[:, :1024].T), ("wvT", wkv[:, 1024:].T), ("wo", a["L0_xattn_Wo"])):
        d["L0_xattn_" + n] = w.reshape(8, P, P).transpose(1, 0, 2)
    null = [np.concatenate([v, v]) for v in a["L0_xattn_null_kv"]]
    d["L0_xattn_cols"] = np.stack([a["L0_xattn_ln1_s"], a["L0_xattn_ln1_b"], a["L0_xattn_lnc_s"], *null, null[0]], 1)
    d["L0_xattn_mask"] = a["mask_BxS2_bf1"].view(np.uint8)
    for n in ("lno_s", "lno_b", "lnc_s", "lnc_b"):
        d["L0_xattn_" + n] = a["L0_xattn_" + n]
    d["L0_attn_qkv"] = a["L0_attn_Wqkv"][:2 * P].reshape(2, P, P).transpose(1, 0, 2)
    d["L0_attn_v"], d["L0_attn_out"] = a["L0_attn_Wqkv"][2 * P:].T, a["L0_attn_Wout"].T
    d["L0_attn_proj"] = a["L0_attn_proj"].reshape(P, 64)
    d["L0_attn_bqk"] = a["L0_attn_bqkv"][:2 * P].reshape(2, P).T
    d["L0_attn_bv"], d["L0_attn_bout"] = a["L0_attn_bqkv"][2 * P:], a["L0_attn_bout"]
    for n in "qkvo":
        d["L3_attn_W" + n] = a["L3_attn_W" + n].T

    def by_chunk(w):
        n = -(-w.shape[0] // P)
        out = np.zeros((n * P, P), w.dtype)
        out[:w.shape[0]] = w
        return out.reshape(n, P, P).transpose(1, 0, 2)

    g, u = (a[f"L0_ffn_w_{n}"].T.reshape(P, 2, 1, 192) for n in ("gate", "up"))
    d["L0_ffn_up"] = np.concatenate([g, u], 2).reshape(P, -1)
    d["L0_ffn_down"] = by_chunk(a["L0_ffn_w_down"].T)
    g = np.concatenate([a["L1_ffn_w_gate"], a["L1_ffn_sw_gate"][None]])
    u = np.concatenate([a["L1_ffn_w_up"], a["L1_ffn_sw_up"][None]])
    d["L1_ffn_up"] = np.stack([g, u], 2).transpose(1, 0, 2, 3).reshape(P, -1)
    d["L1_ffn_down"] = by_chunk(np.concatenate([a["L1_ffn_w_down"], a["L1_ffn_sw_down"][None]]).reshape(-1, P))
    d["L1_ffn_router_w"], d["L1_ffn_router_b"] = a["L1_ffn_router_w"], a["L1_ffn_router_b"]
    g = np.concatenate([a["L2_ffn_ew1"], a["L2_ffn_fc1"][None]]).transpose(2, 0, 1)
    u = np.concatenate([a["L2_ffn_ew3"], a["L2_ffn_fc2"][None]]).transpose(2, 0, 1)
    d["L2_ffn_up"] = np.stack([g, u], 2).reshape(P, -1)
    d["L2_ffn_down"] = by_chunk(np.concatenate([a["L2_ffn_ew2"], a["L2_ffn_fc3"][None]]).transpose(0, 2, 1).reshape(-1, P))
    d["L2_ffn_gate_w"], d["L2_ffn_gate_b"] = a["L2_ffn_gate_w"].T, a["L2_ffn_gate_b"]
    d["L3_ffn_up"] = np.concatenate([a["L3_ffn_W_up"].transpose(1, 0, 2).reshape(P, -1), a["L3_ffn_Ws_up"]], 1)
    d["L3_ffn_down"] = by_chunk(np.concatenate([a["L3_ffn_W_down"].reshape(-1, P), a["L3_ffn_Ws_down"]]))
    d["L3_ffn_centroids"], d["L3_ffn_expert_biases"] = a["L3_ffn_centroids"].T, a["L3_ffn_expert_biases"]
    return {n: np.ascontiguousarray(v) for n, v in d.items()}


def kernel(**inputs):
    import concourse.bacc as _bacc
    from concourse import mybir as _mybir
    from concourse.bass_utils import run_bass_kernel_spmd as _run

    nc = _bacc.Bacc("TRN2", target_bir_lowering=False, num_devices=1)
    arrays, dram = {}, {}
    for name, v in lay_out(inputs).items():
        arrays[f"in_{name}"] = v
        dram[name] = nc.dram_tensor(f"in_{name}", v.shape, _mybir.dt.from_np(v.dtype), kind="ExternalInput").ap()
    out = nc.dram_tensor("out_0", (P, TILES, P), F32, kind="ExternalOutput").ap()
    perceiver(nc, dram, out)
    r = _run(nc, [arrays], core_ids=[0])
    return np.ascontiguousarray(r.results[0]["out_0"].transpose(1, 0, 2)).reshape(BATCH, SEQ, P)
```
